# Optimizing a Trainium2 kernel written in Bass

```python
import numpy as np
import jax
import jax.numpy as jnp

def _softmax(x, axis=-1):
    return jax.nn.softmax(x, axis=axis)

def _gelu(x):
    return jax.nn.gelu(x, approximate=True)

def _silu(x):
    return jax.nn.silu(x)

def _sigmoid(x):
    return jax.nn.sigmoid(x)

def _layernorm(x, axis=-1, eps=1e-05):
    m = jnp.mean(x, axis=axis, keepdims=True)
    v = jnp.var(x, axis=axis, keepdims=True)
    return (x - m) / jnp.sqrt(v + eps)

def _scatter_add(tgt, idx, src, axis=0):
    return tgt.at[idx].add(src)

def _segment_sum(src, seg, n):
    return jax.ops.segment_sum(src, seg, n)
kernel_name = 'mk_vit_tower_d4_tok_img1024_r4_225faa'

def setup_inputs(seed: int=0):
    np.random.seed(seed)
    _w = jnp.asarray

    def _rec_inputs():
        import jax
        import jax.numpy as jnp
        _rk = jax.random.key(seed)
        x = -0.00016672 + 0.999947 * jax.random.normal(jax.random.fold_in(_rk, 1), (32, 3, 96, 96), jnp.float32)
        return x
    x = _rec_inputs()

    def _L0_tok_setup():
        import jax, jax.numpy as jnp
        import numpy as np
        P = 16
        Q_EPS = 1e-05

        def _rms_norm(x):
            return x * jax.lax.rsqrt(jnp.mean(x * x, axis=-1, keepdims=True) + 1e-06)

        def _act_quant(x):
            scale = 127.0 / jnp.clip(jnp.max(jnp.abs(x), axis=-1, keepdims=True), Q_EPS, None)
            return jnp.clip(jnp.round(x * scale), -128.0, 127.0) / scale

        def _weight_quant(w):
            scale = 1.0 / jnp.clip(jnp.mean(jnp.abs(w)), Q_EPS, None)
            return jnp.clip(jnp.round(w * scale), -1.0, 1.0) / scale
        key = jax.random.key(seed)
        k1, k2, k3, k4 = jax.random.split(key, 4)
        B, C, H, W = (64, 3, 96, 96)
        D = 256
        Din = P * P * C
        return {'x': jax.random.normal(k1, (B, C, H, W), jnp.float32), 'weight': jax.random.normal(k2, (D, Din), jnp.float32) * 0.02, 'class_token': jax.random.normal(k3, (1, 1, D), jnp.float32), 'pos_embedding': jax.random.normal(k4, (1, 1, D), jnp.float32)}
    _L0_tok_all = _L0_tok_setup()
    _L0_tok_in = {k: v for k, v in _L0_tok_all.items() if k in ('weight', 'class_token', 'pos_embedding')}
    del _L0_tok_all

    def _L0_attn_setup():
        import jax, jax.numpy as jnp
        import numpy as np
        NUM_HEADS = 16

        def _sinusoid_rel_pos(seq_len, dim):
            pos = jnp.arange(seq_len - 1, -1, -1, dtype=jnp.float32)
            inv_freq = 1.0 / 10000.0 ** (jnp.arange(0, dim, 2, dtype=jnp.float32) / dim)
            ang = pos[:, None] * inv_freq[None, :]
            return jnp.concatenate([jnp.sin(ang), jnp.cos(ang)], axis=-1)

        def _rel_shift(x):
            B, H, S, L = x.shape
            x = jnp.pad(x, ((0, 0), (0, 0), (0, 0), (1, 0)))
            x = x.reshape(B, H, L + 1, S)
            return x[:, :, 1:S + 1, :]
        key = jax.random.key(seed)
        ks = jax.random.split(key, 8)
        B, S, C = (2, 512, 256)
        Dk, Dv, H = (256, 256, NUM_HEADS)
        dk = Dk // H
        scale = 0.02
        return {'x': jax.random.normal(ks[0], (B, S, C), dtype=jnp.float32), 'Wq': jax.random.normal(ks[1], (C, Dk), dtype=jnp.float32) * scale, 'Wk': jax.random.normal(ks[2], (C, Dk), dtype=jnp.float32) * scale, 'Wv': jax.random.normal(ks[3], (C, Dv), dtype=jnp.float32) * scale, 'u': jax.random.normal(ks[4], (H, dk), dtype=jnp.float32) * scale, 'v': jax.random.normal(ks[5], (H, dk), dtype=jnp.float32) * scale, 'Wo': jax.random.normal(ks[6], (Dv, C), dtype=jnp.float32) * scale, 'bo': jnp.zeros((C,), dtype=jnp.float32)}
    _L0_attn_all = _L0_attn_setup()
    _L0_attn_in = {k: v for k, v in _L0_attn_all.items() if k in ('Wq', 'Wk', 'Wv', 'u', 'v', 'Wo', 'bo')}
    del _L0_attn_all

    def _L0_ffn_setup():
        import jax, jax.numpy as jnp
        import numpy as np
        B, S, D_MODEL, D_HIDDEN = (4, 512, 256, 1024)

        def act_quant(x):
            scale = 127.0 / jnp.clip(jnp.max(jnp.abs(x), axis=-1, keepdims=True), 1e-05)
            return jnp.clip(jnp.round(x * scale), -128, 127) / scale

        def weight_quant(w):
            scale = 1.0 / jnp.clip(jnp.mean(jnp.abs(w)), 1e-05)
            return jnp.clip(jnp.round(w * scale), -1, 1) / scale

        def bit_linear(x, w):
            xq = x + jax.lax.stop_gradient(act_quant(x) - x)
            wq = w + jax.lax.stop_gradient(weight_quant(w) - w)
            return jnp.einsum('bsd,hd->bsh', xq, wq)

        def depthwise_conv1d(x_bcl, w, b):
            y = jax.lax.conv_general_dilated(x_bcl, w, window_strides=(1,), padding=[(1, 1)], dimension_numbers=('NCH', 'OIH', 'NCH'), feature_group_count=x_bcl.shape[1])
            return y + b[None, :, None]
        key = jax.random.key(seed)
        ks = jax.random.split(key, 5)
        lim1 = 1.0 / np.sqrt(D_MODEL)
        lim2 = 1.0 / np.sqrt(D_HIDDEN)
        limc = 1.0 / np.sqrt(3.0)
        return {'x': jax.random.normal(ks[0], (B, S, D_MODEL), dtype=jnp.float32), 'w1': jax.random.uniform(ks[1], (D_HIDDEN, D_MODEL), jnp.float32, -lim1, lim1), 'conv_w': jax.random.uniform(ks[2], (D_HIDDEN, 1, 3), jnp.float32, -limc, limc), 'conv_b': jax.random.uniform(ks[3], (D_HIDDEN,), jnp.float32, -limc, limc), 'w2': jax.random.uniform(ks[4], (D_MODEL, D_HIDDEN), jnp.float32, -lim2, lim2)}
    _L0_ffn_all = _L0_ffn_setup()
    _L0_ffn_in = {k: v for k, v in _L0_ffn_all.items() if k in ('w1', 'conv_w', 'conv_b', 'w2')}
    del _L0_ffn_all

    def _L1_attn_setup():
        import jax, jax.numpy as jnp
        import numpy as np
        BATCH, SEQ, DMODEL, NSTATE = (4, 512, 256, 16)
        key = jax.random.key(seed)
        ks = jax.random.split(key, 6)

        def lin_w(k, out_d, in_d):
            return jax.random.uniform(k, (out_d, in_d), jnp.float32, -1.0, 1.0) / np.sqrt(in_d).astype(np.float32)
        return {'x': jax.random.normal(ks[0], (BATCH, SEQ, DMODEL), jnp.float32), 'W1': lin_w(ks[1], DMODEL, DMODEL), 'b1': jnp.zeros((DMODEL,), jnp.float32), 'W2': lin_w(ks[2], NSTATE, DMODEL), 'b2': jnp.zeros((NSTATE,), jnp.float32), 'W3': lin_w(ks[3], NSTATE, DMODEL), 'b3': jnp.zeros((NSTATE,), jnp.float32), 'A': jax.random.uniform(ks[4], (DMODEL, NSTATE), jnp.float32, -1.0, 1.0) * np.sqrt(6.0 / (DMODEL + NSTATE)).astype(np.float32)}
    _L1_attn_all = _L1_attn_setup()
    _L1_attn_in = {k: v for k, v in _L1_attn_all.items() if k in ('W1', 'b1', 'W2', 'b2', 'W3', 'b3', 'A')}
    del _L1_attn_all

    def _L1_ffn_setup():
        import jax, jax.numpy as jnp
        import numpy as np
        B, S, D, F, E = (4, 512, 256, 1024, 4)
        key = jax.random.key(seed)
        ks = jax.random.split(key, 8)
        sd = 1.0 / np.sqrt(D)
        sf = 1.0 / np.sqrt(F)
        return {'x': jax.random.normal(ks[0], (B, S, D), dtype=jnp.float32), 'W1': jax.random.uniform(ks[1], (E, D, F), jnp.float32, -sd, sd), 'b1': jax.random.uniform(ks[2], (E, F), jnp.float32, -sd, sd), 'W2': jax.random.uniform(ks[3], (E, F, D), jnp.float32, -sf, sf), 'b2': jax.random.uniform(ks[4], (E, D), jnp.float32, -sf, sf), 'Wu': jax.random.uniform(ks[5], (D, 1), jnp.float32, -sd, sd), 'bu': jax.random.uniform(ks[6], (1,), jnp.float32, -sd, sd)}
    _L1_ffn_all = _L1_ffn_setup()
    _L1_ffn_in = {k: v for k, v in _L1_ffn_all.items() if k in ('W1', 'b1', 'W2', 'b2', 'Wu', 'bu')}
    del _L1_ffn_all

    def _L2_attn_setup():
        import jax, jax.numpy as jnp
        import numpy as np
        D_CONV = 4
        DT_RANK = 64
        D_STATE = 16

        def _selective_scan(u, delta, A, Bm, Cm, D):
            b, l, d = u.shape
            n = A.shape[1]
            deltaA = jnp.exp(jnp.einsum('bld,dn->bldn', delta, A))
            dBu = delta[..., None] * Bm[:, :, None, :] * u[..., None]

            def step(state, inp):
                dA_t, dBu_t, C_t = inp
                state = dA_t * state + dBu_t
                y_t = jnp.einsum('bdn,bn->bd', state, C_t)
                return (state, y_t)
            init = jnp.zeros((b, d, n), u.dtype)
            xs = (jnp.swapaxes(deltaA, 0, 1), jnp.swapaxes(dBu, 0, 1), jnp.swapaxes(Cm, 0, 1))
            _, ys = jax.lax.scan(step, init, xs)
            y = jnp.swapaxes(ys, 0, 1)
            return y + u * D
        key = jax.random.key(seed)
        ks = jax.random.split(key, 10)
        d_model, d_in, L, B = (256, 512, 256, 2)
        s = 0.02
        x = jax.random.normal(ks[0], (B, L, d_model), jnp.float32)
        W_in = jax.random.normal(ks[1], (d_model, 2 * d_in), jnp.float32) * s
        conv_w = jax.random.normal(ks[2], (D_CONV, 1, d_in), jnp.float32) * s
        conv_b = jax.random.normal(ks[3], (d_in,), jnp.float32) * s
        W_x = jax.random.normal(ks[4], (d_in, DT_RANK + 2 * D_STATE), jnp.float32) * s
        W_dt = jax.random.normal(ks[5], (DT_RANK, d_in), jnp.float32) * s
        b_dt = jax.random.normal(ks[6], (d_in,), jnp.float32) * s
        A_log = jnp.log(jnp.tile(jnp.arange(1, D_STATE + 1, dtype=jnp.float32), (d_in, 1)))
        D = jnp.ones((d_in,), jnp.float32)
        W_out = jax.random.normal(ks[7], (d_in, d_model), jnp.float32) * s
        return {'x': x, 'W_in': W_in, 'conv_w': conv_w, 'conv_b': conv_b, 'W_x': W_x, 'W_dt': W_dt, 'b_dt': b_dt, 'A_log': A_log, 'D': D, 'W_out': W_out}
    _L2_attn_all = _L2_attn_setup()
    _L2_attn_in = {k: v for k, v in _L2_attn_all.items() if k in ('W_in', 'conv_w', 'conv_b', 'W_x', 'W_dt', 'b_dt', 'A_log', 'D', 'W_out')}
    del _L2_attn_all

    def _L2_ffn_setup():
        import math
        import jax, jax.numpy as jnp
        from jax import lax
        import numpy as np
        E = 16
        K = 2
        CF = 1.25
        key = jax.random.key(seed)
        k0, k1, k2, k3, k4 = jax.random.split(key, 5)
        B, S, D, H = (2, 512, 256, 256)
        scale = 0.02
        return {'x': jax.random.normal(k0, (B, S, D), dtype=jnp.float32), 'router_w': jax.random.normal(k1, (D, E), dtype=jnp.float32) * scale, 'gate_w': jax.random.normal(k2, (E, D, H), dtype=jnp.float32) * scale, 'up_w': jax.random.normal(k3, (E, D, H), dtype=jnp.float32) * scale, 'down_w': jax.random.normal(k4, (E, H, D), dtype=jnp.float32) * scale}
    _L2_ffn_all = _L2_ffn_setup()
    _L2_ffn_in = {k: v for k, v in _L2_ffn_all.items() if k in ('router_w', 'gate_w', 'up_w', 'down_w')}
    del _L2_ffn_all

    def _L3_attn_setup():
        import jax, jax.numpy as jnp
        import numpy as np
        HID = 256
        HK, HV = (4, 8)
        DK, DV = (128, 128)
        KEY_DIM = HK * DK
        VAL_DIM = HV * DV
        CONV_DIM = 2 * KEY_DIM + VAL_DIM
        KCONV = 4
        NEXP, TOPK, INTER = (8, 2, 128)
        EPS = 1e-06

        def zrms(x, w):
            v = jnp.mean(x * x, axis=-1, keepdims=True)
            return x * jax.lax.rsqrt(v + EPS) * (1.0 + w)

        def causal_dwconv(x, w):
            xp = jnp.pad(x, ((0, 0), (KCONV - 1, 0), (0, 0)))
            kern = w.T[:, None, :]
            return jax.lax.conv_general_dilated(xp, kern, (1,), 'VALID', dimension_numbers=('NHC', 'HIO', 'NHC'), feature_group_count=CONV_DIM)

        def gated_delta_rule(q, k, v, g, beta):
            B = q.shape[0]
            S0 = jnp.zeros((B, HV, DK, DV), q.dtype)

            def step(S, inp):
                qt, kt, vt, gt, bt = inp
                S = S * jnp.exp(gt)[..., None, None]
                kv = jnp.einsum('bhk,bhkv->bhv', kt, S)
                delta = (vt - kv) * bt[..., None]
                S = S + jnp.einsum('bhk,bhv->bhkv', kt, delta)
                o = jnp.einsum('bhk,bhkv->bhv', qt, S)
                return (S, o)
            xs = tuple((jnp.moveaxis(a, 1, 0) for a in (q, k, v, g, beta)))
            _, o = jax.lax.scan(step, S0, xs)
            return jnp.moveaxis(o, 0, 1)

        def _reference_tuple_inner(hidden_states, w_ln1, w_ln2, W_qkvz, W_ba, conv_w, dt_bias, A_log, gate_norm_w, W_out, W_router, W_gate_e, W_up_e, W_down_e):
            B, S, _ = hidden_states.shape
            resid = hidden_states
            x = zrms(hidden_states, w_ln1)
            qkvz = x @ W_qkvz
            q, k, v, z = jnp.split(qkvz, [KEY_DIM, 2 * KEY_DIM, 2 * KEY_DIM + VAL_DIM], axis=-1)
            b, a = jnp.split(x @ W_ba, 2, axis=-1)
            beta = jax.nn.sigmoid(b)
            g = -jnp.exp(A_log) * jax.nn.softplus(a + dt_bias)
            mixed = jnp.concatenate([q, k, v], axis=-1)
            mixed = jax.nn.silu(causal_dwconv(mixed, conv_w))
            q, k, v = jnp.split(mixed, [KEY_DIM, 2 * KEY_DIM], axis=-1)
            q = q.reshape(B, S, HK, DK)
            k = k.reshape(B, S, HK, DK)
            v = v.reshape(B, S, HV, DV)
            rep = HV // HK
            q = jnp.repeat(q, rep, axis=2)
            k = jnp.repeat(k, rep, axis=2)
            q = q * jax.lax.rsqrt(jnp.sum(q * q, -1, keepdims=True) + EPS)
            k = k * jax.lax.rsqrt(jnp.sum(k * k, -1, keepdims=True) + EPS)
            q = q * DK ** (-0.5)
            core = gated_delta_rule(q, k, v, g, beta)
            core = core * jax.lax.rsqrt(jnp.mean(core * core, -1, keepdims=True) + EPS) * gate_norm_w
            core = core * jax.nn.silu(z.reshape(B, S, HV, DV))
            h = resid + core.reshape(B, S, VAL_DIM) @ W_out
            resid = h
            x = zrms(h, w_ln2)
            probs = jax.nn.softmax(x @ W_router, axis=-1)
            topv, topi = jax.lax.top_k(probs, TOPK)
            topv = topv / jnp.sum(topv, -1, keepdims=True)
            route = jnp.sum(jax.nn.one_hot(topi, NEXP, dtype=x.dtype) * topv[..., None], axis=-2)
            gate_h = jnp.einsum('bsh,ehi->bsei', x, W_gate_e)
            up_h = jnp.einsum('bsh,ehi->bsei', x, W_up_e)
            exp_out = jnp.einsum('bsei,eih->bseh', jax.nn.silu(gate_h) * up_h, W_down_e)
            moe_out = jnp.einsum('bseh,bse->bsh', exp_out, route)
            return (resid + moe_out, topi)
        key = jax.random.key(seed)
        ks = jax.random.split(key, 12)

        def lin(k, shape, fan_in):
            return jax.random.normal(k, shape, jnp.float32) * fan_in ** (-0.5)
        return {'hidden_states': jax.random.normal(ks[0], (1, 512, HID), jnp.float32), 'w_ln1': jnp.zeros((HID,), jnp.float32), 'w_ln2': jnp.zeros((HID,), jnp.float32), 'W_qkvz': lin(ks[1], (HID, 2 * KEY_DIM + 2 * VAL_DIM), HID), 'W_ba': lin(ks[2], (HID, 2 * HV), HID), 'conv_w': jax.random.normal(ks[3], (CONV_DIM, KCONV), jnp.float32) * KCONV ** (-0.5), 'dt_bias': jax.random.normal(ks[4], (HV,), jnp.float32) * 0.1, 'A_log': jnp.log(jax.random.uniform(ks[5], (HV,), jnp.float32, 1.0, 16.0)), 'gate_norm_w': jnp.ones((DV,), jnp.float32), 'W_out': lin(ks[6], (VAL_DIM, HID), VAL_DIM), 'W_router': lin(ks[7], (HID, NEXP), HID), 'W_gate_e': lin(ks[8], (NEXP, HID, INTER), HID), 'W_up_e': lin(ks[9], (NEXP, HID, INTER), HID), 'W_down_e': lin(ks[10], (NEXP, INTER, HID), INTER)}
    _L3_attn_all = _L3_attn_setup()
    _L3_attn_in = {k: v for k, v in _L3_attn_all.items() if k in ('w_ln1', 'w_ln2', 'W_qkvz', 'W_ba', 'conv_w', 'dt_bias', 'A_log', 'gate_norm_w', 'W_out', 'W_router', 'W_gate_e', 'W_up_e', 'W_down_e')}
    del _L3_attn_all

    def _L3_ffn_setup():
        import jax, jax.numpy as jnp
        import numpy as np
        B, T, C = (2, 512, 256)
        H, D = (16, 64)
        CR = 8
        R = C // CR
        ROPE = D // 2
        NOPE = D - ROPE
        E, K, I, S = (8, 2, 128, 1)
        THETA = 100000.0
        EPS = 1e-05

        def _rmsnorm(x, w):
            rms = jnp.sqrt(jnp.mean(x * x, axis=-1, keepdims=True) + EPS)
            return w * (x / rms)

        def _rope(xh):
            d = xh.shape[-1]
            t = jnp.arange(xh.shape[2], dtype=jnp.float32)
            freqs = 1.0 / THETA ** (jnp.arange(0, d, 2, dtype=jnp.float32) / d)
            ang = jnp.outer(t, freqs)
            cos, sin = (jnp.cos(ang), jnp.sin(ang))
            xr = xh.reshape(xh.shape[:-1] + (d // 2, 2))
            x0, x1 = (xr[..., 0], xr[..., 1])
            rot = jnp.stack([x0 * cos - x1 * sin, x0 * sin + x1 * cos], axis=-1)
            return rot.reshape(xh.shape)

        def _attention(x, Wq, Wkva, Wkvb, Wo):
            b, t, _ = x.shape
            q = (x @ Wq).reshape(b, t, H, D).transpose(0, 2, 1, 3)
            ckv = x @ Wkva
            kv_latent, k_rope = (ckv[:, :, :R], ckv[:, :, R:])
            kv = (kv_latent @ Wkvb).reshape(b, t, H, NOPE).transpose(0, 2, 1, 3)
            k_rope = jnp.broadcast_to(k_rope[:, None, :, :], (b, H, t, ROPE))
            q_nope, q_rope = (q[..., :NOPE], q[..., NOPE:])
            q = jnp.concatenate([q_nope, _rope(q_rope)], axis=-1)
            k = jnp.concatenate([kv, _rope(k_rope)], axis=-1)
            v = jnp.concatenate([kv, jnp.zeros_like(k_rope)], axis=-1)
            att = jnp.einsum('bhqd,bhkd->bhqk', q, k) / jnp.sqrt(jnp.float32(D))
            mask = jnp.tril(jnp.ones((t, t), dtype=bool))
            att = jnp.where(mask, att, jnp.float32(-jnp.inf))
            att = jax.nn.softmax(att, axis=-1)
            y = jnp.einsum('bhqk,bhkd->bhqd', att, v)
            y = y.transpose(0, 2, 1, 3).reshape(b, t, H * D)
            return y @ Wo

        def _experts(x_flat, Wg, Wu, Wd):
            g = jax.nn.silu(jnp.einsum('nc,eci->nei', x_flat, Wg))
            u = jnp.einsum('nc,eci->nei', x_flat, Wu)
            return jnp.einsum('nei,eic->nec', g * u, Wd)

        def _moe(x, Wgate, expert_bias, Wg, Wu, Wd, sWg, sWu, sWd):
            b, t, c = x.shape
            xf = x.reshape(-1, c)
            shared = jnp.mean(_experts(xf, sWg, sWu, sWd), axis=1)
            logits = xf @ Wgate + expert_bias
            probs = jax.nn.softmax(logits, axis=-1)
            topk_p, topk_i = jax.lax.top_k(probs, K)
            topk_p = topk_p / jnp.sum(topk_p, axis=-1, keepdims=True)
            comb = jnp.sum(jax.nn.one_hot(topk_i, E, dtype=xf.dtype) * topk_p[..., None], axis=1)
            routed = jnp.einsum('ne,nec->nc', comb, _experts(xf, Wg, Wu, Wd))
            return (shared + routed).reshape(b, t, c)
        key = jax.random.key(seed)
        ks = jax.random.split(key, 16)
        w = lambda k, shp: jax.random.normal(k, shp, dtype=jnp.float32) * 0.02
        return {'x': jax.random.normal(ks[0], (B, T, C), dtype=jnp.float32), 'w_ln1': jnp.ones((C,), jnp.float32), 'Wq': w(ks[1], (C, H * D)), 'Wkva': w(ks[2], (C, R + ROPE)), 'Wkvb': w(ks[3], (R, H * NOPE)), 'Wo': w(ks[4], (H * D, C)), 'w_ln2': jnp.ones((C,), jnp.float32), 'Wgate': w(ks[5], (C, E)), 'expert_bias': jnp.zeros((E,), jnp.float32), 'Wg': w(ks[6], (E, C, I)), 'Wu': w(ks[7], (E, C, I)), 'Wd': w(ks[8], (E, I, C)), 'sWg': w(ks[9], (S, C, I)), 'sWu': w(ks[10], (S, C, I)), 'sWd': w(ks[11], (S, I, C))}
    _L3_ffn_all = _L3_ffn_setup()
    _L3_ffn_in = {k: v for k, v in _L3_ffn_all.items() if k in ('w_ln1', 'Wq', 'Wkva', 'Wkvb', 'Wo', 'w_ln2', 'Wgate', 'expert_bias', 'Wg', 'Wu', 'Wd', 'sWg', 'sWu', 'sWd')}
    del _L3_ffn_all
    return {'x': x, 'L0_tok_weight': _L0_tok_in['weight'], 'L0_tok_class_token': _L0_tok_in['class_token'], 'L0_tok_pos_embedding': _L0_tok_in['pos_embedding'], 'L0_attn_Wq': _L0_attn_in['Wq'], 'L0_attn_Wk': _L0_attn_in['Wk'], 'L0_attn_Wv': _L0_attn_in['Wv'], 'L0_attn_u': _L0_attn_in['u'], 'L0_attn_v': _L0_attn_in['v'], 'L0_attn_Wo': _L0_attn_in['Wo'], 'L0_attn_bo': _L0_attn_in['bo'], 'L0_ffn_w1': _L0_ffn_in['w1'], 'L0_ffn_conv_w': _L0_ffn_in['conv_w'], 'L0_ffn_conv_b': _L0_ffn_in['conv_b'], 'L0_ffn_w2': _L0_ffn_in['w2'], 'L1_attn_W1': _L1_attn_in['W1'], 'L1_attn_b1': _L1_attn_in['b1'], 'L1_attn_W2': _L1_attn_in['W2'], 'L1_attn_b2': _L1_attn_in['b2'], 'L1_attn_W3': _L1_attn_in['W3'], 'L1_attn_b3': _L1_attn_in['b3'], 'L1_attn_A': _L1_attn_in['A'], 'L1_ffn_W1': _L1_ffn_in['W1'], 'L1_ffn_b1': _L1_ffn_in['b1'], 'L1_ffn_W2': _L1_ffn_in['W2'], 'L1_ffn_b2': _L1_ffn_in['b2'], 'L1_ffn_Wu': _L1_ffn_in['Wu'], 'L1_ffn_bu': _L1_ffn_in['bu'], 'L2_attn_W_in': _L2_attn_in['W_in'], 'L2_attn_conv_w': _L2_attn_in['conv_w'], 'L2_attn_conv_b': _L2_attn_in['conv_b'], 'L2_attn_W_x': _L2_attn_in['W_x'], 'L2_attn_W_dt': _L2_attn_in['W_dt'], 'L2_attn_b_dt': _L2_attn_in['b_dt'], 'L2_attn_A_log': _L2_attn_in['A_log'], 'L2_attn_D': _L2_attn_in['D'], 'L2_attn_W_out': _L2_attn_in['W_out'], 'L2_ffn_router_w': _L2_ffn_in['router_w'], 'L2_ffn_gate_w': _L2_ffn_in['gate_w'], 'L2_ffn_up_w': _L2_ffn_in['up_w'], 'L2_ffn_down_w': _L2_ffn_in['down_w'], 'L3_attn_w_ln1': _L3_attn_in['w_ln1'], 'L3_attn_w_ln2': _L3_attn_in['w_ln2'], 'L3_attn_W_qkvz': _L3_attn_in['W_qkvz'], 'L3_attn_W_ba': _L3_attn_in['W_ba'], 'L3_attn_conv_w': _L3_attn_in['conv_w'], 'L3_attn_dt_bias': _L3_attn_in['dt_bias'], 'L3_attn_A_log': _L3_attn_in['A_log'], 'L3_attn_gate_norm_w': _L3_attn_in['gate_norm_w'], 'L3_attn_W_out': _L3_attn_in['W_out'], 'L3_attn_W_router': _L3_attn_in['W_router'], 'L3_attn_W_gate_e': _L3_attn_in['W_gate_e'], 'L3_attn_W_up_e': _L3_attn_in['W_up_e'], 'L3_attn_W_down_e': _L3_attn_in['W_down_e'], 'L3_ffn_w_ln1': _L3_ffn_in['w_ln1'], 'L3_ffn_Wq': _L3_ffn_in['Wq'], 'L3_ffn_Wkva': _L3_ffn_in['Wkva'], 'L3_ffn_Wkvb': _L3_ffn_in['Wkvb'], 'L3_ffn_Wo': _L3_ffn_in['Wo'], 'L3_ffn_w_ln2': _L3_ffn_in['w_ln2'], 'L3_ffn_Wgate': _L3_ffn_in['Wgate'], 'L3_ffn_expert_bias': _L3_ffn_in['expert_bias'], 'L3_ffn_Wg': _L3_ffn_in['Wg'], 'L3_ffn_Wu': _L3_ffn_in['Wu'], 'L3_ffn_Wd': _L3_ffn_in['Wd'], 'L3_ffn_sWg': _L3_ffn_in['sWg'], 'L3_ffn_sWu': _L3_ffn_in['sWu'], 'L3_ffn_sWd': _L3_ffn_in['sWd']}

def reference(x, L0_tok_weight, L0_tok_class_token, L0_tok_pos_embedding, L0_attn_Wq, L0_attn_Wk, L0_attn_Wv, L0_attn_u, L0_attn_v, L0_attn_Wo, L0_attn_bo, L0_ffn_w1, L0_ffn_conv_w, L0_ffn_conv_b, L0_ffn_w2, L1_attn_W1, L1_attn_b1, L1_attn_W2, L1_attn_b2, L1_attn_W3, L1_attn_b3, L1_attn_A, L1_ffn_W1, L1_ffn_b1, L1_ffn_W2, L1_ffn_b2, L1_ffn_Wu, L1_ffn_bu, L2_attn_W_in, L2_attn_conv_w, L2_attn_conv_b, L2_attn_W_x, L2_attn_W_dt, L2_attn_b_dt, L2_attn_A_log, L2_attn_D, L2_attn_W_out, L2_ffn_router_w, L2_ffn_gate_w, L2_ffn_up_w, L2_ffn_down_w, L3_attn_w_ln1, L3_attn_w_ln2, L3_attn_W_qkvz, L3_attn_W_ba, L3_attn_conv_w, L3_attn_dt_bias, L3_attn_A_log, L3_attn_gate_norm_w, L3_attn_W_out, L3_attn_W_router, L3_attn_W_gate_e, L3_attn_W_up_e, L3_attn_W_down_e, L3_ffn_w_ln1, L3_ffn_Wq, L3_ffn_Wkva, L3_ffn_Wkvb, L3_ffn_Wo, L3_ffn_w_ln2, L3_ffn_Wgate, L3_ffn_expert_bias, L3_ffn_Wg, L3_ffn_Wu, L3_ffn_Wd, L3_ffn_sWg, L3_ffn_sWu, L3_ffn_sWd):
    import jax
    import jax.numpy as jnp

    def _L0_tok_ref(x, weight, class_token, pos_embedding):
        import jax, jax.numpy as jnp
        import numpy as np
        P = 16
        Q_EPS = 1e-05

        def _rms_norm(x):
            return x * jax.lax.rsqrt(jnp.mean(x * x, axis=-1, keepdims=True) + 1e-06)

        def _act_quant(x):
            scale = 127.0 / jnp.clip(jnp.max(jnp.abs(x), axis=-1, keepdims=True), Q_EPS, None)
            return jnp.clip(jnp.round(x * scale), -128.0, 127.0) / scale

        def _weight_quant(w):
            scale = 1.0 / jnp.clip(jnp.mean(jnp.abs(w)), Q_EPS, None)
            return jnp.clip(jnp.round(w * scale), -1.0, 1.0) / scale
        B, C, H, W = x.shape
        h, w = (H // P, W // P)
        patches = x.reshape(B, C, h, P, w, P).transpose(0, 2, 4, 3, 5, 1).reshape(B, h * w, P * P * C)
        xn = _rms_norm(patches)
        xq = xn + jax.lax.stop_gradient(_act_quant(xn) - xn)
        wq = weight + jax.lax.stop_gradient(_weight_quant(weight) - weight)
        proj = jnp.einsum('bnd,od->bno', xq, wq)
        cls = jnp.broadcast_to(class_token, (B, 1, proj.shape[-1]))
        out = jnp.concatenate([cls, proj], axis=1) + pos_embedding
        return out

    def _L0_attn_ref(x, Wq, Wk, Wv, u, v, Wo, bo):
        import jax, jax.numpy as jnp
        import numpy as np
        NUM_HEADS = 16

        def _sinusoid_rel_pos(seq_len, dim):
            pos = jnp.arange(seq_len - 1, -1, -1, dtype=jnp.float32)
            inv_freq = 1.0 / 10000.0 ** (jnp.arange(0, dim, 2, dtype=jnp.float32) / dim)
            ang = pos[:, None] * inv_freq[None, :]
            return jnp.concatenate([jnp.sin(ang), jnp.cos(ang)], axis=-1)

        def _rel_shift(x):
            B, H, S, L = x.shape
            x = jnp.pad(x, ((0, 0), (0, 0), (0, 0), (1, 0)))
            x = x.reshape(B, H, L + 1, S)
            return x[:, :, 1:S + 1, :]
        B, S, C = x.shape
        H = NUM_HEADS
        dk = Wq.shape[1] // H
        dv = Wv.shape[1] // H
        Q = (x @ Wq).reshape(B, S, H, dk).transpose(0, 2, 1, 3)
        K = (x @ Wk).reshape(B, S, H, dk).transpose(0, 2, 1, 3)
        V = (x @ Wv).reshape(B, S, H, dv).transpose(0, 2, 1, 3)
        r = _sinusoid_rel_pos(S, dk)
        term1 = jnp.einsum('bhqd,bhkd->bhqk', Q, K)
        term2 = jnp.einsum('bhqd,kd->bhqk', Q, r)
        term3 = jnp.einsum('hd,bhkd->bhk', u, K)[:, :, None, :]
        term4 = jnp.einsum('hd,kd->hk', v, r)[None, :, None, :]
        scores = (term1 + term3 + _rel_shift(term2 + term4)) / jnp.sqrt(jnp.asarray(dk, dtype=x.dtype))
        attn = jax.nn.softmax(scores, axis=-1)
        out = jnp.einsum('bhqk,bhkd->bqhd', attn, V).reshape(B, S, H * dv)
        return out @ Wo + bo

    def _L0_ffn_ref(x, w1, conv_w, conv_b, w2):
        import jax, jax.numpy as jnp
        import numpy as np
        B, S, D_MODEL, D_HIDDEN = (4, 512, 256, 1024)

        def act_quant(x):
            scale = 127.0 / jnp.clip(jnp.max(jnp.abs(x), axis=-1, keepdims=True), 1e-05)
            return jnp.clip(jnp.round(x * scale), -128, 127) / scale

        def weight_quant(w):
            scale = 1.0 / jnp.clip(jnp.mean(jnp.abs(w)), 1e-05)
            return jnp.clip(jnp.round(w * scale), -1, 1) / scale

        def bit_linear(x, w):
            xq = x + jax.lax.stop_gradient(act_quant(x) - x)
            wq = w + jax.lax.stop_gradient(weight_quant(w) - w)
            return jnp.einsum('bsd,hd->bsh', xq, wq)

        def depthwise_conv1d(x_bcl, w, b):
            y = jax.lax.conv_general_dilated(x_bcl, w, window_strides=(1,), padding=[(1, 1)], dimension_numbers=('NCH', 'OIH', 'NCH'), feature_group_count=x_bcl.shape[1])
            return y + b[None, :, None]
        h = bit_linear(x, w1)
        h = depthwise_conv1d(h.transpose(0, 2, 1), conv_w, conv_b)
        h = h.transpose(0, 2, 1)
        h = jax.nn.silu(h)
        return bit_linear(h, w2)

    def _L1_attn_ref(x, W1, b1, W2, b2, W3, b3, A):
        import jax, jax.numpy as jnp
        import numpy as np
        BATCH, SEQ, DMODEL, NSTATE = (4, 512, 256, 16)
        Bmat = x @ W2.T + b2
        Cmat = x @ W3.T + b3
        delta = jax.nn.softplus(x @ W1.T + b1)
        bc = jnp.einsum('bln,bln->bl', Bmat, Cmat)
        y = x * delta * bc[..., None]
        return y

    def _L1_ffn_ref(x, W1, b1, W2, b2, Wu, bu):
        import jax, jax.numpy as jnp
        import numpy as np
        B, S, D, F, E = (4, 512, 256, 1024, 4)
        n_exp = W1.shape[0]
        seq = x.shape[1]
        u = jax.nn.sigmoid(jnp.einsum('bsd,do->bso', x, Wu) + bu)[..., 0]
        k = jnp.clip(jnp.ceil(u * n_exp), 1, n_exp).astype(jnp.int32)
        h = jax.nn.relu(jnp.einsum('bsd,edf->bsef', x, W1) + b1)
        y = jnp.einsum('bsef,efd->bsed', h, W2) + b2
        s_idx = jnp.arange(seq)
        out = jnp.zeros_like(x)
        for i in range(1, n_exp + 1):
            e_idx = (s_idx + i - 1) % n_exp
            y_i = jnp.take_along_axis(y, e_idx[None, :, None, None], axis=2)[:, :, 0, :]
            w = jnp.where(k >= i, u / i, 0.0)
            out = out + w[..., None] * y_i
        return out

    def _L2_attn_ref(x, W_in, conv_w, conv_b, W_x, W_dt, b_dt, A_log, D, W_out):
        import jax, jax.numpy as jnp
        import numpy as np
        D_CONV = 4
        DT_RANK = 64
        D_STATE = 16

        def _selective_scan(u, delta, A, Bm, Cm, D):
            b, l, d = u.shape
            n = A.shape[1]
            deltaA = jnp.exp(jnp.einsum('bld,dn->bldn', delta, A))
            dBu = delta[..., None] * Bm[:, :, None, :] * u[..., None]

            def step(state, inp):
                dA_t, dBu_t, C_t = inp
                state = dA_t * state + dBu_t
                y_t = jnp.einsum('bdn,bn->bd', state, C_t)
                return (state, y_t)
            init = jnp.zeros((b, d, n), u.dtype)
            xs = (jnp.swapaxes(deltaA, 0, 1), jnp.swapaxes(dBu, 0, 1), jnp.swapaxes(Cm, 0, 1))
            _, ys = jax.lax.scan(step, init, xs)
            y = jnp.swapaxes(ys, 0, 1)
            return y + u * D
        B, L, _ = x.shape
        d_in = W_in.shape[1] // 2
        x_and_res = x @ W_in
        x_, res = jnp.split(x_and_res, [d_in], axis=-1)
        x_pad = jnp.pad(x_, ((0, 0), (D_CONV - 1, 0), (0, 0)))
        x_conv = jax.lax.conv_general_dilated(x_pad, conv_w, window_strides=(1,), padding='VALID', dimension_numbers=('NWC', 'WIO', 'NWC'), feature_group_count=d_in)
        x_conv = x_conv[:, :L, :] + conv_b
        x_conv = jax.nn.silu(x_conv)
        A = -jnp.exp(A_log)
        x_dbl = x_conv @ W_x
        delta, Bm, Cm = jnp.split(x_dbl, [DT_RANK, DT_RANK + D_STATE], axis=-1)
        delta = jax.nn.softplus(delta @ W_dt + b_dt)
        y = _selective_scan(x_conv, delta, A, Bm, Cm, D)
        y = y * jax.nn.silu(res)
        return y @ W_out

    def _L2_ffn_ref(x, router_w, gate_w, up_w, down_w):
        import math
        import jax, jax.numpy as jnp
        from jax import lax
        import numpy as np
        E = 16
        K = 2
        CF = 1.25
        B, S, D = x.shape
        xf = x.reshape(-1, D)
        T = B * S
        capacity = max(1, math.ceil(T * K / E * CF))
        Cbuf = K * capacity
        logits = xf @ router_w
        probs = jax.nn.softmax(logits, axis=-1)
        w, idx = lax.top_k(probs, K)
        oh = jax.nn.one_hot(idx, E, dtype=w.dtype)
        rank = jnp.cumsum(oh, axis=0) - oh
        myrank = jnp.sum(rank * oh, axis=-1)
        keep = myrank < capacity
        w = jnp.where(keep, w, 0.0)
        flat_e = idx.reshape(-1)
        flat_w = w.reshape(-1)
        keep_f = keep.reshape(-1)
        tok = jnp.repeat(jnp.arange(T, dtype=jnp.int32), K)
        ohk = jax.nn.one_hot(flat_e, E, dtype=jnp.int32) * keep_f[:, None].astype(jnp.int32)
        pos = jnp.cumsum(ohk, axis=0) - ohk
        slot = jnp.sum(pos * ohk, axis=-1)
        e_idx = jnp.where(keep_f, flat_e, E)
        dispatch = jnp.full((E + 1, Cbuf), T, dtype=jnp.int32).at[e_idx, slot].set(tok)
        wbuf = jnp.zeros((E + 1, Cbuf), dtype=w.dtype).at[e_idx, slot].set(flat_w)
        dispatch = dispatch[:E]
        wbuf = wbuf[:E]
        x_pad = jnp.concatenate([xf, jnp.zeros((1, D), xf.dtype)], axis=0)
        xe = x_pad[dispatch]
        gate = jnp.einsum('ecd,edh->ech', xe, gate_w)
        up = jnp.einsum('ecd,edh->ech', xe, up_w)
        hidden = jax.nn.silu(gate) * up
        out = jnp.einsum('ech,ehd->ecd', hidden, down_w)
        out = out * wbuf[:, :, None]
        combined = jnp.zeros((T + 1, D), dtype=xf.dtype).at[dispatch.reshape(-1)].add(out.reshape(-1, D))
        return combined[:T].reshape(B, S, D)

    def _L3_attn_ref(hidden_states, w_ln1, w_ln2, W_qkvz, W_ba, conv_w, dt_bias, A_log, gate_norm_w, W_out, W_router, W_gate_e, W_up_e, W_down_e):
        import jax, jax.numpy as jnp
        import numpy as np
        HID = 256
        HK, HV = (4, 8)
        DK, DV = (128, 128)
        KEY_DIM = HK * DK
        VAL_DIM = HV * DV
        CONV_DIM = 2 * KEY_DIM + VAL_DIM
        KCONV = 4
        NEXP, TOPK, INTER = (8, 2, 128)
        EPS = 1e-06

        def zrms(x, w):
            v = jnp.mean(x * x, axis=-1, keepdims=True)
            return x * jax.lax.rsqrt(v + EPS) * (1.0 + w)

        def causal_dwconv(x, w):
            xp = jnp.pad(x, ((0, 0), (KCONV - 1, 0), (0, 0)))
            kern = w.T[:, None, :]
            return jax.lax.conv_general_dilated(xp, kern, (1,), 'VALID', dimension_numbers=('NHC', 'HIO', 'NHC'), feature_group_count=CONV_DIM)

        def gated_delta_rule(q, k, v, g, beta):
            B = q.shape[0]
            S0 = jnp.zeros((B, HV, DK, DV), q.dtype)

            def step(S, inp):
                qt, kt, vt, gt, bt = inp
                S = S * jnp.exp(gt)[..., None, None]
                kv = jnp.einsum('bhk,bhkv->bhv', kt, S)
                delta = (vt - kv) * bt[..., None]
                S = S + jnp.einsum('bhk,bhv->bhkv', kt, delta)
                o = jnp.einsum('bhk,bhkv->bhv', qt, S)
                return (S, o)
            xs = tuple((jnp.moveaxis(a, 1, 0) for a in (q, k, v, g, beta)))
            _, o = jax.lax.scan(step, S0, xs)
            return jnp.moveaxis(o, 0, 1)

        def _reference_tuple_inner(hidden_states, w_ln1, w_ln2, W_qkvz, W_ba, conv_w, dt_bias, A_log, gate_norm_w, W_out, W_router, W_gate_e, W_up_e, W_down_e):
            B, S, _ = hidden_states.shape
            resid = hidden_states
            x = zrms(hidden_states, w_ln1)
            qkvz = x @ W_qkvz
            q, k, v, z = jnp.split(qkvz, [KEY_DIM, 2 * KEY_DIM, 2 * KEY_DIM + VAL_DIM], axis=-1)
            b, a = jnp.split(x @ W_ba, 2, axis=-1)
            beta = jax.nn.sigmoid(b)
            g = -jnp.exp(A_log) * jax.nn.softplus(a + dt_bias)
            mixed = jnp.concatenate([q, k, v], axis=-1)
            mixed = jax.nn.silu(causal_dwconv(mixed, conv_w))
            q, k, v = jnp.split(mixed, [KEY_DIM, 2 * KEY_DIM], axis=-1)
            q = q.reshape(B, S, HK, DK)
            k = k.reshape(B, S, HK, DK)
            v = v.reshape(B, S, HV, DV)
            rep = HV // HK
            q = jnp.repeat(q, rep, axis=2)
            k = jnp.repeat(k, rep, axis=2)
            q = q * jax.lax.rsqrt(jnp.sum(q * q, -1, keepdims=True) + EPS)
            k = k * jax.lax.rsqrt(jnp.sum(k * k, -1, keepdims=True) + EPS)
            q = q * DK ** (-0.5)
            core = gated_delta_rule(q, k, v, g, beta)
            core = core * jax.lax.rsqrt(jnp.mean(core * core, -1, keepdims=True) + EPS) * gate_norm_w
            core = core * jax.nn.silu(z.reshape(B, S, HV, DV))
            h = resid + core.reshape(B, S, VAL_DIM) @ W_out
            resid = h
            x = zrms(h, w_ln2)
            probs = jax.nn.softmax(x @ W_router, axis=-1)
            topv, topi = jax.lax.top_k(probs, TOPK)
            topv = topv / jnp.sum(topv, -1, keepdims=True)
            route = jnp.sum(jax.nn.one_hot(topi, NEXP, dtype=x.dtype) * topv[..., None], axis=-2)
            gate_h = jnp.einsum('bsh,ehi->bsei', x, W_gate_e)
            up_h = jnp.einsum('bsh,ehi->bsei', x, W_up_e)
            exp_out = jnp.einsum('bsei,eih->bseh', jax.nn.silu(gate_h) * up_h, W_down_e)
            moe_out = jnp.einsum('bseh,bse->bsh', exp_out, route)
            return (resid + moe_out, topi)
        return _reference_tuple_inner(hidden_states, w_ln1, w_ln2, W_qkvz, W_ba, conv_w, dt_bias, A_log, gate_norm_w, W_out, W_router, W_gate_e, W_up_e, W_down_e)[0]

    def _L3_ffn_ref(x, w_ln1, Wq, Wkva, Wkvb, Wo, w_ln2, Wgate, expert_bias, Wg, Wu, Wd, sWg, sWu, sWd):
        import jax, jax.numpy as jnp
        import numpy as np
        B, T, C = (2, 512, 256)
        H, D = (16, 64)
        CR = 8
        R = C // CR
        ROPE = D // 2
        NOPE = D - ROPE
        E, K, I, S = (8, 2, 128, 1)
        THETA = 100000.0
        EPS = 1e-05

        def _rmsnorm(x, w):
            rms = jnp.sqrt(jnp.mean(x * x, axis=-1, keepdims=True) + EPS)
            return w * (x / rms)

        def _rope(xh):
            d = xh.shape[-1]
            t = jnp.arange(xh.shape[2], dtype=jnp.float32)
            freqs = 1.0 / THETA ** (jnp.arange(0, d, 2, dtype=jnp.float32) / d)
            ang = jnp.outer(t, freqs)
            cos, sin = (jnp.cos(ang), jnp.sin(ang))
            xr = xh.reshape(xh.shape[:-1] + (d // 2, 2))
            x0, x1 = (xr[..., 0], xr[..., 1])
            rot = jnp.stack([x0 * cos - x1 * sin, x0 * sin + x1 * cos], axis=-1)
            return rot.reshape(xh.shape)

        def _attention(x, Wq, Wkva, Wkvb, Wo):
            b, t, _ = x.shape
            q = (x @ Wq).reshape(b, t, H, D).transpose(0, 2, 1, 3)
            ckv = x @ Wkva
            kv_latent, k_rope = (ckv[:, :, :R], ckv[:, :, R:])
            kv = (kv_latent @ Wkvb).reshape(b, t, H, NOPE).transpose(0, 2, 1, 3)
            k_rope = jnp.broadcast_to(k_rope[:, None, :, :], (b, H, t, ROPE))
            q_nope, q_rope = (q[..., :NOPE], q[..., NOPE:])
            q = jnp.concatenate([q_nope, _rope(q_rope)], axis=-1)
            k = jnp.concatenate([kv, _rope(k_rope)], axis=-1)
            v = jnp.concatenate([kv, jnp.zeros_like(k_rope)], axis=-1)
            att = jnp.einsum('bhqd,bhkd->bhqk', q, k) / jnp.sqrt(jnp.float32(D))
            mask = jnp.tril(jnp.ones((t, t), dtype=bool))
            att = jnp.where(mask, att, jnp.float32(-jnp.inf))
            att = jax.nn.softmax(att, axis=-1)
            y = jnp.einsum('bhqk,bhkd->bhqd', att, v)
            y = y.transpose(0, 2, 1, 3).reshape(b, t, H * D)
            return y @ Wo

        def _experts(x_flat, Wg, Wu, Wd):
            g = jax.nn.silu(jnp.einsum('nc,eci->nei', x_flat, Wg))
            u = jnp.einsum('nc,eci->nei', x_flat, Wu)
            return jnp.einsum('nei,eic->nec', g * u, Wd)

        def _moe(x, Wgate, expert_bias, Wg, Wu, Wd, sWg, sWu, sWd):
            b, t, c = x.shape
            xf = x.reshape(-1, c)
            shared = jnp.mean(_experts(xf, sWg, sWu, sWd), axis=1)
            logits = xf @ Wgate + expert_bias
            probs = jax.nn.softmax(logits, axis=-1)
            topk_p, topk_i = jax.lax.top_k(probs, K)
            topk_p = topk_p / jnp.sum(topk_p, axis=-1, keepdims=True)
            comb = jnp.sum(jax.nn.one_hot(topk_i, E, dtype=xf.dtype) * topk_p[..., None], axis=1)
            routed = jnp.einsum('ne,nec->nc', comb, _experts(xf, Wg, Wu, Wd))
            return (shared + routed).reshape(b, t, c)
        x = x + _attention(_rmsnorm(x, w_ln1), Wq, Wkva, Wkvb, Wo)
        residual = x
        xn = _rmsnorm(x, w_ln2)
        x_out = _moe(xn, Wgate, expert_bias, Wg, Wu, Wd, sWg, sWu, sWd)
        return residual + x_out
    h = _L0_tok_ref(x, L0_tok_weight, L0_tok_class_token, L0_tok_pos_embedding)
    h = h + _L0_attn_ref(_layernorm(h, axis=-1), L0_attn_Wq, L0_attn_Wk, L0_attn_Wv, L0_attn_u, L0_attn_v, L0_attn_Wo, L0_attn_bo)
    h = h + _L0_ffn_ref(_layernorm(h, axis=-1), L0_ffn_w1, L0_ffn_conv_w, L0_ffn_conv_b, L0_ffn_w2)
    h = h + _L1_attn_ref(_layernorm(h, axis=-1), L1_attn_W1, L1_attn_b1, L1_attn_W2, L1_attn_b2, L1_attn_W3, L1_attn_b3, L1_attn_A)
    h = h + _L1_ffn_ref(_layernorm(h, axis=-1), L1_ffn_W1, L1_ffn_b1, L1_ffn_W2, L1_ffn_b2, L1_ffn_Wu, L1_ffn_bu)
    h = h + _L2_attn_ref(_layernorm(h, axis=-1), L2_attn_W_in, L2_attn_conv_w, L2_attn_conv_b, L2_attn_W_x, L2_attn_W_dt, L2_attn_b_dt, L2_attn_A_log, L2_attn_D, L2_attn_W_out)
    h = h + _L2_ffn_ref(_layernorm(h, axis=-1), L2_ffn_router_w, L2_ffn_gate_w, L2_ffn_up_w, L2_ffn_down_w)
    h = h + _L3_attn_ref(_layernorm(h, axis=-1), L3_attn_w_ln1, L3_attn_w_ln2, L3_attn_W_qkvz, L3_attn_W_ba, L3_attn_conv_w, L3_attn_dt_bias, L3_attn_A_log, L3_attn_gate_norm_w, L3_attn_W_out, L3_attn_W_router, L3_attn_W_gate_e, L3_attn_W_up_e, L3_attn_W_down_e)
    h = h + _L3_ffn_ref(_layernorm(h, axis=-1), L3_ffn_w_ln1, L3_ffn_Wq, L3_ffn_Wkva, L3_ffn_Wkvb, L3_ffn_Wo, L3_ffn_w_ln2, L3_ffn_Wgate, L3_ffn_expert_bias, L3_ffn_Wg, L3_ffn_Wu, L3_ffn_Wd, L3_ffn_sWg, L3_ffn_sWu, L3_ffn_sWd)
    return h

_drawn_inputs = setup_inputs


def setup_inputs(seed=0):
    import zlib

    import numpy as np

    out = dict(_drawn_inputs(seed))
    spreads = {'L0_attn_bo': (0.0, 0.1),
     'L1_attn_b1': (0.0, 0.1),
     'L1_attn_b2': (0.0, 0.1),
     'L1_attn_b3': (0.0, 0.671),
     'L2_attn_D': (1.0, 0.6),
     'L3_attn_w_ln1': (0.0, 0.461),
     'L3_attn_w_ln2': (0.0, 0.591),
     'L3_attn_gate_norm_w': (1.0, 0.6),
     'L3_ffn_w_ln1': (1.0, 0.6),
     'L3_ffn_w_ln2': (1.0, 0.6),
     'L3_ffn_expert_bias': (0.0, 0.8)}
    factors = {'L0_attn_Wq': 8.0,
     'L0_attn_Wk': 8.0,
     'L0_attn_u': 8.0,
     'L0_attn_v': 8.0,
     'L1_ffn_W1': 7.733,
     'L1_ffn_b1': 26.398,
     'L1_ffn_W2': 6.817,
     'L1_ffn_b2': 50.138,
     'L1_ffn_Wu': 5.905,
     'L2_attn_W_in': 8.0,
     'L2_attn_conv_w': 8.0,
     'L2_attn_conv_b': 8.0,
     'L2_attn_W_x': 8.0,
     'L2_attn_W_dt': 8.0,
     'L2_attn_b_dt': 8.0,
     'L2_attn_A_log': 8.0,
     'L2_attn_W_out': 8.0,
     'L2_ffn_router_w': 8.0,
     'L2_ffn_gate_w': 8.0,
     'L2_ffn_up_w': 8.0,
     'L2_ffn_down_w': 8.0,
     'L3_attn_W_ba': 2.958,
     'L3_attn_dt_bias': 40.378,
     'L3_attn_A_log': 6.632,
     'L3_ffn_Wq': 8.0,
     'L3_ffn_Wkva': 8.0,
     'L3_ffn_Wkvb': 8.0,
     'L3_ffn_Wo': 8.0,
     'L3_ffn_Wgate': 8.0,
     'L3_ffn_Wg': 8.0,
     'L3_ffn_Wu': 8.0,
     'L3_ffn_Wd': 8.0,
     'L3_ffn_sWg': 8.0,
     'L3_ffn_sWu': 8.0,
     'L3_ffn_sWd': 8.0}
    for name, (base, spread) in spreads.items():
        noise = np.random.default_rng([zlib.crc32(name.encode()), seed]).standard_normal(out[name].shape)
        drawn = base * np.exp(spread * noise) if base else spread * noise
        out[name] = jnp.asarray(drawn.astype(out[name].dtype))
    for name, factor in factors.items():
        out[name] = (out[name] * factor).astype(out[name].dtype)
    return out
```

```python
import math
from contextlib import ExitStack

import concourse.bass as bass
import numpy as np
from concourse import mybir

ALU = mybir.AluOpType
ACT = mybir.ActivationFunctionType
F32 = mybir.dt.float32
BF16 = mybir.dt.bfloat16
U32 = mybir.dt.uint32
X = mybir.AxisListType.X

P = 128
B, S, D = 32, 37, 256
G = 3
TT = G * S
NT = 11
T = NT * TT
KC = D // P
NCH = 3
CH = T // NCH
BANK = 512
ROUND = 12582912.0


def sems(nc, stack, names):
    made = {n: nc.alloc_semaphore(n) for n in names.split()}
    for sem in made.values():
        nc.gpsimd.nop().then_inc(sem, 1)
    nc.all_engine_barrier()
    stack.callback(lambda: nc.clear_and_free_semaphores(list(made.values())))
    return made


def bufs(nc, stack):
    def sb(name, shape, dt=F32):
        return stack.enter_context(nc.sbuf_tensor(name, shape, dt))

    def ps(name, shape, dt=F32):
        return stack.enter_context(nc.psum_tensor(name, shape, dt))

    return sb, ps


def chain(eng, sem, at=0):
    n = [0]

    def link(ins):
        n[0] += 1
        ins.then_inc(sem, 1)
        eng.wait_ge(sem, at + n[0] + 1)

    link.count = lambda: n[0]
    return link


def norm_transpose(nc, name, h, xT, ident, eps, center, w_dram=None, w_plus=0.0, x_tok=None, turn=True):
    with ExitStack() as stack:
        sb, ps = bufs(nc, stack)
        s = sems(nc, stack, " ".join(f"{name}_{x}" for x in (
            "w_loaded", "w_ready", "v", "var_ready", "rstd_ready", "x_ready", "turned", "done")))
        s = {k[len(name) + 1:]: v for k, v in s.items()}
        xc = sb(f"{name}_xc", [TT, NT, D])
        xn = x_tok if x_tok is not None else sb(f"{name}_xn", [TT, NT, D])
        mean = sb(f"{name}_mean", [TT, NT])
        var = sb(f"{name}_var", [TT, NT])
        half = sb(f"{name}_half", [TT, NT])
        rstd = sb(f"{name}_rstd", [TT, NT])
        w = sb(f"{name}_w", [P, KC])
        pt = ps(f"{name}_pt", [P, KC * NCH, BANK])
        groups = [(0, 4), (4, 8), (8, NT)]
        block = stack.enter_context(nc.Block())

        @block.sync
        def _(sp):
            if w_dram is not None:
                sp.dma_start(w[:, :], w_dram).then_inc(s["w_loaded"], 16)

        @block.vector
        def _(dve):
            link = chain(dve, s["v"])
            nc.vector.memset(half[:, :], -0.5)
            src = h
            if center:
                link(nc.vector.tensor_reduce(mean[:, :], h[:, :, :], X, ALU.add))
                link(nc.vector.tensor_scalar(mean[:, :], mean[:, :], 1.0 / D, None, ALU.mult))
                link(nc.vector.tensor_tensor(xc[:, :, :], h[:, :, :],
                                             mean[:, :].unsqueeze(2).broadcast_to([TT, NT, D]), ALU.subtract))
                src = xc
            link(nc.vector.tensor_tensor(xn[:, :, :], src[:, :, :], src[:, :, :], ALU.mult))
            link(nc.vector.tensor_reduce(var[:, :], xn[:, :, :], X, ALU.add))
            nc.vector.tensor_scalar(var[:, :], var[:, :], 1.0 / D, eps, ALU.mult, ALU.add).then_inc(s["var_ready"], 1)
            if w_dram is not None:
                dve.wait_ge(s["w_loaded"], 17)
                nc.vector.tensor_scalar(w[:, :], w[:, :], w_plus, None, ALU.add).then_inc(s["w_ready"], 1)
                dve.wait_ge(s["w_ready"], 2)
            dve.wait_ge(s["rstd_ready"], 2)
            nc.vector.tensor_tensor(xn[:, :, :], src[:, :, :],
                                    rstd[:, :].unsqueeze(2).broadcast_to([TT, NT, D]), ALU.mult).then_inc(s["x_ready"], 1)
            for g, (a, b) in enumerate(groups if turn else []):
                dve.wait_ge(s["turned"], g + 2)
                nc.vector.tensor_scalar(xT[:, 0, a * TT:b * TT], pt[:, g, 0:(b - a) * TT],
                                        w[:, 0:1] if w_dram is not None else 1.0, None, ALU.mult).then_inc(s["done"], 1)

        @block.gpsimd
        def _(pool):
            pool.wait_ge(s["var_ready"], 2)
            nc.gpsimd.tensor_tensor(rstd[:, :], var[:, :], half[:, :], ALU.pow).then_inc(s["rstd_ready"], 1)

        @block.tensor
        def _(pe):
            pe.wait_ge(s["x_ready"], 2)
            for k in range(KC):
                for g, (a, b) in enumerate(groups if turn else []):
                    for t in range(a, b):
                        last = nc.tensor.transpose(pt[:, k * NCH + g, (t - a) * TT:(t - a + 1) * TT],
                                                   xn[:, t, k * P:(k + 1) * P], ident[0:TT, 0:TT])
                    last.then_inc(s["turned"], 1)

        @block.scalar
        def _(act):
            if w_dram is not None:
                act.wait_ge(s["w_ready"], 2)
            for g, (a, b) in enumerate(groups if turn else []):
                act.wait_ge(s["turned"], NCH + g + 2)
                nc.scalar.activation(xT[:, 1, a * TT:b * TT], pt[:, NCH + g, 0:(b - a) * TT], ACT.Copy,
                                     scale=w[:, 1:2] if w_dram is not None else 1.0).then_inc(s["done"], 1)


def stage_tok(nc, d, h, ident):
    DIN = 768
    NK = DIN // P
    with ExitStack() as stack:
        sb, ps = bufs(nc, stack)
        s = sems(nc, stack, "tok_w_in tok_x_in tok_add_in tok_v tok_a tok_wsum tok_wtot tok_wq_ready tok_ss "
                            "tok_ms tok_r tok_q_ready tok_turned tok_qT tok_mm tok_hdone tok_half")
        w = sb("tok_w", [P, NK, D])
        wa = sb("tok_wa", [P, NK * D])
        wq = sb("tok_wq", [P, NK, D], BF16)
        ones = sb("tok_ones", [P, P])
        wsum = sb("tok_wsum_b", [P, 1])
        wmean = sb("tok_wmean", [P, 1])
        wscale = sb("tok_wscale", [P, 1])
        x = sb("tok_x", [TT, NT, DIN])
        junk = sb("tok_junk", [TT, DIN])
        add = sb("tok_addend", [TT, NT, D])
        pos = sb("tok_pos", [TT, D])
        ss = sb("tok_ssb", [TT, NT])
        ms = sb("tok_msb", [TT, NT])
        mx = sb("tok_mx", [TT, NT])
        half = sb("tok_halfb", [TT, NT])
        r = sb("tok_rb", [TT, NT])
        sc = sb("tok_sc", [TT, NT])
        inv = sb("tok_inv", [TT, NT])
        q = sb("tok_q", [TT, DIN])
        qb = sb("tok_qb", [TT, DIN], BF16)
        identb = sb("tok_identb", [P, P], BF16)
        qT = sb("tok_qTb", [P, NK, TT], BF16)
        pw = ps("tok_pw", [P, BANK])
        pt = ps("tok_pt", [P, 2, 1024], BF16)
        po = ps("tok_po", [P, BANK])
        block = stack.enter_context(nc.Block())

        @block.sync
        def _(sp):
            sp.dma_start(w[:, :, :], d["tok_w"]).then_inc(s["tok_w_in"], 16)
            sp.dma_start(x[:, :, :], d["patches"]).then_inc(s["tok_x_in"], 16)
            sp.dma_start(add[:, :, :], d["tok_addend"]).then_inc(s["tok_add_in"], 16)
            sp.dma_start(pos[:, :], d["tok_pos"]).then_inc(s["tok_add_in"], 16)

        @block.scalar
        def _(act):
            act.wait_ge(s["tok_w_in"], 17)
            nc.scalar.activation(wa[:, :], w[:, :, :].rearrange("p k d -> p (k d)"), ACT.Abs,
                                 accum_out=wsum[:, :]).then_inc(s["tok_wsum"], 1)
            act.wait_ge(s["tok_x_in"], 17)
            for t in range(NT):
                last = nc.scalar.activation(junk[:, :], x[:, t, :], ACT.Square, accum_out=ss[:, t:t + 1])
                if t < NT - 1:
                    last.then_inc(s["tok_a"], 1)
                    act.wait_ge(s["tok_a"], t + 2)
            last.then_inc(s["tok_ss"], 1)

        @block.gpsimd
        def _(pool):
            pool.wait_ge(s["tok_ms"], 2)
            nc.gpsimd.tensor_tensor(r[:, :], ms[:, :], half[:, :], ALU.pow).then_inc(s["tok_r"], 1)

        @block.tensor
        def _(pe):
            pe.wait_ge(s["tok_half"], 2)
            pe.wait_ge(s["tok_wsum"], 2)
            nc.tensor.matmul(pw[:, 0:1], ones[:, :], wsum[:, :], start=True, stop=True).then_inc(s["tok_wtot"], 1)
            pe.wait_ge(s["tok_wq_ready"], 2)
            with pe.Fori(0, NT) as i:
                pe.wait_ge(s["tok_q_ready"], i + 2)
                pe.wait_ge(s["tok_qT"], i + 1)
                for k in range(NK):
                    last = nc.tensor.transpose(pt[:, 0, k * P:k * P + TT], qb[:, k * P:(k + 1) * P],
                                               identb[0:TT, 0:TT])
                last.then_inc(s["tok_turned"], 1)
                pe.wait_ge(s["tok_qT"], i + 2)
                pe.wait_ge(s["tok_hdone"], i + 1)
                for k in range(NK):
                    last = nc.tensor.matmul(po[0:TT, 0:D], qT[:, k, :], wq[:, k, :], start=(k == 0),
                                            stop=(k == NK - 1))
                last.then_inc(s["tok_mm"], 1)

        @block.vector
        def _(dve):
            link = chain(dve, s["tok_v"])
            nc.vector.memset(half[:, :], -0.5)
            nc.vector.tensor_copy(identb[:, :], ident[:, :])
            nc.vector.memset(ones[:, :], 1.0).then_inc(s["tok_half"], 1)
            dve.wait_ge(s["tok_wtot"], 2)
            link(nc.vector.tensor_scalar(wmean[:, :], pw[:, 0:1], 1.0 / (D * DIN), 1e-5, ALU.mult, ALU.max))
            link(nc.vector.reciprocal(wscale[:, :], wmean[:, :]))
            wf = w[:, :, :]
            link(nc.vector.tensor_scalar(wf, wf, wscale[:, 0:1], None, ALU.mult))
            link(nc.vector.tensor_scalar(wf, wf, ROUND, -ROUND, ALU.add, ALU.add))
            nc.vector.tensor_scalar(wq[:, :, :], wf, 1.0, -1.0, ALU.min, ALU.max).then_inc(s["tok_wq_ready"], 1)
            dve.wait_ge(s["tok_x_in"], 17)
            link(nc.vector.tensor_reduce(mx[:, :], x[:, :, :], X, ALU.max, apply_absolute_value=True))
            dve.wait_ge(s["tok_ss"], 2)
            nc.vector.tensor_scalar(ms[:, :], ss[:, :], 1.0 / DIN, 1e-6, ALU.mult, ALU.add).then_inc(s["tok_ms"], 1)
            dve.wait_ge(s["tok_r"], 2)
            link(nc.vector.tensor_tensor(mx[:, :], mx[:, :], r[:, :], ALU.mult))
            link(nc.vector.tensor_scalar(mx[:, :], mx[:, :], 1e-5, None, ALU.max))
            link(nc.vector.reciprocal(sc[:, :], mx[:, :]))
            link(nc.vector.tensor_scalar(sc[:, :], sc[:, :], 127.0, None, ALU.mult))
            link(nc.vector.tensor_scalar(inv[:, :], mx[:, :], 1.0 / 127.0, wmean[0:TT, 0:1], ALU.mult, ALU.mult))
            link(nc.vector.tensor_tensor(x[:, :, :], x[:, :, :],
                                         r[:, :].unsqueeze(2).broadcast_to([TT, NT, DIN]), ALU.mult))
            link(nc.vector.tensor_tensor(x[:, :, :], x[:, :, :],
                                         sc[:, :].unsqueeze(2).broadcast_to([TT, NT, DIN]), ALU.mult))
            link(nc.vector.tensor_scalar(x[:, :, :], x[:, :, :], ROUND, -ROUND, ALU.add, ALU.add))
            dve.wait_ge(s["tok_add_in"], 33)
            link(nc.vector.tensor_tensor(h[:, :, :], add[:, :, :],
                                         pos[:, :].unsqueeze(1).broadcast_to([TT, NT, D]), ALU.add))
            with dve.Fori(0, NT) as i:
                nc.vector.tensor_scalar(qb[:, :], x[:, bass.ds(i, 1), :].rearrange("p a d -> p (a d)"),
                                        127.0, -128.0, ALU.min, ALU.max).then_inc(s["tok_q_ready"], 1)
                dve.wait_ge(s["tok_turned"], i + 2)
                dve.wait_ge(s["tok_mm"], i + 1)
                nc.vector.tensor_copy(qT[:, :, :], pt[:, 0, 0:NK * P].rearrange("p (k t) -> p k t", t=P)[:, :, 0:TT]
                                      ).then_inc(s["tok_qT"], 1)
                dve.wait_ge(s["tok_mm"], i + 2)
                ht = h[:, bass.ds(i, 1), :].rearrange("p a d -> p (a d)")
                nc.vector.scalar_tensor_tensor(ht, po[0:TT, 0:D],
                                               inv[:, bass.ds(i, 1)], ht, ALU.mult, ALU.add).then_inc(s["tok_hdone"], 1)


def flat2(ap):
    return ap.rearrange("p a d -> p (a d)")


def stage_attn0(nc, d, h, xT, ident):
    H, HG = 16, 8
    QG = 4
    NB = H // QG
    W = QG * S
    PG = (H + G - 1) // G
    norm_transpose(nc, "an", h, xT, ident, 1e-5, True)
    with ExitStack() as stack:
        sb, ps = bufs(nc, stack)
        s = sems(nc, stack, "a_in a_const a_zero a_qk_mm a_qk_done a_sw_mm a_sw_done a_qpad "
                            "a_qu_tile a_xrep a_kexp a_rot a_scores a_v_mm a_vexp a_probs a_max a_exp "
                            "a_turned a_pT a_pv a_oT a_out_mm a_hdone a_v1 a_v2")
        wq, wk, wv = (sb(f"a_w{n}", [P, KC, D]) for n in "qkv")
        wo = sb("a_wo", [G * 16, PG, D])
        bo = sb("a_bo", [TT, D])
        uv = sb("a_uv", [P, 2, KC])
        perm = sb("a_perm", [P, P])
        tab = sb("a_tab", [P, 4, TT])
        texp = sb("a_texp", [P, HG, S])
        hmask = sb("a_hmask", [P, HG])
        vmask = sb("a_vmask", [TT, D])
        band = sb("a_band", [TT, 2, S])
        qu = sb("a_qu", [P, KC, T])
        qv = sb("a_qv", [P, KC, T + 1])
        sw = sb("a_sw", [P, KC, T + 1])
        kT = sb("a_kT", [P, KC, T])
        qum = sb("a_qum", [P, KC, G * TT])
        kexp = sb("a_kexp", [P, KC, G, HG, S])
        xrep = sb("a_xrep", [P, KC, G, G, S])
        r = [sb(f"a_r{n}", [P, KC, TT]) for n in (1, 2)]
        rt = sb("a_rt", [P, KC, TT])
        m1 = sb("a_m1", [TT, NB, QG, S])
        m2 = sb("a_m2", [TT, NB, QG, S])
        e = sb("a_e", [TT, NB * QG, S])
        mx = sb("a_mx", [TT, H])
        sm = sb("a_sm", [TT, H])
        pT = sb("a_pTb", [TT, PG, TT])
        vexp = sb("a_vexpb", [TT, G, D])
        oT = sb("a_oTb", [G * 16, PG, TT])
        tmp = sb("a_tmp", [TT, D])
        psS = ps("a_psS", [P, NB, BANK])
        psT = ps("a_psT", [P, 2, BANK])
        psV = ps("a_psV", [P, 2, BANK])
        block = stack.enter_context(nc.Block())

        @block.sync
        def _(sp):
            for dst, src in ((wq, "a_wq"), (wk, "a_wk"), (wv, "a_wv"), (wo, "a_wo"), (tab, "a_tab"),
                             (texp, "a_texp"), (band, "a_band"), (uv, "a_uv")):
                sp.dma_start(dst[:, :, :], d[src]).then_inc(s["a_in"], 16)
            for dst, src in ((bo, "a_bo"), (perm, "a_perm"), (hmask, "a_hmask"), (vmask, "a_vmask")):
                sp.dma_start(dst[:, :], d[src]).then_inc(s["a_in"], 16)

        @block.tensor
        def _(pe):
            pe.wait_ge(s["a_in"], 16 * 12 + 1)
            n = 0
            for w in (wq, wk):
                for c in range(KC):
                    for t in range(NCH):
                        if n >= 4:
                            pe.wait_ge(s["a_qk_done"], n - 2)
                        for k in range(KC):
                            last = nc.tensor.matmul(psS[:, n % 4, 0:CH], w[:, k, c * P:(c + 1) * P],
                                                    xT[:, k, t * CH:(t + 1) * CH], start=(k == 0), stop=(k == KC - 1))
                        last.then_inc(s["a_qk_mm"], 1)
                        n += 1
            pe.wait_ge(s["a_qk_done"], n + 1)
            for m in range(KC * NCH):
                if m >= 4:
                    pe.wait_ge(s["a_sw_done"], m - 2)
                c, t = divmod(m, NCH)
                nc.tensor.matmul(psS[:, m % 4, 0:CH], perm[:, :], qv[:, c, t * CH:(t + 1) * CH],
                                 start=True, stop=True).then_inc(s["a_sw_mm"], 1)
            pe.wait_ge(s["a_sw_done"], KC * NCH + 1)
            with pe.Fori(0, NT) as i:
                pe.wait_ge(s["a_qu_tile"], i + 2)
                pe.wait_ge(s["a_kexp"], i + 2)
                pe.wait_ge(s["a_rot"], i + 2)
                pe.wait_ge(s["a_probs"], i + 1)
                for g in range(NB):
                    c, o = divmod(g, 2)
                    for q in range(G):
                        nc.tensor.matmul(psS[0:TT, g, 0:W], qum[:, c, q * TT:(q + 1) * TT],
                                         kexp[:, c, q, o * QG:(o + 1) * QG, :].rearrange("p h j -> p (h j)"),
                                         start=(q == 0), stop=(q == G - 1))
                    for m in range(2):
                        last = nc.tensor.matmul(psS[0:TT, g, (m + 1) * W:(m + 2) * W], r[m][:, c, :],
                                                flat2(texp[:, o * QG:(o + 1) * QG, :]), start=True, stop=True)
                last.then_inc(s["a_scores"], 1)
                pe.wait_ge(s["a_xrep"], i + 2)
                pe.wait_ge(s["a_hdone"], i + 1)
                for q in range(G):
                    for k in range(KC):
                        last = nc.tensor.matmul(psV[0:TT, q // 2, (q % 2) * D:(q % 2 + 1) * D],
                                                xrep[:, k, q, :, :].rearrange("p a j -> p (a j)"), wv[:, k, :],
                                                start=(k == 0), stop=(k == KC - 1))
                last.then_inc(s["a_v_mm"], 1)
                pe.wait_ge(s["a_probs"], i + 2)
                pe.wait_ge(s["a_oT"], i + 1)
                for g in range(PG):
                    n = min(G, H - G * g) * S
                    last = nc.tensor.transpose(psT[0:n, g // 4, (g % 4) * TT:(g % 4 + 1) * TT],
                                               e[:, G * g:G * g + n // S, :].rearrange("p h j -> p (h j)"),
                                               ident[0:TT, 0:TT])
                last.then_inc(s["a_turned"], 1)
                pe.wait_ge(s["a_pT"], i + 2)
                pe.wait_ge(s["a_vexp"], i + 2)
                for g in range(PG):
                    m = min(G, H - G * g)
                    for q in range(G):
                        last = nc.tensor.matmul(psT[0:m * 16, g // 4, (g % 4) * TT + q * S:(g % 4) * TT + (q + 1) * S],
                                                vexp[0:m * S, q, g * 48:g * 48 + m * 16],
                                                pT[0:m * S, g, q * S:(q + 1) * S], start=True, stop=True)
                last.then_inc(s["a_pv"], 1)
                pe.wait_ge(s["a_oT"], i + 2)
                for g in range(PG):
                    m = min(G, H - G * g) * 16
                    last = nc.tensor.matmul(psV[0:TT, 1, D:2 * D], oT[0:m, g, :], wo[0:m, g, :],
                                            start=(g == 0), stop=(g == PG - 1))
                last.then_inc(s["a_out_mm"], 1)

        @block.scalar
        def _(act):
            act.wait_ge(s["a_qpad"], 2)
            for m in range(KC * NCH):
                c, t = divmod(m, NCH)
                act.wait_ge(s["a_sw_mm"], m + 2)
                nc.scalar.activation(sw[:, c, t * CH:(t + 1) * CH], psS[:, m % 4, 0:CH], ACT.Copy
                                     ).then_inc(s["a_sw_done"], 1)
            with act.Fori(0, NT) as i:
                act.wait_ge(s["a_max"], i + 2)
                nc.scalar.activation(e[:, :, :], m1[:, :, :, :].rearrange("p b h j -> p (b h) j"), ACT.Exp,
                                     scale=0.25).then_inc(s["a_exp"], 1)
                act.wait_ge(s["a_turned"], i + 2)
                nc.scalar.activation(pT[:, 0:4, :].rearrange("p g t -> p (g t)"), psT[0:TT, 0, 0:4 * TT], ACT.Copy
                                     ).then_inc(s["a_v2"], 1)
                nc.scalar.activation(pT[:, 4, :], psT[0:TT, 1, 0:TT], ACT.Copy).then_inc(s["a_v2"], 1)
                nc.scalar.activation(pT[0:S, 5, :], psT[0:S, 1, TT:2 * TT], ACT.Copy).then_inc(s["a_v2"], 1)
                act.wait_ge(s["a_v2"], 3 * i + 4)
                nc.scalar.nop().then_inc(s["a_pT"], 1)
                act.wait_ge(s["a_pv"], i + 2)
                nc.scalar.activation(oT[:, 0:4, :].rearrange("p g t -> p (g t)"), psT[0:48, 0, 0:4 * TT], ACT.Copy)
                nc.scalar.activation(oT[:, 4, :], psT[0:48, 1, 0:TT], ACT.Copy)
                nc.scalar.activation(oT[0:16, 5, :], psT[0:16, 1, TT:2 * TT], ACT.Copy).then_inc(s["a_oT"], 1)

        @block.gpsimd
        def _(pool):
            nc.gpsimd.memset(qum[:, :, :], 0.0)
            nc.gpsimd.memset(qv[:, :, T:T + 1], 0.0).then_inc(s["a_zero"], 1)
            nc.gpsimd.memset(sw[:, :, T:T + 1], 0.0).then_inc(s["a_qpad"], 1)
            pool.wait_ge(s["a_zero"], 2)
            pool.wait_ge(s["a_qk_done"], 2 * KC * NCH + 1)
            pool.wait_ge(s["a_in"], 16 * 12 + 1)
            with pool.Fori(0, NT) as i:
                pool.wait_ge(s["a_scores"], i + 1)
                for c in range(KC):
                    src = kT[:, c, bass.ds(i * TT, TT)].rearrange("p (q j) -> p q j", q=G)
                    for q in range(G):
                        last = nc.gpsimd.tensor_tensor(
                            kexp[:, c, q, :, :], src[:, q, :].unsqueeze(1).broadcast_to([P, HG, S]),
                            hmask[:, :].unsqueeze(2).broadcast_to([P, HG, S]), ALU.mult)
                last.then_inc(s["a_kexp"], 1)
                pool.wait_ge(s["a_v_mm"], i + 1)
                for c in range(KC):
                    for q in range(G):
                        last = nc.gpsimd.tensor_copy(xrep[:, c, q, :, :],
                                                     xT[:, c, bass.ds(i * TT + q * S, S)].unsqueeze(1)
                                                     .broadcast_to([P, G, S]))
                last.then_inc(s["a_xrep"], 1)

        @block.vector
        def _(dve):
            dve.wait_ge(s["a_in"], 16 * 12 + 1)
            dve.wait_ge(s["a_zero"], 2)
            n = 0
            for w in range(2):
                for c in range(KC):
                    for t in range(NCH):
                        dve.wait_ge(s["a_qk_mm"], n + 2)
                        src = psS[:, n % 4, 0:CH]
                        at = slice(t * CH, (t + 1) * CH)
                        if w == 0:
                            nc.vector.tensor_scalar(qu[:, c, at], src, uv[:, 0, c:c + 1], None, ALU.add)
                            last = nc.vector.tensor_scalar(qv[:, c, at], src, uv[:, 1, c:c + 1], None, ALU.add)
                        else:
                            last = nc.vector.tensor_copy(kT[:, c, at], src)
                        last.then_inc(s["a_qk_done"], 1)
                        n += 1
            dve.wait_ge(s["a_qk_done"], n + 1)
            dve.wait_ge(s["a_sw_done"], KC * NCH + 1)
            V1 = 15
            with dve.Fori(0, NT) as i:
                link = chain(dve, s["a_v1"], i * V1)
                dve.wait_ge(s["a_scores"], i + 1)
                for c in range(KC):
                    own = qum[:, c, :].rearrange("p (q x) -> p q x", q=G)
                    for q in range(G):
                        last = nc.vector.tensor_copy(qum[:, c, q * (TT + S):q * (TT + S) + S],
                                                     qu[:, c, bass.ds(i * TT + q * S, S)])
                last.then_inc(s["a_qu_tile"], 1)
                for m in range(2):
                    at = bass.ds(i * TT + m, TT)
                    link(nc.vector.tensor_tensor(r[m][:, :, :], qv[:, :, at],
                                                 tab[:, 2 * m:2 * m + 1, :].broadcast_to([P, KC, TT]), ALU.mult))
                    link(nc.vector.tensor_tensor(rt[:, :, :], sw[:, :, at],
                                                 tab[:, 2 * m + 1:2 * m + 2, :].broadcast_to([P, KC, TT]), ALU.mult))
                    link(nc.vector.tensor_tensor(r[m][:, :, :], r[m][:, :, :], rt[:, :, :], ALU.add))
                nc.vector.nop().then_inc(s["a_rot"], 1)
                dve.wait_ge(s["a_scores"], i + 2)
                dve.wait_ge(s["a_exp"], i + 1)
                part = [psS[0:TT, :, m * W:(m + 1) * W].rearrange("p b (h j) -> p b h j", j=S) for m in range(3)]
                for m, dst in ((1, m1), (2, m2)):
                    for g in range(NB):
                        last = nc.vector.tensor_tensor(dst[:, g, :, :], part[m][:, g, :, :],
                                                       band[:, m - 1:m, :].broadcast_to([TT, QG, S]), ALU.mult)
                    link(last)
                link(nc.vector.tensor_tensor(m1[:, :, :, :].rearrange("p b h j -> p (b h j)"),
                                             m1[:, :, :, :].rearrange("p b h j -> p (b h j)"),
                                             m2[:, :, :, :].rearrange("p b h j -> p (b h j)"), ALU.add))
                link(nc.vector.tensor_tensor(m1[:, :, :, :].rearrange("p b h j -> p b (h j)"),
                                             m1[:, :, :, :].rearrange("p b h j -> p b (h j)"),
                                             psS[0:TT, :, 0:W], ALU.add))
                sc = m1[:, :, :, :].rearrange("p b h j -> p (b h) j")
                link(nc.vector.tensor_reduce(mx[:, :], sc, X, ALU.max))
                nc.vector.tensor_tensor(sc, sc, mx[:, :].unsqueeze(2).broadcast_to([TT, H, S]),
                                        ALU.subtract).then_inc(s["a_max"], 1)
                dve.wait_ge(s["a_exp"], i + 2)
                link(nc.vector.tensor_reduce(sm[:, :], e[:, :, :], X, ALU.add))
                link(nc.vector.reciprocal(sm[:, :], sm[:, :]))
                nc.vector.tensor_tensor(e[:, :, :], e[:, :, :], sm[:, :].unsqueeze(2).broadcast_to([TT, H, S]),
                                        ALU.mult).then_inc(s["a_probs"], 1)
                dve.wait_ge(s["a_v_mm"], i + 2)
                for q in range(G):
                    last = nc.vector.tensor_tensor(vexp[:, q, :], psV[0:TT, q // 2, (q % 2) * D:(q % 2 + 1) * D],
                                                   vmask[:, :], ALU.mult)
                last.then_inc(s["a_vexp"], 1)
                dve.wait_ge(s["a_out_mm"], i + 2)
                link(nc.vector.tensor_tensor(tmp[:, :], psV[0:TT, 1, D:2 * D], bo[:, :], ALU.add))
                ht = flat2(h[:, bass.ds(i, 1), :])
                nc.vector.tensor_tensor(ht, ht, tmp[:, :], ALU.add).then_inc(s["a_hdone"], 1)
                link(nc.vector.nop())
            assert link.count() == V1


def layout_attn0(i, o):
    f = np.float32
    for n in "qkv":
        o[f"a_w{n}"] = cols(i[f"L0_attn_W{n}"], KC)
    wo = np.zeros((6, 48, D), f)
    wo.reshape(288, D)[:D] = i["L0_attn_Wo"]
    o["a_wo"] = wo.transpose(1, 0, 2)
    o["a_bo"] = rep(i["L0_attn_bo"])
    o["a_uv"] = np.stack([i["L0_attn_u"].reshape(KC, P).T, i["L0_attn_v"].reshape(KC, P).T], 1)
    o["a_perm"] = np.eye(P, dtype=f)[np.arange(P) ^ 8]
    freq = 1.0 / 10000.0 ** (np.arange(0, 16, 2) / 16)
    w = np.tile(freq, P // 8)[:, None]
    sine = (np.arange(P) % 16 < 8)[:, None]
    pos = np.tile(np.arange(S), G)[None, :]
    tab = []
    for a in (pos, pos + S + 1):
        tab += [np.sin(a * w), np.where(sine, 1, -1) * np.cos(a * w)]
    o["a_tab"] = np.stack(tab, 1).astype(f)
    j = np.arange(S)[None, :]
    t = np.where(sine, np.cos(j * w), np.sin(j * w))
    own = (np.arange(P)[:, None] // 16 == np.arange(8)[None, :])
    o["a_texp"] = (own[:, :, None] * t[:, None, :]).astype(f)
    o["a_hmask"] = own.astype(f)
    o["a_vmask"] = (np.arange(TT)[:, None] // S == (np.arange(D)[None, :] // 16) % G).astype(f)
    q = np.tile(np.arange(S), G)[:, None]
    o["a_band"] = np.stack([j <= q, j >= q + 2], 1).astype(f)


def stage_ffn0(nc, d, h, xT, ident):
    F = 1024
    FC = F // P
    SP = S + 2
    with ExitStack() as stack:
        sb, ps = bufs(nc, stack)
        x = sb("f_x", [TT, NT, D])
        norm_transpose(nc, "fn", h, xT, ident, 1e-5, True, x_tok=x, turn=False)
        s = sems(nc, stack, "f_in f_v f_v2 f_v3 f_ones f_wsum f_wtot f_wq f_xq f_turned f_qT f_diag f_bc_mm f_bc "
                            "f_h_mm f_hp f_edge f_conv1 f_conv3 f_silu f_amax f_max_turned f_max f_diag2 f_bc2_mm "
                            "f_hq f_out_mm f_hdone f_a")
        w1 = sb("f_w1", [P, KC * F])
        w2 = sb("f_w2", [P, FC * D])
        w1q = sb("f_w1q", [P, KC, F], BF16)
        w2q = sb("f_w2q", [P, FC, D], BF16)
        cw = sb("f_cw", [P, FC, 3])
        cb = sb("f_cb", [P, FC])
        ones = sb("f_ones_b", [P, P])
        wsum = sb("f_wsum_b", [P, 2])
        wmean = sb("f_wmean", [P, 2])
        wscale = sb("f_wscale", [P, 2])
        mx = sb("f_mx", [TT, NT])
        sc = sb("f_sc", [TT, NT])
        inv = sb("f_inv", [TT, NT])
        xb = sb("f_xb", [TT, NT, D], BF16)
        identb = sb("f_identb", [P, P], BF16)
        qT = sb("f_qTb", [P, KC, T], BF16)
        diag = sb("f_diagb", [TT, NT, TT])
        bc = sb("f_bcb", [P, T])
        hp = sb("f_hpb", [P, B + 1, SP])
        acc = sb("f_acc", [P, B + 1, S])
        act1 = sb("f_act", [P, FC, T])
        amax = sb("f_amaxb", [P, T])
        hq = sb("f_hqb", [P, FC, T], BF16)
        pm = ps("f_pm", [P, NCH, BANK])
        pt = ps("f_pt", [P, 4, 2 * BANK], BF16)
        po = ps("f_po", [P, BANK])
        groups = [(0, 4), (4, 8), (8, NT)]
        SL = TT + 1
        ph = [(0, 9), (9, NT)]
        block = stack.enter_context(nc.Block())

        @block.sync
        def _(sp):
            for dst, src in ((w1[:, :], "f_w1"), (w2[:, :], "f_w2"), (cw[:, :, :], "f_cw"), (cb[:, :], "f_cb")):
                sp.dma_start(dst, d[src]).then_inc(s["f_in"], 16)

        @block.scalar
        def _(act):
            act.wait_ge(s["f_in"], 65)
            nc.scalar.activation(act1[:, 0:2, :].rearrange("p c t -> p (c t)")[:, 0:KC * F], w1[:, :], ACT.Abs,
                                 accum_out=wsum[:, 0:1])
            nc.scalar.activation(act1[:, 2:4, :].rearrange("p c t -> p (c t)")[:, 0:FC * D], w2[:, :], ACT.Abs,
                                 accum_out=wsum[:, 1:2]).then_inc(s["f_wsum"], 1)
            for g in range(4):
                act.wait_ge(s["f_turned"], g + 2)
                k, b = divmod(g, 2)
                lo, hi = ph[b]
                nc.scalar.activation(qT[:, k, lo * TT:hi * TT].rearrange("p (t x) -> p t x", x=TT),
                                     pt[:, g, 0:(hi - lo) * SL].rearrange("p (t x) -> p t x", x=SL)[:, :, 0:TT], ACT.Copy
                                     ).then_inc(s["f_qT"], 1)
            act.wait_ge(s["f_wsum"], 2)
            with act.Fori(0, FC) as c:
                act.wait_ge(s["f_hp"], 3 * c + 4)
                act.wait_ge(s["f_silu"], c + 1)
                nc.scalar.activation(acc[:, :, :], hp[:, :, 0:S], ACT.Identity, scale=cw[:, bass.ds(c, 1), 0:1]
                                     .rearrange("p a b -> p (a b)"), bias=cb[:, bass.ds(c, 1)]).then_inc(s["f_conv1"], 1)
                act.wait_ge(s["f_conv3"], c + 2)
                nc.scalar.activation(flat2(act1[:, bass.ds(c, 1), :]), acc[:, :, :].rearrange("p b j -> p (b j)"),
                                     ACT.Silu).then_inc(s["f_silu"], 1)

        @block.tensor
        def _(pe):
            pe.wait_ge(s["f_ones"], 2)
            pe.wait_ge(s["f_wsum"], 2)
            nc.tensor.matmul(po[:, 0:2], ones[:, :], wsum[:, :], start=True, stop=True).then_inc(s["f_wtot"], 1)
            pe.wait_ge(s["f_xq"], 2)
            for k in range(KC):
                for b, (lo, hi) in enumerate(ph):
                    for t in range(lo, hi):
                        last = nc.tensor.transpose(pt[:, 2 * k + b, (t - lo) * SL:(t - lo) * SL + TT],
                                                   xb[:, t, k * P:(k + 1) * P], identb[0:TT, 0:TT])
                    last.then_inc(s["f_turned"], 1)
            pe.wait_ge(s["f_diag"], 2)
            for g, (a, b) in enumerate(groups):
                last = nc.tensor.matmul(pm[:, g, 0:(b - a) * TT], ones[0:TT, :], flat2(diag[:, a:b, :]),
                                        start=True, stop=True)
            last.then_inc(s["f_bc_mm"], 1)
            pe.wait_ge(s["f_bc"], 2)
            pe.wait_ge(s["f_qT"], 5)
            with pe.Fori(0, FC) as c:
                for t in range(NCH):
                    pe.wait_ge(s["f_hp"], 3 * c + t + 1)
                    for k in range(KC):
                        last = nc.tensor.matmul(pm[:, t, 0:CH], w1q[:, k, bass.ds(c * P, P)],
                                                qT[:, k, t * CH:(t + 1) * CH], start=(k == 0), stop=(k == KC - 1))
                    last.then_inc(s["f_h_mm"], 1)
            pe.wait_ge(s["f_amax"], FC + 1)
            for g, (a, b) in enumerate(groups):
                pe.wait_ge(s["f_max"], g + 1)
                for t in range(a, b):
                    last = nc.tensor.transpose(pm[0:TT, 0, (t - a) * P:(t - a + 1) * P],
                                               amax[:, t * TT:(t + 1) * TT], ident[:, :])
                last.then_inc(s["f_max_turned"], 1)
            pe.wait_ge(s["f_diag2"], 2)
            for g, (a, b) in enumerate(groups):
                last = nc.tensor.matmul(pm[:, g, 0:(b - a) * TT], ones[0:TT, :], flat2(diag[:, a:b, :]),
                                        start=True, stop=True)
            last.then_inc(s["f_bc2_mm"], 1)
            pe.wait_ge(s["f_hq"], 2)
            with pe.Fori(0, NT) as i:
                pe.wait_ge(s["f_hdone"], i + 1)
                for k in range(FC):
                    last = nc.tensor.matmul(po[0:TT, 0:D], hq[:, k, bass.ds(i * TT, TT)], w2q[:, k, :],
                                            start=(k == 0), stop=(k == FC - 1))
                last.then_inc(s["f_out_mm"], 1)

        @block.gpsimd
        def _(pool):
            nc.gpsimd.memset(hp[:, :, :], 0.0).then_inc(s["f_edge"], 1)

        @block.vector
        def _(dve):
            link = chain(dve, s["f_v"])
            nc.vector.memset(ones[:, :], 1.0).then_inc(s["f_ones"], 1)
            link(nc.vector.tensor_copy(identb[:, :], ident[:, :]))
            link(nc.vector.tensor_reduce(mx[:, :], x[:, :, :], X, ALU.max, apply_absolute_value=True))
            link(nc.vector.tensor_scalar(mx[:, :], mx[:, :], 1e-5, None, ALU.max))
            link(nc.vector.reciprocal(sc[:, :], mx[:, :]))
            link(nc.vector.tensor_scalar(sc[:, :], sc[:, :], 127.0, None, ALU.mult))
            link(nc.vector.tensor_tensor(x[:, :, :], x[:, :, :], sc[:, :].unsqueeze(2).broadcast_to([TT, NT, D]),
                                         ALU.mult))
            link(nc.vector.tensor_scalar(x[:, :, :], x[:, :, :], ROUND, -ROUND, ALU.add, ALU.add))
            nc.vector.tensor_scalar(xb[:, :, :], x[:, :, :], 127.0, -128.0, ALU.min, ALU.max).then_inc(s["f_xq"], 1)
            dve.wait_ge(s["f_wtot"], 2)
            link(nc.vector.tensor_scalar(wmean[:, :], po[:, 0:2], 1.0 / (F * D), 1e-5, ALU.mult, ALU.max))
            link(nc.vector.reciprocal(wscale[:, :], wmean[:, :]))
            for n, (w, wq) in enumerate(((w1, w1q), (w2, w2q))):
                link(nc.vector.tensor_scalar(w[:, :], w[:, :], wscale[:, n:n + 1], None, ALU.mult))
                link(nc.vector.tensor_scalar(w[:, :], w[:, :], ROUND, -ROUND, ALU.add, ALU.add))
                link(nc.vector.tensor_scalar(flat2(wq[:, :, :]), w[:, :], 1.0, -1.0, ALU.min, ALU.max))
            link(nc.vector.tensor_scalar(inv[:, :], mx[:, :], 1.0 / 127.0, wmean[0:TT, 0:1], ALU.mult, ALU.mult))
            eye = ident[0:TT, 0:TT].unsqueeze(1).broadcast_to([TT, NT, TT])
            nc.vector.tensor_tensor(diag[:, :, :], eye, inv[:, :].unsqueeze(2).broadcast_to([TT, NT, TT]), ALU.mult
                                    ).then_inc(s["f_diag"], 1)
            link(nc.vector.memset(amax[:, :], 0.0))
            dve.wait_ge(s["f_bc_mm"], 2)
            for g, (a, b) in enumerate(groups):
                last = nc.vector.tensor_copy(bc[:, a * TT:b * TT], pm[:, g, 0:(b - a) * TT])
            last.then_inc(s["f_bc"], 1)
            dve.wait_ge(s["f_bc"], 2)
            dve.wait_ge(s["f_edge"], 2)
            NB = (B + 1) // NCH
            with dve.Fori(0, FC) as c:
                link2 = chain(dve, s["f_v2"], 2 * c)
                dve.wait_ge(s["f_conv3"], c + 1)
                dve.wait_ge(s["f_conv1"], c + 1)
                for t in range(NCH):
                    dve.wait_ge(s["f_h_mm"], 3 * c + t + 2)
                    nc.vector.tensor_tensor(hp[:, t * NB:(t + 1) * NB, 1:S + 1],
                                            pm[:, t, 0:CH].rearrange("p (b j) -> p b j", j=S),
                                            bc[:, t * CH:(t + 1) * CH].rearrange("p (b j) -> p b j", j=S),
                                            ALU.mult).then_inc(s["f_hp"], 1)
                dve.wait_ge(s["f_conv1"], c + 2)
                dve.wait_ge(s["f_hp"], 3 * c + 4)
                tap = [flat2(cw[:, bass.ds(c, 1), n:n + 1]) for n in range(3)]
                link2(nc.vector.scalar_tensor_tensor(acc[:, :, :], hp[:, :, 1:S + 1], tap[1], acc[:, :, :],
                                                     ALU.mult, ALU.add))
                nc.vector.scalar_tensor_tensor(acc[:, :, :], hp[:, :, 2:S + 2], tap[2], acc[:, :, :],
                                               ALU.mult, ALU.add).then_inc(s["f_conv3"], 1)
                dve.wait_ge(s["f_silu"], c + 2)
                dve.wait_ge(s["f_amax"], c + 1)
                one = flat2(act1[:, bass.ds(c, 1), :])
                link2(nc.vector.scalar_tensor_tensor(amax[:, :], one, -1.0, amax[:, :], ALU.mult, ALU.max))
                nc.vector.tensor_tensor(amax[:, :], one, amax[:, :], ALU.max).then_inc(s["f_amax"], 1)
            link3 = chain(dve, s["f_v3"])
            for g, (a, b) in enumerate(groups):
                dve.wait_ge(s["f_max_turned"], g + 2)
                nc.vector.tensor_reduce(mx[:, a:b], pm[0:TT, 0, 0:(b - a) * P].rearrange("p (t f) -> p t f", f=P),
                                        X, ALU.max).then_inc(s["f_max"], 1)
            dve.wait_ge(s["f_max"], 4)
            link3(nc.vector.tensor_scalar(mx[:, :], mx[:, :], 1e-5, None, ALU.max))
            link3(nc.vector.reciprocal(sc[:, :], mx[:, :]))
            link3(nc.vector.tensor_scalar(sc[:, :], sc[:, :], 127.0, None, ALU.mult))
            link3(nc.vector.tensor_scalar(inv[:, :], mx[:, :], 1.0 / 127.0, wmean[0:TT, 1:2], ALU.mult, ALU.mult))
            nc.vector.tensor_tensor(diag[:, :, :], eye, sc[:, :].unsqueeze(2).broadcast_to([TT, NT, TT]), ALU.mult
                                    ).then_inc(s["f_diag2"], 1)
            dve.wait_ge(s["f_bc2_mm"], 2)
            for g, (a, b) in enumerate(groups):
                last = nc.vector.tensor_copy(bc[:, a * TT:b * TT], pm[:, g, 0:(b - a) * TT])
            link3(last)
            link3(nc.vector.tensor_tensor(act1[:, :, :], act1[:, :, :],
                                          bc[:, :].unsqueeze(1).broadcast_to([P, FC, T]), ALU.mult))
            link3(nc.vector.tensor_scalar(act1[:, :, :], act1[:, :, :], ROUND, -ROUND, ALU.add, ALU.add))
            nc.vector.tensor_scalar(hq[:, :, :], act1[:, :, :], 127.0, -128.0, ALU.min, ALU.max).then_inc(s["f_hq"], 1)
            with dve.Fori(0, NT) as i:
                dve.wait_ge(s["f_out_mm"], i + 2)
                ht = flat2(h[:, bass.ds(i, 1), :])
                nc.vector.scalar_tensor_tensor(ht, po[0:TT, 0:D], inv[:, bass.ds(i, 1)], ht, ALU.mult, ALU.add
                                               ).then_inc(s["f_hdone"], 1)


def layout_ffn0(i, o):
    o["f_w1"] = cols(i["L0_ffn_w1"].T, KC).reshape(P, -1)
    o["f_w2"] = cols(i["L0_ffn_w2"].T, 8).reshape(P, -1)
    o["f_cw"] = cols(i["L0_ffn_conv_w"].reshape(-1, 3), 8)
    o["f_cb"] = i["L0_ffn_conv_b"].reshape(8, P).T


GROUPS = [(0, 4), (4, 8), (8, NT)]


def projected(nc, name, xT, w_dram, n, bias_dram, dst):
    with ExitStack() as stack:
        sb, ps = bufs(nc, stack)
        s = sems(nc, stack, f"{name}_in {name}_x {name}_mm {name}_done")
        get = s
        s_in, s_x, s_mm, s_done = (get[f"{name}_{k}"] for k in ("in", "x", "mm", "done"))
        w = sb(f"{name}_w", [P, KC, n])
        bias = sb(f"{name}_bias", [TT, n])
        xs = sb(f"{name}_xs", [P, KC, TT])
        pp = ps(f"{name}_pp", [P, BANK])
        block = stack.enter_context(nc.Block())

        @block.sync
        def _(sp):
            sp.dma_start(w[:, :, :], w_dram).then_inc(s_in, 16)
            sp.dma_start(bias[:, :], bias_dram).then_inc(s_in, 16)

        @block.scalar
        def _(act):
            with act.Fori(0, NT) as i:
                act.wait_ge(s_mm, i + 1)
                nc.scalar.activation(xs[:, :, :], xT[:, :, bass.ds(i * TT, TT)], ACT.Copy).then_inc(s_x, 1)

        @block.tensor
        def _(pe):
            pe.wait_ge(s_in, 33)
            with pe.Fori(0, NT) as i:
                pe.wait_ge(s_x, i + 2)
                pe.wait_ge(s_done, i + 1)
                for k in range(KC):
                    last = nc.tensor.matmul(pp[0:TT, 0:n], xs[:, k, :], w[:, k, :], start=(k == 0), stop=(k == KC - 1))
                last.then_inc(s_mm, 1)

        @block.vector
        def _(dve):
            dve.wait_ge(s_in, 33)
            with dve.Fori(0, NT) as i:
                dve.wait_ge(s_mm, i + 2)
                nc.vector.tensor_tensor(flat2(dst[:, bass.ds(i, 1), :]), pp[0:TT, 0:n], bias[:, :], ALU.add
                                        ).then_inc(s_done, 1)


def stage_gate1(nc, d, h, xT, ident):
    N = 16
    W = D + 2 * N
    with ExitStack() as stack:
        sb, ps = bufs(nc, stack)
        x = sb("g_x", [TT, NT, D])
        pre = sb("g_pre", [TT, NT, W])
        norm_transpose(nc, "gn", h, xT, ident, 1e-5, True, x_tok=x)
        projected(nc, "gp", xT, d["g_w"], W, d["g_bias"], pre)
        s = sems(nc, stack, "g_v g_abs g_exp g_ln")
        e = sb("g_e", [TT, NT, D])
        ln = sb("g_lnb", [TT, NT, D])
        u = sb("g_u", [TT, NT, D])
        bc = sb("g_bc", [TT, NT, N])
        sm = sb("g_sm", [TT, NT])
        block = stack.enter_context(nc.Block())

        @block.scalar
        def _(act):
            nc.scalar.activation(e[:, :, :], pre[:, :, 0:D], ACT.Abs).then_inc(s["g_abs"], 1)
            act.wait_ge(s["g_abs"], 2)
            nc.scalar.activation(e[:, :, :], e[:, :, :], ACT.Exp, scale=-1.0).then_inc(s["g_exp"], 1)
            act.wait_ge(s["g_exp"], 2)
            nc.scalar.activation(ln[:, :, :], e[:, :, :], ACT.Ln, bias=1.0).then_inc(s["g_ln"], 1)

        @block.vector
        def _(dve):
            link = chain(dve, s["g_v"])
            link(nc.vector.tensor_tensor(bc[:, :, :], pre[:, :, D:D + N], pre[:, :, D + N:W], ALU.mult))
            link(nc.vector.tensor_reduce(sm[:, :], bc[:, :, :], X, ALU.add))
            dve.wait_ge(s["g_exp"], 2)
            link(nc.vector.tensor_scalar(u[:, :, :], e[:, :, :], 1.0, None, ALU.add))
            link(nc.vector.scalar_tensor_tensor(u[:, :, :], u[:, :, :], -1.0, e[:, :, :], ALU.add, ALU.subtract))
            dve.wait_ge(s["g_ln"], 2)
            link(nc.vector.tensor_tensor(ln[:, :, :], ln[:, :, :], u[:, :, :], ALU.subtract))
            link(nc.vector.scalar_tensor_tensor(ln[:, :, :], pre[:, :, 0:D], 0.0, ln[:, :, :], ALU.max, ALU.add))
            link(nc.vector.tensor_tensor(ln[:, :, :], ln[:, :, :], x[:, :, :], ALU.mult))
            link(nc.vector.tensor_tensor(ln[:, :, :], ln[:, :, :], sm[:, :].unsqueeze(2).broadcast_to([TT, NT, D]),
                                         ALU.mult))
            link(nc.vector.tensor_tensor(h[:, :, :], h[:, :, :], ln[:, :, :], ALU.add))


def experts(nc, name, w_dram, gates, xT, h, E, U, FC, gated, biases=False):
    I = FC * P
    NU = 2 if gated else 1
    UPW = NU * KC * I
    BW = UPW + FC * D
    WC = BW + (FC + D if biases else 0)
    UP = 3 * FC
    with ExitStack() as stack:
        sb, ps = bufs(nc, stack)
        names = ("up_mm act hid free up_free acc down_mm ones " +
                 " ".join(f"w{u} used{u}" for u in range(U))).split()
        made = sems(nc, stack, " ".join(f"{name}_{k}" for k in names))
        s = {k[len(name) + 1:]: v for k, v in made.items()}
        slot = s
        w = [sb(f"{name}_wb{u}", [P, WC]) for u in range(U)]
        hid = [sb(f"{name}_hid{u}", [P, FC, T]) for u in range(U)]
        sg = sb(f"{name}_sg", [P, 2, BANK])
        pu = ps(f"{name}_pu", [P, 2, NU, BANK])
        po = ps(f"{name}_po", [P, 2, BANK])
        ones = sb(f"{name}_onesb", [1, TT])
        block = stack.enter_context(nc.Block())

        @block.sync
        def _(sp):
            with sp.Fori(0, E // U) as i:
                for u in range(U):
                    sp.wait_ge(slot[f"used{u}"], i + 1)
                    sp.dma_start(w[u][:, :], w_dram[bass.ds(i * U + u, 1)].rearrange("a p w -> p (a w)")
                                 ).then_inc(slot[f"w{u}"], 16)

        @block.tensor
        def _(pe):
            pe.wait_ge(s["ones"], 2)

            def up(u, e, g):
                lo, hi = GROUPS[g]
                for f in range(FC):
                    n = g * FC + f
                    pe.wait_ge(s["up_free"], e * UP + n + 2)
                    for m in range(NU):
                        for k in range(KC):
                            at = (m * KC + k) * I + f * P
                            last = nc.tensor.matmul(pu[:, (n + u * UP) % 2, m, 0:(hi - lo) * TT], w[u][:, at:at + P],
                                                    xT[:, k, lo * TT:hi * TT], start=(k == 0), stop=(k == KC - 1))
                    last.then_inc(s["up_mm"], 1)

            def down(u, e, g):
                lo, hi = GROUPS[g]
                pe.wait_ge(s["hid"], e * UP + (g + 1) * FC + 1)
                for t in range(lo, hi):
                    pe.wait_ge(s["free"], e * NT + t + 2)
                    o = po[0:TT, (t + u * NT) % 2, 0:D]
                    if biases:
                        nc.tensor.matmul(o, ones[:, :], w[u][0:1, BW + FC:WC], start=True, stop=False)
                    for f in range(FC):
                        last = nc.tensor.matmul(o, hid[u][:, f, t * TT:(t + 1) * TT],
                                                w[u][:, UPW + f * D:UPW + (f + 1) * D],
                                                start=(f == 0 and not biases), stop=(f == FC - 1))
                    last.then_inc(s["down_mm"], 1)

            with pe.Fori(0, E // U) as i:
                for u in range(U):
                    e = i * U + u
                    pe.wait_ge(slot[f"w{u}"], i * 16 + 17)
                    up(u, e, 0)
                    up(u, e, 1)
                    down(u, e, 0)
                    up(u, e, 2)
                    down(u, e, 1)
                    down(u, e, 2)

        @block.scalar
        def _(act):
            with act.Fori(0, E // U) as i:
                for u in range(U):
                    e = i * U + u
                    for n in range(UP):
                        g, f = divmod(n, FC)
                        lo, hi = GROUPS[g]
                        N = (hi - lo) * TT
                        src = pu[:, (n + u * UP) % 2, 0, 0:N]
                        act.wait_ge(s["up_mm"], e * UP + n + 2)
                        if gated:
                            act.wait_ge(s["up_free"], e * UP + n + 2)
                            nc.scalar.activation(sg[:, (n + u * UP) % 2, 0:N], src, ACT.Silu).then_inc(s["act"], 1)
                        else:
                            if n == 0:
                                act.wait_ge(slot[f"used{u}"], i + 1)
                            nc.scalar.activation(hid[u][:, f, lo * TT:hi * TT], src, ACT.Relu,
                                                 bias=w[u][:, BW + f:BW + f + 1]).then_inc(s["hid"], 1)
                            act.wait_ge(s["hid"], e * UP + n + 2)
                            nc.scalar.nop().then_inc(s["up_free"], 1)

        @block.vector
        def _(dve):
            nc.vector.nop().then_inc(s["up_free"], 2)
            nc.vector.memset(ones[:, :], 1.0).then_inc(s["ones"], 1)
            nc.vector.nop().then_inc(s["free"], 2)
            with dve.Fori(0, E // U) as i:
                for u in range(U):
                    e = i * U + u

                    def products(g, u=u, e=e, i=i):
                        lo, hi = GROUPS[g]
                        N = (hi - lo) * TT
                        for f in range(FC):
                            n = g * FC + f
                            b = (n + u * UP) % 2
                            dve.wait_ge(s["act"], e * UP + n + 2)
                            if n == 0:
                                dve.wait_ge(slot[f"used{u}"], i + 1)
                            nc.vector.tensor_tensor(hid[u][:, f, lo * TT:hi * TT], sg[:, b, 0:N],
                                                    pu[:, b, 1, 0:N], ALU.mult).then_inc(s["hid"], 1)
                            dve.wait_ge(s["hid"], e * UP + n + 2)
                            nc.vector.nop().then_inc(s["up_free"], 1)

                    def add(g, u=u, e=e):
                        lo, hi = GROUPS[g]
                        for t in range(lo, hi):
                            dve.wait_ge(s["down_mm"], e * NT + t + 2)
                            nc.vector.scalar_tensor_tensor(h[:, t, :], po[0:TT, (t + u * NT) % 2, 0:D],
                                                           flat2(gates[:, t:t + 1, bass.ds(e, 1)]), h[:, t, :],
                                                           ALU.mult, ALU.add).then_inc(s["acc"], 1)
                            dve.wait_ge(s["acc"], e * NT + t + 2)
                            nc.vector.nop().then_inc(s["free"], 1)
                        if g == 2:
                            nc.vector.nop().then_inc(slot[f"used{u}"], 1)

                    if gated:
                        products(0)
                        products(1)
                        add(0)
                        products(2)
                        add(1)
                        add(2)
                    else:
                        add(0)
                        add(1)
                        add(2)


def stage_ffn1(nc, d, h, xT, ident):
    E = 4
    with ExitStack() as stack:
        sb, ps = bufs(nc, stack)
        norm_transpose(nc, "en", h, xT, ident, 1e-5, True)
        z = sb("e_z", [TT, NT, 1])
        gates = sb("e_gates", [TT, NT, E])
        projected(nc, "ep", xT, d["e_wu"], 1, d["e_bu"], z)
        with ExitStack() as inner:
            sb2, _ = bufs(nc, inner)
            s = sems(nc, inner, "e_turn_in e_u e_v")
            turn = sb2("e_turn", [TT, E, E])
            u = sb2("e_ub", [TT, NT, 1])
            w = sb2("e_w", [TT, NT, 1])
            t = sb2("e_t", [TT, NT, E])
            block = inner.enter_context(nc.Block())

            @block.sync
            def _(sp):
                sp.dma_start(turn[:, :, :], d["e_turn"]).then_inc(s["e_turn_in"], 16)

            @block.scalar
            def _(act):
                nc.scalar.activation(u[:, :, :], z[:, :, :], ACT.Sigmoid).then_inc(s["e_u"], 1)

            @block.vector
            def _(dve):
                link = chain(dve, s["e_v"])
                dve.wait_ge(s["e_turn_in"], 17)
                dve.wait_ge(s["e_u"], 2)
                for r in range(E):
                    if r == 0:
                        link(nc.vector.tensor_copy(w[:, :, :], u[:, :, :]))
                    else:
                        link(nc.vector.tensor_scalar(w[:, :, :], u[:, :, :], float(E), float(r), ALU.mult, ALU.is_gt))
                        link(nc.vector.tensor_tensor(w[:, :, :], w[:, :, :], u[:, :, :], ALU.mult))
                        link(nc.vector.tensor_scalar(w[:, :, :], w[:, :, :], 1.0 / (r + 1), None, ALU.mult))
                    dst = gates if r == 0 else t
                    link(nc.vector.tensor_tensor(dst[:, :, :], w[:, :, :].broadcast_to([TT, NT, E]),
                                                 turn[:, r:r + 1, :].broadcast_to([TT, NT, E]), ALU.mult))
                    if r:
                        link(nc.vector.tensor_tensor(gates[:, :, :], gates[:, :, :], t[:, :, :], ALU.add))
        experts(nc, "e", d["e_w"], gates, xT, h, E, 2, 8, False, True)


def layout_l1(i, o):
    o["g_w"] = cols(np.concatenate([i[f"L1_attn_W{n}"].T for n in (1, 2, 3)], 1), KC)
    o["g_bias"] = rep(np.concatenate([i[f"L1_attn_b{n}"] for n in (1, 2, 3)]))
    o["e_wu"] = cols(i["L1_ffn_Wu"], KC)
    o["e_bu"] = rep(i["L1_ffn_bu"])
    pos = np.tile(np.arange(S), G)[:, None, None]
    r, e = np.arange(4)[None, :, None], np.arange(4)[None, None, :]
    o["e_turn"] = ((pos + r) % 4 == e).astype(np.float32)
    b2 = np.zeros((4, P, D), np.float32)
    b2[:, 0] = i["L1_ffn_b2"]
    o["e_w"] = np.concatenate([up_cols(i["L1_ffn_W1"]), up_cols(i["L1_ffn_W2"]),
                               i["L1_ffn_b1"].reshape(4, 8, P).transpose(0, 2, 1), b2], 2)


def up_cols(w):
    e, k, n = w.shape
    return w.reshape(e, k // P, P, n).transpose(0, 2, 1, 3).reshape(e, P, -1)


def stage_scan(nc, d, h, xT, ident):
    DI, R, N, K = 512, 64, 16, 4
    C = DI // P
    SP = S + K - 1
    NB = (B + 1) // NCH
    W = C * CH
    with ExitStack() as stack:
        sb, ps = bufs(nc, stack)
        norm_transpose(nc, "sn", h, xT, ident, 1e-5, True)
        xc = sb("s_xc", [P, NCH, C, CH])
        res = sb("s_res", [P, NCH, C, CH])
        delta = sb("s_delta", [P, NCH, C, CH])
        a = sb("s_a", [P, N, C])
        dd = sb("s_d", [P, C])
        xdbl = sb("s_xdbl", [R + 2 * N, T])
        bc_dram = nc.dram_tensor("s_bc", (NCH, N, 2, CH), F32, kind="Internal").ap()
        with ExitStack() as inner:
            sb2, ps2 = bufs(nc, inner)
            s = sems(nc, inner, "s_in s_edge s_px_mm s_x s_tap0 s_taps s_xc_done s_res_done s_dbl_mm s_dbl s_dt_mm "
                                "s_dt s_e s_ln s_v s_a_exp s_bc_out s_dve")
            w_in = sb2("s_w_in", [P, KC, 2 * DI])
            w_x = sb2("s_w_x", [P, C, R + 2 * N])
            w_dt = sb2("s_w_dt", [R, DI])
            cw = sb2("s_cw", [P, C, K])
            cb = sb2("s_cb", [P, C])
            b_dt = sb2("s_b_dt", [P, C])
            xp = [sb2(f"s_xp{n}", [P, B + 1, SP]) for n in range(2)]
            acc = [sb2(f"s_acc{n}", [P, B + 1, S]) for n in range(2)]
            e = sb2("s_eb", [P, NCH, C, CH])
            ln = sb2("s_lnb", [P, NCH, C, CH])
            pp = ps2("s_pp", [P, 6, BANK])
            block = inner.enter_context(nc.Block())

            @block.sync
            def _(sp):
                for dst, src in ((w_in[:, :, :], "s_w_in"), (w_x[:, :, :], "s_w_x"), (w_dt[:, :], "s_w_dt"),
                                 (cw[:, :, :], "s_cw"), (cb[:, :], "s_cb"), (b_dt[:, :], "s_b_dt"),
                                 (a[:, :, :], "s_a"), (dd[:, :], "s_d")):
                    sp.dma_start(dst, d[src]).then_inc(s["s_in"], 16)
                sp.wait_ge(s["s_dbl"], NCH + 1)
                for t in range(NCH):
                    for m in range(2):
                        sp.dma_start(bc_dram[t, :, m, :], xdbl[R + m * N:R + (m + 1) * N, t * CH:(t + 1) * CH]
                                     ).then_inc(s["s_bc_out"], 16)
                sp.wait_ge(s["s_bc_out"], 6 * 16 + 1)

            @block.tensor
            def _(pe):
                pe.wait_ge(s["s_in"], 129)
                for n in range(2 * C * NCH):
                    j, t = divmod(n, NCH)
                    if n >= 6:
                        m = n - 5
                        pe.wait_ge(s["s_x"], m + 1) if m <= C * NCH else pe.wait_ge(s["s_res_done"], m - C * NCH + 1)
                    for k in range(KC):
                        last = nc.tensor.matmul(pp[:, n % 6, 0:CH], w_in[:, k, j * P:(j + 1) * P],
                                                xT[:, k, t * CH:(t + 1) * CH], start=(k == 0), stop=(k == KC - 1))
                    last.then_inc(s["s_px_mm"], 1)
                pe.wait_ge(s["s_xc_done"], C + 1)
                pe.wait_ge(s["s_res_done"], C * NCH + 1)
                for t in range(NCH):
                    for c in range(C):
                        last = nc.tensor.matmul(pp[0:R + 2 * N, t, 0:CH], w_x[:, c, :], xc[:, t, c, :],
                                                start=(c == 0), stop=(c == C - 1))
                    last.then_inc(s["s_dbl_mm"], 1)
                for n in range(C * NCH):
                    t, c = divmod(n, C)
                    pe.wait_ge(s["s_dbl"], t + 2)
                    if n >= 3:
                        pe.wait_ge(s["s_dt"], n - 1)
                    nc.tensor.matmul(pp[:, 3 + n % 3, 0:CH], w_dt[:, c * P:(c + 1) * P], xdbl[0:R, t * CH:(t + 1) * CH],
                                     start=True, stop=True).then_inc(s["s_dt_mm"], 1)

            @block.scalar
            def _(act):
                act.wait_ge(s["s_in"], 129)
                nc.scalar.activation(a[:, :, :], a[:, :, :], ACT.Exp).then_inc(s["s_a_exp"], 1)
                for c in range(C):
                    act.wait_ge(s["s_x"], 3 * c + 4)
                    nc.scalar.activation(acc[c % 2][:, :, :], xp[c % 2][:, :, 0:S], ACT.Identity, scale=cw[:, c, 0:1],
                                         bias=cb[:, c:c + 1]).then_inc(s["s_tap0"], 1)
                    act.wait_ge(s["s_taps"], c + 2)
                    nc.scalar.activation(xc[:, :, c, :], acc[c % 2][:, :, :].rearrange("p (t b) j -> p t (b j)", t=NCH),
                                         ACT.Silu).then_inc(s["s_xc_done"], 1)
                for n in range(C * NCH):
                    c, t = divmod(n, NCH)
                    act.wait_ge(s["s_px_mm"], C * NCH + n + 2)
                    nc.scalar.activation(res[:, t, c, :], pp[:, (C * NCH + n) % 6, 0:CH], ACT.Silu
                                         ).then_inc(s["s_res_done"], 1)
                for t in range(NCH):
                    act.wait_ge(s["s_dbl_mm"], t + 2)
                    nc.scalar.activation(xdbl[:, t * CH:(t + 1) * CH], pp[0:R + 2 * N, t, 0:CH], ACT.Copy
                                         ).then_inc(s["s_dbl"], 1)
                act.wait_ge(s["s_dt"], C * NCH + 1)
                nc.scalar.activation(e[:, :, :, :], delta[:, :, :, :], ACT.Abs).then_inc(s["s_e"], 1)
                act.wait_ge(s["s_e"], 2)
                nc.scalar.activation(e[:, :, :, :], e[:, :, :, :], ACT.Exp, scale=-1.0).then_inc(s["s_e"], 1)
                act.wait_ge(s["s_e"], 3)
                nc.scalar.activation(ln[:, :, :, :], e[:, :, :, :], ACT.Ln, bias=1.0).then_inc(s["s_ln"], 1)

            @block.gpsimd
            def _(pool):
                for n in range(2):
                    nc.gpsimd.memset(xp[n][:, :, :], 0.0).then_inc(s["s_edge"], 1)

            @block.vector
            def _(dve):
                link = chain(dve, s["s_v"])
                dve.wait_ge(s["s_edge"], 3)
                for c in range(C):
                    if c >= 2:
                        dve.wait_ge(s["s_tap0"], c)
                        dve.wait_ge(s["s_taps"], c)
                    for t in range(NCH):
                        dve.wait_ge(s["s_px_mm"], 3 * c + t + 2)
                        nc.vector.tensor_copy(xp[c % 2][:, t * NB:(t + 1) * NB, K - 1:SP],
                                              pp[:, (3 * c + t) % 6, 0:CH].rearrange("p (b j) -> p b j", j=S)
                                              ).then_inc(s["s_x"], 1)
                    dve.wait_ge(s["s_x"], 3 * c + 4)
                    dve.wait_ge(s["s_tap0"], c + 2)
                    for k in range(1, K):
                        ins = nc.vector.scalar_tensor_tensor(acc[c % 2][:, :, :], xp[c % 2][:, :, k:k + S],
                                                             cw[:, c, k:k + 1], acc[c % 2][:, :, :], ALU.mult, ALU.add)
                        if k < K - 1:
                            link(ins)
                        else:
                            ins.then_inc(s["s_taps"], 1)
                dve.wait_ge(s["s_a_exp"], 2)
                link(nc.vector.tensor_scalar(a[:, :, :], a[:, :, :], -1.0, None, ALU.mult))
                for n in range(C * NCH):
                    t, c = divmod(n, C)
                    dve.wait_ge(s["s_dt_mm"], n + 2)
                    nc.vector.tensor_scalar(delta[:, t, c, :], pp[:, 3 + n % 3, 0:CH], b_dt[:, c:c + 1], None, ALU.add
                                            ).then_inc(s["s_dt"], 1)
                u, lf, ef, df = (x[:, :, :, :].rearrange("p t c n -> p (t c n)") for x in (e, ln, e, delta))
                tmp = flat2(acc[0][:, :, :])
                dve.wait_ge(s["s_ln"], 2)
                for t in range(NCH * C):
                    at = slice(t * CH, (t + 1) * CH)
                    one = tmp[:, (t % 3) * CH:(t % 3 + 1) * CH]
                    link(nc.vector.tensor_scalar(one, ef[:, at], 1.0, None, ALU.add))
                    link(nc.vector.scalar_tensor_tensor(ef[:, at], one, -1.0, ef[:, at], ALU.add, ALU.subtract))
                link(nc.vector.tensor_tensor(lf, lf, ef, ALU.subtract))
                link(nc.vector.scalar_tensor_tensor(df, df, 0.0, lf, ALU.max, ALU.add))

        with ExitStack() as inner:
            sb2, ps2 = bufs(nc, inner)
            s = sems(nc, inner, "c_du c_exp c_start c_zero c_y_mm c_y c_v c_ym c_w c_out_mm c_out " +
                     " ".join(f"c_bc{u} c_da{u} c_dbu{u} c_scan{u} c_yt{u} c_sum{u}" for u in range(2)))
            v = s
            du = sb2("c_dub", [P, NCH, C, CH])
            bc = [sb2(f"c_bcb{u}", [P, 2, CH]) for u in range(2)]
            da = [sb2(f"c_dab{u}", [P, W]) for u in range(2)]
            dbu = [sb2(f"c_dbub{u}", [P, W]) for u in range(2)]
            st = [sb2(f"c_st{u}", [P, W]) for u in range(2)]
            yt = [sb2(f"c_ytb{u}", [P, W]) for u in range(2)]
            zero = sb2("c_zerob", [P, CH])
            w_out = sb2("c_w_out", [P, C, D])
            ycol = sb2("c_ycol", [P, C, T])
            pc = ps2("c_pc", [P, C, BANK])
            po = ps2("c_po", [P, 2, BANK])
            block = inner.enter_context(nc.Block())

            @block.sync
            def _(sp):
                sp.dma_start(w_out[:, :, :], d["s_w_out"]).then_inc(s["c_w"], 16)
                for t in range(NCH):
                    with sp.Fori(0, N // 2) as i:
                        for u in range(2):
                            sp.wait_ge(v[f"c_dbu{u}"], t * 8 + i + 1)
                            sp.wait_ge(v[f"c_yt{u}"], t * 8 + i + 1)
                            sp.dma_start(bc[u][:, :, :].rearrange("p m n -> p (m n)"),
                                         bc_dram[t, bass.ds(2 * i + u, 1)].rearrange("a m n -> a (m n)")
                                         .broadcast_to([P, 2 * CH])).then_inc(v[f"c_bc{u}"], 16)

            @block.scalar
            def _(act):
                for t in range(NCH):
                    with act.Fori(0, N // 2) as i:
                        for u in range(2):
                            act.wait_ge(v[f"c_scan{u}"], t * 8 + i + 1)
                            for c in range(C):
                                last = nc.scalar.activation(da[u][:, c * CH:(c + 1) * CH], delta[:, t, c, :], ACT.Exp,
                                                            scale=flat2(a[:, bass.ds(2 * i + u, 1), c:c + 1]))
                            last.then_inc(s["c_exp"], 1)

            @block.gpsimd
            def _(pool):
                pool.wait_ge(s["c_du"], 2)
                for t in range(NCH):
                    with pool.Fori(0, N // 2) as i:
                        for u in range(2):
                            pool.wait_ge(v[f"c_scan{u}"], t * 8 + i + 1)
                            pool.wait_ge(v[f"c_bc{u}"], (t * 8 + i) * 16 + 17)
                            pool.wait_ge(s["c_exp"], t * 16 + 2 * i + u + 2)
                            nc.gpsimd.tensor_tensor(dbu[u][:, :].rearrange("p (c n) -> p c n", c=C), du[:, t, :, :],
                                                    bc[u][:, 0:1, :].broadcast_to([P, C, CH]), ALU.mult
                                                    ).then_inc(v[f"c_dbu{u}"], 1)
                            nc.gpsimd.memset(da[u][:, :].rearrange("p (b j) -> p b j", j=S)[:, :, 0:1], 0.0
                                             ).then_inc(v[f"c_da{u}"], 1)

            @block.tensor
            def _(pe):
                pe.wait_ge(s["c_zero"], 2)
                for t in range(NCH):
                    pe.wait_ge(s["c_y"], t + 1)
                    for c in range(C):
                        nc.tensor.matmul(pc[:, c, 0:CH], ident[:, :], zero[:, :], start=True, stop=False,
                                         skip_group_check=True)
                    with pe.Fori(0, N // 2) as i:
                        for u in range(2):
                            pe.wait_ge(v[f"c_yt{u}"], t * 8 + i + 2)
                            for c in range(C):
                                last = nc.tensor.matmul(pc[:, c, 0:CH], ident[:, :], yt[u][:, c * CH:(c + 1) * CH],
                                                        start=False, stop=False, skip_group_check=True)
                            last.then_inc(v[f"c_sum{u}"], 1)
                    for c in range(C):
                        last = nc.tensor.matmul(pc[:, c, 0:CH], ident[:, :], zero[:, :], start=False, stop=True,
                                                skip_group_check=True)
                    last.then_inc(s["c_y_mm"], 1)
                pe.wait_ge(s["c_w"], 17)
                pe.wait_ge(s["c_ym"], 2)
                for n in range(NT):
                    if n >= 2:
                        pe.wait_ge(s["c_out"], n)
                    for c in range(C):
                        last = nc.tensor.matmul(po[0:TT, n % 2, 0:D], ycol[:, c, n * TT:(n + 1) * TT], w_out[:, c, :],
                                                start=(c == 0), stop=(c == C - 1))
                    last.then_inc(s["c_out_mm"], 1)

            @block.vector
            def _(dve):
                link = chain(dve, s["c_v"])
                nc.vector.memset(zero[:, :], 0.0).then_inc(s["c_zero"], 1)
                nc.vector.tensor_tensor(du[:, :, :, :].rearrange("p t c n -> p (t c n)"),
                                        delta[:, :, :, :].rearrange("p t c n -> p (t c n)"),
                                        xc[:, :, :, :].rearrange("p t c n -> p (t c n)"), ALU.mult
                                        ).then_inc(s["c_du"], 1)
                for t in range(NCH):
                    with dve.Fori(0, N // 2) as i:
                        for u in range(2):
                            m = t * 8 + i
                            dve.wait_ge(v[f"c_da{u}"], m + 2)
                            dve.wait_ge(v[f"c_dbu{u}"], m + 2)
                            dve.wait_ge(v[f"c_yt{u}"], m + 1)
                            nc.vector.tensor_tensor_scan(st[u][:, :], da[u][:, :], dbu[u][:, :], 0.0, ALU.mult, ALU.add
                                                         ).then_inc(v[f"c_scan{u}"], 1)
                            dve.wait_ge(v[f"c_scan{u}"], m + 2)
                            dve.wait_ge(v[f"c_bc{u}"], m * 16 + 17)
                            dve.wait_ge(v[f"c_sum{u}"], m + 1)
                            nc.vector.tensor_tensor(yt[u][:, :].rearrange("p (c n) -> p c n", c=C),
                                                    st[u][:, :].rearrange("p (c n) -> p c n", c=C),
                                                    bc[u][:, 1:2, :].broadcast_to([P, C, CH]), ALU.mult
                                                    ).then_inc(v[f"c_yt{u}"], 1)
                    dve.wait_ge(s["c_y_mm"], t + 2)
                    for c in range(C):
                        last = nc.vector.scalar_tensor_tensor(ycol[:, c, t * CH:(t + 1) * CH], xc[:, t, c, :],
                                                              dd[:, c:c + 1], pc[:, c, 0:CH], ALU.mult, ALU.add)
                    last.then_inc(s["c_y"], 1)
                dve.wait_ge(s["c_y"], NCH + 1)
                nc.vector.tensor_tensor(ycol[:, :, :].rearrange("p c (t n) -> p t c n", t=NCH),
                                        ycol[:, :, :].rearrange("p c (t n) -> p t c n", t=NCH), res[:, :, :, :],
                                        ALU.mult).then_inc(s["c_ym"], 1)
                for n in range(NT):
                    dve.wait_ge(s["c_out_mm"], n + 2)
                    nc.vector.tensor_tensor(h[:, n, :], h[:, n, :], po[0:TT, n % 2, 0:D], ALU.add).then_inc(s["c_out"], 1)


def layout_scan(i, o):
    o["s_w_in"] = cols(i["L2_attn_W_in"], KC)
    o["s_w_x"] = cols(i["L2_attn_W_x"], 4)
    o["s_w_dt"] = i["L2_attn_W_dt"]
    o["s_cw"] = i["L2_attn_conv_w"].reshape(4, 4, P).transpose(2, 1, 0)
    o["s_cb"] = i["L2_attn_conv_b"].reshape(4, P).T
    o["s_b_dt"] = i["L2_attn_b_dt"].reshape(4, P).T
    o["s_a"] = i["L2_attn_A_log"].reshape(4, P, 16).transpose(1, 2, 0)
    o["s_d"] = i["L2_attn_D"].reshape(4, P).T
    o["s_w_out"] = cols(i["L2_attn_W_out"], 4)


def top2_gates(nc, name, logits, gates, iota_dram, ident, E, capacity=None):
    with ExitStack() as stack:
        sb, ps = bufs(nc, stack)
        made = sems(nc, stack, " ".join(f"{name}_{k}" for k in "iota v max exp hot turned cum back m8 idx".split()))
        s = {k[len(name) + 1:]: x for k, x in made.items()}
        iota = sb(f"{name}_iotab", [TT, E])
        mx = sb(f"{name}_mx", [TT, NT])
        p = sb(f"{name}_p", [TT, NT, E])
        m8 = sb(f"{name}_m8b", [TT, NT, 8])
        idx = sb(f"{name}_idxb", [TT, NT, 8], U32)
        pick = sb(f"{name}_pick", [TT, NT, 2])
        hot = sb(f"{name}_hotb", [TT, NT, 2, E])
        hotT = sb(f"{name}_hotT", [2 * E, T])
        cum = sb(f"{name}_cumb", [2 * E, T])
        one = sb(f"{name}_one", [2 * E, T])
        pt = ps(f"{name}_pt", [P, NCH, BANK])
        pb = ps(f"{name}_pb", [P, BANK])
        block = stack.enter_context(nc.Block())

        @block.sync
        def _(sp):
            sp.dma_start(iota[:, :], iota_dram).then_inc(s["iota"], 16)

        @block.scalar
        def _(act):
            act.wait_ge(s["max"], 2)
            nc.scalar.activation(p[:, :, :], p[:, :, :], ACT.Exp).then_inc(s["exp"], 1)

        @block.tensor
        def _(pe):
            if capacity is not None:
                pe.wait_ge(s["hot"], 2)
                for g, (a, b) in enumerate(GROUPS):
                    for t in range(a, b):
                        last = nc.tensor.transpose(pt[0:2 * E, g, (t - a) * TT:(t - a + 1) * TT],
                                                   hot[:, t, :, :].rearrange("p k e -> p (k e)"), ident[0:TT, 0:TT])
                last.then_inc(s["turned"], 1)
                pe.wait_ge(s["cum"], 2)
                for t in range(NT):
                    last = nc.tensor.transpose(pb[0:TT, t * 2 * E:(t + 1) * 2 * E], cum[:, t * TT:(t + 1) * TT],
                                               ident[0:2 * E, 0:2 * E])
                last.then_inc(s["back"], 1)

        @block.vector
        def _(dve):
            link = chain(dve, s["v"])
            wide = [TT, NT, E]
            link(nc.vector.tensor_reduce(mx[:, :], logits[:, :, :], X, ALU.max))
            nc.vector.tensor_tensor(p[:, :, :], logits[:, :, :], mx[:, :].unsqueeze(2).broadcast_to(wide),
                                    ALU.subtract).then_inc(s["max"], 1)
            dve.wait_ge(s["exp"], 2)
            link(nc.vector.tensor_reduce(mx[:, :], p[:, :, :], X, ALU.add))
            link(nc.vector.reciprocal(mx[:, :], mx[:, :]))
            link(nc.vector.tensor_tensor(p[:, :, :], p[:, :, :], mx[:, :].unsqueeze(2).broadcast_to(wide), ALU.mult))
            for t in range(NT):
                last = nc.vector.max(m8[:, t, :], p[:, t, :])
            last.then_inc(s["m8"], 1)
            dve.wait_ge(s["m8"], 2)
            for t in range(NT):
                last = nc.vector.max_index(idx[:, t, :], m8[:, t, :], p[:, t, :])
            last.then_inc(s["idx"], 1)
            dve.wait_ge(s["idx"], 2)
            link(nc.vector.tensor_copy(pick[:, :, :], idx[:, :, 0:2]))
            dve.wait_ge(s["iota"], 17)
            for k in range(2):
                last = nc.vector.tensor_tensor(hot[:, :, k, :], pick[:, :, k:k + 1].broadcast_to(wide),
                                               iota[:, :].unsqueeze(1).broadcast_to(wide), ALU.is_equal)
            if capacity is None:
                link(last)
                link(nc.vector.tensor_tensor(mx[:, :].unsqueeze(2), m8[:, :, 0:1], m8[:, :, 1:2], ALU.add))
                link(nc.vector.reciprocal(mx[:, :], mx[:, :]))
                link(nc.vector.tensor_tensor(pick[:, :, :], m8[:, :, 0:2],
                                             mx[:, :].unsqueeze(2).broadcast_to([TT, NT, 2]), ALU.mult))
                w = pick
            else:
                last.then_inc(s["hot"], 1)
                link(nc.vector.memset(one[:, :], 1.0))
                dve.wait_ge(s["turned"], 2)
                for g, (a, b) in enumerate(GROUPS):
                    last = nc.vector.tensor_copy(hotT[:, a * TT:b * TT], pt[0:2 * E, g, 0:(b - a) * TT])
                link(last)
                link(nc.vector.tensor_tensor_scan(cum[:, :], one[:, :], hotT[:, :], 0.0, ALU.mult, ALU.add))
                nc.vector.scalar_tensor_tensor(cum[:, :], cum[:, :], float(capacity), hotT[:, :], ALU.is_le, ALU.mult
                                               ).then_inc(s["cum"], 1)
                dve.wait_ge(s["back"], 2)
                link(nc.vector.tensor_copy(hot[:, :, :, :].rearrange("p t k e -> p (t k e)"), pb[0:TT, 0:NT * 2 * E]))
                w = m8
            for k in range(2):
                last = nc.vector.tensor_tensor(hot[:, :, k, :], hot[:, :, k, :],
                                               w[:, :, k:k + 1].broadcast_to(wide), ALU.mult)
            link(last)
            link(nc.vector.tensor_tensor(gates[:, :, 0:E], hot[:, :, 0, :], hot[:, :, 1, :], ALU.add))
            if gates.shape[2] > E:
                link(nc.vector.memset(gates[:, :, E:], 1.0))


def stage_moe2(nc, d, h, xT, ident):
    E = 16
    capacity = max(1, math.ceil(B * S * 2 / E * 1.25))
    with ExitStack() as stack:
        sb, _ = bufs(nc, stack)
        norm_transpose(nc, "mn", h, xT, ident, 1e-5, True)
        logits = sb("m_logits", [TT, NT, E])
        gates = sb("m_gates", [TT, NT, E])
        projected(nc, "mp", xT, d["m_router"], E, d["m_zero"], logits)
        top2_gates(nc, "mt", logits, gates, d["m_iota"], ident, E, capacity)
        experts(nc, "m", d["m_w"], gates, xT, h, E, 2, 2, True)


def layout_moe2(i, o):
    o["m_router"] = cols(i["L2_ffn_router_w"], KC)
    o["m_zero"] = rep(np.zeros(16, np.float32))
    o["m_iota"] = rep(np.arange(16, dtype=np.float32))
    o["m_w"] = np.concatenate([up_cols(i[f"L2_ffn_{n}_w"]) for n in ("gate", "up", "down")], 2)


def stage_delta(nc, d, h, xT, ident):
    HK, HV, DK, K = 4, 8, 128, 4
    CV = 2 * HK + HV
    NB = (B + 1) // NCH
    SP = S + K - 1
    W2 = HK * TT
    with ExitStack() as stack:
        sb, ps = bufs(nc, stack)
        norm_transpose(nc, "dn", h, xT, ident, 1e-6, False, w_dram=d["d_ln1"], w_plus=1.0)
        ba = sb("d_ba", [TT, NT, 2 * HV])
        projected(nc, "dp", xT, d["d_w_ba"], 2 * HV, d["d_b_ba"], ba)
        mix = sb("d_mix", [P, CV, T])
        beta = sb("d_beta", [TT, NT, HV])
        g = sb("d_g", [TT, NT, HV])
        pT = sb("d_pT", [TT, NT, HV, TT])
        a_dram = nc.dram_tensor("d_a", (B + 1, HV, S, S), F32, kind="Internal").ap()
        t_dram = nc.dram_tensor("d_t", (B + 1, HV, S, S), F32, kind="Internal").ap()

        with ExitStack() as inner:
            sb2, ps2 = bufs(nc, inner)
            s = sems(nc, inner, "dc_in dc_edge dc_v dc_v2 dc_beta dc_e dc_ln dc_al "
                                + " ".join(f"dc_w{u} dc_mm{u} dc_x{u} dc_tap{u} dc_taps{u} dc_done{u}" for u in range(2)))
            v = s
            w = [sb2(f"dc_wb{u}", [P, KC * P]) for u in range(2)]
            cw = [sb2(f"dc_cw{u}", [P, K]) for u in range(2)]
            xp = [sb2(f"dc_xp{u}", [P, B + 1, SP]) for u in range(2)]
            acc = [sb2(f"dc_acc{u}", [P, B + 1, S]) for u in range(2)]
            al = sb2("dc_alb", [TT, HV])
            e = sb2("dc_eb", [TT, NT, HV])
            ln = sb2("dc_lnb", [TT, NT, HV])
            uu = sb2("dc_u", [TT, NT, HV])
            pp = [ps2(f"dc_pp{u}", [P, NCH, BANK]) for u in range(2)]
            block = inner.enter_context(nc.Block())

            @block.sync
            def _(sp):
                sp.dma_start(al[:, :], d["d_a_log"]).then_inc(s["dc_in"], 16)
                with sp.Fori(0, CV // 2) as i:
                    for u in range(2):
                        sp.wait_ge(v[f"dc_done{u}"], i + 1)
                        sp.dma_start(w[u][:, :], d["d_w_qkv"][bass.ds(2 * i + u, 1)].rearrange("a p n -> p (a n)")
                                     ).then_inc(v[f"dc_w{u}"], 16)
                        sp.dma_start(cw[u][:, :], d["d_cw"][bass.ds(2 * i + u, 1)].rearrange("a p n -> p (a n)")
                                     ).then_inc(v[f"dc_w{u}"], 16)

            @block.tensor
            def _(pe):
                with pe.Fori(0, CV // 2) as i:
                    for u in range(2):
                        pe.wait_ge(v[f"dc_w{u}"], i * 32 + 33)
                        pe.wait_ge(v[f"dc_x{u}"], i + 1)
                        for t in range(NCH):
                            for k in range(KC):
                                last = nc.tensor.matmul(pp[u][:, t, 0:CH], w[u][:, k * P:(k + 1) * P],
                                                        xT[:, k, t * CH:(t + 1) * CH], start=(k == 0),
                                                        stop=(k == KC - 1))
                        last.then_inc(v[f"dc_mm{u}"], 1)

            @block.scalar
            def _(act):
                act.wait_ge(s["dc_in"], 17)
                nc.scalar.activation(al[:, :], al[:, :], ACT.Exp).then_inc(s["dc_al"], 1)
                nc.scalar.activation(e[:, :, :], ba[:, :, HV:], ACT.Abs).then_inc(s["dc_e"], 1)
                act.wait_ge(s["dc_e"], 2)
                nc.scalar.activation(e[:, :, :], e[:, :, :], ACT.Exp, scale=-1.0).then_inc(s["dc_e"], 1)
                act.wait_ge(s["dc_e"], 3)
                nc.scalar.activation(ln[:, :, :], e[:, :, :], ACT.Ln, bias=1.0).then_inc(s["dc_ln"], 1)
                nc.scalar.activation(beta[:, :, :], ba[:, :, 0:HV], ACT.Sigmoid).then_inc(s["dc_beta"], 1)
                act.wait_ge(s["dc_edge"], 3)
                with act.Fori(0, CV // 2) as i:
                    for u in range(2):
                        act.wait_ge(v[f"dc_mm{u}"], i + 2)
                        act.wait_ge(v[f"dc_done{u}"], i + 1)
                        nc.scalar.activation(xp[u][:, :, K - 1:SP].rearrange("p (t b) j -> p t b j", t=NCH),
                                             pp[u][:, :, 0:CH].rearrange("p t (b j) -> p t b j", j=S), ACT.Copy
                                             ).then_inc(v[f"dc_x{u}"], 1)
                        act.wait_ge(v[f"dc_x{u}"], i + 2)
                        act.wait_ge(v[f"dc_w{u}"], i * 32 + 33)
                        nc.scalar.activation(acc[u][:, :, :], xp[u][:, :, 0:S], ACT.Copy, scale=cw[u][:, 0:1]
                                             ).then_inc(v[f"dc_tap{u}"], 1)
                    for u in range(2):
                        act.wait_ge(v[f"dc_taps{u}"], i + 2)
                        nc.scalar.activation(flat2(mix[:, bass.ds(2 * i + u, 1), :]), flat2(acc[u][:, :, :]), ACT.Silu
                                             ).then_inc(v[f"dc_done{u}"], 1)

            @block.gpsimd
            def _(pool):
                for u in range(2):
                    nc.gpsimd.memset(xp[u][:, :, :], 0.0).then_inc(s["dc_edge"], 1)

            @block.vector
            def _(dve):
                link = chain(dve, s["dc_v"])
                dve.wait_ge(s["dc_ln"], 2)
                dve.wait_ge(s["dc_al"], 2)
                link(nc.vector.tensor_scalar(uu[:, :, :], e[:, :, :], 1.0, None, ALU.add))
                link(nc.vector.scalar_tensor_tensor(uu[:, :, :], uu[:, :, :], -1.0, e[:, :, :], ALU.add, ALU.subtract))
                link(nc.vector.tensor_tensor(ln[:, :, :], ln[:, :, :], uu[:, :, :], ALU.subtract))
                link(nc.vector.scalar_tensor_tensor(ln[:, :, :], ba[:, :, HV:], 0.0, ln[:, :, :], ALU.max, ALU.add))
                link(nc.vector.tensor_tensor(g[:, :, :], ln[:, :, :],
                                             al[:, :].unsqueeze(1).broadcast_to([TT, NT, HV]), ALU.mult))
                link(nc.vector.tensor_scalar(g[:, :, :], g[:, :, :], -1.0, None, ALU.mult))
                with dve.Fori(0, CV // 2) as i:
                    link2 = chain(dve, s["dc_v2"], 4 * i)
                    for u in range(2):
                        dve.wait_ge(v[f"dc_tap{u}"], i + 2)
                        for k in range(1, K):
                            ins = nc.vector.scalar_tensor_tensor(acc[u][:, :, :], xp[u][:, :, k:k + S],
                                                                 cw[u][:, k:k + 1], acc[u][:, :, :], ALU.mult, ALU.add)
                            link2(ins) if k < K - 1 else ins.then_inc(v[f"dc_taps{u}"], 1)

        with ExitStack() as inner:
            sb2, ps2 = bufs(nc, inner)
            s = sems(nc, inner, "dl_in dl_sq dl_sum dl_ss dl_half dl_r dl_bc_mm dl_bc dl_v")
            sel = sb2("dl_sel", [P, 8, 8])
            spread = sb2("dl_spread", [8, 8, P])
            sq = sb2("dl_sqb", [P, 8, T])
            ss = sb2("dl_ssb", [8, T])
            half = sb2("dl_halfb", [8, T])
            pp = ps2("dl_pp", [P, 3, BANK])
            pb = ps2("dl_pb", [P, 4, BANK])
            block = inner.enter_context(nc.Block())

            @block.sync
            def _(sp):
                sp.dma_start(sel[:, :, :], d["d_sel"]).then_inc(s["dl_in"], 16)
                sp.dma_start(spread[:, :, :], d["d_spread"]).then_inc(s["dl_in"], 16)

            @block.scalar
            def _(act):
                for c in range(8):
                    nc.scalar.activation(sq[:, c, :], mix[:, c, :], ACT.Square).then_inc(s["dl_sq"], 1)

            @block.gpsimd
            def _(pool):
                pool.wait_ge(s["dl_ss"], 2)
                nc.gpsimd.tensor_tensor(ss[:, :], ss[:, :], half[:, :], ALU.pow).then_inc(s["dl_r"], 1)

            @block.tensor
            def _(pe):
                pe.wait_ge(s["dl_in"], 33)
                pe.wait_ge(s["dl_sq"], 9)
                for t in range(NCH):
                    for c in range(8):
                        last = nc.tensor.matmul(pp[0:8, t, 0:CH], sel[:, c, :], sq[:, c, t * CH:(t + 1) * CH],
                                                start=(c == 0), stop=(c == 7))
                last.then_inc(s["dl_sum"], 1)
                pe.wait_ge(s["dl_r"], 2)
                for n in range(8 * NCH):
                    c, t = divmod(n, NCH)
                    if n >= 4:
                        pe.wait_ge(s["dl_bc"], n - 2)
                    nc.tensor.matmul(pb[:, n % 4, 0:CH], spread[:, c, :], ss[:, t * CH:(t + 1) * CH], start=True,
                                     stop=True).then_inc(s["dl_bc_mm"], 1)

            @block.vector
            def _(dve):
                nc.vector.memset(half[:, :], -0.5)
                dve.wait_ge(s["dl_sum"], 2)
                for t in range(NCH):
                    last = nc.vector.tensor_scalar(ss[:, t * CH:(t + 1) * CH], pp[0:8, t, 0:CH], 1e-6, None, ALU.add)
                last.then_inc(s["dl_ss"], 1)
                for n in range(8 * NCH):
                    c, t = divmod(n, NCH)
                    dve.wait_ge(s["dl_bc_mm"], n + 2)
                    at = mix[:, c, t * CH:(t + 1) * CH]
                    nc.vector.tensor_tensor(at, at, pb[:, n % 4, 0:CH], ALU.mult).then_inc(s["dl_bc"], 1)

        with ExitStack() as inner:
            sb2, ps2 = bufs(nc, inner)
            s = sems(nc, inner, "da_in da_gm da_ks da_dec_mm da_kk_mm da_exp da_mask da_a da_v da_out da_p")
            m = sb2("da_masks", [TT, 3, TT])
            gm = sb2("da_gmb", [TT, 2, HV, TT])
            ks = sb2("da_ksb", [P, HK, TT])
            ex = sb2("da_ex", [TT, 2, HV, TT])
            am = sb2("da_am", [TT, HV, TT])
            pd = ps2("da_pd", [P, 4, BANK])
            pk = ps2("da_pk", [P, 2, BANK])
            block = inner.enter_context(nc.Block())
            wide = [TT, HV, TT]

            @block.sync
            def _(sp):
                sp.dma_start(m[:, :, :], d["d_masks"]).then_inc(s["da_in"], 16)
                with sp.Fori(0, NT) as i:
                    sp.wait_ge(s["da_a"], i + 2)
                    for q in range(G):
                        at = slice(q * S, (q + 1) * S)
                        sp.dma_start(a_dram[bass.ds(i * G + q, 1)].rearrange("b h i j -> i (b h) j"), am[at, :, at]
                                     ).then_inc(s["da_out"], 16)
                sp.wait_ge(s["da_out"], NT * G * 16 + 1)

            @block.gpsimd
            def _(pool):
                pool.wait_ge(s["da_in"], 17)
                with pool.Fori(0, NT) as i:
                    pool.wait_ge(s["da_dec_mm"], i + 1)
                    gt = flat2(g[:, bass.ds(i, 1), :]).unsqueeze(2).broadcast_to(wide)
                    for n in range(2):
                        last = nc.gpsimd.tensor_tensor(gm[:, n, :, :], gt, m[:, n:n + 1, :].broadcast_to(wide),
                                                       ALU.mult)
                    last.then_inc(s["da_gm"], 1)
                    pool.wait_ge(s["da_exp"], i + 2)
                    nc.gpsimd.tensor_tensor(ex[:, 0, :, :], ex[:, 0, :, :], m[:, 0:1, :].broadcast_to(wide), ALU.mult)
                    nc.gpsimd.tensor_tensor(ex[:, 1, :, :], ex[:, 1, :, :], m[:, 1:2, :].broadcast_to(wide), ALU.mult
                                            ).then_inc(s["da_mask"], 1)

            @block.tensor
            def _(pe):
                pe.wait_ge(s["da_in"], 17)
                with pe.Fori(0, NT) as i:
                    pe.wait_ge(s["da_gm"], i + 2)
                    pe.wait_ge(s["da_exp"], i + 1)
                    for n in range(2):
                        for o in range(2):
                            last = nc.tensor.matmul(pd[0:TT, 2 * n + o, 0:W2], m[:, 1 - n, :],
                                                    flat2(gm[:, n, o * HK:(o + 1) * HK, :]), start=True, stop=True)
                    last.then_inc(s["da_dec_mm"], 1)
                    pe.wait_ge(s["da_ks"], i + 2)
                    pe.wait_ge(s["da_p"], i + 1)
                    for n in range(2):
                        for c in range(HK):
                            src = mix[:, n * HK + c, bass.ds(i * TT, TT)]
                            last = nc.tensor.matmul(pk[0:TT, n, c * TT:(c + 1) * TT], ks[:, c, :], src, start=True,
                                                    stop=True)
                    last.then_inc(s["da_kk_mm"], 1)

            @block.scalar
            def _(act):
                with act.Fori(0, NT) as i:
                    act.wait_ge(s["da_kk_mm"], i + 1)
                    nc.scalar.activation(ks[:, :, :], mix[:, HK:2 * HK, bass.ds(i * TT, TT)], ACT.Copy
                                         ).then_inc(s["da_ks"], 1)
                    act.wait_ge(s["da_dec_mm"], i + 2)
                    act.wait_ge(s["da_p"], i + 1)
                    for n in range(2):
                        last = nc.scalar.activation(ex[:, n, :, :].rearrange("p (o h) x -> p o (h x)", o=2),
                                                    pd[0:TT, 2 * n:2 * n + 2, 0:W2], ACT.Exp)
                    last.then_inc(s["da_exp"], 1)

            @block.vector
            def _(dve):
                with dve.Fori(0, NT) as i:
                    link = chain(dve, s["da_v"], 2 * i)
                    dve.wait_ge(s["da_mask"], i + 2)
                    dve.wait_ge(s["da_kk_mm"], i + 2)
                    dve.wait_ge(s["da_out"], i * G * 16 + 1)
                    rep2 = [TT, HK, 2, TT]
                    kk = [pk[0:TT, n, 0:W2].rearrange("p (c x) -> p c x", x=TT).unsqueeze(2).broadcast_to(rep2)
                          for n in range(2)]
                    link(nc.vector.tensor_tensor(am[:, :, :].rearrange("p (c r) x -> p c r x", r=2),
                                                 ex[:, 1, :, :].rearrange("p (c r) x -> p c r x", r=2), kk[1], ALU.mult))
                    nc.vector.tensor_tensor(am[:, :, :], am[:, :, :],
                                            flat2(beta[:, bass.ds(i, 1), :]).unsqueeze(2).broadcast_to(wide), ALU.mult
                                            ).then_inc(s["da_a"], 1)
                    link(nc.vector.tensor_tensor(pT[:, bass.ds(i, 1), :, :].rearrange("p a (c r) x -> p (a c) r x", r=2),
                                                 ex[:, 0, :, :].rearrange("p (c r) x -> p c r x", r=2), kk[0],
                                                 ALU.mult))
                    nc.vector.nop().then_inc(s["da_p"], 1)

        with ExitStack() as inner:
            sb2, ps2 = bufs(nc, inner)
            s = sems(nc, inner, "di_in di_zero di_v di_out")
            NG = B * HV // P
            a = sb2("di_a", [P, NG, S, S])
            tT = sb2("di_tT", [P, NG, S, S])
            pr = sb2("di_pr", [P, NG * S * S])
            block = inner.enter_context(nc.Block())
            split = [x[0:B].rearrange("b h i j -> (b h) (i j)").rearrange("(g p) n -> p g n", g=NG)
                     for x in (a_dram, t_dram)]

            @block.sync
            def _(sp):
                sp.dma_start(a[:, :, :, :].rearrange("p g i j -> p g (i j)"), split[0]).then_inc(s["di_in"], 16)
                sp.wait_ge(s["di_v"], 2 * S)
                sp.dma_start(split[1], tT[:, :, :, :].rearrange("p g i j -> p g (i j)")).then_inc(s["di_out"], 16)
                sp.dma_start(t_dram[B:B + 1].rearrange("b h i j -> (b h) (i j)"),
                             tT[0:HV, 0, :, :].rearrange("p i j -> p (i j)")).then_inc(s["di_out"], 16)
                sp.wait_ge(s["di_out"], 33)

            @block.gpsimd
            def _(pool):
                nc.gpsimd.memset(tT[:, :, :, :], 0.0).then_inc(s["di_zero"], 1)

            @block.vector
            def _(dve):
                link = chain(dve, s["di_v"])
                dve.wait_ge(s["di_zero"], 2)
                link(nc.vector.memset(tT[:, :, :, :].rearrange("p g i j -> p g (i j)")[:, :, 0:S * S:S + 1], 1.0))
                dve.wait_ge(s["di_in"], 17)
                for i in range(1, S):
                    one = pr[:, 0:NG * i * i].rearrange("p (g c j) -> p g c j", g=NG, c=i)
                    link(nc.vector.tensor_tensor(one, tT[:, :, 0:i, 0:i],
                                                 a[:, :, i:i + 1, 0:i].broadcast_to([P, NG, i, i]), ALU.mult))
                    link(nc.vector.tensor_reduce(tT[:, :, 0:i, i:i + 1].rearrange("p g c a -> p g (c a)"), one, X,
                                                 ALU.add, negate=True))

        with ExitStack() as inner:
            sb2, ps2 = bufs(nc, inner)
            s = sems(nc, inner, "do_in do_zero do_t do_vs do_ps do_xs do_v_mm do_vb do_u_mm do_u do_o_mm do_z_mm "
                                "do_sq do_ms do_r do_z do_core do_c_mm do_c do_out_mm do_h do_v do_half")
            wz = sb2("do_wz", [P, KC, HV * DK])
            wo = sb2("do_wo", [P, HV, D])
            gw = sb2("do_gw", [TT, DK])
            tm = sb2("do_tm", [TT, HV, TT])
            vs = sb2("do_vsb", [P, HV, TT])
            pm = sb2("do_pm", [TT, HV, TT])
            xs = sb2("do_xsb", [P, KC, TT])
            vb = sb2("do_vbb", [TT, HV, DK])
            ub = sb2("do_ub", [TT, HV, DK])
            sq = sb2("do_sqb", [TT, HV, DK])
            ms = sb2("do_msb", [TT, HV])
            half = sb2("do_halfb", [TT, HV])
            zs = sb2("do_zs", [TT, HV, DK])
            cT = sb2("do_cT", [P, HV, TT])
            pv, pu, po, pz = (ps2(f"do_p{n}", [P, 2, BANK]) for n in "vuoz")
            block = inner.enter_context(nc.Block())
            wide = [TT, HV, DK]

            def heads(p):
                return p[0:TT, :, :].rearrange("p o (h x) -> p (o h) x", x=DK)

            @block.sync
            def _(sp):
                sp.dma_start(wz[:, :, :], d["d_w_z"]).then_inc(s["do_in"], 16)
                sp.dma_start(wo[:, :, :], d["d_w_out"]).then_inc(s["do_in"], 16)
                sp.dma_start(gw[:, :], d["d_gw"]).then_inc(s["do_in"], 16)
                sp.wait_ge(s["do_zero"], 2)
                with sp.Fori(0, NT) as i:
                    sp.wait_ge(s["do_u_mm"], i + 1)
                    for q in range(G):
                        at = slice(q * S, (q + 1) * S)
                        sp.dma_start(tm[at, :, at], t_dram[bass.ds(i * G + q, 1)].rearrange("b h i j -> i (b h) j")
                                     ).then_inc(s["do_t"], 16)

            @block.gpsimd
            def _(pool):
                nc.gpsimd.memset(tm[:, :, :], 0.0).then_inc(s["do_zero"], 1)
                pool.wait_ge(s["do_half"], 2)
                with pool.Fori(0, NT) as i:
                    pool.wait_ge(s["do_v_mm"], i + 1)
                    nc.gpsimd.tensor_copy(vs[:, :, :], mix[:, 2 * HK:CV, bass.ds(i * TT, TT)]).then_inc(s["do_vs"], 1)
                    pool.wait_ge(s["do_z_mm"], i + 1)
                    nc.gpsimd.tensor_copy(xs[:, :, :], xT[:, :, bass.ds(i * TT, TT)]).then_inc(s["do_xs"], 1)
                    pool.wait_ge(s["do_o_mm"], i + 1)
                    nc.gpsimd.tensor_copy(pm[:, :, :], pT[:, bass.ds(i, 1), :, :].rearrange("p a h x -> p (a h) x")
                                          ).then_inc(s["do_ps"], 1)
                    pool.wait_ge(s["do_ms"], i + 2)
                    nc.gpsimd.tensor_tensor(ms[:, :], ms[:, :], half[:, :], ALU.pow).then_inc(s["do_r"], 1)

            @block.tensor
            def _(pe):
                pe.wait_ge(s["do_in"], 49)
                with pe.Fori(0, NT) as i:
                    pe.wait_ge(s["do_vs"], i + 2)
                    pe.wait_ge(s["do_c"], i + 1)
                    for c in range(HV):
                        last = nc.tensor.transpose(pv[0:TT, c // 4, (c % 4) * DK:(c % 4 + 1) * DK], vs[:, c, :],
                                                   ident[:, :])
                    last.then_inc(s["do_v_mm"], 1)
                    pe.wait_ge(s["do_xs"], i + 2)
                    pe.wait_ge(s["do_z"], i + 1)
                    for o in range(2):
                        for k in range(KC):
                            last = nc.tensor.matmul(pz[0:TT, o, :], xs[:, k, :], wz[:, k, o * BANK:(o + 1) * BANK],
                                                    start=(k == 0), stop=(k == KC - 1))
                    last.then_inc(s["do_z_mm"], 1)
                    pe.wait_ge(s["do_vb"], i + 2)
                    pe.wait_ge(s["do_t"], (i + 1) * G * 16 + 1)
                    pe.wait_ge(s["do_h"], i + 1)
                    for c in range(HV):
                        last = nc.tensor.matmul(pu[0:TT, c // 4, (c % 4) * DK:(c % 4 + 1) * DK], tm[:, c, :],
                                                vb[:, c, :], start=True, stop=True)
                    last.then_inc(s["do_u_mm"], 1)
                    pe.wait_ge(s["do_u"], i + 2)
                    pe.wait_ge(s["do_ps"], i + 2)
                    for c in range(HV):
                        last = nc.tensor.matmul(po[0:TT, c // 4, (c % 4) * DK:(c % 4 + 1) * DK], pm[:, c, :],
                                                ub[:, c, :], start=True, stop=True)
                    last.then_inc(s["do_o_mm"], 1)
                    pe.wait_ge(s["do_core"], i + 2)
                    for c in range(HV):
                        last = nc.tensor.transpose(pv[:, c // 4, (c % 4) * TT:(c % 4 + 1) * TT], zs[:, c, :],
                                                   ident[0:TT, 0:TT])
                    last.then_inc(s["do_c_mm"], 1)
                    pe.wait_ge(s["do_c"], i + 2)
                    for c in range(HV):
                        last = nc.tensor.matmul(pu[0:TT, 0, 0:D], cT[:, c, :], wo[:, c, :], start=(c == 0),
                                                stop=(c == HV - 1))
                    last.then_inc(s["do_out_mm"], 1)

            @block.scalar
            def _(act):
                with act.Fori(0, NT) as i:
                    act.wait_ge(s["do_z_mm"], i + 2)
                    act.wait_ge(s["do_c_mm"], i + 1)
                    nc.scalar.activation(zs[:, :, :], heads(pz), ACT.Silu).then_inc(s["do_z"], 1)
                    act.wait_ge(s["do_u_mm"], i + 2)
                    nc.scalar.activation(ub[:, :, :], heads(pu), ACT.Copy).then_inc(s["do_u"], 1)
                    act.wait_ge(s["do_o_mm"], i + 2)
                    nc.scalar.activation(sq[:, :, :], heads(po), ACT.Square).then_inc(s["do_sq"], 1)
                    act.wait_ge(s["do_c_mm"], i + 2)
                    nc.scalar.activation(cT[:, :, :].rearrange("p (o h) x -> p o (h x)", o=2), pv[:, :, 0:W2], ACT.Copy
                                         ).then_inc(s["do_c"], 1)

            @block.vector
            def _(dve):
                dve.wait_ge(s["do_in"], 49)
                nc.vector.memset(half[:, :], -0.5).then_inc(s["do_half"], 1)
                with dve.Fori(0, NT) as i:
                    link = chain(dve, s["do_v"], 4 * i)
                    dve.wait_ge(s["do_v_mm"], i + 2)
                    nc.vector.tensor_tensor(vb[:, :, :], heads(pv),
                                            flat2(beta[:, bass.ds(i, 1), :]).unsqueeze(2).broadcast_to(wide), ALU.mult
                                            ).then_inc(s["do_vb"], 1)
                    dve.wait_ge(s["do_z"], i + 2)
                    link(nc.vector.tensor_tensor(zs[:, :, :], zs[:, :, :],
                                                 gw[:, :].unsqueeze(1).broadcast_to(wide), ALU.mult))
                    dve.wait_ge(s["do_sq"], i + 2)
                    link(nc.vector.tensor_reduce(ms[:, :], sq[:, :, :], X, ALU.add))
                    nc.vector.tensor_scalar(ms[:, :], ms[:, :], 1.0 / DK, 1e-6, ALU.mult, ALU.add).then_inc(s["do_ms"], 1)
                    link(nc.vector.tensor_tensor(zs[:, :, :], zs[:, :, :], heads(po), ALU.mult))
                    dve.wait_ge(s["do_r"], i + 2)
                    nc.vector.tensor_tensor(zs[:, :, :], zs[:, :, :], ms[:, :].unsqueeze(2).broadcast_to(wide), ALU.mult
                                            ).then_inc(s["do_core"], 1)
                    dve.wait_ge(s["do_out_mm"], i + 2)
                    ht = flat2(h[:, bass.ds(i, 1), :])
                    nc.vector.tensor_tensor(ht, ht, pu[0:TT, 0, 0:D], ALU.add).then_inc(s["do_h"], 1)
                    link(nc.vector.nop())


def stage_moe3(nc, d, h, xT, ident):
    with ExitStack() as stack:
        sb, ps = bufs(nc, stack)
        E = 8
        norm_transpose(nc, "dm", h, xT, ident, 1e-6, False, w_dram=d["d_ln2"], w_plus=1.0)
        logits = sb("d_logits", [TT, NT, E])
        gates = sb("d_gates", [TT, NT, E])
        projected(nc, "dr", xT, d["d_router"], E, d["m_zero"][:, 0:E], logits)
        top2_gates(nc, "dt", logits, gates, d["m_iota"][:, 0:E], ident, E)
        experts(nc, "de", d["d_w_e"], gates, xT, h, E, 2, 1, True)


def layout_delta(i, o):
    f = np.float32
    o["d_ln1"] = i["L3_attn_w_ln1"].reshape(KC, P).T
    o["d_ln2"] = i["L3_attn_w_ln2"].reshape(KC, P).T
    o["d_w_ba"] = cols(i["L3_attn_W_ba"], KC)
    o["d_b_ba"] = rep(np.concatenate([np.zeros(8, f), i["L3_attn_dt_bias"]]))
    w = i["L3_attn_W_qkvz"]
    o["d_w_qkv"] = w[:, :2048].reshape(KC, P, 16, P).transpose(2, 1, 0, 3).reshape(16, P, KC * P)
    o["d_w_z"] = cols(w[:, 2048:], KC)
    o["d_cw"] = i["L3_attn_conv_w"].reshape(16, P, 4)
    o["d_a_log"] = rep(i["L3_attn_A_log"])
    eye = np.eye(8, dtype=f)
    o["d_sel"] = np.broadcast_to(eye, (P, 8, 8))
    scale = np.where(np.arange(8) < 4, P ** -0.5, 1.0)
    o["d_spread"] = np.broadcast_to((eye * scale[None]).astype(f)[:, :, None], (8, 8, P))
    a = np.arange(TT)[:, None]
    b = np.arange(TT)[None, :]
    same = a // S == b // S
    o["d_masks"] = np.stack([same & (a <= b), same & (a > b), same & (a < b)], 1).astype(f)
    o["d_w_out"] = cols(i["L3_attn_W_out"], 8)
    o["d_gw"] = rep(i["L3_attn_gate_norm_w"])
    o["d_router"] = cols(i["L3_attn_W_router"], KC)
    o["d_w_e"] = np.concatenate([up_cols(i[f"L3_attn_W_{n}_e"]) for n in ("gate", "up", "down")], 2)


def stage_mla(nc, d, h, xT, ident):
    H, HD, NOPE = 16, 64, 32
    C = H * HD // P
    PG = (H + G - 1) // G
    GN = G * NOPE
    with ExitStack() as stack:
        sb, ps = bufs(nc, stack)
        norm_transpose(nc, "ln", h, xT, ident, 1e-5, False, w_dram=d["l_ln1"])
        q = sb("l_q", [P, C, T])
        kT = sb("l_kT", [P, C, T])
        ckv = sb("l_ckv", [HD, T])
        seqs = [P, T // S, S]

        with ExitStack() as inner:
            sb2, ps2 = bufs(nc, inner)
            s = sems(nc, inner, "lp_in lp_mm lp_raw lp_sw_mm lp_rot lp_v lp_k_mm lp_k lp_done")
            wq = sb2("lp_wq", [P, KC, H * HD])
            wkva = sb2("lp_wkva", [P, KC, HD])
            wk = sb2("lp_wk", [HD, H * HD])
            perm = sb2("lp_perm", [P, P])
            tab = sb2("lp_tab", [P, 2, S])
            raw = [sb2(f"lp_raw{n}", [P, T]) for n in range(2)]
            sw = sb2("lp_sw", [P, T])
            pp = ps2("lp_pp", [P, NCH, BANK])
            pw = ps2("lp_pw", [P, NCH, BANK])
            block = inner.enter_context(nc.Block())
            jobs = [(wkva, HD, 0, ckv)] + [(wq, P, c * P, q[:, c, :]) for c in range(C)]

            @block.sync
            def _(sp):
                for dst, src in ((wq[:, :, :], "l_wq"), (wkva[:, :, :], "l_wkva"), (wk[:, :], "l_wk"),
                                 (perm[:, :], "l_perm"), (tab[:, :, :], "l_tab")):
                    sp.dma_start(dst, d[src]).then_inc(s["lp_in"], 16)

            @block.tensor
            def _(pe):
                pe.wait_ge(s["lp_in"], 81)

                def swap(n):
                    m = jobs[n][1]
                    pe.wait_ge(s["lp_raw"], n + 2)
                    if n:
                        pe.wait_ge(s["lp_rot"], n + 1)
                    for t in range(NCH):
                        last = nc.tensor.matmul(pw[0:m, t, 0:CH], perm[0:m, 0:m], raw[n % 2][0:m, t * CH:(t + 1) * CH],
                                                start=True, stop=True)
                    last.then_inc(s["lp_sw_mm"], 1)

                for n, (w, m, at, _) in enumerate(jobs):
                    if n:
                        pe.wait_ge(s["lp_raw"], n + 1)
                    for t in range(NCH):
                        for k in range(KC):
                            last = nc.tensor.matmul(pp[0:m, t, 0:CH], w[:, k, at:at + m],
                                                    xT[:, k, t * CH:(t + 1) * CH], start=(k == 0), stop=(k == KC - 1))
                    last.then_inc(s["lp_mm"], 1)
                    if n:
                        swap(n - 1)
                swap(len(jobs) - 1)
                pe.wait_ge(s["lp_rot"], len(jobs) + 1)
                for c in range(C):
                    if c >= 2:
                        pe.wait_ge(s["lp_k"], c)
                    for t in range(NCH):
                        last = nc.tensor.matmul((pp, pw)[c % 2][:, t, 0:CH], wk[:, c * P:(c + 1) * P],
                                                ckv[:, t * CH:(t + 1) * CH], start=True, stop=True)
                    last.then_inc(s["lp_k_mm"], 1)

            @block.scalar
            def _(act):
                for n, (_, m, _, _) in enumerate(jobs):
                    act.wait_ge(s["lp_mm"], n + 2)
                    if n >= 2:
                        act.wait_ge(s["lp_rot"], n)
                    nc.scalar.activation(raw[n % 2][0:m, :].rearrange("p (t n) -> p t n", t=NCH), pp[0:m, :, 0:CH],
                                         ACT.Copy).then_inc(s["lp_raw"], 1)
                for c in range(C):
                    act.wait_ge(s["lp_k_mm"], c + 2)
                    nc.scalar.activation(kT[:, c, :].rearrange("p (t n) -> p t n", t=NCH),
                                         (pp, pw)[c % 2][:, :, 0:CH], ACT.Copy).then_inc(s["lp_k"], 1)

            @block.vector
            def _(dve):
                link = chain(dve, s["lp_v"])
                dve.wait_ge(s["lp_in"], 81)
                for n, (_, m, _, dst) in enumerate(jobs):
                    one = dst if n else dst[:, :]
                    fac = [tab[0:m, k:k + 1, :].broadcast_to([m, T // S, S]) for k in range(2)]
                    dve.wait_ge(s["lp_sw_mm"], n + 2)
                    link(nc.vector.tensor_tensor(one.rearrange("p (b j) -> p b j", j=S),
                                                 raw[n % 2][0:m, :].rearrange("p (b j) -> p b j", j=S), fac[0],
                                                 ALU.mult))
                    for t in range(NCH):
                        last = nc.vector.tensor_tensor(
                            sw[0:m, t * CH:(t + 1) * CH].rearrange("p (b j) -> p b j", j=S),
                            pw[0:m, t, 0:CH].rearrange("p (b j) -> p b j", j=S), fac[1][:, 0:T // S // NCH, :],
                            ALU.mult)
                    link(last)
                    nc.vector.tensor_tensor(one, one, sw[0:m, :], ALU.add).then_inc(s["lp_rot"], 1)
                    dve.wait_ge(s["lp_rot"], n + 2)

        with ExitStack() as inner:
            sb2, ps2 = bufs(nc, inner)
            s = sems(nc, inner, "la_in la_zero la_qm la_kx la_lat la_s_mm la_max la_exp la_probs la_v_mm la_vexp "
                                "la_turned la_pT la_pv la_oT la_out_mm la_h la_v la_cp")
            wv = sb2("la_wv", [NOPE, H * NOPE])
            wo = sb2("la_wo", [GN, PG, D])
            vmask = sb2("la_vmask", [TT, H * NOPE])
            neg = sb2("la_neg", [TT, S])
            qm = sb2("la_qmb", [P, C, G * TT])
            kx = sb2("la_kxb", [P, C, 2, TT])
            lat = sb2("la_latb", [NOPE, G, G, S])
            sc = sb2("la_sc", [TT, H, S])
            e = sb2("la_e", [TT, H, S])
            mx = sb2("la_mx", [TT, H])
            pT = sb2("la_pTb", [TT, PG, TT])
            vexp = sb2("la_vexpb", [TT, G, H * NOPE])
            oT = sb2("la_oTb", [GN, PG, TT])
            psS = ps2("la_psS", [P, 2, BANK])
            psT = ps2("la_psT", [P, 2, BANK])
            psV = ps2("la_psV", [P, G, BANK])
            psO = ps2("la_psO", [P, BANK])
            block = inner.enter_context(nc.Block())
            W = C // 2 * 2 * S

            @block.sync
            def _(sp):
                for dst, src in ((wv[:, :], "l_wv"), (wo[:, :, :], "l_wo"), (vmask[:, :], "l_vmask"),
                                 (neg[:, :], "l_neg")):
                    sp.dma_start(dst, d[src]).then_inc(s["la_in"], 16)

            @block.gpsimd
            def _(pool):
                nc.gpsimd.memset(qm[:, :, :], 0.0)
                nc.gpsimd.memset(kx[:, :, :, :], 0.0).then_inc(s["la_zero"], 1)
                pool.wait_ge(s["la_zero"], 2)
                with pool.Fori(0, NT) as i:
                    pool.wait_ge(s["la_s_mm"], i + 1)
                    for n in range(G):
                        last = nc.gpsimd.tensor_copy(qm[:, :, n * (TT + S):n * (TT + S) + S],
                                                     q[:, :, bass.ds(i * TT + n * S, S)])
                    last.then_inc(s["la_qm"], 1)
                    pool.wait_ge(s["la_v_mm"], i + 1)
                    for n in range(G):
                        last = nc.gpsimd.tensor_copy(lat[:, n, :, :], ckv[0:NOPE, bass.ds(i * TT + n * S, S)]
                                                     .unsqueeze(1).broadcast_to([NOPE, G, S]))
                    last.then_inc(s["la_lat"], 1)

            @block.scalar
            def _(act):
                act.wait_ge(s["la_zero"], 2)
                with act.Fori(0, NT) as i:
                    act.wait_ge(s["la_s_mm"], i + 1)
                    for n in range(2):
                        at = slice(n * HD, (n + 1) * HD)
                        last = nc.scalar.activation(kx[at, :, n, :], kT[at, :, bass.ds(i * TT, TT)], ACT.Copy)
                    last.then_inc(s["la_kx"], 1)
                    act.wait_ge(s["la_max"], i + 2)
                    nc.scalar.activation(e[:, :, :], sc[:, :, :], ACT.Exp, scale=HD ** -0.5).then_inc(s["la_exp"], 1)
                    act.wait_ge(s["la_turned"], i + 2)
                    nc.scalar.activation(pT[:, 0:4, :].rearrange("p g t -> p (g t)"), psT[0:TT, 0, 0:4 * TT], ACT.Copy)
                    nc.scalar.activation(pT[:, 4, :], psT[0:TT, 1, 0:TT], ACT.Copy)
                    nc.scalar.activation(pT[0:S, 5, :], psT[0:S, 1, TT:2 * TT], ACT.Copy).then_inc(s["la_pT"], 1)
                    act.wait_ge(s["la_pv"], i + 2)
                    nc.scalar.activation(oT[:, 0:4, :].rearrange("p g t -> p (g t)"), psT[0:GN, 0, 0:4 * TT], ACT.Copy)
                    nc.scalar.activation(oT[:, 4, :], psT[0:GN, 1, 0:TT], ACT.Copy)
                    nc.scalar.activation(oT[0:NOPE, 5, :], psT[0:NOPE, 1, TT:2 * TT], ACT.Copy).then_inc(s["la_oT"], 1)

            @block.tensor
            def _(pe):
                pe.wait_ge(s["la_in"], 65)
                with pe.Fori(0, NT) as i:
                    pe.wait_ge(s["la_qm"], i + 2)
                    pe.wait_ge(s["la_kx"], i + 2)
                    pe.wait_ge(s["la_probs"], i + 1)
                    for c in range(C):
                        o = (c % 4) * 2 * S
                        for n in range(G):
                            last = nc.tensor.matmul(psS[0:TT, c // 4, o:o + 2 * S], qm[:, c, n * TT:(n + 1) * TT],
                                                    kx[:, c, :, n * S:(n + 1) * S], start=(n == 0), stop=(n == G - 1))
                    last.then_inc(s["la_s_mm"], 1)
                    pe.wait_ge(s["la_lat"], i + 2)
                    pe.wait_ge(s["la_vexp"], i + 1)
                    for n in range(G):
                        last = nc.tensor.matmul(psV[0:TT, n, :], lat[:, n, :, :].rearrange("p a j -> p (a j)"),
                                                wv[:, :], start=True, stop=True)
                    last.then_inc(s["la_v_mm"], 1)
                    pe.wait_ge(s["la_probs"], i + 2)
                    pe.wait_ge(s["la_oT"], i + 1)
                    for g in range(PG):
                        m = min(G, H - G * g)
                        last = nc.tensor.transpose(psT[0:m * S, g // 4, (g % 4) * TT:(g % 4 + 1) * TT],
                                                   e[:, G * g:G * g + m, :].rearrange("p h j -> p (h j)"),
                                                   ident[0:TT, 0:TT])
                    last.then_inc(s["la_turned"], 1)
                    pe.wait_ge(s["la_pT"], i + 2)
                    pe.wait_ge(s["la_vexp"], i + 2)
                    for g in range(PG):
                        m = min(G, H - G * g)
                        for n in range(G):
                            o = (g % 4) * TT + n * S
                            last = nc.tensor.matmul(psT[0:m * NOPE, g // 4, o:o + S],
                                                    vexp[0:m * S, n, g * GN:g * GN + m * NOPE],
                                                    pT[0:m * S, g, n * S:(n + 1) * S], start=True, stop=True)
                    last.then_inc(s["la_pv"], 1)
                    pe.wait_ge(s["la_oT"], i + 2)
                    pe.wait_ge(s["la_h"], i + 1)
                    for g in range(PG):
                        m = min(G, H - G * g) * NOPE
                        last = nc.tensor.matmul(psO[0:TT, 0:D], oT[0:m, g, :], wo[0:m, g, :], start=(g == 0),
                                                stop=(g == PG - 1))
                    last.then_inc(s["la_out_mm"], 1)

            @block.vector
            def _(dve):
                dve.wait_ge(s["la_in"], 65)
                V = 6
                with dve.Fori(0, NT) as i:
                    link = chain(dve, s["la_v"], i * V)
                    dve.wait_ge(s["la_s_mm"], i + 2)
                    for o in range(2):
                        last = nc.vector.tensor_tensor(sc[:, o * 8:(o + 1) * 8, :],
                                                       psS[0:TT, o, 0:W].rearrange("p (h j) -> p h j", j=S),
                                                       neg[:, :].unsqueeze(1).broadcast_to([TT, 8, S]), ALU.add)
                    link(last)
                    link(nc.vector.tensor_reduce(mx[:, :], sc[:, :, :], X, ALU.max))
                    wide = mx[:, :].unsqueeze(2).broadcast_to([TT, H, S])
                    nc.vector.tensor_tensor(sc[:, :, :], sc[:, :, :], wide, ALU.subtract).then_inc(s["la_max"], 1)
                    dve.wait_ge(s["la_v_mm"], i + 2)
                    dve.wait_ge(s["la_pv"], i + 1)
                    nc.vector.tensor_tensor(vexp[:, :, :], psV[0:TT, :, :],
                                            vmask[:, :].unsqueeze(1).broadcast_to([TT, G, H * NOPE]), ALU.mult
                                            ).then_inc(s["la_vexp"], 1)
                    dve.wait_ge(s["la_exp"], i + 2)
                    link(nc.vector.tensor_reduce(mx[:, :], e[:, :, :], X, ALU.add))
                    link(nc.vector.reciprocal(mx[:, :], mx[:, :]))
                    link(nc.vector.tensor_tensor(e[:, :, :], e[:, :, :], wide, ALU.mult))
                    nc.vector.nop().then_inc(s["la_probs"], 1)
                    dve.wait_ge(s["la_out_mm"], i + 2)
                    ht = flat2(h[:, bass.ds(i, 1), :])
                    nc.vector.tensor_tensor(ht, ht, psO[0:TT, 0:D], ALU.add).then_inc(s["la_h"], 1)
                    link(nc.vector.nop())
                assert link.count() == V


def stage_moe4(nc, d, h, xT, ident):
    with ExitStack() as stack:
        sb, ps = bufs(nc, stack)
        E = 8
        norm_transpose(nc, "lm", h, xT, ident, 1e-5, False, w_dram=d["l_ln2"])
        logits = sb("l_logits", [TT, NT, E])
        gates = sb("l_gates", [TT, NT, E])
        one = sb("l_one", [TT, NT, 1])
        projected(nc, "lr", xT, d["l_router"], E, d["l_bias"], logits)
        top2_gates(nc, "lt", logits, gates, d["m_iota"][:, 0:E], ident, E)
        experts(nc, "le", d["l_w_e"], gates, xT, h, E, 2, 1, True)
        with ExitStack() as inner:
            s = sems(nc, inner, "l_one_set")
            block = inner.enter_context(nc.Block())

            @block.vector
            def _(dve):
                nc.vector.memset(one[:, :, :], 1.0).then_inc(s["l_one_set"], 1)
        experts(nc, "ls", d["l_w_s"], one, xT, h, 1, 1, 1, True)


def layout_mla(i, o):
    f = np.float32
    o["l_ln1"] = i["L3_ffn_w_ln1"].reshape(KC, P).T
    o["l_ln2"] = i["L3_ffn_w_ln2"].reshape(KC, P).T
    o["l_wq"] = cols(i["L3_ffn_Wq"], KC)
    o["l_wkva"] = cols(i["L3_ffn_Wkva"], KC)
    wk = np.zeros((64, 16, 64), f)
    wk[:32, :, :32] = i["L3_ffn_Wkvb"].reshape(32, 16, 32)
    wk[32:, :, 32:] = np.eye(32, dtype=f)[:, None, :]
    o["l_wk"] = wk.reshape(64, 1024)
    o["l_wv"] = i["L3_ffn_Wkvb"]
    o["l_perm"] = np.eye(P, dtype=f)[np.arange(P) ^ 1]
    freq = 1.0 / 100000.0 ** (np.arange(0, 32, 2, dtype=np.float32) / 32)
    p = np.arange(P)
    rope = (p % 64 >= 32)[:, None]
    ang = np.arange(S)[None, :] * freq[(p % 32) // 2][:, None]
    sign = np.where(p % 2 == 0, -1, 1)[:, None]
    o["l_tab"] = np.stack([np.where(rope, np.cos(ang), 1), np.where(rope, sign * np.sin(ang), 0)], 1).astype(f)
    wo = np.zeros((18, 32, D), f)
    wo[:16] = i["L3_ffn_Wo"].reshape(16, 64, D)[:, :32]
    o["l_wo"] = wo.reshape(6, 96, D).transpose(1, 0, 2)
    o["l_vmask"] = (np.arange(TT)[:, None] // S == (np.arange(512)[None, :] // 32) % G).astype(f)
    pos = np.tile(np.arange(S), G)[:, None]
    o["l_neg"] = np.where(np.arange(S)[None, :] <= pos, 0, -1e30).astype(f)
    o["l_router"] = cols(i["L3_ffn_Wgate"], KC)
    o["l_bias"] = rep(i["L3_ffn_expert_bias"])
    o["l_w_e"] = np.concatenate([up_cols(i[f"L3_ffn_{n}"]) for n in ("Wg", "Wu", "Wd")], 2)
    o["l_w_s"] = np.concatenate([up_cols(i[f"L3_ffn_s{n}"]) for n in ("Wg", "Wu", "Wd")], 2)


def on_normed(name, *parts):
    def stage(nc, d, h, xT, ident):
        with ExitStack() as stack:
            sb, _ = bufs(nc, stack)
            r = sb(f"{name}_r", [TT, NT, D])
            norm_transpose(nc, f"{name}_ln", h, xT, ident, 1e-5, True, x_tok=r, turn=False)
            for part in parts:
                part(nc, d, r, xT, ident)
            s = sems(nc, stack, f"{name}_added")
            block = stack.enter_context(nc.Block())

            @block.vector
            def _(dve):
                nc.vector.tensor_tensor(h[:, :, :], h[:, :, :], r[:, :, :], ALU.add).then_inc(
                    s[f"{name}_added"], 1)
    return stage


STAGES = [lambda nc, d, h, xT, ident: stage_tok(nc, d, h, ident), stage_attn0, stage_ffn0, stage_gate1, stage_ffn1,
          stage_scan, stage_moe2, on_normed("l6", stage_delta, stage_moe3),
          on_normed("l7", stage_mla, stage_moe4)]
LAYOUTS = [layout_attn0, layout_ffn0, layout_l1, layout_scan, layout_moe2, layout_delta, layout_mla]


def cols(a, k):
    return a.reshape(k, -1, a.shape[1]).transpose(1, 0, 2)


def rep(a, n=TT):
    return np.broadcast_to(a.reshape(1, -1), (n, a.size))


def tiles(a):
    return a.reshape(NT, TT, -1).transpose(1, 0, 2)


def layout(i):
    f = np.float32
    o = {}
    pat = np.zeros((B + 1, S, 768), f)
    pat[:B, 1:] = i["x"].reshape(B, 3, 6, 16, 6, 16).transpose(0, 2, 4, 3, 5, 1).reshape(B, 36, 768)
    o["patches"] = tiles(pat.reshape(T, 768))
    add = np.zeros((B + 1, S, D), f)
    add[:B, 0] = i["L0_tok_class_token"].reshape(D)
    o["tok_addend"] = tiles(add.reshape(T, D))
    o["tok_pos"] = rep(i["L0_tok_pos_embedding"])
    o["tok_w"] = cols(i["L0_tok_weight"].T, 6)
    for g in LAYOUTS:
        g(i, o)
    return {k: np.ascontiguousarray(v) for k, v in o.items()}


def build(nc, d, out, stages=None, h0=None):
    with ExitStack() as stack:
        sb, _ = bufs(nc, stack)
        h = sb("h", [TT, NT, D])
        xT = sb("xT", [P, KC, T])
        ident = sb("ident", [P, P])
        with ExitStack() as s0:
            s = sems(nc, s0, "start_zero start_ident start_h0")
            block = s0.enter_context(nc.Block())

            @block.gpsimd
            def _(pool):
                nc.gpsimd.memset(ident[:, :], 0.0).then_inc(s["start_zero"], 1)
                pool.wait_ge(s["start_zero"], 2)
                nc.gpsimd.affine_select(out=ident[:, :], in_=ident[:, :], compare_op=ALU.not_equal, fill=1.0,
                                        base=0, pattern=[[-1, P]], channel_multiplier=1).then_inc(s["start_ident"], 1)
                pool.wait_ge(s["start_ident"], 2)

            if h0 is not None:
                @block.sync
                def _(sp):
                    sp.dma_start(h[:, :, :], h0).then_inc(s["start_h0"], 16)
                    sp.wait_ge(s["start_h0"], 17)
        for n, stage in enumerate(STAGES):
            if stages is None or n in stages:
                stage(nc, d, h, xT, ident)
        with ExitStack() as s1:
            s = sems(nc, s1, "out_written")
            block = s1.enter_context(nc.Block())
            flat = out.rearrange("b s d -> (b s) d")

            @block.sync
            def _(sp):
                n = NT - 1
                sp.dma_start(flat[0:n * TT, :].rearrange("(t p) d -> p t d", p=TT), h[:, 0:n, :]
                             ).then_inc(s["out_written"], 16)
                rest = B * S - n * TT
                sp.dma_start(flat[n * TT:B * S, :], h[0:rest, n, :]).then_inc(s["out_written"], 16)
                sp.wait_ge(s["out_written"], 33)


def kernel(**inputs):
    import concourse.bacc as _bacc
    from concourse.bass_utils import run_bass_kernel_spmd as _run

    nc = _bacc.Bacc("TRN2", target_bir_lowering=False, num_devices=1)
    arrays, d = {}, {}
    for name, a in layout({k: np.asarray(v) for k, v in inputs.items()}).items():
        arrays[f"in_{name}"] = a
        d[name] = nc.dram_tensor(f"in_{name}", a.shape, mybir.dt.from_np(a.dtype), kind="ExternalInput").ap()
    out = nc.dram_tensor("out_0", (B, S, D), F32, kind="ExternalOutput").ap()
    build(nc, d, out)
    r = _run(nc, [arrays], core_ids=[0])
    return r.results[0]["out_0"]
```

```python
import math
from contextlib import ExitStack

import concourse.bass as bass
import numpy as np
from concourse import mybir

ALU = mybir.AluOpType
ACT = mybir.ActivationFunctionType
F32 = mybir.dt.float32
F32R = mybir.dt.float32r
BF16 = mybir.dt.bfloat16
U32 = mybir.dt.uint32
X = mybir.AxisListType.X

P = 128
B, S, D = 32, 37, 256
G = 3
TT = G * S
NT = 11
T = NT * TT
KC = D // P
NCH = 3
CH = T // NCH
BANK = 512
ROUND = 12582912.0


def sems(nc, stack, names):
    made = {n: nc.alloc_semaphore(n) for n in names.split()}
    for sem in made.values():
        nc.gpsimd.nop().then_inc(sem, 1)
    nc.all_engine_barrier()
    stack.callback(lambda: nc.clear_and_free_semaphores(list(made.values())))
    return made


def bufs(nc, stack):
    def sb(name, shape, dt=F32):
        return stack.enter_context(nc.sbuf_tensor(name, shape, dt))

    def ps(name, shape, dt=F32):
        return stack.enter_context(nc.psum_tensor(name, shape, dt))

    return sb, ps


def chain(eng, sem, at=0):
    n = [0]

    def link(ins):
        n[0] += 1
        ins.then_inc(sem, 1)
        eng.wait_ge(sem, at + n[0] + 1)

    link.count = lambda: n[0]
    return link


def flat2(ap):
    return ap.rearrange("p a d -> p (a d)")


def span(i, n):
    return slice(i * n, (i + 1) * n) if isinstance(i, int) else bass.ds(i * n if n > 1 else i, n)


def norm_transpose(nc, name, h, xT, ident, eps, center, w_dram=None, w_plus=0.0, x_tok=None, turn=True,
                   loads=()):
    with ExitStack() as stack:
        sb, ps = bufs(nc, stack)
        s = sems(nc, stack, " ".join(f"{name}_{x}" for x in (
            "w_loaded", "loaded", "w_ready", "v", "var_ready", "rstd_ready", "shift_ready", "x_even", "x_odd", "turned",
            "done")))
        s = {k[len(name) + 1:]: v for k, v in s.items()}
        xn = x_tok if x_tok is not None else sb(f"{name}_xn", [TT, NT, D])
        stats = sb(f"{name}_stats", [TT, NT, 6])
        mv = sb(f"{name}_mv", [TT, NT, 2])
        var = sb(f"{name}_var", [TT, NT])
        half = sb(f"{name}_half", [TT, NT])
        rstd = sb(f"{name}_rstd", [TT, NT])
        shift = sb(f"{name}_shift", [TT, NT])
        w = sb(f"{name}_w", [P, KC])
        pt = ps(f"{name}_pt", [P, KC * NCH, BANK])
        groups = [(0, 4), (4, 8), (8, NT)] if turn else []
        block = stack.enter_context(nc.Block())

        @block.sync
        def _(sp):
            if w_dram is not None:
                sp.dma_start(w[:, :], w_dram).then_inc(s["w_loaded"], 16)
            for dst, src in loads:
                sp.dma_start(dst, src).then_inc(s["loaded"], 16)
            if loads:
                sp.wait_ge(s["loaded"], 16 * len(loads) + 1)

        @block.vector
        def _(dve):
            link = chain(dve, s["v"])
            nc.vector.memset(half[:, :], -0.5)
            for t in range(NT):
                last = nc.vector.bn_stats(stats[:, t, :], h[:, t, :])
            link(last)
            for t in range(NT):
                last = nc.vector.bn_aggr(mv[:, t, :], stats[:, t, :])
            link(last)
            mean, v = (mv[:, :, k:k + 1].rearrange("p t a -> p (t a)") for k in range(2))
            if center:
                nc.vector.tensor_scalar(var[:, :], v, 1.0, eps, ALU.mult, ALU.add).then_inc(s["var_ready"], 1)
            else:
                link(nc.vector.tensor_tensor(shift[:, :], mean, mean, ALU.mult))
                nc.vector.scalar_tensor_tensor(var[:, :], v, eps, shift[:, :], ALU.add, ALU.add
                                               ).then_inc(s["var_ready"], 1)
            if w_dram is not None:
                dve.wait_ge(s["w_loaded"], 17)
                nc.vector.tensor_scalar(w[:, :], w[:, :], w_plus, None, ALU.add).then_inc(s["w_ready"], 1)
                dve.wait_ge(s["w_ready"], 2)
            dve.wait_ge(s["rstd_ready"], 2)
            if center:
                nc.vector.scalar_tensor_tensor(shift[:, :], mean, -1.0, rstd[:, :], ALU.mult, ALU.mult
                                               ).then_inc(s["shift_ready"], 1)
            for t in range(0, NT, 2):
                if center:
                    ins = nc.vector.tensor_scalar(xn[:, t, :], h[:, t, :], mv[:, t, 0:1], rstd[:, t:t + 1],
                                                  ALU.subtract, ALU.mult)
                else:
                    ins = nc.vector.tensor_scalar(xn[:, t, :], h[:, t, :], rstd[:, t:t + 1], None, ALU.mult)
                ins.then_inc(s["x_even"], 1)
            for g, (a, b) in enumerate(groups):
                dve.wait_ge(s["turned"], KC * g + 2)
                nc.vector.tensor_scalar(xT[:, 0, a * TT:b * TT], pt[:, g, 0:(b - a) * TT],
                                        w[:, 0:1] if w_dram is not None else 1.0, None, ALU.mult
                                        ).then_inc(s["done"], 1)

        @block.gpsimd
        def _(pool):
            pool.wait_ge(s["var_ready"], 2)
            nc.gpsimd.tensor_tensor(rstd[:, :], var[:, :], half[:, :], ALU.pow).then_inc(s["rstd_ready"], 1)

        @block.tensor
        def _(pe):
            for g, (a, b) in enumerate(groups):
                for k in range(KC):
                    for t in range(a, b):
                        if k == 0:
                            pe.wait_ge(s["x_odd" if t % 2 else "x_even"], t // 2 + 2)
                        last = nc.tensor.transpose(pt[:, k * NCH + g, (t - a) * TT:(t - a + 1) * TT],
                                                   xn[:, t, k * P:(k + 1) * P], ident[0:TT, 0:TT])
                    last.then_inc(s["turned"], 1)

        @block.scalar
        def _(act):
            act.wait_ge(s["rstd_ready"], 2)
            if center:
                act.wait_ge(s["shift_ready"], 2)
            for t in range(1, NT, 2):
                if center:
                    ins = nc.scalar.activation(xn[:, t, :], h[:, t, :], ACT.Identity, scale=rstd[:, t:t + 1],
                                               bias=shift[:, t:t + 1])
                else:
                    ins = nc.scalar.activation(xn[:, t, :], h[:, t, :], ACT.Copy, scale=rstd[:, t:t + 1])
                ins.then_inc(s["x_odd"], 1)
            if w_dram is not None:
                act.wait_ge(s["w_ready"], 2)
            for g, (a, b) in enumerate(groups):
                act.wait_ge(s["turned"], KC * g + 3)
                nc.scalar.activation(xT[:, 1, a * TT:b * TT], pt[:, NCH + g, 0:(b - a) * TT], ACT.Copy,
                                     scale=w[:, 1:2] if w_dram is not None else 1.0).then_inc(s["done"], 1)


def stage_tok(nc, d, h, ident):
    DIN = 768
    NK = DIN // P
    with ExitStack() as stack:
        sb, ps = bufs(nc, stack)
        s = sems(nc, stack, "tok_w_in tok_add_in tok_v tok_v2 tok_a tok_wsum tok_wtot tok_wq_ready tok_ss tok_ms "
                            "tok_r tok_xr tok_rounded tok_q_ready tok_turned tok_qT tok_mm tok_base tok_hdone "
                            "tok_half tok_x0 tok_x1 tok_x2")
        w = sb("tok_w", [P, NK, D])
        wa = sb("tok_wa", [P, NK * D])
        wq = sb("tok_wq", [P, NK, D], BF16)
        ones = sb("tok_ones", [P, P])
        wsum = sb("tok_wsum_b", [P, 1])
        wmean = sb("tok_wmean", [P, 1])
        wscale = sb("tok_wscale", [P, 1])
        x = sb("tok_x", [TT, NT, DIN])
        junk = sb("tok_junk", [TT, 2, DIN])
        add = sb("tok_addend", [TT, NT, D])
        pos = sb("tok_pos", [TT, D])
        ss = sb("tok_ssb", [TT, NT])
        ms = sb("tok_msb", [TT, NT])
        mx = sb("tok_mx", [TT, NT])
        half = sb("tok_halfb", [TT, NT])
        r = sb("tok_rb", [TT, NT])
        back = sb("tok_back", [TT, 1])
        sc = sb("tok_sc", [TT, NT])
        inv = sb("tok_inv", [TT, NT])
        qb = sb("tok_qb", [TT, NT, DIN], BF16)
        identb = sb("tok_identb", [P, P], BF16)
        qT = sb("tok_qTb", [P, NT, NK * TT], BF16)
        pw = ps("tok_pw", [P, BANK])
        pt = ps("tok_pt", [P, 2, 1024], BF16)
        po = ps("tok_po", [P, BANK])
        parts = [(0, 4), (4, 8), (8, NT)]
        AHEAD = 3
        block = stack.enter_context(nc.Block())

        @block.sync
        def _(sp):
            sp.dma_start(w[:, :, :], d["tok_w"]).then_inc(s["tok_w_in"], 16)
            for g, (a, b) in enumerate(parts):
                sp.dma_start(x[:, a:b, :], d["patches"][:, a:b, :]).then_inc(s[f"tok_x{g}"], 16)
            sp.dma_start(add[:, :, :], d["tok_addend"]).then_inc(s["tok_add_in"], 16)
            sp.dma_start(pos[:, :], d["tok_pos"]).then_inc(s["tok_add_in"], 16)

        @block.scalar
        def _(act):
            act.wait_ge(s["tok_w_in"], 17)
            nc.scalar.activation(wa[:, :], w[:, :, :].rearrange("p k d -> p (k d)"), ACT.Abs,
                                 accum_out=wsum[:, :]).then_inc(s["tok_wsum"], 1)
            for g, (a, b) in enumerate(parts):
                act.wait_ge(s[f"tok_x{g}"], 17)
                for t in range(a, b):
                    if t >= 2:
                        act.wait_ge(s["tok_ss"], t)
                    nc.scalar.activation(junk[:, t % 2, :], x[:, t, :], ACT.Square, accum_out=ss[:, t:t + 1]
                                         ).then_inc(s["tok_ss"], 1)

            def scaled(i):
                nc.scalar.activation(flat2(x[:, span(i, 1), :]), flat2(x[:, span(i, 1), :]), ACT.Copy,
                                     scale=r[:, span(i, 1)]).then_inc(s["tok_xr"], 1)

            def copy(i):
                act.wait_ge(s["tok_turned"], i + 2)
                nc.scalar.activation(flat2(qT[:, span(i, 1), :]).rearrange("p (k t) -> p k t", t=TT),
                                     pt[:, 0, 0:NK * P].rearrange("p (k t) -> p k t", t=P)[:, :, 0:TT], ACT.Copy
                                     ).then_inc(s["tok_qT"], 1)

            act.wait_ge(s["tok_r"], 2)
            for i in range(AHEAD):
                scaled(i)
            with act.Fori(AHEAD, NT) as i:
                scaled(i)
                copy(i - AHEAD)
            for i in range(NT - AHEAD, NT):
                copy(i)

        @block.gpsimd
        def _(pool):
            pool.wait_ge(s["tok_add_in"], 33)
            nc.gpsimd.tensor_tensor(h[:, :, :], add[:, :, :], pos[:, :].unsqueeze(1).broadcast_to([TT, NT, D]),
                                    ALU.add).then_inc(s["tok_base"], 1)
            pool.wait_ge(s["tok_ms"], 2)
            nc.gpsimd.tensor_tensor(r[:, :], ms[:, :], half[:, :], ALU.pow).then_inc(s["tok_r"], 1)
            with pool.Fori(0, NT) as i:
                pool.wait_ge(s["tok_rounded"], i + 2)
                nc.gpsimd.tensor_tensor(flat2(qb[:, bass.ds(i, 1), :]), flat2(x[:, bass.ds(i, 1), :]),
                                        back[:, :].broadcast_to([TT, DIN]), ALU.add).then_inc(s["tok_q_ready"], 1)

        @block.tensor
        def _(pe):
            pe.wait_ge(s["tok_half"], 2)
            pe.wait_ge(s["tok_wsum"], 2)
            nc.tensor.matmul(pw[:, 0:1], ones[:, :], wsum[:, :], start=True, stop=True).then_inc(s["tok_wtot"], 1)
            pe.wait_ge(s["tok_wq_ready"], 2)

            def turn(i):
                pe.wait_ge(s["tok_q_ready"], i + 2)
                pe.wait_ge(s["tok_qT"], i + 1)
                one = flat2(qb[:, span(i, 1), :])
                for k in range(NK):
                    last = nc.tensor.transpose(pt[:, 0, k * P:k * P + TT], one[:, k * P:(k + 1) * P],
                                               identb[0:TT, 0:TT])
                last.then_inc(s["tok_turned"], 1)

            def product(i):
                pe.wait_ge(s["tok_qT"], i + 2)
                pe.wait_ge(s["tok_hdone"], i + 1)
                one = flat2(qT[:, span(i, 1), :])
                for k in range(NK):
                    last = nc.tensor.matmul(po[0:TT, 0:D], one[:, k * TT:(k + 1) * TT], wq[:, k, :], start=(k == 0),
                                            stop=(k == NK - 1))
                last.then_inc(s["tok_mm"], 1)

            turn(0)
            with pe.Fori(1, NT) as i:
                turn(i)
                product(i - 1)
            product(NT - 1)

        @block.vector
        def _(dve):
            link = chain(dve, s["tok_v"])
            nc.vector.memset(half[:, :], -0.5)
            nc.vector.memset(back[:, :], -ROUND)
            nc.vector.tensor_copy(identb[:, :], ident[:, :])
            nc.vector.memset(ones[:, :], 1.0).then_inc(s["tok_half"], 1)
            dve.wait_ge(s["tok_wtot"], 2)
            link(nc.vector.tensor_scalar(wmean[:, :], pw[:, 0:1], 1.0 / (D * DIN), 1e-5, ALU.mult, ALU.max))
            link(nc.vector.reciprocal(wscale[:, :], wmean[:, :]))
            wf = w[:, :, :]
            link(nc.vector.tensor_scalar(wf, wf, wscale[:, 0:1], None, ALU.mult))
            link(nc.vector.tensor_scalar(wf, wf, ROUND, -ROUND, ALU.add, ALU.add))
            nc.vector.tensor_scalar(wq[:, :, :], wf, 1.0, -1.0, ALU.min, ALU.max).then_inc(s["tok_wq_ready"], 1)
            for g, (a, b) in enumerate(parts):
                dve.wait_ge(s[f"tok_x{g}"], 17)
                last = nc.vector.tensor_reduce(mx[:, a:b], x[:, a:b, :], X, ALU.max, apply_absolute_value=True)
            link(last)
            dve.wait_ge(s["tok_ss"], NT + 1)
            nc.vector.tensor_scalar(ms[:, :], ss[:, :], 1.0 / DIN, 1e-6, ALU.mult, ALU.add).then_inc(s["tok_ms"], 1)
            dve.wait_ge(s["tok_r"], 2)
            link(nc.vector.tensor_tensor(mx[:, :], mx[:, :], r[:, :], ALU.mult))
            link(nc.vector.tensor_scalar(mx[:, :], mx[:, :], 1e-5, None, ALU.max))
            link(nc.vector.reciprocal(sc[:, :], mx[:, :]))
            link(nc.vector.tensor_scalar(sc[:, :], sc[:, :], 127.0, None, ALU.mult))
            link(nc.vector.tensor_scalar(inv[:, :], mx[:, :], 1.0 / 127.0, wmean[0:TT, 0:1], ALU.mult, ALU.mult))

            def rounded(i):
                dve.wait_ge(s["tok_xr"], i + 2)
                one = flat2(x[:, span(i, 1), :])
                nc.vector.tensor_scalar(one, one, sc[:, span(i, 1)], 127.0, ALU.mult, ALU.min).then_inc(s["tok_v2"], 1)
                dve.wait_ge(s["tok_v2"], i + 2)
                nc.vector.tensor_scalar(one, one, -128.0, ROUND, ALU.max, ALU.add).then_inc(s["tok_rounded"], 1)

            def add(i):
                dve.wait_ge(s["tok_mm"], i + 2)
                ht = flat2(h[:, span(i, 1), :])
                nc.vector.scalar_tensor_tensor(ht, po[0:TT, 0:D], inv[:, span(i, 1)], ht, ALU.mult, ALU.add
                                               ).then_inc(s["tok_hdone"], 1)

            for i in range(AHEAD):
                rounded(i)
            dve.wait_ge(s["tok_base"], 2)
            with dve.Fori(AHEAD, NT) as i:
                rounded(i)
                add(i - AHEAD)
            for i in range(NT - AHEAD, NT):
                add(i)


def stage_attn0(nc, d, h, xT, ident):
    H, HG = 16, 8
    QG = 4
    NB = H // QG
    W = QG * S
    PG = (H + G - 1) // G
    with ExitStack() as stack:
        sb, ps = bufs(nc, stack)
        wq, wk, wv = (sb(f"a_w{n}", [P, KC, D]) for n in "qkv")
        wo = sb("a_wo", [G * 16, PG, D])
        bo = sb("a_bo", [TT, D])
        uv = sb("a_uv", [P, 2, KC])
        perm = sb("a_perm", [P, P])
        tab = sb("a_tab", [P, 4, TT])
        texp = sb("a_texp", [P, HG, S])
        hmask = sb("a_hmask", [P, HG])
        vmask = sb("a_vmask", [TT, D])
        band = sb("a_band", [TT, 2, S])
        norm_transpose(nc, "an", h, xT, ident, 1e-5, True, loads=[(x[:, :, :], d[f"a_{n}"]) for n, x in (
            ("wq", wq), ("wk", wk), ("wv", wv), ("wo", wo), ("tab", tab), ("texp", texp), ("band", band), ("uv", uv))]
            + [(x[:, :], d[f"a_{n}"]) for n, x in (("bo", bo), ("perm", perm), ("hmask", hmask), ("vmask", vmask))])
        s = sems(nc, stack, "a_zero a_qk_mm a_qk_done a_sw_mm a_sw_done a_qpad "
                            "a_qu_tile a_xrep a_kexp a_rot a_scores a_v_mm a_vexp a_probs a_max a_exp "
                            "a_turned a_summed a_pT a_pv a_oT a_out_mm a_hdone a_v1 a_v2")
        qu = sb("a_qu", [P, KC, T])
        qv = sb("a_qv", [P, KC, T + 1])
        sw = sb("a_sw", [P, KC, T + 1])
        kT = sb("a_kT", [P, KC, T])
        qum = sb("a_qum", [P, KC, G * TT])
        kexp = sb("a_kexp", [P, KC, G, HG, S])
        xrep = sb("a_xrep", [P, KC, G, G, S])
        r = [sb(f"a_r{n}", [P, KC, TT]) for n in (1, 2)]
        rt = [sb(f"a_rt{n}", [P, KC, TT]) for n in (1, 2)]
        m1 = sb("a_m1", [TT, NB, QG, S])
        m2 = sb("a_m2", [TT, NB, QG, S])
        e = sb("a_e", [TT, NB * QG, S])
        mx = sb("a_mx", [TT, H])
        sm = sb("a_sm", [TT, H])
        pT = sb("a_pTb", [TT, PG, TT])
        vexp = sb("a_vexpb", [TT, G, D])
        oT = sb("a_oTb", [G * 16, PG, TT])
        tmp = sb("a_tmp", [TT, D])
        psS = ps("a_psS", [P, NB, BANK])
        psT = ps("a_psT", [P, 2, BANK])
        psV = ps("a_psV", [P, 2, BANK])
        block = stack.enter_context(nc.Block())

        @block.tensor
        def _(pe):
            n = 0
            for w in (wq, wk):
                for c in range(KC):
                    for t in range(NCH):
                        if n >= 4:
                            pe.wait_ge(s["a_qk_done"], n - 2)
                        for k in range(KC):
                            last = nc.tensor.matmul(psS[:, n % 4, 0:CH], w[:, k, c * P:(c + 1) * P],
                                                    xT[:, k, t * CH:(t + 1) * CH], start=(k == 0), stop=(k == KC - 1))
                        last.then_inc(s["a_qk_mm"], 1)
                        n += 1
            pe.wait_ge(s["a_qk_done"], n + 1)
            for m in range(KC * NCH):
                if m >= 4:
                    pe.wait_ge(s["a_sw_done"], m - 2)
                c, t = divmod(m, NCH)
                nc.tensor.matmul(psS[:, m % 4, 0:CH], perm[:, :], qv[:, c, t * CH:(t + 1) * CH],
                                 start=True, stop=True).then_inc(s["a_sw_mm"], 1)
            pe.wait_ge(s["a_sw_done"], KC * NCH + 1)
            def scores(i):
                pe.wait_ge(s["a_qu_tile"], i + 2)
                pe.wait_ge(s["a_kexp"], i + 2)
                pe.wait_ge(s["a_rot"], i + 2)
                pe.wait_ge(s["a_summed"], i + 1)
                for g in range(NB):
                    c, o = divmod(g, 2)
                    for q in range(G):
                        nc.tensor.matmul(psS[0:TT, g, 0:W], qum[:, c, q * TT:(q + 1) * TT],
                                         kexp[:, c, q, o * QG:(o + 1) * QG, :].rearrange("p h j -> p (h j)"),
                                         start=(q == 0), stop=(q == G - 1))
                    for m in range(2):
                        last = nc.tensor.matmul(psS[0:TT, g, (m + 1) * W:(m + 2) * W], r[m][:, c, :],
                                                flat2(texp[:, o * QG:(o + 1) * QG, :]), start=True, stop=True)
                last.then_inc(s["a_scores"], 1)

            def values(i):
                pe.wait_ge(s["a_xrep"], i + 2)
                pe.wait_ge(s["a_vexp"], i + 1)
                for q in range(G):
                    for k in range(KC):
                        last = nc.tensor.matmul(psV[0:TT, q // 2, (q % 2) * D:(q % 2 + 1) * D],
                                                xrep[:, k, q, :, :].rearrange("p a j -> p (a j)"), wv[:, k, :],
                                                start=(k == 0), stop=(k == KC - 1))
                last.then_inc(s["a_v_mm"], 1)

            def turn(i):
                pe.wait_ge(s["a_probs"], i + 2)
                pe.wait_ge(s["a_hdone"], i + 1)
                for g in range(PG):
                    n = min(G, H - G * g) * S
                    last = nc.tensor.transpose(psT[0:n, g // 4, (g % 4) * TT:(g % 4 + 1) * TT],
                                               e[:, G * g:G * g + n // S, :].rearrange("p h j -> p (h j)"),
                                               ident[0:TT, 0:TT])
                last.then_inc(s["a_turned"], 1)

            def mix_values(i):
                pe.wait_ge(s["a_pT"], i + 2)
                pe.wait_ge(s["a_vexp"], i + 2)
                for g in range(PG):
                    m = min(G, H - G * g)
                    for q in range(G):
                        last = nc.tensor.matmul(psT[0:m * 16, g // 4, (g % 4) * TT + q * S:(g % 4) * TT + (q + 1) * S],
                                                vexp[0:m * S, q, g * 48:g * 48 + m * 16],
                                                pT[0:m * S, g, q * S:(q + 1) * S], start=True, stop=True)
                last.then_inc(s["a_pv"], 1)

            def project(i):
                pe.wait_ge(s["a_oT"], i + 2)
                for g in range(PG):
                    m = min(G, H - G * g) * 16
                    last = nc.tensor.matmul(psT[0:TT, 1, 0:D], oT[0:m, g, :], wo[0:m, g, :],
                                            start=(g == 0), stop=(g == PG - 1))
                last.then_inc(s["a_out_mm"], 1)

            scores(0)
            values(0)
            with pe.Fori(1, NT) as i:
                scores(i)
                turn(i - 1)
                mix_values(i - 1)
                values(i)
                project(i - 1)
            turn(NT - 1)
            mix_values(NT - 1)
            project(NT - 1)

        @block.scalar
        def _(act):
            act.wait_ge(s["a_qpad"], 2)
            for m in range(KC * NCH):
                c, t = divmod(m, NCH)
                act.wait_ge(s["a_sw_mm"], m + 2)
                nc.scalar.activation(sw[:, c, t * CH:(t + 1) * CH], psS[:, m % 4, 0:CH], ACT.Copy
                                     ).then_inc(s["a_sw_done"], 1)
            with act.Fori(0, NT) as i:
                act.wait_ge(s["a_max"], i + 2)
                act.wait_ge(s["a_turned"], i + 1)
                nc.scalar.activation(e[:, :, :], m1[:, :, :, :].rearrange("p b h j -> p (b h) j"), ACT.Exp,
                                     scale=0.25).then_inc(s["a_exp"], 1)
                act.wait_ge(s["a_turned"], i + 2)
                nc.scalar.activation(pT[:, 0:4, :].rearrange("p g t -> p (g t)"), psT[0:TT, 0, 0:4 * TT], ACT.Copy
                                     ).then_inc(s["a_v2"], 1)
                nc.scalar.activation(pT[:, 4, :], psT[0:TT, 1, 0:TT], ACT.Copy).then_inc(s["a_v2"], 1)
                nc.scalar.activation(pT[0:S, 5, :], psT[0:S, 1, TT:2 * TT], ACT.Copy).then_inc(s["a_v2"], 1)
                act.wait_ge(s["a_v2"], 3 * i + 4)
                nc.scalar.nop().then_inc(s["a_pT"], 1)
                act.wait_ge(s["a_pv"], i + 2)
                nc.scalar.activation(oT[:, 0:4, :].rearrange("p g t -> p (g t)"), psT[0:48, 0, 0:4 * TT], ACT.Copy)
                nc.scalar.activation(oT[:, 4, :], psT[0:48, 1, 0:TT], ACT.Copy)
                nc.scalar.activation(oT[0:16, 5, :], psT[0:16, 1, TT:2 * TT], ACT.Copy).then_inc(s["a_oT"], 1)

        @block.gpsimd
        def _(pool):
            nc.gpsimd.memset(qum[:, :, :], 0.0)
            nc.gpsimd.memset(qv[:, :, T:T + 1], 0.0).then_inc(s["a_zero"], 1)
            nc.gpsimd.memset(sw[:, :, T:T + 1], 0.0).then_inc(s["a_qpad"], 1)
            pool.wait_ge(s["a_zero"], 2)
            pool.wait_ge(s["a_qk_done"], 2 * KC * NCH + 1)
            with pool.Fori(0, NT) as i:
                pool.wait_ge(s["a_scores"], i + 1)
                for c in range(KC):
                    src = kT[:, c, bass.ds(i * TT, TT)].rearrange("p (q j) -> p q j", q=G)
                    for q in range(G):
                        last = nc.gpsimd.tensor_tensor(
                            kexp[:, c, q, :, :], src[:, q, :].unsqueeze(1).broadcast_to([P, HG, S]),
                            hmask[:, :].unsqueeze(2).broadcast_to([P, HG, S]), ALU.mult)
                last.then_inc(s["a_kexp"], 1)
                pool.wait_ge(s["a_v_mm"], i + 1)
                for c in range(KC):
                    for q in range(G):
                        last = nc.gpsimd.tensor_copy(xrep[:, c, q, :, :],
                                                     xT[:, c, bass.ds(i * TT + q * S, S)].unsqueeze(1)
                                                     .broadcast_to([P, G, S]))
                last.then_inc(s["a_xrep"], 1)

        @block.vector
        def _(dve):
            dve.wait_ge(s["a_zero"], 2)
            n = 0
            for w in range(2):
                for c in range(KC):
                    for t in range(NCH):
                        dve.wait_ge(s["a_qk_mm"], n + 2)
                        src = psS[:, n % 4, 0:CH]
                        at = slice(t * CH, (t + 1) * CH)
                        if w == 0:
                            nc.vector.tensor_scalar(qu[:, c, at], src, uv[:, 0, c:c + 1], None, ALU.add)
                            last = nc.vector.tensor_scalar(qv[:, c, at], src, uv[:, 1, c:c + 1], None, ALU.add)
                        else:
                            last = nc.vector.tensor_copy(kT[:, c, at], src)
                        last.then_inc(s["a_qk_done"], 1)
                        n += 1
            dve.wait_ge(s["a_qk_done"], n + 1)
            dve.wait_ge(s["a_sw_done"], KC * NCH + 1)
            def rotate(i):
                dve.wait_ge(s["a_scores"], i + 1)
                for c in range(KC):
                    for q in range(G):
                        last = nc.vector.tensor_copy(qum[:, c, q * (TT + S):q * (TT + S) + S],
                                                     qu[:, c, bass.ds(i * TT + q * S, S)])
                last.then_inc(s["a_qu_tile"], 1)
                for m in range(2):
                    at = bass.ds(i * TT + m, TT)
                    nc.vector.tensor_tensor(r[m][:, :, :], qv[:, :, at],
                                            tab[:, 2 * m:2 * m + 1, :].broadcast_to([P, KC, TT]), ALU.mult)
                    link(nc.vector.tensor_tensor(rt[m][:, :, :], sw[:, :, at],
                                                 tab[:, 2 * m + 1:2 * m + 2, :].broadcast_to([P, KC, TT]), ALU.mult))
                for m in range(2):
                    ins = nc.vector.tensor_tensor(r[m][:, :, :], r[m][:, :, :], rt[m][:, :, :], ALU.add)
                ins.then_inc(s["a_rot"], 1)

            def softmax(i):
                dve.wait_ge(s["a_scores"], i + 2)
                dve.wait_ge(s["a_exp"], i + 1)
                part = [psS[0:TT, :, m * W:(m + 1) * W].rearrange("p b (h j) -> p b h j", j=S) for m in range(3)]
                for m, dst in ((1, m1), (2, m2)):
                    last = nc.vector.tensor_tensor(dst[:, :, :, :], part[m],
                                                   band[:, m - 1:m, :].unsqueeze(1).broadcast_to([TT, NB, QG, S]),
                                                   ALU.mult)
                link(last)
                link(nc.vector.tensor_tensor(m2[:, :, :, :].rearrange("p b h j -> p b (h j)"),
                                             m2[:, :, :, :].rearrange("p b h j -> p b (h j)"),
                                             psS[0:TT, :, 0:W], ALU.add))
                nc.vector.nop().then_inc(s["a_summed"], 1)
                link(nc.vector.tensor_tensor(m1[:, :, :, :].rearrange("p b h j -> p (b h j)"),
                                             m1[:, :, :, :].rearrange("p b h j -> p (b h j)"),
                                             m2[:, :, :, :].rearrange("p b h j -> p (b h j)"), ALU.add))
                sc = m1[:, :, :, :].rearrange("p b h j -> p (b h) j")
                link(nc.vector.tensor_reduce(mx[:, :], sc, X, ALU.max))
                nc.vector.tensor_tensor(sc, sc, mx[:, :].unsqueeze(2).broadcast_to([TT, H, S]),
                                        ALU.subtract).then_inc(s["a_max"], 1)

            def probs(i):
                dve.wait_ge(s["a_exp"], i + 2)
                link(nc.vector.tensor_reduce(sm[:, :], e[:, :, :], X, ALU.add))
                link(nc.vector.reciprocal(sm[:, :], sm[:, :]))
                nc.vector.tensor_tensor(e[:, :, :], e[:, :, :], sm[:, :].unsqueeze(2).broadcast_to([TT, H, S]),
                                        ALU.mult).then_inc(s["a_probs"], 1)

            def values(i):
                dve.wait_ge(s["a_v_mm"], i + 2)
                dve.wait_ge(s["a_pv"], i + 1)
                for q in range(G):
                    last = nc.vector.tensor_tensor(vexp[:, q, :], psV[0:TT, q // 2, (q % 2) * D:(q % 2 + 1) * D],
                                                   vmask[:, :], ALU.mult)
                last.then_inc(s["a_vexp"], 1)

            def add(i):
                dve.wait_ge(s["a_out_mm"], i + 2)
                link(nc.vector.tensor_tensor(tmp[:, :], psT[0:TT, 1, 0:D], bo[:, :], ALU.add))
                ht = h[:, i, :] if isinstance(i, int) else flat2(h[:, bass.ds(i, 1), :])
                nc.vector.tensor_tensor(ht, ht, tmp[:, :], ALU.add).then_inc(s["a_hdone"], 1)

            link = chain(dve, s["a_v1"])
            rotate(0)
            ROT = link.count()
            softmax(0)
            rotate(1)
            probs(0)
            values(0)
            V0 = link.count()
            V1 = V0 - ROT + 1
            with dve.Fori(1, NT - 1) as i:
                link = chain(dve, s["a_v1"], (i - 1) * V1 + V0)
                softmax(i)
                rotate(i + 1)
                probs(i)
                values(i)
                add(i - 1)
            assert link.count() == V1, link.count()
            link = chain(dve, s["a_v1"], (NT - 2) * V1 + V0)
            softmax(NT - 1)
            probs(NT - 1)
            values(NT - 1)
            add(NT - 2)
            add(NT - 1)


def layout_attn0(i, o):
    f = np.float32
    for n in "qkv":
        o[f"a_w{n}"] = cols(i[f"L0_attn_W{n}"], KC)
    wo = np.zeros((6, 48, D), f)
    wo.reshape(288, D)[:D] = i["L0_attn_Wo"]
    o["a_wo"] = wo.transpose(1, 0, 2)
    o["a_bo"] = rep(i["L0_attn_bo"])
    o["a_uv"] = np.stack([i["L0_attn_u"].reshape(KC, P).T, i["L0_attn_v"].reshape(KC, P).T], 1)
    o["a_perm"] = np.eye(P, dtype=f)[np.arange(P) ^ 8]
    freq = 1.0 / 10000.0 ** (np.arange(0, 16, 2) / 16)
    w = np.tile(freq, P // 8)[:, None]
    sine = (np.arange(P) % 16 < 8)[:, None]
    pos = np.tile(np.arange(S), G)[None, :]
    tab = []
    for a in (pos, pos + S + 1):
        tab += [np.sin(a * w), np.where(sine, 1, -1) * np.cos(a * w)]
    o["a_tab"] = np.stack(tab, 1).astype(f)
    j = np.arange(S)[None, :]
    t = np.where(sine, np.cos(j * w), np.sin(j * w))
    own = (np.arange(P)[:, None] // 16 == np.arange(8)[None, :])
    o["a_texp"] = (own[:, :, None] * t[:, None, :]).astype(f)
    o["a_hmask"] = own.astype(f)
    o["a_vmask"] = (np.arange(TT)[:, None] // S == (np.arange(D)[None, :] // 16) % G).astype(f)
    q = np.tile(np.arange(S), G)[:, None]
    o["a_band"] = np.stack([j <= q, j >= q + 2], 1).astype(f)


def stage_ffn0(nc, d, h, xT, ident):
    F = 1024
    FC = F // P
    SP = S + 2
    with ExitStack() as stack:
        sb, ps = bufs(nc, stack)
        x = sb("f_x", [TT, NT, D])
        w1 = sb("f_w1", [P, KC * F])
        w2 = sb("f_w2", [P, FC * D])
        cw = sb("f_cw", [P, FC, 3])
        cb = sb("f_cb", [P, FC])
        norm_transpose(nc, "fn", h, xT, ident, 1e-5, True, x_tok=x, turn=False, loads=[
            (w1[:, :], d["f_w1"]), (w2[:, :], d["f_w2"]), (cw[:, :, :], d["f_cw"]), (cb[:, :], d["f_cb"])])
        s = sems(nc, stack, "f_v f_v2 f_v3 f_ones f_wsum f_wtot f_wq f_xq f_turned f_qT f_diag f_bc_mm f_bc "
                            "f_h_mm f_hp f_edge f_conv1 f_conv3 f_silu f_amax f_max_turned f_max f_diag2 f_bc2_mm "
                            "f_bc2 f_scaled f_hq f_out_mm f_hdone f_a")
        w1q = sb("f_w1q", [P, KC, F], BF16)
        w2q = sb("f_w2q", [P, FC, D], BF16)
        ones = sb("f_ones_b", [P, P])
        wsum = sb("f_wsum_b", [P, 2])
        wmean = sb("f_wmean", [P, 2])
        wscale = sb("f_wscale", [P, 2])
        mx = sb("f_mx", [TT, NT])
        sc = sb("f_sc", [TT, NT])
        inv = sb("f_inv", [TT, NT])
        xb = sb("f_xb", [TT, NT, D], BF16)
        identb = sb("f_identb", [P, P], BF16)
        qT = sb("f_qTb", [P, KC, T], BF16)
        diag = sb("f_diagb", [TT, NT, TT])
        bc = sb("f_bcb", [P, T])
        hp = [sb(f"f_hpb{u}", [P, B + 1, SP]) for u in range(2)]
        acc = [sb(f"f_acc{u}", [P, B + 1, S]) for u in range(2)]
        act1 = sb("f_act", [P, FC, T])
        amax = sb("f_amaxb", [P, T])
        hq = sb("f_hqb", [P, FC, T], BF16)
        pm = ps("f_pm", [P, NCH, BANK])
        pt = ps("f_pt", [P, 4, 2 * BANK], BF16)
        po = ps("f_po", [P, BANK])
        groups = [(0, 4), (4, 8), (8, NT)]
        SL = TT + 1
        ph = [(0, 9), (9, NT)]
        MP = 3
        block = stack.enter_context(nc.Block())

        @block.scalar
        def _(act):
            nc.scalar.activation(act1[:, 0:2, :].rearrange("p c t -> p (c t)")[:, 0:KC * F], w1[:, :], ACT.Abs,
                                 accum_out=wsum[:, 0:1])
            nc.scalar.activation(act1[:, 2:4, :].rearrange("p c t -> p (c t)")[:, 0:FC * D], w2[:, :], ACT.Abs,
                                 accum_out=wsum[:, 1:2]).then_inc(s["f_wsum"], 1)
            for g in range(4):
                act.wait_ge(s["f_turned"], g + 2)
                k, b = divmod(g, 2)
                lo, hi = ph[b]
                nc.scalar.activation(qT[:, k, lo * TT:hi * TT].rearrange("p (t x) -> p t x", x=TT),
                                     pt[:, g, 0:(hi - lo) * SL].rearrange("p (t x) -> p t x", x=SL)[:, :, 0:TT], ACT.Copy
                                     ).then_inc(s["f_qT"], 1)
            act.wait_ge(s["f_wsum"], 2)

            def first_tap(c, u):
                act.wait_ge(s["f_hp"], 3 * c + 4)
                act.wait_ge(s["f_silu"], c)
                nc.scalar.activation(acc[u][:, :, :], hp[u][:, :, 0:S], ACT.Identity, scale=flat2(cw[:, span(c, 1), 0:1]),
                                     bias=cb[:, span(c, 1)]).then_inc(s["f_conv1"], 1)

            def silu(c, u):
                act.wait_ge(s["f_conv3"], c + 2)
                nc.scalar.activation(flat2(act1[:, span(c, 1), :]), acc[u][:, :, :].rearrange("p b j -> p (b j)"),
                                     ACT.Silu).then_inc(s["f_silu"], 1)

            act.wait_ge(s["f_hp"], 4)
            nc.scalar.activation(acc[0][:, :, :], hp[0][:, :, 0:S], ACT.Identity, scale=cw[:, 0, 0:1],
                                 bias=cb[:, 0:1]).then_inc(s["f_conv1"], 1)
            first_tap(1, 1)
            silu(0, 0)
            with act.Fori(1, FC // 2) as i:
                for u in range(2):
                    first_tap(2 * i + u, u)
                    silu(2 * i + u - 1, 1 - u)
            silu(FC - 1, 1)

        @block.tensor
        def _(pe):
            pe.wait_ge(s["f_ones"], 2)
            pe.wait_ge(s["f_wsum"], 2)
            nc.tensor.matmul(po[:, 0:2], ones[:, :], wsum[:, :], start=True, stop=True).then_inc(s["f_wtot"], 1)
            pe.wait_ge(s["f_xq"], 2)
            for k in range(KC):
                for b, (lo, hi) in enumerate(ph):
                    for t in range(lo, hi):
                        last = nc.tensor.transpose(pt[:, 2 * k + b, (t - lo) * SL:(t - lo) * SL + TT],
                                                   xb[:, t, k * P:(k + 1) * P], identb[0:TT, 0:TT])
                    last.then_inc(s["f_turned"], 1)
            pe.wait_ge(s["f_diag"], 2)
            for g, (a, b) in enumerate(groups):
                last = nc.tensor.matmul(pm[:, g, 0:(b - a) * TT], ones[0:TT, :], flat2(diag[:, a:b, :]),
                                        start=True, stop=True)
            last.then_inc(s["f_bc_mm"], 1)
            pe.wait_ge(s["f_bc"], 2)
            pe.wait_ge(s["f_qT"], 5)
            with pe.Fori(0, FC) as c:
                for t in range(NCH):
                    pe.wait_ge(s["f_hp"], 3 * c + t + 1)
                    for k in range(KC):
                        last = nc.tensor.matmul(pm[:, t, 0:CH], w1q[:, k, bass.ds(c * P, P)],
                                                qT[:, k, t * CH:(t + 1) * CH], start=(k == 0), stop=(k == KC - 1))
                    last.then_inc(s["f_h_mm"], 1)
            pe.wait_ge(s["f_amax"], FC + 1)
            for g, (a, b) in enumerate(groups):
                pe.wait_ge(s["f_max"], g + 1)
                for t in range(a, b):
                    last = nc.tensor.transpose(pm[0:TT, 0, (t - a) * P:(t - a + 1) * P],
                                               amax[:, t * TT:(t + 1) * TT], ident[:, :])
                last.then_inc(s["f_max_turned"], 1)
            pe.wait_ge(s["f_diag2"], 2)
            for g, (a, b) in enumerate(groups):
                last = nc.tensor.matmul(pm[:, g, 0:(b - a) * TT], ones[0:TT, :], flat2(diag[:, a:b, :]),
                                        start=True, stop=True)
            last.then_inc(s["f_bc2_mm"], 1)
            pe.wait_ge(s["f_bc2"], NCH + 1)
            for g, (a, b) in enumerate(groups):
                pe.wait_ge(s["f_hq"], g + 2)
                for n in range(a, b):
                    if n >= NCH:
                        pe.wait_ge(s["f_hdone"], n - NCH + 2)
                    for k in range(FC):
                        last = nc.tensor.matmul(pm[0:TT, n % NCH, 0:D], hq[:, k, n * TT:(n + 1) * TT], w2q[:, k, :],
                                                start=(k == 0), stop=(k == FC - 1))
                    last.then_inc(s["f_out_mm"], 1)

        @block.gpsimd
        def _(pool):
            for u in range(2):
                nc.gpsimd.memset(hp[u][:, :, :], 0.0).then_inc(s["f_edge"], 1)
            for g, (a, b) in enumerate(groups):
                pool.wait_ge(s["f_bc2"], g + 2)
                nc.gpsimd.tensor_tensor(act1[:, 0:MP, a * TT:b * TT], act1[:, 0:MP, a * TT:b * TT],
                                        bc[:, a * TT:b * TT].unsqueeze(1).broadcast_to([P, MP, (b - a) * TT]), ALU.mult
                                        ).then_inc(s["f_scaled"], 1)

        @block.vector
        def _(dve):
            link = chain(dve, s["f_v"])
            nc.vector.memset(ones[:, :], 1.0).then_inc(s["f_ones"], 1)
            link(nc.vector.tensor_copy(identb[:, :], ident[:, :]))
            link(nc.vector.tensor_reduce(mx[:, :], x[:, :, :], X, ALU.max, apply_absolute_value=True))
            link(nc.vector.tensor_scalar(mx[:, :], mx[:, :], 1e-5, None, ALU.max))
            link(nc.vector.reciprocal(sc[:, :], mx[:, :]))
            link(nc.vector.tensor_scalar(sc[:, :], sc[:, :], 127.0, None, ALU.mult))
            link(nc.vector.tensor_tensor(x[:, :, :], x[:, :, :], sc[:, :].unsqueeze(2).broadcast_to([TT, NT, D]),
                                         ALU.mult))
            link(nc.vector.tensor_scalar(x[:, :, :], x[:, :, :], ROUND, -ROUND, ALU.add, ALU.add))
            nc.vector.tensor_scalar(xb[:, :, :], x[:, :, :], 127.0, -128.0, ALU.min, ALU.max).then_inc(s["f_xq"], 1)
            dve.wait_ge(s["f_wtot"], 2)
            link(nc.vector.tensor_scalar(wmean[:, :], po[:, 0:2], 1.0 / (F * D), 1e-5, ALU.mult, ALU.max))
            link(nc.vector.reciprocal(wscale[:, :], wmean[:, :]))
            for n, (w, wq) in enumerate(((w1, w1q), (w2, w2q))):
                link(nc.vector.tensor_scalar(w[:, :], w[:, :], wscale[:, n:n + 1], None, ALU.mult))
                link(nc.vector.tensor_scalar(w[:, :], w[:, :], ROUND, -ROUND, ALU.add, ALU.add))
                link(nc.vector.tensor_scalar(flat2(wq[:, :, :]), w[:, :], 1.0, -1.0, ALU.min, ALU.max))
            link(nc.vector.tensor_scalar(inv[:, :], mx[:, :], 1.0 / 127.0, wmean[0:TT, 0:1], ALU.mult, ALU.mult))
            eye = ident[0:TT, 0:TT].unsqueeze(1).broadcast_to([TT, NT, TT])
            nc.vector.tensor_tensor(diag[:, :, :], eye, inv[:, :].unsqueeze(2).broadcast_to([TT, NT, TT]), ALU.mult
                                    ).then_inc(s["f_diag"], 1)
            link(nc.vector.memset(amax[:, :], 0.0))
            dve.wait_ge(s["f_bc_mm"], 2)
            for g, (a, b) in enumerate(groups):
                last = nc.vector.tensor_copy(bc[:, a * TT:b * TT], pm[:, g, 0:(b - a) * TT])
            last.then_inc(s["f_bc"], 1)
            dve.wait_ge(s["f_bc"], 2)
            dve.wait_ge(s["f_edge"], 3)
            NB = (B + 1) // NCH

            def widened(c, u):
                if u is not None:
                    dve.wait_ge(s["f_conv3"], c)
                for t in range(NCH):
                    dve.wait_ge(s["f_h_mm"], 3 * c + t + 2)
                    nc.vector.tensor_tensor(hp[u or 0][:, t * NB:(t + 1) * NB, 1:S + 1],
                                            pm[:, t, 0:CH].rearrange("p (b j) -> p b j", j=S),
                                            bc[:, t * CH:(t + 1) * CH].rearrange("p (b j) -> p b j", j=S),
                                            ALU.mult).then_inc(s["f_hp"], 1)

            def taps(c, u):
                dve.wait_ge(s["f_conv1"], c + 2)
                dve.wait_ge(s["f_hp"], 3 * c + 4)
                tap = [flat2(cw[:, span(c, 1), n:n + 1]) for n in range(3)]
                link2(nc.vector.scalar_tensor_tensor(acc[u][:, :, :], hp[u][:, :, 1:S + 1], tap[1], acc[u][:, :, :],
                                                     ALU.mult, ALU.add))
                nc.vector.scalar_tensor_tensor(acc[u][:, :, :], hp[u][:, :, 2:S + 2], tap[2], acc[u][:, :, :],
                                               ALU.mult, ALU.add).then_inc(s["f_conv3"], 1)

            def largest(c):
                dve.wait_ge(s["f_silu"], c + 2)
                dve.wait_ge(s["f_amax"], c + 1)
                one = flat2(act1[:, span(c, 1), :])
                link2(nc.vector.scalar_tensor_tensor(amax[:, :], one, -1.0, amax[:, :], ALU.mult, ALU.max))
                nc.vector.tensor_tensor(amax[:, :], one, amax[:, :], ALU.max).then_inc(s["f_amax"], 1)

            link2 = chain(dve, s["f_v2"])
            widened(0, None)
            widened(1, 1)
            taps(0, 0)
            with dve.Fori(1, FC // 2) as i:
                link2 = chain(dve, s["f_v2"], 4 * (i - 1) + 1)
                for u in range(2):
                    widened(2 * i + u, u)
                    taps(2 * i + u - 1, 1 - u)
                    largest(2 * i + u - 2)
            link2 = chain(dve, s["f_v2"], 4 * (FC // 2 - 1) + 1)
            taps(FC - 1, 1)
            largest(FC - 2)
            largest(FC - 1)
            link3 = chain(dve, s["f_v3"])
            for g, (a, b) in enumerate(groups):
                dve.wait_ge(s["f_max_turned"], g + 2)
                nc.vector.tensor_reduce(mx[:, a:b], pm[0:TT, 0, 0:(b - a) * P].rearrange("p (t f) -> p t f", f=P),
                                        X, ALU.max).then_inc(s["f_max"], 1)
            dve.wait_ge(s["f_max"], 4)
            link3(nc.vector.tensor_scalar(mx[:, :], mx[:, :], 1e-5, None, ALU.max))
            link3(nc.vector.reciprocal(sc[:, :], mx[:, :]))
            link3(nc.vector.tensor_scalar(sc[:, :], sc[:, :], 127.0, None, ALU.mult))
            link3(nc.vector.tensor_scalar(inv[:, :], mx[:, :], 1.0 / 127.0, wmean[0:TT, 1:2], ALU.mult, ALU.mult))
            nc.vector.tensor_tensor(diag[:, :, :], eye, sc[:, :].unsqueeze(2).broadcast_to([TT, NT, TT]), ALU.mult
                                    ).then_inc(s["f_diag2"], 1)
            dve.wait_ge(s["f_bc2_mm"], 2)
            for g, (a, b) in enumerate(groups):
                nc.vector.tensor_copy(bc[:, a * TT:b * TT], pm[:, g, 0:(b - a) * TT]).then_inc(s["f_bc2"], 1)

            def add(g):
                for n in range(*groups[g]):
                    dve.wait_ge(s["f_out_mm"], n + 2)
                    nc.vector.scalar_tensor_tensor(h[:, n, :], pm[0:TT, n % NCH, 0:D], inv[:, n:n + 1], h[:, n, :],
                                                   ALU.mult, ALU.add).then_inc(s["f_hdone"], 1)

            for g, (a, b) in enumerate(groups):
                part = act1[:, :, a * TT:b * TT]
                dve.wait_ge(s["f_bc2"], g + 2)
                link3(nc.vector.tensor_tensor(part[:, MP:, :], part[:, MP:, :],
                                              bc[:, a * TT:b * TT].unsqueeze(1).broadcast_to([P, FC - MP, (b - a) * TT]),
                                              ALU.mult))
                dve.wait_ge(s["f_scaled"], g + 2)
                link3(nc.vector.tensor_scalar(part, part, ROUND, -ROUND, ALU.add, ALU.add))
                nc.vector.tensor_scalar(hq[:, :, a * TT:b * TT], part, 127.0, -128.0, ALU.min, ALU.max
                                        ).then_inc(s["f_hq"], 1)
                if g:
                    add(g - 1)
            add(NCH - 1)


def layout_ffn0(i, o):
    o["f_w1"] = cols(i["L0_ffn_w1"].T, KC).reshape(P, -1)
    o["f_w2"] = cols(i["L0_ffn_w2"].T, 8).reshape(P, -1)
    o["f_cw"] = cols(i["L0_ffn_conv_w"].reshape(-1, 3), 8)
    o["f_cb"] = i["L0_ffn_conv_b"].reshape(8, P).T


GROUPS = [(0, 4), (4, 8), (8, NT)]


def linear(sb, name, w_dram, n, bias_dram):
    w = sb(f"{name}_w", [P, KC, n])
    bias = sb(f"{name}_bias", [TT, n])
    return (w, bias, n), [(w[:, :, :], w_dram), (bias[:, :], bias_dram)]


def projected(nc, name, xT, layer, dst):
    w, bias, n = layer
    with ExitStack() as stack:
        _, ps = bufs(nc, stack)
        s = sems(nc, stack, f"{name}_mm {name}_done")
        s_mm, s_done = (s[f"{name}_{k}"] for k in ("mm", "done"))
        per = BANK // n
        parts = [(a, min(a + per, NT)) for a in range(0, NT, per)]
        NBK = min(4, len(parts))
        pp = ps(f"{name}_pp", [P, NBK, BANK])
        block = stack.enter_context(nc.Block())

        @block.tensor
        def _(pe):
            for m, (a, b) in enumerate(parts):
                if m >= NBK:
                    pe.wait_ge(s_done, m - NBK + 2)
                for t in range(a, b):
                    for k in range(KC):
                        last = nc.tensor.matmul(pp[0:TT, m % NBK, (t - a) * n:(t - a + 1) * n],
                                                xT[:, k, t * TT:(t + 1) * TT], w[:, k, :], start=(k == 0),
                                                stop=(k == KC - 1))
                last.then_inc(s_mm, 1)

        @block.vector
        def _(dve):
            for m, (a, b) in enumerate(parts):
                dve.wait_ge(s_mm, m + 2)
                nc.vector.tensor_tensor(dst[:, a:b, :],
                                        pp[0:TT, m % NBK, 0:(b - a) * n].rearrange("p (t n) -> p t n", n=n),
                                        bias[:, :].unsqueeze(1).broadcast_to([TT, b - a, n]), ALU.add
                                        ).then_inc(s_done, 1)


def stage_gate1(nc, d, h, xT, ident):
    N = 16
    W = D + 2 * N
    with ExitStack() as stack:
        sb, ps = bufs(nc, stack)
        x = sb("g_x", [TT, NT, D])
        pre = sb("g_pre", [TT, NT, W])
        layer, loads = linear(sb, "gp", d["g_w"], W, d["g_bias"])
        norm_transpose(nc, "gn", h, xT, ident, 1e-5, True, x_tok=x, loads=loads)
        projected(nc, "gp", xT, layer, pre)
        s = sems(nc, stack, "g_v g_abs g_exp g_ln")
        e = sb("g_e", [TT, NT, D])
        ln = sb("g_lnb", [TT, NT, D])
        u = sb("g_u", [TT, NT, D])
        bc = sb("g_bc", [TT, NT, N])
        sm = sb("g_sm", [TT, NT])
        block = stack.enter_context(nc.Block())

        @block.scalar
        def _(act):
            nc.scalar.activation(e[:, :, :], pre[:, :, 0:D], ACT.Abs).then_inc(s["g_abs"], 1)
            act.wait_ge(s["g_abs"], 2)
            nc.scalar.activation(e[:, :, :], e[:, :, :], ACT.Exp, scale=-1.0).then_inc(s["g_exp"], 1)
            act.wait_ge(s["g_exp"], 2)
            nc.scalar.activation(ln[:, :, :], e[:, :, :], ACT.Ln, bias=1.0).then_inc(s["g_ln"], 1)

        @block.vector
        def _(dve):
            link = chain(dve, s["g_v"])
            link(nc.vector.tensor_tensor(bc[:, :, :], pre[:, :, D:D + N], pre[:, :, D + N:W], ALU.mult))
            link(nc.vector.tensor_reduce(sm[:, :], bc[:, :, :], X, ALU.add))
            dve.wait_ge(s["g_exp"], 2)
            link(nc.vector.tensor_scalar(u[:, :, :], e[:, :, :], 1.0, None, ALU.add))
            link(nc.vector.scalar_tensor_tensor(u[:, :, :], u[:, :, :], -1.0, e[:, :, :], ALU.add, ALU.subtract))
            dve.wait_ge(s["g_ln"], 2)
            link(nc.vector.tensor_tensor(ln[:, :, :], ln[:, :, :], u[:, :, :], ALU.subtract))
            link(nc.vector.scalar_tensor_tensor(ln[:, :, :], pre[:, :, 0:D], 0.0, ln[:, :, :], ALU.max, ALU.add))
            link(nc.vector.tensor_tensor(ln[:, :, :], ln[:, :, :], x[:, :, :], ALU.mult))
            link(nc.vector.tensor_tensor(ln[:, :, :], ln[:, :, :], sm[:, :].unsqueeze(2).broadcast_to([TT, NT, D]),
                                         ALU.mult))
            link(nc.vector.tensor_tensor(h[:, :, :], h[:, :, :], ln[:, :, :], ALU.add))


def split_x(nc, name, xT, xh, xl):
    with ExitStack() as stack:
        s = sems(nc, stack, f"{name}_high {name}_low")
        block = stack.enter_context(nc.Block())

        @block.scalar
        def _(act):
            for k in range(KC):
                nc.scalar.activation(xh[:, k, :], xT[:, k, :], ACT.Copy).then_inc(s[f"{name}_high"], 1)

        @block.vector
        def _(dve):
            for k in range(KC):
                dve.wait_ge(s[f"{name}_high"], k + 2)
                nc.vector.tensor_tensor(xl[:, k, :], xT[:, k, :], xh[:, k, :].bitcast(F32), ALU.subtract
                                        ).then_inc(s[f"{name}_low"], 1)


def experts(nc, name, w_dram, gates, xh, xl, h, E, U, FC, gated, up_bias=None):
    I = FC * P
    NU = 2 if gated else 1
    UPW = NU * KC * I
    BW = UPW + FC * D
    biases = up_bias is not None
    WC = BW + (D if biases else 0)
    UP = 3 * FC
    NS = 3
    LAG = 1 if FC > 2 else 2
    RB = min(2, (U + 1) // 2)
    with ExitStack() as stack:
        sb, ps = bufs(nc, stack)
        names = ("up_mm act prod high low acc down_mm ones ones_r bias_in " +
                 " ".join(f"used{u}" for u in range(U)) + " " +
                 " ".join(f"w{r} wh{r} split{r}" for r in range(RB))).split()
        made = sems(nc, stack, " ".join(f"{name}_{k}" for k in names))
        s = {k[len(name) + 1:]: v for k, v in made.items()}
        w = [sb(f"{name}_wb{r}", [P, WC]) for r in range(RB)]
        wh = [sb(f"{name}_whb{u}", [P, WC], F32R) for u in range(U)]
        wl = [sb(f"{name}_wlb{u}", [P, WC], F32R) for u in range(U)]
        HW = (LAG + 1) * 4 * TT if LAG == 1 else T
        hh = sb(f"{name}_hh", [P, FC, HW], F32R)
        hl = sb(f"{name}_hl", [P, FC, HW], F32R)
        sg = sb(f"{name}_sg", [P, NS, 4 * TT])
        pu = ps(f"{name}_pu", [P, 2, NU, BANK])
        po = ps(f"{name}_po", [P, 4, BANK])
        if biases:
            b1 = sb(f"{name}_b1", [P, E * FC])
            ones = sb(f"{name}_onesb", [1, TT])
            ones_r = sb(f"{name}_onesr", [1, TT], F32R)
        block = stack.enter_context(nc.Block())
        L = E // U - 1
        units = [(u, g) for u in range(U) for g in range(3)]
        LEAD = max(1, U // 2)

        def ahead(seq, i, j, n):
            r, k = divmod(j + n, len(seq))
            if r and isinstance(i, int) and i == L:
                return None
            return (i + r,) + seq[k]

        def raw(i, u):
            return u % RB, i * (U // RB) + u // RB

        def hid_at(u, g):
            return GROUPS[g][0] * TT if LAG == 2 else (u * 3 + g) % 2 * 4 * TT

        def slot(t, u, g):
            bank, half = divmod(t - GROUPS[g][0], 2)
            return po[0:TT, (u * 3 + g) % 2 * 2 + bank, half * D:(half + 1) * D]

        @block.sync
        def _(sp):
            if biases:
                sp.dma_start(b1[:, :], up_bias).then_inc(s["bias_in"], 16)
            with sp.Fori(0, E // U) as i:
                for u in range(U):
                    r, q = raw(i, u)
                    sp.wait_ge(s[f"split{r}"], q + 1)
                    sp.dma_start(w[r][:, :], w_dram[bass.ds(i * U + u, 1)].rearrange("a p w -> p (a w)")
                                 ).then_inc(s[f"w{r}"], 16)

        @block.gpsimd
        def _(pool):
            with pool.Fori(0, E // U) as i:
                for u in range(U):
                    r, q = raw(i, u)
                    pool.wait_ge(s[f"wh{r}"], q + 2)
                    nc.gpsimd.tensor_tensor(wl[u][:, :], w[r][:, :], wh[u][:, :].bitcast(F32), ALU.subtract
                                            ).then_inc(s[f"split{r}"], 1)

        @block.tensor
        def _(pe):
            def up(i, u, g):
                lo, hi = GROUPS[g]
                N = (hi - lo) * TT
                N += N % 2
                e = i * U + u
                if g == 0:
                    r, q = raw(i, u)
                    pe.wait_ge(s[f"split{r}"], q + 2)
                for f in range(FC):
                    n = g * FC + f
                    pe.wait_ge(s["prod"], e * UP + n + 1)
                    for m in range(NU):
                        dst = pu[:, (n + u * UP) % 2, m, 0:N]
                        for k in range(KC):
                            at = (m * KC + k) * I + f * P
                            w_hi, w_lo = wh[u][:, at:at + P], wl[u][:, at:at + P]
                            x_hi, x_lo = xh[:, k, lo * TT:lo * TT + N], xl[:, k, lo * TT:lo * TT + N]
                            nc.tensor.matmul(dst, w_lo, x_hi, start=(k == 0), stop=False)
                            nc.tensor.matmul(dst, w_hi, x_lo, start=False, stop=False)
                            last = nc.tensor.matmul(dst, w_hi, x_hi, start=False, stop=(k == KC - 1))
                    last.then_inc(s["up_mm"], 1)

            def down(i, u, g):
                lo, hi = GROUPS[g]
                e = i * U + u
                pe.wait_ge(s["low"], e * UP + (g + 1) * FC + 3)
                for t in range(lo, hi):
                    if (t - lo) % 2 == 0:
                        a, b = GROUPS[(g + 1) % 3]
                        pe.wait_ge(s["acc"], (e - (g < 2)) * NT + min(a + t - lo + 2, b) + 11)
                    o = slot(t, u, g)
                    if biases:
                        nc.tensor.matmul(o, ones_r[:, :], wh[u][0:1, BW:WC], start=True, stop=False)
                        nc.tensor.matmul(o, ones_r[:, :], wl[u][0:1, BW:WC], start=False, stop=False)
                    for f in range(FC):
                        at = UPW + f * D
                        w_hi, w_lo = wh[u][:, at:at + D], wl[u][:, at:at + D]
                        o_h = hid_at(u, g) + (t - lo) * TT
                        h_hi, h_lo = (x[:, f, o_h:o_h + TT] for x in (hh, hl))
                        nc.tensor.matmul(o, h_lo, w_hi, start=(f == 0 and not biases), stop=False)
                        nc.tensor.matmul(o, h_hi, w_lo, start=False, stop=False)
                        last = nc.tensor.matmul(o, h_hi, w_hi, start=False, stop=(f == FC - 1))
                    last.then_inc(s["down_mm"], 1)

            def turn(i):
                for j, (u, g) in enumerate(units):
                    nxt = ahead(units, i, j, 1)
                    if nxt is not None and LAG == 1:
                        up(*nxt)
                    down(i, u, g)
                    nxt = ahead(units, i, j, 2)
                    if nxt is not None and LAG == 2:
                        up(*nxt)

            if biases:
                pe.wait_ge(s["ones_r"], 2)
            up(0, 0, 0)
            if LAG == 2:
                up(0, 0, 1)
            if L:
                with pe.Fori(0, L) as i:
                    turn(i)
            turn(L)

        @block.scalar
        def _(act):
            def weights(i, u):
                r, q = raw(i, u)
                act.wait_ge(s[f"w{r}"], q * 16 + 17)
                act.wait_ge(s[f"used{u}"], i + 1)
                nc.scalar.activation(wh[u][:, :], w[r][:, :], ACT.Copy).then_inc(s[f"wh{r}"], 1)

            def main(i, u, n):
                g, f = divmod(n, FC)
                lo, hi = GROUPS[g]
                N = (hi - lo) * TT
                e = i * U + u
                act.wait_ge(s["up_mm"], e * UP + n + 2)
                act.wait_ge(s["low"], e * UP + n + 1)
                src = pu[:, (n + u * UP) % 2, 0, 0:N]
                if gated:
                    nc.scalar.activation(sg[:, n % NS, 0:N], src, ACT.Silu).then_inc(s["act"], 1)
                else:
                    nc.scalar.activation(sg[:, n % NS, 0:N], src, ACT.Relu, bias=b1[:, span(e * FC + f, 1)]
                                         ).then_inc(s["prod"], 1)

            def high(i, u, n):
                g, f = divmod(n, FC)
                lo, hi = GROUPS[g]
                e = i * U + u
                act.wait_ge(s["prod"], e * UP + n + 3)
                at = hid_at(u, g)
                nc.scalar.activation(hh[:, f, at:at + (hi - lo) * TT], sg[:, n % NS, 0:(hi - lo) * TT], ACT.Copy
                                     ).then_inc(s["high"], 1)

            def unit(i, u, g):
                for n in range(g * FC, (g + 1) * FC):
                    main(i, u, n)
                    high(i, u, n)
                if g == (0 if U > 2 else 1):
                    nxt = ahead([(x,) for x in range(U)], i, u, LEAD)
                    if nxt is not None:
                        weights(*nxt)

            if biases:
                act.wait_ge(s["bias_in"], 17)
            for u in range(LEAD):
                weights(0, u)
            if L:
                with act.Fori(0, L) as i:
                    for u, g in units:
                        unit(i, u, g)
            for u, g in units:
                unit(L, u, g)

        @block.vector
        def _(dve):
            nc.vector.nop().then_inc(s["prod"], 1)
            nc.vector.nop().then_inc(s["low"], 2)
            nc.vector.nop().then_inc(s["acc"], 10)
            if biases:
                nc.vector.memset(ones[:, :], 1.0).then_inc(s["ones"], 1)
                dve.wait_ge(s["ones"], 2)
                nc.vector.tensor_copy(ones_r[:, :], ones[:, :]).then_inc(s["ones_r"], 1)

            def add(i, u, g):
                lo, hi = GROUPS[g]
                e = i * U + u
                dve.wait_ge(s["acc"], e * NT + hi)
                for t in range(lo, hi):
                    if (t - lo) % 2 == 0:
                        dve.wait_ge(s["down_mm"], e * NT + min(t + 2, hi) + 1)
                    nc.vector.scalar_tensor_tensor(h[:, t, :], slot(t, u, g), flat2(gates[:, t:t + 1, span(e, 1)]),
                                                   h[:, t, :], ALU.mult, ALU.add).then_inc(s["acc"], 1)
                if g == 2:
                    nc.vector.nop().then_inc(s[f"used{u}"], 1)

            def unit(i, u, g, before):
                lo, hi = GROUPS[g]
                N = (hi - lo) * TT
                for f in range(FC):
                    n = g * FC + f
                    m = (i * U + u) * UP + n
                    if gated:
                        dve.wait_ge(s["act"], m + 2)
                        nc.vector.tensor_tensor(sg[:, n % NS, 0:N], sg[:, n % NS, 0:N],
                                                pu[:, (n + u * UP) % 2, 1, 0:N], ALU.mult).then_inc(s["prod"], 1)
                    if f == 0 and before is not None and LAG == 2:
                        add(*before)
                    dve.wait_ge(s["high"], m + 2)
                    at = slice(hid_at(u, g), hid_at(u, g) + N)
                    nc.vector.tensor_tensor(hl[:, f, at], sg[:, n % NS, 0:N], hh[:, f, at].bitcast(F32), ALU.subtract
                                            ).then_inc(s["low"], 1)
                if before is not None and LAG == 1:
                    add(*before)

            def turn(i):
                for j, (u, g) in enumerate(units):
                    nxt = ahead(units, i, j, LAG)
                    if nxt is not None:
                        unit(*nxt, before=(i, u, g))
                    else:
                        add(i, u, g)

            unit(0, 0, 0, None)
            if LAG == 2:
                unit(0, 0, 1, None)
            if L:
                with dve.Fori(0, L) as i:
                    turn(i)
            turn(L)


def stage_ffn1(nc, d, h, xT, ident):
    E = 4
    with ExitStack() as stack:
        sb, ps = bufs(nc, stack)
        layer, loads = linear(sb, "ep", d["e_wu"], 1, d["e_bu"])
        turn = sb("e_turn", [TT, E, E])
        norm_transpose(nc, "en", h, xT, ident, 1e-5, True, loads=loads + [(turn[:, :, :], d["e_turn"])])
        z = sb("e_z", [TT, NT, 1])
        gates = sb("e_gates", [TT, NT, E])
        projected(nc, "ep", xT, layer, z)
        with ExitStack() as inner:
            sb2, _ = bufs(nc, inner)
            s = sems(nc, inner, "e_u e_v")
            u = sb2("e_ub", [TT, NT, 1])
            w = sb2("e_w", [TT, NT, 1])
            t = sb2("e_t", [TT, NT, E])
            block = inner.enter_context(nc.Block())

            @block.scalar
            def _(act):
                nc.scalar.activation(u[:, :, :], z[:, :, :], ACT.Sigmoid).then_inc(s["e_u"], 1)

            @block.vector
            def _(dve):
                link = chain(dve, s["e_v"])
                dve.wait_ge(s["e_u"], 2)
                for r in range(E):
                    if r == 0:
                        link(nc.vector.tensor_copy(w[:, :, :], u[:, :, :]))
                    else:
                        link(nc.vector.tensor_scalar(w[:, :, :], u[:, :, :], float(E), float(r), ALU.mult, ALU.is_gt))
                        link(nc.vector.tensor_tensor(w[:, :, :], w[:, :, :], u[:, :, :], ALU.mult))
                        link(nc.vector.tensor_scalar(w[:, :, :], w[:, :, :], 1.0 / (r + 1), None, ALU.mult))
                    dst = gates if r == 0 else t
                    link(nc.vector.tensor_tensor(dst[:, :, :], w[:, :, :].broadcast_to([TT, NT, E]),
                                                 turn[:, r:r + 1, :].broadcast_to([TT, NT, E]), ALU.mult))
                    if r:
                        link(nc.vector.tensor_tensor(gates[:, :, :], gates[:, :, :], t[:, :, :], ALU.add))
        xh, xl = (sb(f"e_x{n}", [P, KC, T + 1], F32R) for n in "hl")
        split_x(nc, "ex", xT, xh, xl)
        experts(nc, "e", d["e_w"], gates, xh, xl, h, E, 2, 8, False, d["e_b1"])


def layout_l1(i, o):
    o["g_w"] = cols(np.concatenate([i[f"L1_attn_W{n}"].T for n in (1, 2, 3)], 1), KC)
    o["g_bias"] = rep(np.concatenate([i[f"L1_attn_b{n}"] for n in (1, 2, 3)]))
    o["e_wu"] = cols(i["L1_ffn_Wu"], KC)
    o["e_bu"] = rep(i["L1_ffn_bu"])
    pos = np.tile(np.arange(S), G)[:, None, None]
    r, e = np.arange(4)[None, :, None], np.arange(4)[None, None, :]
    o["e_turn"] = ((pos + r) % 4 == e).astype(np.float32)
    b2 = np.zeros((4, P, D), np.float32)
    b2[:, 0] = i["L1_ffn_b2"]
    o["e_w"] = np.concatenate([up_cols(i["L1_ffn_W1"]), up_cols(i["L1_ffn_W2"]), b2], 2)
    o["e_b1"] = i["L1_ffn_b1"].reshape(4 * 8, P).T


def up_cols(w):
    e, k, n = w.shape
    return w.reshape(e, k // P, P, n).transpose(0, 2, 1, 3).reshape(e, P, -1)


def stage_scan(nc, d, h, xT, ident):
    DI, R, N, K = 512, 64, 16, 4
    C = DI // P
    SP = S + K - 1
    NB = (B + 1) // NCH
    W = C * CH
    with ExitStack() as stack:
        sb, ps = bufs(nc, stack)
        xc = sb("s_xc", [P, NCH, C, CH])
        res = sb("s_res", [P, NCH, C, CH])
        delta = sb("s_delta", [P, NCH, C, CH])
        a = sb("s_a", [P, N, C])
        dd = sb("s_d", [P, C])
        xdbl = sb("s_xdbl", [R + 2 * N, T])
        bc_dram = nc.dram_tensor("s_bc", (NCH, N, 2, CH), F32, kind="Internal").ap()
        with ExitStack() as inner:
            sb2, ps2 = bufs(nc, inner)
            w_in = sb2("s_w_in", [P, KC, 2 * DI])
            w_x = sb2("s_w_x", [P, C, R + 2 * N])
            w_dt = sb2("s_w_dt", [R, DI])
            cw = sb2("s_cw", [P, C, K])
            cb = sb2("s_cb", [P, C])
            b_dt = sb2("s_b_dt", [P, C])
            norm_transpose(nc, "sn", h, xT, ident, 1e-5, True, loads=[
                (w_in[:, :, :], d["s_w_in"]), (w_x[:, :, :], d["s_w_x"]), (w_dt[:, :], d["s_w_dt"]),
                (cw[:, :, :], d["s_cw"]), (cb[:, :], d["s_cb"]), (b_dt[:, :], d["s_b_dt"]),
                (a[:, :, :], d["s_a"]), (dd[:, :], d["s_d"])])
            s = sems(nc, inner, "s_edge s_px_mm s_x s_tap0 s_taps s_xc_done s_res_done s_dbl_mm s_dbl s_dt_mm "
                                "s_dt s_e s_ln s_v s_a_exp s_bc_out s_dve")
            xp = [sb2(f"s_xp{n}", [P, B + 1, SP]) for n in range(2)]
            acc = [sb2(f"s_acc{n}", [P, B + 1, S]) for n in range(2)]
            e = sb2("s_eb", [P, NCH, C, CH])
            ln = sb2("s_lnb", [P, NCH, C, CH])
            pp = ps2("s_pp", [P, 6, BANK])
            block = inner.enter_context(nc.Block())

            @block.sync
            def _(sp):
                sp.wait_ge(s["s_dbl"], NCH + 1)
                for t in range(NCH):
                    for m in range(2):
                        sp.dma_start(bc_dram[t, :, m, :], xdbl[R + m * N:R + (m + 1) * N, t * CH:(t + 1) * CH]
                                     ).then_inc(s["s_bc_out"], 16)
                sp.wait_ge(s["s_bc_out"], 6 * 16 + 1)

            @block.tensor
            def _(pe):
                for n in range(2 * C * NCH):
                    j, t = divmod(n, NCH)
                    if n >= 6:
                        m = n - 5
                        pe.wait_ge(s["s_x"], m + 1) if m <= C * NCH else pe.wait_ge(s["s_res_done"], m - C * NCH + 1)
                    for k in range(KC):
                        last = nc.tensor.matmul(pp[:, n % 6, 0:CH], w_in[:, k, j * P:(j + 1) * P],
                                                xT[:, k, t * CH:(t + 1) * CH], start=(k == 0), stop=(k == KC - 1))
                    last.then_inc(s["s_px_mm"], 1)
                pe.wait_ge(s["s_xc_done"], C + 1)
                pe.wait_ge(s["s_res_done"], C * NCH + 1)
                for t in range(NCH):
                    for c in range(C):
                        last = nc.tensor.matmul(pp[0:R + 2 * N, t, 0:CH], w_x[:, c, :], xc[:, t, c, :],
                                                start=(c == 0), stop=(c == C - 1))
                    last.then_inc(s["s_dbl_mm"], 1)
                for n in range(C * NCH):
                    t, c = divmod(n, C)
                    pe.wait_ge(s["s_dbl"], t + 2)
                    if n >= 3:
                        pe.wait_ge(s["s_dt"], n - 1)
                    nc.tensor.matmul(pp[:, 3 + n % 3, 0:CH], w_dt[:, c * P:(c + 1) * P], xdbl[0:R, t * CH:(t + 1) * CH],
                                     start=True, stop=True).then_inc(s["s_dt_mm"], 1)

            @block.scalar
            def _(act):
                nc.scalar.activation(a[:, :, :], a[:, :, :], ACT.Exp).then_inc(s["s_a_exp"], 1)
                for c in range(C):
                    act.wait_ge(s["s_x"], 3 * c + 4)
                    nc.scalar.activation(acc[c % 2][:, :, :], xp[c % 2][:, :, 0:S], ACT.Identity, scale=cw[:, c, 0:1],
                                         bias=cb[:, c:c + 1]).then_inc(s["s_tap0"], 1)
                    act.wait_ge(s["s_taps"], c + 2)
                    nc.scalar.activation(xc[:, :, c, :], acc[c % 2][:, :, :].rearrange("p (t b) j -> p t (b j)", t=NCH),
                                         ACT.Silu).then_inc(s["s_xc_done"], 1)
                for n in range(C * NCH):
                    c, t = divmod(n, NCH)
                    act.wait_ge(s["s_px_mm"], C * NCH + n + 2)
                    nc.scalar.activation(res[:, t, c, :], pp[:, (C * NCH + n) % 6, 0:CH], ACT.Silu
                                         ).then_inc(s["s_res_done"], 1)
                for t in range(NCH):
                    act.wait_ge(s["s_dbl_mm"], t + 2)
                    nc.scalar.activation(xdbl[:, t * CH:(t + 1) * CH], pp[0:R + 2 * N, t, 0:CH], ACT.Copy
                                         ).then_inc(s["s_dbl"], 1)
                act.wait_ge(s["s_dt"], C * NCH + 1)
                nc.scalar.activation(e[:, :, :, :], delta[:, :, :, :], ACT.Abs).then_inc(s["s_e"], 1)
                act.wait_ge(s["s_e"], 2)
                nc.scalar.activation(e[:, :, :, :], e[:, :, :, :], ACT.Exp, scale=-1.0).then_inc(s["s_e"], 1)
                act.wait_ge(s["s_e"], 3)
                nc.scalar.activation(ln[:, :, :, :], e[:, :, :, :], ACT.Ln, bias=1.0).then_inc(s["s_ln"], 1)

            @block.gpsimd
            def _(pool):
                for n in range(2):
                    nc.gpsimd.memset(xp[n][:, :, :], 0.0).then_inc(s["s_edge"], 1)

            @block.vector
            def _(dve):
                link = chain(dve, s["s_v"])
                dve.wait_ge(s["s_edge"], 3)
                for c in range(C):
                    if c >= 2:
                        dve.wait_ge(s["s_tap0"], c)
                        dve.wait_ge(s["s_taps"], c)
                    for t in range(NCH):
                        dve.wait_ge(s["s_px_mm"], 3 * c + t + 2)
                        nc.vector.tensor_copy(xp[c % 2][:, t * NB:(t + 1) * NB, K - 1:SP],
                                              pp[:, (3 * c + t) % 6, 0:CH].rearrange("p (b j) -> p b j", j=S)
                                              ).then_inc(s["s_x"], 1)
                    dve.wait_ge(s["s_x"], 3 * c + 4)
                    dve.wait_ge(s["s_tap0"], c + 2)
                    for k in range(1, K):
                        ins = nc.vector.scalar_tensor_tensor(acc[c % 2][:, :, :], xp[c % 2][:, :, k:k + S],
                                                             cw[:, c, k:k + 1], acc[c % 2][:, :, :], ALU.mult, ALU.add)
                        if k < K - 1:
                            link(ins)
                        else:
                            ins.then_inc(s["s_taps"], 1)
                dve.wait_ge(s["s_a_exp"], 2)
                link(nc.vector.tensor_scalar(a[:, :, :], a[:, :, :], -1.0, None, ALU.mult))
                for n in range(C * NCH):
                    t, c = divmod(n, C)
                    dve.wait_ge(s["s_dt_mm"], n + 2)
                    nc.vector.tensor_scalar(delta[:, t, c, :], pp[:, 3 + n % 3, 0:CH], b_dt[:, c:c + 1], None, ALU.add
                                            ).then_inc(s["s_dt"], 1)
                u, lf, ef, df = (x[:, :, :, :].rearrange("p t c n -> p (t c n)") for x in (e, ln, e, delta))
                tmp = flat2(acc[0][:, :, :])
                dve.wait_ge(s["s_ln"], 2)
                for t in range(NCH * C):
                    at = slice(t * CH, (t + 1) * CH)
                    one = tmp[:, (t % 3) * CH:(t % 3 + 1) * CH]
                    link(nc.vector.tensor_scalar(one, ef[:, at], 1.0, None, ALU.add))
                    link(nc.vector.scalar_tensor_tensor(ef[:, at], one, -1.0, ef[:, at], ALU.add, ALU.subtract))
                link(nc.vector.tensor_tensor(lf, lf, ef, ALU.subtract))
                link(nc.vector.scalar_tensor_tensor(df, df, 0.0, lf, ALU.max, ALU.add))

        with ExitStack() as inner:
            sb2, ps2 = bufs(nc, inner)
            NBC = 4
            s = sems(nc, inner, "c_du c_exp c_start c_zero c_y_mm c_y c_v c_ym c_w c_out_mm c_out " +
                     " ".join(f"c_da{u} c_dbu{u} c_scan{u} c_yt{u} c_sum{u}" for u in range(2)) +
                     "".join(f" c_bc{b}" for b in range(NBC)))
            v = s
            du = sb2("c_dub", [P, NCH, C, CH])
            bc = [sb2(f"c_bcb{b}", [P, 2, CH]) for b in range(NBC)]
            da = [sb2(f"c_dab{u}", [P, W]) for u in range(2)]
            dbu = [sb2(f"c_dbub{u}", [P, W]) for u in range(2)]
            st = [sb2(f"c_st{u}", [P, W]) for u in range(2)]
            yt = [sb2(f"c_ytb{u}", [P, W]) for u in range(2)]
            zero = sb2("c_zerob", [P, CH], BF16)
            w_out = sb2("c_w_out", [P, C, D])
            ycol = sb2("c_ycol", [P, C, T])
            pc = ps2("c_pc", [P, C, BANK])
            po = ps2("c_po", [P, 2, BANK])
            block = inner.enter_context(nc.Block())

            @block.sync
            def _(sp):
                sp.dma_start(w_out[:, :, :], d["s_w_out"]).then_inc(s["c_w"], 16)

                def load(t, i, b):
                    sp.dma_start(bc[b][:, :, :].rearrange("p m n -> p (m n)"),
                                 bc_dram[t, span(NBC * i + b, 1)].rearrange("a m n -> a (m n)")
                                 .broadcast_to([P, 2 * CH])).then_inc(s[f"c_bc{b}"], 16)

                for b in range(NBC):
                    load(0, 0, b)
                for t in range(NCH):
                    with sp.Fori(0 if t else 1, N // NBC) as i:
                        for b in range(NBC):
                            m = t * 8 + 2 * i + b // 2
                            sp.wait_ge(s[f"c_dbu{b % 2}"], m)
                            sp.wait_ge(s[f"c_yt{b % 2}"], m)
                            load(t, i, b)

            @block.scalar
            def _(act):
                for t in range(NCH):
                    with act.Fori(0, N // 2) as i:
                        for u in range(2):
                            act.wait_ge(v[f"c_scan{u}"], t * 8 + i + 1)
                            for c in range(C):
                                last = nc.scalar.activation(da[u][:, c * CH:(c + 1) * CH], delta[:, t, c, :], ACT.Exp,
                                                            scale=flat2(a[:, bass.ds(2 * i + u, 1), c:c + 1]))
                            last.then_inc(s["c_exp"], 1)

            @block.gpsimd
            def _(pool):
                pool.wait_ge(s["c_du"], 2)
                for t in range(NCH):
                    with pool.Fori(0, N // NBC) as i:
                        for b in range(NBC):
                            u = b % 2
                            pool.wait_ge(v[f"c_scan{u}"], t * 8 + 2 * i + b // 2 + 1)
                            pool.wait_ge(v[f"c_bc{b}"], (t * (N // NBC) + i) * 16 + 17)
                            pool.wait_ge(s["c_exp"], t * 16 + NBC * i + b + 2)
                            nc.gpsimd.tensor_tensor(dbu[u][:, :].rearrange("p (c n) -> p c n", c=C), du[:, t, :, :],
                                                    bc[b][:, 0:1, :].broadcast_to([P, C, CH]), ALU.mult
                                                    ).then_inc(v[f"c_dbu{u}"], 1)
                            nc.gpsimd.memset(da[u][:, :].rearrange("p (b j) -> p b j", j=S)[:, :, 0:1], 0.0
                                             ).then_inc(v[f"c_da{u}"], 1)

            @block.tensor
            def _(pe):
                pe.wait_ge(s["c_zero"], 2)
                for t in range(NCH):
                    pe.wait_ge(s["c_y"], t + 1)
                    for c in range(C):
                        nc.tensor.matmul(pc[:, c, 0:CH], zero[:, 0:P], zero[:, :], start=True, stop=False,
                                         skip_group_check=True)
                    with pe.Fori(0, N // 2) as i:
                        for u in range(2):
                            pe.wait_ge(v[f"c_yt{u}"], t * 8 + i + 2)
                            for c in range(C):
                                last = nc.tensor.matmul(pc[:, c, 0:CH], ident[:, :], yt[u][:, c * CH:(c + 1) * CH],
                                                        start=False, stop=False, skip_group_check=True)
                            last.then_inc(v[f"c_sum{u}"], 1)
                    for c in range(C):
                        last = nc.tensor.matmul(pc[:, c, 0:CH], zero[:, 0:P], zero[:, :], start=False, stop=True,
                                                skip_group_check=True)
                    last.then_inc(s["c_y_mm"], 1)
                pe.wait_ge(s["c_w"], 17)
                pe.wait_ge(s["c_ym"], 2)
                for n in range(NT):
                    if n >= 2:
                        pe.wait_ge(s["c_out"], n)
                    for c in range(C):
                        last = nc.tensor.matmul(po[0:TT, n % 2, 0:D], ycol[:, c, n * TT:(n + 1) * TT], w_out[:, c, :],
                                                start=(c == 0), stop=(c == C - 1))
                    last.then_inc(s["c_out_mm"], 1)

            @block.vector
            def _(dve):
                link = chain(dve, s["c_v"])
                nc.vector.memset(zero[:, :], 0.0).then_inc(s["c_zero"], 1)
                nc.vector.tensor_tensor(du[:, :, :, :].rearrange("p t c n -> p (t c n)"),
                                        delta[:, :, :, :].rearrange("p t c n -> p (t c n)"),
                                        xc[:, :, :, :].rearrange("p t c n -> p (t c n)"), ALU.mult
                                        ).then_inc(s["c_du"], 1)
                for t in range(NCH):
                    with dve.Fori(0, N // NBC) as i:
                        for b in range(NBC):
                            u = b % 2
                            m = t * 8 + 2 * i + b // 2
                            dve.wait_ge(v[f"c_da{u}"], m + 2)
                            dve.wait_ge(v[f"c_dbu{u}"], m + 2)
                            dve.wait_ge(v[f"c_yt{u}"], m + 1)
                            nc.vector.tensor_tensor_scan(st[u][:, :], da[u][:, :], dbu[u][:, :], 0.0, ALU.mult, ALU.add
                                                         ).then_inc(v[f"c_scan{u}"], 1)
                            dve.wait_ge(v[f"c_scan{u}"], m + 2)
                            dve.wait_ge(v[f"c_bc{b}"], (t * (N // NBC) + i) * 16 + 17)
                            dve.wait_ge(v[f"c_sum{u}"], m + 1)
                            nc.vector.tensor_tensor(yt[u][:, :].rearrange("p (c n) -> p c n", c=C),
                                                    st[u][:, :].rearrange("p (c n) -> p c n", c=C),
                                                    bc[b][:, 1:2, :].broadcast_to([P, C, CH]), ALU.mult
                                                    ).then_inc(v[f"c_yt{u}"], 1)
                    dve.wait_ge(s["c_y_mm"], t + 2)
                    for c in range(C):
                        last = nc.vector.scalar_tensor_tensor(ycol[:, c, t * CH:(t + 1) * CH], xc[:, t, c, :],
                                                              dd[:, c:c + 1], pc[:, c, 0:CH], ALU.mult, ALU.add)
                    last.then_inc(s["c_y"], 1)
                dve.wait_ge(s["c_y"], NCH + 1)
                nc.vector.tensor_tensor(ycol[:, :, :].rearrange("p c (t n) -> p t c n", t=NCH),
                                        ycol[:, :, :].rearrange("p c (t n) -> p t c n", t=NCH), res[:, :, :, :],
                                        ALU.mult).then_inc(s["c_ym"], 1)
                for n in range(NT):
                    dve.wait_ge(s["c_out_mm"], n + 2)
                    nc.vector.tensor_tensor(h[:, n, :], h[:, n, :], po[0:TT, n % 2, 0:D], ALU.add).then_inc(s["c_out"], 1)


def layout_scan(i, o):
    o["s_w_in"] = cols(i["L2_attn_W_in"], KC)
    o["s_w_x"] = cols(i["L2_attn_W_x"], 4)
    o["s_w_dt"] = i["L2_attn_W_dt"]
    o["s_cw"] = i["L2_attn_conv_w"].reshape(4, 4, P).transpose(2, 1, 0)
    o["s_cb"] = i["L2_attn_conv_b"].reshape(4, P).T
    o["s_b_dt"] = i["L2_attn_b_dt"].reshape(4, P).T
    o["s_a"] = i["L2_attn_A_log"].reshape(4, P, 16).transpose(1, 2, 0)
    o["s_d"] = i["L2_attn_D"].reshape(4, P).T
    o["s_w_out"] = cols(i["L2_attn_W_out"], 4)


def router(sb, name, w_dram, bias_dram, iota_dram, E):
    layer, loads = linear(sb, name, w_dram, E, bias_dram)
    iota = sb(f"{name}_iota", [TT, E])
    return layer, iota, loads + [(iota[:, :], iota_dram)]


def top2_gates(nc, name, logits, gates, iota, ident, E, capacity=None):
    with ExitStack() as stack:
        sb, ps = bufs(nc, stack)
        made = sems(nc, stack, " ".join(f"{name}_{k}" for k in "v max exp hot turned cum back m8 idx".split()))
        s = {k[len(name) + 1:]: x for k, x in made.items()}
        mx = sb(f"{name}_mx", [TT, NT])
        p = sb(f"{name}_p", [TT, NT, E])
        m8 = sb(f"{name}_m8b", [TT, NT, 8])
        idx = sb(f"{name}_idxb", [TT, NT, 8], U32)
        pick = sb(f"{name}_pick", [TT, NT, 2])
        hot = sb(f"{name}_hotb", [TT, NT, 2, E])
        hotT = sb(f"{name}_hotT", [2 * E, T])
        cum = sb(f"{name}_cumb", [2 * E, T])
        one = sb(f"{name}_one", [2 * E, T])
        pt = ps(f"{name}_pt", [P, NCH, BANK])
        pb = ps(f"{name}_pb", [P, BANK])
        block = stack.enter_context(nc.Block())

        @block.scalar
        def _(act):
            act.wait_ge(s["max"], 2)
            nc.scalar.activation(p[:, :, :], p[:, :, :], ACT.Exp).then_inc(s["exp"], 1)

        @block.tensor
        def _(pe):
            if capacity is not None:
                pe.wait_ge(s["hot"], 2)
                for g, (a, b) in enumerate(GROUPS):
                    for t in range(a, b):
                        last = nc.tensor.transpose(pt[0:2 * E, g, (t - a) * TT:(t - a + 1) * TT],
                                                   hot[:, t, :, :].rearrange("p k e -> p (k e)"), ident[0:TT, 0:TT])
                last.then_inc(s["turned"], 1)
                pe.wait_ge(s["cum"], 2)
                for t in range(NT):
                    last = nc.tensor.transpose(pb[0:TT, t * 2 * E:(t + 1) * 2 * E], cum[:, t * TT:(t + 1) * TT],
                                               ident[0:2 * E, 0:2 * E])
                last.then_inc(s["back"], 1)

        @block.vector
        def _(dve):
            link = chain(dve, s["v"])
            wide = [TT, NT, E]
            link(nc.vector.tensor_reduce(mx[:, :], logits[:, :, :], X, ALU.max))
            nc.vector.tensor_tensor(p[:, :, :], logits[:, :, :], mx[:, :].unsqueeze(2).broadcast_to(wide),
                                    ALU.subtract).then_inc(s["max"], 1)
            dve.wait_ge(s["exp"], 2)
            link(nc.vector.tensor_reduce(mx[:, :], p[:, :, :], X, ALU.add))
            link(nc.vector.reciprocal(mx[:, :], mx[:, :]))
            link(nc.vector.tensor_tensor(p[:, :, :], p[:, :, :], mx[:, :].unsqueeze(2).broadcast_to(wide), ALU.mult))
            for t in range(NT):
                last = nc.vector.max(m8[:, t, :], p[:, t, :])
            last.then_inc(s["m8"], 1)
            dve.wait_ge(s["m8"], 2)
            for t in range(NT):
                last = nc.vector.max_index(idx[:, t, :], m8[:, t, :], p[:, t, :])
            last.then_inc(s["idx"], 1)
            dve.wait_ge(s["idx"], 2)
            link(nc.vector.tensor_copy(pick[:, :, :], idx[:, :, 0:2]))
            for k in range(2):
                last = nc.vector.tensor_tensor(hot[:, :, k, :], pick[:, :, k:k + 1].broadcast_to(wide),
                                               iota[:, :].unsqueeze(1).broadcast_to(wide), ALU.is_equal)
            if capacity is None:
                link(last)
                link(nc.vector.tensor_tensor(mx[:, :].unsqueeze(2), m8[:, :, 0:1], m8[:, :, 1:2], ALU.add))
                link(nc.vector.reciprocal(mx[:, :], mx[:, :]))
                link(nc.vector.tensor_tensor(pick[:, :, :], m8[:, :, 0:2],
                                             mx[:, :].unsqueeze(2).broadcast_to([TT, NT, 2]), ALU.mult))
                w = pick
            else:
                last.then_inc(s["hot"], 1)
                link(nc.vector.memset(one[:, :], 1.0))
                dve.wait_ge(s["turned"], 2)
                for g, (a, b) in enumerate(GROUPS):
                    last = nc.vector.tensor_copy(hotT[:, a * TT:b * TT], pt[0:2 * E, g, 0:(b - a) * TT])
                link(last)
                link(nc.vector.tensor_tensor_scan(cum[:, :], one[:, :], hotT[:, :], 0.0, ALU.mult, ALU.add))
                nc.vector.scalar_tensor_tensor(cum[:, :], cum[:, :], float(capacity), hotT[:, :], ALU.is_le, ALU.mult
                                               ).then_inc(s["cum"], 1)
                dve.wait_ge(s["back"], 2)
                link(nc.vector.tensor_copy(hot[:, :, :, :].rearrange("p t k e -> p (t k e)"), pb[0:TT, 0:NT * 2 * E]))
                w = m8
            for k in range(2):
                last = nc.vector.tensor_tensor(hot[:, :, k, :], hot[:, :, k, :],
                                               w[:, :, k:k + 1].broadcast_to(wide), ALU.mult)
            link(last)
            link(nc.vector.tensor_tensor(gates[:, :, 0:E], hot[:, :, 0, :], hot[:, :, 1, :], ALU.add))
            if gates.shape[2] > E:
                link(nc.vector.memset(gates[:, :, E:], 1.0))


def stage_moe2(nc, d, h, xT, ident):
    E = 16
    capacity = max(1, math.ceil(B * S * 2 / E * 1.25))
    with ExitStack() as stack:
        sb, _ = bufs(nc, stack)
        layer, iota, loads = router(sb, "mp", d["m_router"], d["m_zero"], d["m_iota"], E)
        norm_transpose(nc, "mn", h, xT, ident, 1e-5, True, loads=loads)
        logits = sb("m_logits", [TT, NT, E])
        gates = sb("m_gates", [TT, NT, E])
        projected(nc, "mp", xT, layer, logits)
        top2_gates(nc, "mt", logits, gates, iota, ident, E, capacity)
        xh, xl = (sb(f"m_x{n}", [P, KC, T + 1], F32R) for n in "hl")
        split_x(nc, "mx", xT, xh, xl)
        experts(nc, "m", d["m_w"], gates, xh, xl, h, E, 4, 2, True)


def layout_moe2(i, o):
    o["m_router"] = cols(i["L2_ffn_router_w"], KC)
    o["m_zero"] = rep(np.zeros(16, np.float32))
    o["m_iota"] = rep(np.arange(16, dtype=np.float32))
    o["m_w"] = np.concatenate([up_cols(i[f"L2_ffn_{n}_w"]) for n in ("gate", "up", "down")], 2)


def stage_delta(nc, d, h, xT, ident):
    HK, HV, DK, K = 4, 8, 128, 4
    CV = 2 * HK + HV
    NB = (B + 1) // NCH
    SP = S + K - 1
    W2 = HK * TT
    with ExitStack() as stack:
        sb, ps = bufs(nc, stack)
        layer, loads = linear(sb, "dp", d["d_w_ba"], 2 * HV, d["d_b_ba"])
        norm_transpose(nc, "dn", h, xT, ident, 1e-6, False, w_dram=d["d_ln1"], w_plus=1.0, loads=loads)
        ba = sb("d_ba", [TT, NT, 2 * HV])
        projected(nc, "dp", xT, layer, ba)
        mix = sb("d_mix", [P, CV, T])
        beta = sb("d_beta", [TT, NT, HV])
        g = sb("d_g", [TT, NT, HV])
        pT = sb("d_pT", [TT, NT, HV, TT])
        a_dram = nc.dram_tensor("d_a", (B + 1, HV, S, S), F32, kind="Internal").ap()
        t_dram = nc.dram_tensor("d_t", (B + 1, HV, S, S), F32, kind="Internal").ap()

        with ExitStack() as inner:
            sb2, ps2 = bufs(nc, inner)
            s = sems(nc, inner, "dc_in dc_edge dc_v dc_v2 dc_beta dc_e dc_ln dc_al "
                                + " ".join(f"dc_w{u} dc_mm{u} dc_x{u} dc_tap{u} dc_taps{u} dc_done{u}" for u in range(2)))
            v = s
            w = [sb2(f"dc_wb{u}", [P, KC * P]) for u in range(2)]
            cw = sb2("dc_cw", [P, CV, K])
            xp = [sb2(f"dc_xp{u}", [P, B + 1, SP]) for u in range(2)]
            acc = [sb2(f"dc_acc{u}", [P, B + 1, S]) for u in range(2)]
            al = sb2("dc_alb", [TT, HV])
            e = sb2("dc_eb", [TT, NT, HV])
            ln = sb2("dc_lnb", [TT, NT, HV])
            uu = sb2("dc_u", [TT, NT, HV])
            pp = [ps2(f"dc_pp{u}", [P, NCH, BANK]) for u in range(2)]
            block = inner.enter_context(nc.Block())

            @block.sync
            def _(sp):
                sp.dma_start(al[:, :], d["d_a_log"]).then_inc(s["dc_in"], 16)
                sp.dma_start(cw[:, :, :], d["d_cw"]).then_inc(s["dc_in"], 16)
                with sp.Fori(0, CV // 2) as i:
                    for u in range(2):
                        sp.wait_ge(v[f"dc_mm{u}"], i + 1)
                        sp.dma_start(w[u][:, :], d["d_w_qkv"][bass.ds(2 * i + u, 1)].rearrange("a p n -> p (a n)")
                                     ).then_inc(v[f"dc_w{u}"], 16)

            @block.tensor
            def _(pe):
                with pe.Fori(0, CV // 2) as i:
                    for u in range(2):
                        pe.wait_ge(v[f"dc_w{u}"], i * 16 + 17)
                        pe.wait_ge(v[f"dc_x{u}"], i + 1)
                        for t in range(NCH):
                            for k in range(KC):
                                last = nc.tensor.matmul(pp[u][:, t, 0:CH], w[u][:, k * P:(k + 1) * P],
                                                        xT[:, k, t * CH:(t + 1) * CH], start=(k == 0),
                                                        stop=(k == KC - 1))
                        last.then_inc(v[f"dc_mm{u}"], 1)

            @block.scalar
            def _(act):
                act.wait_ge(s["dc_in"], 33)
                nc.scalar.activation(al[:, :], al[:, :], ACT.Exp).then_inc(s["dc_al"], 1)
                nc.scalar.activation(e[:, :, :], ba[:, :, HV:], ACT.Abs).then_inc(s["dc_e"], 1)
                act.wait_ge(s["dc_e"], 2)
                nc.scalar.activation(e[:, :, :], e[:, :, :], ACT.Exp, scale=-1.0).then_inc(s["dc_e"], 1)
                act.wait_ge(s["dc_e"], 3)
                nc.scalar.activation(ln[:, :, :], e[:, :, :], ACT.Ln, bias=1.0).then_inc(s["dc_ln"], 1)
                nc.scalar.activation(beta[:, :, :], ba[:, :, 0:HV], ACT.Sigmoid).then_inc(s["dc_beta"], 1)
                act.wait_ge(s["dc_edge"], 3)

                def first_tap(i, u):
                    act.wait_ge(v[f"dc_mm{u}"], i + 2)
                    act.wait_ge(v[f"dc_taps{u}"], i + 1)
                    nc.scalar.activation(xp[u][:, :, K - 1:SP].rearrange("p (t b) j -> p t b j", t=NCH),
                                         pp[u][:, :, 0:CH].rearrange("p t (b j) -> p t b j", j=S), ACT.Copy
                                         ).then_inc(v[f"dc_x{u}"], 1)
                    act.wait_ge(v[f"dc_x{u}"], i + 2)
                    act.wait_ge(v[f"dc_done{u}"], i + 1)
                    nc.scalar.activation(acc[u][:, :, :], xp[u][:, :, 0:S], ACT.Copy,
                                         scale=flat2(cw[:, span(2 * i + u, 1), 0:1])).then_inc(v[f"dc_tap{u}"], 1)

                def silu(i, u):
                    act.wait_ge(v[f"dc_taps{u}"], i + 2)
                    nc.scalar.activation(flat2(mix[:, span(2 * i + u, 1), :]), flat2(acc[u][:, :, :]), ACT.Silu
                                         ).then_inc(v[f"dc_done{u}"], 1)

                first_tap(0, 0)
                first_tap(0, 1)
                silu(0, 0)
                with act.Fori(1, CV // 2) as i:
                    first_tap(i, 0)
                    silu(i - 1, 1)
                    first_tap(i, 1)
                    silu(i, 0)
                silu(CV // 2 - 1, 1)

            @block.gpsimd
            def _(pool):
                for u in range(2):
                    nc.gpsimd.memset(xp[u][:, :, :], 0.0).then_inc(s["dc_edge"], 1)

            @block.vector
            def _(dve):
                link = chain(dve, s["dc_v"])
                dve.wait_ge(s["dc_ln"], 2)
                dve.wait_ge(s["dc_in"], 33)
                dve.wait_ge(s["dc_al"], 2)
                link(nc.vector.tensor_scalar(uu[:, :, :], e[:, :, :], 1.0, None, ALU.add))
                link(nc.vector.scalar_tensor_tensor(uu[:, :, :], uu[:, :, :], -1.0, e[:, :, :], ALU.add, ALU.subtract))
                link(nc.vector.tensor_tensor(ln[:, :, :], ln[:, :, :], uu[:, :, :], ALU.subtract))
                link(nc.vector.scalar_tensor_tensor(ln[:, :, :], ba[:, :, HV:], 0.0, ln[:, :, :], ALU.max, ALU.add))
                link(nc.vector.tensor_tensor(g[:, :, :], ln[:, :, :],
                                             al[:, :].unsqueeze(1).broadcast_to([TT, NT, HV]), ALU.mult))
                link(nc.vector.tensor_scalar(g[:, :, :], g[:, :, :], -1.0, None, ALU.mult))
                with dve.Fori(0, CV // 2) as i:
                    link2 = chain(dve, s["dc_v2"], 4 * i)
                    for u in range(2):
                        dve.wait_ge(v[f"dc_tap{u}"], i + 2)
                        for k in range(1, K):
                            ins = nc.vector.scalar_tensor_tensor(acc[u][:, :, :], xp[u][:, :, k:k + S],
                                                                 flat2(cw[:, span(2 * i + u, 1), k:k + 1]), acc[u][:, :, :], ALU.mult, ALU.add)
                            link2(ins) if k < K - 1 else ins.then_inc(v[f"dc_taps{u}"], 1)

        with ExitStack() as inner:
            sb2, ps2 = bufs(nc, inner)
            s = sems(nc, inner, "dl_in dl_sq dl_sum dl_ss dl_root dl_r dl_bc_mm dl_bc dl_v")
            sel = sb2("dl_sel", [P, 8, 8])
            spread = sb2("dl_spread", [8, 8, P])
            sq = sb2("dl_sqb", [P, 8, T])
            ss = sb2("dl_ssb", [8, T])
            root = sb2("dl_rootb", [8, T])
            r = sb2("dl_rb", [8, T])
            pp = ps2("dl_pp", [P, 3, BANK])
            pb = ps2("dl_pb", [P, 4, BANK])
            block = inner.enter_context(nc.Block())

            @block.sync
            def _(sp):
                sp.dma_start(sel[:, :, :], d["d_sel"]).then_inc(s["dl_in"], 16)
                sp.dma_start(spread[:, :, :], d["d_spread"]).then_inc(s["dl_in"], 16)

            @block.scalar
            def _(act):
                for c in range(8):
                    nc.scalar.activation(sq[:, c, :], mix[:, c, :], ACT.Square).then_inc(s["dl_sq"], 1)
                act.wait_ge(s["dl_ss"], 2)
                nc.scalar.activation(root[:, :], ss[:, :], ACT.Sqrt).then_inc(s["dl_root"], 1)

            @block.tensor
            def _(pe):
                pe.wait_ge(s["dl_in"], 33)
                pe.wait_ge(s["dl_sq"], 9)
                for t in range(NCH):
                    for c in range(8):
                        last = nc.tensor.matmul(pp[0:8, t, 0:CH], sel[:, c, :], sq[:, c, t * CH:(t + 1) * CH],
                                                start=(c == 0), stop=(c == 7))
                last.then_inc(s["dl_sum"], 1)
                pe.wait_ge(s["dl_r"], 2)
                for n in range(8 * NCH):
                    c, t = divmod(n, NCH)
                    if n >= 4:
                        pe.wait_ge(s["dl_bc"], n - 2)
                    nc.tensor.matmul(pb[:, n % 4, 0:CH], spread[:, c, :], r[:, t * CH:(t + 1) * CH], start=True,
                                     stop=True).then_inc(s["dl_bc_mm"], 1)

            @block.vector
            def _(dve):
                link = chain(dve, s["dl_v"])
                dve.wait_ge(s["dl_sum"], 2)
                for t in range(NCH):
                    last = nc.vector.tensor_scalar(ss[:, t * CH:(t + 1) * CH], pp[0:8, t, 0:CH], 1e-6, None, ALU.add)
                last.then_inc(s["dl_ss"], 1)
                dve.wait_ge(s["dl_root"], 2)
                link(nc.vector.reciprocal(r[:, :], root[:, :]))
                link(nc.vector.tensor_tensor(root[:, :], ss[:, :], r[:, :], ALU.mult))
                link(nc.vector.tensor_tensor(root[:, :], root[:, :], r[:, :], ALU.mult))
                link(nc.vector.tensor_scalar(root[:, :], root[:, :], -0.5, 1.5, ALU.mult, ALU.add))
                nc.vector.tensor_tensor(r[:, :], r[:, :], root[:, :], ALU.mult).then_inc(s["dl_r"], 1)
                for n in range(8 * NCH):
                    c, t = divmod(n, NCH)
                    dve.wait_ge(s["dl_bc_mm"], n + 2)
                    at = mix[:, c, t * CH:(t + 1) * CH]
                    nc.vector.tensor_tensor(at, at, pb[:, n % 4, 0:CH], ALU.mult).then_inc(s["dl_bc"], 1)

        with ExitStack() as inner:
            sb2, ps2 = bufs(nc, inner)
            s = sems(nc, inner, "da_in da_gm da_ks da_dec_mm da_kk_mm da_exp da_mask da_a da_v da_out da_p")
            m = sb2("da_masks", [TT, 3, TT])
            gm = sb2("da_gmb", [TT, 2, HV, TT])
            ks = sb2("da_ksb", [P, HK, TT])
            ex = sb2("da_ex", [TT, 2, HV, TT])
            am = sb2("da_am", [TT, HV, TT])
            pd = ps2("da_pd", [P, 4, BANK])
            pk = ps2("da_pk", [P, 2, BANK])
            block = inner.enter_context(nc.Block())
            wide = [TT, HV, TT]

            @block.sync
            def _(sp):
                sp.dma_start(m[:, :, :], d["d_masks"]).then_inc(s["da_in"], 16)
                with sp.Fori(0, NT) as i:
                    sp.wait_ge(s["da_a"], i + 2)
                    for q in range(G):
                        at = slice(q * S, (q + 1) * S)
                        sp.dma_start(a_dram[bass.ds(i * G + q, 1)].rearrange("b h i j -> i (b h) j"), am[at, :, at]
                                     ).then_inc(s["da_out"], 16)
                sp.wait_ge(s["da_out"], NT * G * 16 + 1)

            @block.gpsimd
            def _(pool):
                pool.wait_ge(s["da_in"], 17)

                def masked_gates(i):
                    pool.wait_ge(s["da_dec_mm"], i + 1)
                    gt = flat2(g[:, span(i, 1), :]).unsqueeze(2).broadcast_to(wide)
                    for n in range(2):
                        last = nc.gpsimd.tensor_tensor(gm[:, n, :, :], gt, m[:, n:n + 1, :].broadcast_to(wide),
                                                       ALU.mult)
                    last.then_inc(s["da_gm"], 1)

                def mask(i):
                    pool.wait_ge(s["da_exp"], i + 2)
                    nc.gpsimd.tensor_tensor(ex[:, 0, :, :], ex[:, 0, :, :], m[:, 0:1, :].broadcast_to(wide), ALU.mult
                                            ).then_inc(s["da_mask"], 1)

                masked_gates(0)
                with pool.Fori(0, NT - 1) as i:
                    masked_gates(i + 1)
                    mask(i)
                mask(NT - 1)

            @block.tensor
            def _(pe):
                pe.wait_ge(s["da_in"], 17)
                with pe.Fori(0, NT) as i:
                    pe.wait_ge(s["da_gm"], i + 2)
                    pe.wait_ge(s["da_exp"], i + 1)
                    for n in range(2):
                        for o in range(2):
                            last = nc.tensor.matmul(pd[0:TT, 2 * n + o, 0:W2], m[:, 1 - n, :],
                                                    flat2(gm[:, n, o * HK:(o + 1) * HK, :]), start=True, stop=True)
                    last.then_inc(s["da_dec_mm"], 1)
                    pe.wait_ge(s["da_ks"], i + 2)
                    pe.wait_ge(s["da_p"], i + 1)
                    for n in range(2):
                        for c in range(HK):
                            src = mix[:, n * HK + c, bass.ds(i * TT, TT)]
                            last = nc.tensor.matmul(pk[0:TT, n, c * TT:(c + 1) * TT], ks[:, c, :], src, start=True,
                                                    stop=True)
                    last.then_inc(s["da_kk_mm"], 1)

            @block.scalar
            def _(act):
                with act.Fori(0, NT) as i:
                    act.wait_ge(s["da_kk_mm"], i + 1)
                    nc.scalar.activation(ks[:, :, :], mix[:, HK:2 * HK, bass.ds(i * TT, TT)], ACT.Copy
                                         ).then_inc(s["da_ks"], 1)
                    act.wait_ge(s["da_dec_mm"], i + 2)
                    act.wait_ge(s["da_p"], i + 1)
                    for n in range(2):
                        last = nc.scalar.activation(ex[:, n, :, :].rearrange("p (o h) x -> p o (h x)", o=2),
                                                    pd[0:TT, 2 * n:2 * n + 2, 0:W2], ACT.Exp)
                    last.then_inc(s["da_exp"], 1)

            @block.vector
            def _(dve):
                dve.wait_ge(s["da_in"], 17)
                V = 3
                with dve.Fori(0, NT) as i:
                    link = chain(dve, s["da_v"], V * i)
                    dve.wait_ge(s["da_exp"], i + 2)
                    link(nc.vector.tensor_tensor(ex[:, 1, :, :], ex[:, 1, :, :], m[:, 1:2, :].broadcast_to(wide),
                                                 ALU.mult))
                    dve.wait_ge(s["da_kk_mm"], i + 2)
                    dve.wait_ge(s["da_out"], i * G * 16 + 1)
                    rep2 = [TT, HK, 2, TT]
                    kk = [pk[0:TT, n, 0:W2].rearrange("p (c x) -> p c x", x=TT).unsqueeze(2).broadcast_to(rep2)
                          for n in range(2)]
                    link(nc.vector.tensor_tensor(am[:, :, :].rearrange("p (c r) x -> p c r x", r=2),
                                                 ex[:, 1, :, :].rearrange("p (c r) x -> p c r x", r=2), kk[1], ALU.mult))
                    dve.wait_ge(s["da_mask"], i + 2)
                    link(nc.vector.tensor_tensor(pT[:, bass.ds(i, 1), :, :].rearrange("p a (c r) x -> p (a c) r x", r=2),
                                                 ex[:, 0, :, :].rearrange("p (c r) x -> p c r x", r=2), kk[0],
                                                 ALU.mult))
                    nc.vector.nop().then_inc(s["da_p"], 1)
                    nc.vector.tensor_tensor(am[:, :, :], am[:, :, :],
                                            flat2(beta[:, bass.ds(i, 1), :]).unsqueeze(2).broadcast_to(wide), ALU.mult
                                            ).then_inc(s["da_a"], 1)
                assert link.count() == V

        with ExitStack() as inner:
            sb2, ps2 = bufs(nc, inner)
            s = sems(nc, inner, "di_in di_zero di_v di_out")
            NG = B * HV // P
            a = sb2("di_a", [P, NG, S, S])
            tT = sb2("di_tT", [P, NG, S, S])
            pr = sb2("di_pr", [P, NG * S * S])
            block = inner.enter_context(nc.Block())
            split = [x[0:B].rearrange("b h i j -> (b h) (i j)").rearrange("(g p) n -> p g n", g=NG)
                     for x in (a_dram, t_dram)]

            @block.sync
            def _(sp):
                sp.dma_start(a[:, :, :, :].rearrange("p g i j -> p g (i j)"), split[0]).then_inc(s["di_in"], 16)
                sp.wait_ge(s["di_v"], 2 * S)
                sp.dma_start(split[1], tT[:, :, :, :].rearrange("p g i j -> p g (i j)")).then_inc(s["di_out"], 16)
                sp.dma_start(t_dram[B:B + 1].rearrange("b h i j -> (b h) (i j)"),
                             tT[0:HV, 0, :, :].rearrange("p i j -> p (i j)")).then_inc(s["di_out"], 16)
                sp.wait_ge(s["di_out"], 33)

            @block.gpsimd
            def _(pool):
                nc.gpsimd.memset(tT[:, :, :, :], 0.0).then_inc(s["di_zero"], 1)

            @block.vector
            def _(dve):
                link = chain(dve, s["di_v"])
                dve.wait_ge(s["di_zero"], 2)
                link(nc.vector.memset(tT[:, :, :, :].rearrange("p g i j -> p g (i j)")[:, :, 0:S * S:S + 1], 1.0))
                dve.wait_ge(s["di_in"], 17)
                for i in range(1, S):
                    one = pr[:, 0:NG * i * i].rearrange("p (g c j) -> p g c j", g=NG, c=i)
                    link(nc.vector.tensor_tensor(one, tT[:, :, 0:i, 0:i],
                                                 a[:, :, i:i + 1, 0:i].broadcast_to([P, NG, i, i]), ALU.mult))
                    link(nc.vector.tensor_reduce(tT[:, :, 0:i, i:i + 1].rearrange("p g c a -> p g (c a)"), one, X,
                                                 ALU.add, negate=True))

        with ExitStack() as inner:
            sb2, ps2 = bufs(nc, inner)
            s = sems(nc, inner, "do_in do_zero do_t do_vs do_ps do_xs do_v_mm do_vb do_u_mm do_u do_o_mm do_z_mm "
                                "do_sq do_ms do_r do_z do_g do_core do_c_mm do_c do_out_mm do_h do_v do_half")
            wz = sb2("do_wz", [P, KC, HV * DK])
            wo = sb2("do_wo", [P, HV, D])
            gw = sb2("do_gw", [TT, DK])
            tm = sb2("do_tm", [TT, HV, TT])
            vs = sb2("do_vsb", [P, HV, TT])
            pm = sb2("do_pm", [TT, HV, TT])
            xs = sb2("do_xsb", [P, KC, TT])
            vb = sb2("do_vbb", [TT, HV, DK])
            ub = sb2("do_ub", [TT, HV, DK])
            sq = sb2("do_sqb", [TT, HV, DK])
            ms = sb2("do_msb", [TT, HV])
            half = sb2("do_halfb", [TT, HV])
            zs = sb2("do_zs", [TT, HV, DK])
            core = sb2("do_coreb", [TT, HV, DK])
            cT = sb2("do_cT", [P, HV, TT])
            pv, pu, po, pz = (ps2(f"do_p{n}", [P, 2, BANK]) for n in "vuoz")
            block = inner.enter_context(nc.Block())
            wide = [TT, HV, DK]

            def heads(p):
                return p[0:TT, :, :].rearrange("p o (h x) -> p (o h) x", x=DK)

            @block.sync
            def _(sp):
                sp.dma_start(wz[:, :, :], d["d_w_z"]).then_inc(s["do_in"], 16)
                sp.dma_start(wo[:, :, :], d["d_w_out"]).then_inc(s["do_in"], 16)
                sp.dma_start(gw[:, :], d["d_gw"]).then_inc(s["do_in"], 16)
                sp.wait_ge(s["do_zero"], 2)
                with sp.Fori(0, NT) as i:
                    sp.wait_ge(s["do_u_mm"], i + 1)
                    for q in range(G):
                        at = slice(q * S, (q + 1) * S)
                        sp.dma_start(tm[at, :, at], t_dram[bass.ds(i * G + q, 1)].rearrange("b h i j -> i (b h) j")
                                     ).then_inc(s["do_t"], 16)

            @block.gpsimd
            def _(pool):
                nc.gpsimd.memset(tm[:, :, :], 0.0).then_inc(s["do_zero"], 1)
                pool.wait_ge(s["do_half"], 2)

                def stage_v(i):
                    pool.wait_ge(s["do_v_mm"], i + 1)
                    nc.gpsimd.tensor_copy(vs[:, :, :], mix[:, 2 * HK:CV, span(i, TT)]).then_inc(s["do_vs"], 1)

                def stage_x(i):
                    pool.wait_ge(s["do_z_mm"], i + 1)
                    nc.gpsimd.tensor_copy(xs[:, :, :], xT[:, :, span(i, TT)]).then_inc(s["do_xs"], 1)

                def stage_p(i):
                    pool.wait_ge(s["do_o_mm"], i + 1)
                    nc.gpsimd.tensor_copy(pm[:, :, :], pT[:, span(i, 1), :, :].rearrange("p a h x -> p (a h) x")
                                          ).then_inc(s["do_ps"], 1)

                def power(i):
                    pool.wait_ge(s["do_ms"], i + 2)
                    nc.gpsimd.tensor_tensor(ms[:, :], ms[:, :], half[:, :], ALU.pow).then_inc(s["do_r"], 1)

                stage_v(0)
                stage_x(0)
                stage_p(0)
                with pool.Fori(1, NT) as i:
                    stage_v(i)
                    stage_x(i)
                    power(i - 1)
                    stage_p(i)
                power(NT - 1)

            @block.tensor
            def _(pe):
                pe.wait_ge(s["do_in"], 49)

                def turn_v(i):
                    pe.wait_ge(s["do_vs"], i + 2)
                    for c in range(HV):
                        last = nc.tensor.transpose(pv[0:TT, c // 4, (c % 4) * DK:(c % 4 + 1) * DK], vs[:, c, :],
                                                   ident[:, :])
                    last.then_inc(s["do_v_mm"], 1)

                def gates_z(i):
                    pe.wait_ge(s["do_xs"], i + 2)
                    if not isinstance(i, int):
                        pe.wait_ge(s["do_h"], i)
                    for o in range(2):
                        for k in range(KC):
                            last = nc.tensor.matmul(pz[0:TT, o, :], xs[:, k, :], wz[:, k, o * BANK:(o + 1) * BANK],
                                                    start=(k == 0), stop=(k == KC - 1))
                    last.then_inc(s["do_z_mm"], 1)

                def updates(i):
                    pe.wait_ge(s["do_vb"], i + 2)
                    pe.wait_ge(s["do_t"], (i + 1) * G * 16 + 1)
                    pe.wait_ge(s["do_u"], i + 1)
                    for c in range(HV):
                        last = nc.tensor.matmul(pu[0:TT, c // 4, (c % 4) * DK:(c % 4 + 1) * DK], tm[:, c, :],
                                                vb[:, c, :], start=True, stop=True)
                    last.then_inc(s["do_u_mm"], 1)

                def outputs(i):
                    pe.wait_ge(s["do_u"], i + 2)
                    pe.wait_ge(s["do_ps"], i + 2)
                    pe.wait_ge(s["do_core"], i + 1)
                    for c in range(HV):
                        last = nc.tensor.matmul(po[0:TT, c // 4, (c % 4) * DK:(c % 4 + 1) * DK], pm[:, c, :],
                                                ub[:, c, :], start=True, stop=True)
                    last.then_inc(s["do_o_mm"], 1)

                def turn_core(i, ahead):
                    pe.wait_ge(s["do_core"], i + 2)
                    pe.wait_ge(s["do_vb"], i + ahead + 2)
                    for c in range(HV):
                        last = nc.tensor.transpose(pv[:, c // 4, (c % 4) * TT:(c % 4 + 1) * TT], core[:, c, :],
                                                   ident[0:TT, 0:TT])
                    last.then_inc(s["do_c_mm"], 1)

                def project(i, ahead):
                    pe.wait_ge(s["do_c"], i + 2)
                    pe.wait_ge(s["do_z"], i + ahead + 2)
                    for c in range(HV):
                        last = nc.tensor.matmul(pz[0:TT, 0, 0:D], cT[:, c, :], wo[:, c, :], start=(c == 0),
                                                stop=(c == HV - 1))
                    last.then_inc(s["do_out_mm"], 1)

                turn_v(0)
                gates_z(0)
                updates(0)
                outputs(0)
                with pe.Fori(1, NT) as i:
                    turn_v(i)
                    gates_z(i)
                    updates(i)
                    turn_core(i - 1, 1)
                    outputs(i)
                    project(i - 1, 1)
                turn_core(NT - 1, 0)
                project(NT - 1, 0)

            @block.scalar
            def _(act):
                def silu_z(i):
                    act.wait_ge(s["do_z_mm"], i + 2)
                    act.wait_ge(s["do_g"], i + 1)
                    nc.scalar.activation(zs[:, :, :], heads(pz), ACT.Silu).then_inc(s["do_z"], 1)

                def copy_u(i):
                    act.wait_ge(s["do_u_mm"], i + 2)
                    act.wait_ge(s["do_o_mm"], i + 1)
                    nc.scalar.activation(ub[:, :, :], heads(pu), ACT.Copy).then_inc(s["do_u"], 1)

                def squares(i):
                    act.wait_ge(s["do_o_mm"], i + 2)
                    act.wait_ge(s["do_ms"], i + 1)
                    nc.scalar.activation(sq[:, :, :], heads(po), ACT.Square).then_inc(s["do_sq"], 1)

                def copy_core(i):
                    act.wait_ge(s["do_c_mm"], i + 2)
                    act.wait_ge(s["do_out_mm"], i + 1)
                    nc.scalar.activation(cT[:, :, :].rearrange("p (o h) x -> p o (h x)", o=2), pv[:, :, 0:W2], ACT.Copy
                                         ).then_inc(s["do_c"], 1)

                silu_z(0)
                copy_u(0)
                squares(0)
                with act.Fori(1, NT) as i:
                    silu_z(i)
                    copy_u(i)
                    copy_core(i - 1)
                    squares(i)
                copy_core(NT - 1)

            @block.vector
            def _(dve):
                dve.wait_ge(s["do_in"], 49)
                nc.vector.memset(half[:, :], -0.5).then_inc(s["do_half"], 1)

                def beta_v(i):
                    dve.wait_ge(s["do_v_mm"], i + 2)
                    dve.wait_ge(s["do_u_mm"], i + 1)
                    nc.vector.tensor_tensor(vb[:, :, :], heads(pv),
                                            flat2(beta[:, span(i, 1), :]).unsqueeze(2).broadcast_to(wide), ALU.mult
                                            ).then_inc(s["do_vb"], 1)

                def gate(i):
                    dve.wait_ge(s["do_z"], i + 2)
                    dve.wait_ge(s["do_c_mm"], i + 1)
                    nc.vector.tensor_tensor(core[:, :, :], zs[:, :, :], gw[:, :].unsqueeze(1).broadcast_to(wide),
                                            ALU.mult).then_inc(s["do_g"], 1)

                def mean_square(i):
                    dve.wait_ge(s["do_sq"], i + 2)
                    dve.wait_ge(s["do_core"], i + 1)
                    link(nc.vector.tensor_reduce(ms[:, :], sq[:, :, :], X, ALU.add))
                    nc.vector.tensor_scalar(ms[:, :], ms[:, :], 1.0 / DK, 1e-6, ALU.mult, ALU.add).then_inc(s["do_ms"], 1)

                def norm(i):
                    dve.wait_ge(s["do_g"], i + 2)
                    link(nc.vector.tensor_tensor(core[:, :, :], core[:, :, :], heads(po), ALU.mult))
                    dve.wait_ge(s["do_r"], i + 2)
                    nc.vector.tensor_tensor(core[:, :, :], core[:, :, :], ms[:, :].unsqueeze(2).broadcast_to(wide),
                                            ALU.mult).then_inc(s["do_core"], 1)

                def add(i):
                    dve.wait_ge(s["do_out_mm"], i + 2)
                    ht = flat2(h[:, span(i, 1), :])
                    nc.vector.tensor_tensor(ht, ht, pz[0:TT, 0, 0:D], ALU.add).then_inc(s["do_h"], 1)

                beta_v(0)
                gate(0)
                with dve.Fori(1, NT) as i:
                    link = chain(dve, s["do_v"], (i - 1) * 2)
                    mean_square(i - 1)
                    beta_v(i)
                    norm(i - 1)
                    gate(i)
                    add(i - 1)
                link = chain(dve, s["do_v"], (NT - 1) * 2)
                mean_square(NT - 1)
                norm(NT - 1)
                add(NT - 1)


def stage_moe3(nc, d, h, xT, ident):
    with ExitStack() as stack:
        sb, ps = bufs(nc, stack)
        E = 8
        layer, iota, loads = router(sb, "dr", d["d_router"], d["m_zero"][:, 0:E], d["m_iota"][:, 0:E], E)
        norm_transpose(nc, "dm", h, xT, ident, 1e-6, False, w_dram=d["d_ln2"], w_plus=1.0, loads=loads)
        logits = sb("d_logits", [TT, NT, E])
        gates = sb("d_gates", [TT, NT, E])
        projected(nc, "dr", xT, layer, logits)
        top2_gates(nc, "dt", logits, gates, iota, ident, E)
        xh, xl = (sb(f"d_x{n}", [P, KC, T + 1], F32R) for n in "hl")
        split_x(nc, "dx", xT, xh, xl)
        experts(nc, "de", d["d_w_e"], gates, xh, xl, h, E, 4, 1, True)


def layout_delta(i, o):
    f = np.float32
    o["d_ln1"] = i["L3_attn_w_ln1"].reshape(KC, P).T
    o["d_ln2"] = i["L3_attn_w_ln2"].reshape(KC, P).T
    o["d_w_ba"] = cols(i["L3_attn_W_ba"], KC)
    o["d_b_ba"] = rep(np.concatenate([np.zeros(8, f), i["L3_attn_dt_bias"]]))
    w = i["L3_attn_W_qkvz"]
    o["d_w_qkv"] = w[:, :2048].reshape(KC, P, 16, P).transpose(2, 1, 0, 3).reshape(16, P, KC * P)
    o["d_w_z"] = cols(w[:, 2048:], KC)
    o["d_cw"] = i["L3_attn_conv_w"].reshape(16, P, 4).transpose(1, 0, 2)
    o["d_a_log"] = rep(i["L3_attn_A_log"])
    eye = np.eye(8, dtype=f)
    o["d_sel"] = np.broadcast_to(eye, (P, 8, 8))
    scale = np.where(np.arange(8) < 4, P ** -0.5, 1.0)
    o["d_spread"] = np.broadcast_to((eye * scale[None]).astype(f)[:, :, None], (8, 8, P))
    a = np.arange(TT)[:, None]
    b = np.arange(TT)[None, :]
    same = a // S == b // S
    o["d_masks"] = np.stack([same & (a <= b), same & (a > b), same & (a < b)], 1).astype(f)
    o["d_w_out"] = cols(i["L3_attn_W_out"], 8)
    o["d_gw"] = rep(i["L3_attn_gate_norm_w"])
    o["d_router"] = cols(i["L3_attn_W_router"], KC)
    o["d_w_e"] = np.concatenate([up_cols(i[f"L3_attn_W_{n}_e"]) for n in ("gate", "up", "down")], 2)


def stage_mla(nc, d, h, xT, ident):
    H, HD, NOPE = 16, 64, 32
    C = H * HD // P
    PG = (H + G - 1) // G
    GN = G * NOPE
    with ExitStack() as stack:
        sb, ps = bufs(nc, stack)
        q = sb("l_q", [P, C, T])
        kT = sb("l_kT", [P, C, T])
        ckv = sb("l_ckv", [HD, T])
        seqs = [P, T // S, S]

        with ExitStack() as inner:
            sb2, ps2 = bufs(nc, inner)
            wq = sb2("lp_wq", [P, KC, H * HD])
            wkva = sb2("lp_wkva", [P, KC, HD])
            wk = sb2("lp_wk", [HD, H * HD])
            perm = sb2("lp_perm", [P, P])
            tab = sb2("lp_tab", [P, 2, S])
            norm_transpose(nc, "ln", h, xT, ident, 1e-5, False, w_dram=d["l_ln1"], loads=[
                (wq[:, :, :], d["l_wq"]), (wkva[:, :, :], d["l_wkva"]), (wk[:, :], d["l_wk"]),
                (perm[:, :], d["l_perm"]), (tab[:, :, :], d["l_tab"])])
            s = sems(nc, inner, "lp_mm lp_raw lp_sw_mm lp_rot lp_v lp_k_mm lp_k lp_done")
            raw = [sb2(f"lp_raw{n}", [P, T]) for n in range(2)]
            sw = sb2("lp_sw", [P, T])
            pp = ps2("lp_pp", [P, NCH, BANK])
            pw = ps2("lp_pw", [P, NCH, BANK])
            block = inner.enter_context(nc.Block())
            jobs = [(wkva, HD, 0, ckv)] + [(wq, P, c * P, q[:, c, :]) for c in range(C)]

            @block.tensor
            def _(pe):
                def swap(n):
                    m = jobs[n][1]
                    pe.wait_ge(s["lp_raw"], n + 2)
                    if n:
                        pe.wait_ge(s["lp_rot"], n + 1)
                    for t in range(NCH):
                        last = nc.tensor.matmul(pw[0:m, t, 0:CH], perm[0:m, 0:m], raw[n % 2][0:m, t * CH:(t + 1) * CH],
                                                start=True, stop=True)
                    last.then_inc(s["lp_sw_mm"], 1)

                for n, (w, m, at, _) in enumerate(jobs):
                    if n:
                        pe.wait_ge(s["lp_raw"], n + 1)
                    for t in range(NCH):
                        for k in range(KC):
                            last = nc.tensor.matmul(pp[0:m, t, 0:CH], w[:, k, at:at + m],
                                                    xT[:, k, t * CH:(t + 1) * CH], start=(k == 0), stop=(k == KC - 1))
                    last.then_inc(s["lp_mm"], 1)
                    if n:
                        swap(n - 1)
                swap(len(jobs) - 1)
                pe.wait_ge(s["lp_rot"], len(jobs) + 1)
                for c in range(C):
                    if c >= 2:
                        pe.wait_ge(s["lp_k"], c)
                    for t in range(NCH):
                        last = nc.tensor.matmul((pp, pw)[c % 2][:, t, 0:CH], wk[:, c * P:(c + 1) * P],
                                                ckv[:, t * CH:(t + 1) * CH], start=True, stop=True)
                    last.then_inc(s["lp_k_mm"], 1)

            @block.scalar
            def _(act):
                for n, (_, m, _, _) in enumerate(jobs):
                    act.wait_ge(s["lp_mm"], n + 2)
                    if n >= 2:
                        act.wait_ge(s["lp_rot"], n)
                    nc.scalar.activation(raw[n % 2][0:m, :].rearrange("p (t n) -> p t n", t=NCH), pp[0:m, :, 0:CH],
                                         ACT.Copy).then_inc(s["lp_raw"], 1)
                for c in range(C):
                    act.wait_ge(s["lp_k_mm"], c + 2)
                    nc.scalar.activation(kT[:, c, :].rearrange("p (t n) -> p t n", t=NCH),
                                         (pp, pw)[c % 2][:, :, 0:CH], ACT.Copy).then_inc(s["lp_k"], 1)

            @block.vector
            def _(dve):
                link = chain(dve, s["lp_v"])
                for n, (_, m, _, dst) in enumerate(jobs):
                    one = dst if n else dst[:, :]
                    fac = [tab[0:m, k:k + 1, :].broadcast_to([m, T // S, S]) for k in range(2)]
                    dve.wait_ge(s["lp_sw_mm"], n + 2)
                    link(nc.vector.tensor_tensor(one.rearrange("p (b j) -> p b j", j=S),
                                                 raw[n % 2][0:m, :].rearrange("p (b j) -> p b j", j=S), fac[0],
                                                 ALU.mult))
                    for t in range(NCH):
                        last = nc.vector.tensor_tensor(
                            sw[0:m, t * CH:(t + 1) * CH].rearrange("p (b j) -> p b j", j=S),
                            pw[0:m, t, 0:CH].rearrange("p (b j) -> p b j", j=S), fac[1][:, 0:T // S // NCH, :],
                            ALU.mult)
                    link(last)
                    nc.vector.tensor_tensor(one, one, sw[0:m, :], ALU.add).then_inc(s["lp_rot"], 1)
                    dve.wait_ge(s["lp_rot"], n + 2)

        with ExitStack() as inner:
            sb2, ps2 = bufs(nc, inner)
            s = sems(nc, inner, "la_in la_zero la_qm la_kx la_lat la_s_mm la_max la_exp la_probs la_v_mm la_vexp "
                                "la_turned la_pT la_pv la_oT la_out_mm la_h la_v la_sc")
            wv = sb2("la_wv", [NOPE, H * NOPE])
            wo = sb2("la_wo", [GN, PG, D])
            vmask = sb2("la_vmask", [TT, H * NOPE])
            neg = sb2("la_neg", [TT, S])
            qm = sb2("la_qmb", [P, C, G * TT])
            kx = sb2("la_kxb", [P, C, 2, TT])
            lat = sb2("la_latb", [NOPE, G, G, S])
            sc = sb2("la_sc", [TT, H, S])
            e = sb2("la_e", [TT, H, S])
            mx = sb2("la_mx", [TT, H])
            pT = sb2("la_pTb", [TT, PG, TT])
            vexp = sb2("la_vexpb", [TT, G, H * NOPE])
            oT = sb2("la_oTb", [GN, PG, TT])
            psS = ps2("la_psS", [P, 2, BANK])
            psT = ps2("la_psT", [P, 2, BANK])
            psV = ps2("la_psV", [P, G, BANK])
            psO = ps2("la_psO", [P, BANK])
            block = inner.enter_context(nc.Block())
            W = C // 2 * 2 * S

            @block.sync
            def _(sp):
                for dst, src in ((wv[:, :], "l_wv"), (wo[:, :, :], "l_wo"), (vmask[:, :], "l_vmask"),
                                 (neg[:, :], "l_neg")):
                    sp.dma_start(dst, d[src]).then_inc(s["la_in"], 16)

            @block.gpsimd
            def _(pool):
                nc.gpsimd.memset(qm[:, :, :], 0.0)
                nc.gpsimd.memset(kx[:, :, :, :], 0.0).then_inc(s["la_zero"], 1)
                pool.wait_ge(s["la_zero"], 2)
                with pool.Fori(0, NT) as i:
                    pool.wait_ge(s["la_s_mm"], i + 1)
                    for n in range(G):
                        last = nc.gpsimd.tensor_copy(qm[:, :, n * (TT + S):n * (TT + S) + S],
                                                     q[:, :, bass.ds(i * TT + n * S, S)])
                    last.then_inc(s["la_qm"], 1)
                    pool.wait_ge(s["la_v_mm"], i + 1)
                    for n in range(G):
                        last = nc.gpsimd.tensor_copy(lat[:, n, :, :], ckv[0:NOPE, bass.ds(i * TT + n * S, S)]
                                                     .unsqueeze(1).broadcast_to([NOPE, G, S]))
                    last.then_inc(s["la_lat"], 1)

            @block.scalar
            def _(act):
                act.wait_ge(s["la_zero"], 2)

                def keys(i):
                    act.wait_ge(s["la_s_mm"], i + 1)
                    for n in range(2):
                        at = slice(n * HD, (n + 1) * HD)
                        src = kT[at, :, 0:TT] if isinstance(i, int) else kT[at, :, bass.ds(i * TT, TT)]
                        last = nc.scalar.activation(kx[at, :, n, :], src, ACT.Copy)
                    last.then_inc(s["la_kx"], 1)

                def exponent(i):
                    act.wait_ge(s["la_max"], i + 2)
                    act.wait_ge(s["la_turned"], i + 1)
                    nc.scalar.activation(e[:, :, :], sc[:, :, :], ACT.Exp, scale=HD ** -0.5).then_inc(s["la_exp"], 1)

                def copies(i):
                    act.wait_ge(s["la_turned"], i + 2)
                    nc.scalar.activation(pT[:, 0:4, :].rearrange("p g t -> p (g t)"), psT[0:TT, 0, 0:4 * TT], ACT.Copy)
                    nc.scalar.activation(pT[:, 4, :], psT[0:TT, 1, 0:TT], ACT.Copy)
                    nc.scalar.activation(pT[0:S, 5, :], psT[0:S, 1, TT:2 * TT], ACT.Copy).then_inc(s["la_pT"], 1)
                    act.wait_ge(s["la_pv"], i + 2)
                    nc.scalar.activation(oT[:, 0:4, :].rearrange("p g t -> p (g t)"), psT[0:GN, 0, 0:4 * TT], ACT.Copy)
                    nc.scalar.activation(oT[:, 4, :], psT[0:GN, 1, 0:TT], ACT.Copy)
                    nc.scalar.activation(oT[0:NOPE, 5, :], psT[0:NOPE, 1, TT:2 * TT], ACT.Copy).then_inc(s["la_oT"], 1)

                keys(0)
                with act.Fori(0, NT - 1) as i:
                    exponent(i)
                    keys(i + 1)
                    copies(i)
                exponent(NT - 1)
                copies(NT - 1)

            @block.tensor
            def _(pe):
                pe.wait_ge(s["la_in"], 65)

                def scores(i):
                    pe.wait_ge(s["la_qm"], i + 2)
                    pe.wait_ge(s["la_kx"], i + 2)
                    pe.wait_ge(s["la_sc"], i + 1)
                    for c in range(C):
                        o = (c % 4) * 2 * S
                        for n in range(G):
                            last = nc.tensor.matmul(psS[0:TT, c // 4, o:o + 2 * S], qm[:, c, n * TT:(n + 1) * TT],
                                                    kx[:, c, :, n * S:(n + 1) * S], start=(n == 0), stop=(n == G - 1))
                    last.then_inc(s["la_s_mm"], 1)

                def values(i):
                    pe.wait_ge(s["la_lat"], i + 2)
                    pe.wait_ge(s["la_vexp"], i + 1)
                    for n in range(G):
                        last = nc.tensor.matmul(psV[0:TT, n, :], lat[:, n, :, :].rearrange("p a j -> p (a j)"),
                                                wv[:, :], start=True, stop=True)
                    last.then_inc(s["la_v_mm"], 1)

                def turn(i):
                    pe.wait_ge(s["la_probs"], i + 2)
                    pe.wait_ge(s["la_oT"], i + 1)
                    for g in range(PG):
                        m = min(G, H - G * g)
                        last = nc.tensor.transpose(psT[0:m * S, g // 4, (g % 4) * TT:(g % 4 + 1) * TT],
                                                   e[:, G * g:G * g + m, :].rearrange("p h j -> p (h j)"),
                                                   ident[0:TT, 0:TT])
                    last.then_inc(s["la_turned"], 1)

                def mix_values(i):
                    pe.wait_ge(s["la_pT"], i + 2)
                    pe.wait_ge(s["la_vexp"], i + 2)
                    for g in range(PG):
                        m = min(G, H - G * g)
                        for n in range(G):
                            o = (g % 4) * TT + n * S
                            last = nc.tensor.matmul(psT[0:m * NOPE, g // 4, o:o + S],
                                                    vexp[0:m * S, n, g * GN:g * GN + m * NOPE],
                                                    pT[0:m * S, g, n * S:(n + 1) * S], start=True, stop=True)
                    last.then_inc(s["la_pv"], 1)

                def project(i):
                    pe.wait_ge(s["la_oT"], i + 2)
                    pe.wait_ge(s["la_h"], i + 1)
                    for g in range(PG):
                        m = min(G, H - G * g) * NOPE
                        last = nc.tensor.matmul(psO[0:TT, 0:D], oT[0:m, g, :], wo[0:m, g, :], start=(g == 0),
                                                stop=(g == PG - 1))
                    last.then_inc(s["la_out_mm"], 1)

                scores(0)
                values(0)
                with pe.Fori(1, NT) as i:
                    turn(i - 1)
                    scores(i)
                    mix_values(i - 1)
                    values(i)
                    project(i - 1)
                turn(NT - 1)
                mix_values(NT - 1)
                project(NT - 1)

            @block.vector
            def _(dve):
                dve.wait_ge(s["la_in"], 65)

                def softmax(i):
                    dve.wait_ge(s["la_s_mm"], i + 2)
                    dve.wait_ge(s["la_exp"], i + 1)
                    for o in range(2):
                        last = nc.vector.tensor_tensor(sc[:, o * 8:(o + 1) * 8, :],
                                                       psS[0:TT, o, 0:W].rearrange("p (h j) -> p h j", j=S),
                                                       neg[:, :].unsqueeze(1).broadcast_to([TT, 8, S]), ALU.add)
                    last.then_inc(s["la_sc"], 1)
                    dve.wait_ge(s["la_sc"], i + 2)
                    link(nc.vector.tensor_reduce(mx[:, :], sc[:, :, :], X, ALU.max))
                    nc.vector.tensor_tensor(sc[:, :, :], sc[:, :, :], wide, ALU.subtract).then_inc(s["la_max"], 1)

                def values(i):
                    dve.wait_ge(s["la_v_mm"], i + 2)
                    dve.wait_ge(s["la_pv"], i + 1)
                    nc.vector.tensor_tensor(vexp[:, :, :], psV[0:TT, :, :],
                                            vmask[:, :].unsqueeze(1).broadcast_to([TT, G, H * NOPE]), ALU.mult
                                            ).then_inc(s["la_vexp"], 1)

                def probs(i):
                    dve.wait_ge(s["la_exp"], i + 2)
                    link(nc.vector.tensor_reduce(mx[:, :], e[:, :, :], X, ALU.add))
                    link(nc.vector.reciprocal(mx[:, :], mx[:, :]))
                    link(nc.vector.tensor_tensor(e[:, :, :], e[:, :, :], wide, ALU.mult))
                    nc.vector.nop().then_inc(s["la_probs"], 1)

                def add(i):
                    dve.wait_ge(s["la_out_mm"], i + 2)
                    ht = h[:, i, :] if isinstance(i, int) else flat2(h[:, bass.ds(i, 1), :])
                    nc.vector.tensor_tensor(ht, ht, psO[0:TT, 0:D], ALU.add).then_inc(s["la_h"], 1)

                wide = mx[:, :].unsqueeze(2).broadcast_to([TT, H, S])
                link = chain(dve, s["la_v"])
                softmax(0)
                probs(0)
                values(0)
                V = link.count()
                with dve.Fori(1, NT) as i:
                    link = chain(dve, s["la_v"], i * V)
                    softmax(i)
                    probs(i)
                    values(i)
                    add(i - 1)
                add(NT - 1)


def stage_moe4(nc, d, h, xT, ident):
    with ExitStack() as stack:
        sb, ps = bufs(nc, stack)
        E = 8
        layer, iota, loads = router(sb, "lr", d["l_router"], d["l_bias"], d["m_iota"][:, 0:E], E)
        norm_transpose(nc, "lm", h, xT, ident, 1e-5, False, w_dram=d["l_ln2"], loads=loads)
        logits = sb("l_logits", [TT, NT, E])
        gates = sb("l_gates", [TT, NT, E])
        one = sb("l_one", [TT, NT, 1])
        projected(nc, "lr", xT, layer, logits)
        top2_gates(nc, "lt", logits, gates, iota, ident, E)
        xh, xl = (sb(f"l_x{n}", [P, KC, T + 1], F32R) for n in "hl")
        split_x(nc, "lx", xT, xh, xl)
        experts(nc, "le", d["l_w_e"], gates, xh, xl, h, E, 4, 1, True)
        with ExitStack() as inner:
            s = sems(nc, inner, "l_one_set")
            block = inner.enter_context(nc.Block())

            @block.vector
            def _(dve):
                nc.vector.memset(one[:, :, :], 1.0).then_inc(s["l_one_set"], 1)
        experts(nc, "ls", d["l_w_s"], one, xh, xl, h, 1, 1, 1, True)


def layout_mla(i, o):
    f = np.float32
    o["l_ln1"] = i["L3_ffn_w_ln1"].reshape(KC, P).T
    o["l_ln2"] = i["L3_ffn_w_ln2"].reshape(KC, P).T
    o["l_wq"] = cols(i["L3_ffn_Wq"], KC)
    o["l_wkva"] = cols(i["L3_ffn_Wkva"], KC)
    wk = np.zeros((64, 16, 64), f)
    wk[:32, :, :32] = i["L3_ffn_Wkvb"].reshape(32, 16, 32)
    wk[32:, :, 32:] = np.eye(32, dtype=f)[:, None, :]
    o["l_wk"] = wk.reshape(64, 1024)
    o["l_wv"] = i["L3_ffn_Wkvb"]
    o["l_perm"] = np.eye(P, dtype=f)[np.arange(P) ^ 1]
    freq = 1.0 / 100000.0 ** (np.arange(0, 32, 2, dtype=np.float32) / 32)
    p = np.arange(P)
    rope = (p % 64 >= 32)[:, None]
    ang = np.arange(S)[None, :] * freq[(p % 32) // 2][:, None]
    sign = np.where(p % 2 == 0, -1, 1)[:, None]
    o["l_tab"] = np.stack([np.where(rope, np.cos(ang), 1), np.where(rope, sign * np.sin(ang), 0)], 1).astype(f)
    wo = np.zeros((18, 32, D), f)
    wo[:16] = i["L3_ffn_Wo"].reshape(16, 64, D)[:, :32]
    o["l_wo"] = wo.reshape(6, 96, D).transpose(1, 0, 2)
    o["l_vmask"] = (np.arange(TT)[:, None] // S == (np.arange(512)[None, :] // 32) % G).astype(f)
    pos = np.tile(np.arange(S), G)[:, None]
    o["l_neg"] = np.where(np.arange(S)[None, :] <= pos, 0, -1e30).astype(f)
    o["l_router"] = cols(i["L3_ffn_Wgate"], KC)
    o["l_bias"] = rep(i["L3_ffn_expert_bias"])
    o["l_w_e"] = np.concatenate([up_cols(i[f"L3_ffn_{n}"]) for n in ("Wg", "Wu", "Wd")], 2)
    o["l_w_s"] = np.concatenate([up_cols(i[f"L3_ffn_s{n}"]) for n in ("Wg", "Wu", "Wd")], 2)


def on_normed(name, *parts):
    def stage(nc, d, h, xT, ident):
        with ExitStack() as stack:
            sb, _ = bufs(nc, stack)
            r = sb(f"{name}_r", [TT, NT, D])
            norm_transpose(nc, f"{name}_ln", h, xT, ident, 1e-5, True, x_tok=r, turn=False)
            for part in parts:
                part(nc, d, r, xT, ident)
            s = sems(nc, stack, f"{name}_added")
            block = stack.enter_context(nc.Block())

            @block.vector
            def _(dve):
                nc.vector.tensor_tensor(h[:, :, :], h[:, :, :], r[:, :, :], ALU.add).then_inc(
                    s[f"{name}_added"], 1)
    return stage


STAGES = [lambda nc, d, h, xT, ident: stage_tok(nc, d, h, ident), stage_attn0, stage_ffn0, stage_gate1, stage_ffn1,
          stage_scan, stage_moe2, on_normed("l6", stage_delta, stage_moe3),
          on_normed("l7", stage_mla, stage_moe4)]
LAYOUTS = [layout_attn0, layout_ffn0, layout_l1, layout_scan, layout_moe2, layout_delta, layout_mla]


def cols(a, k):
    return a.reshape(k, -1, a.shape[1]).transpose(1, 0, 2)


def rep(a, n=TT):
    return np.broadcast_to(a.reshape(1, -1), (n, a.size))


def tiles(a):
    return a.reshape(NT, TT, -1).transpose(1, 0, 2)


def layout(i):
    f = np.float32
    o = {}
    pat = np.zeros((B + 1, S, 768), f)
    pat[:B, 1:] = i["x"].reshape(B, 3, 6, 16, 6, 16).transpose(0, 2, 4, 3, 5, 1).reshape(B, 36, 768)
    o["patches"] = tiles(pat.reshape(T, 768))
    add = np.zeros((B + 1, S, D), f)
    add[:B, 0] = i["L0_tok_class_token"].reshape(D)
    o["tok_addend"] = tiles(add.reshape(T, D))
    o["tok_pos"] = rep(i["L0_tok_pos_embedding"])
    o["tok_w"] = cols(i["L0_tok_weight"].T, 6)
    for g in LAYOUTS:
        g(i, o)
    return {k: np.ascontiguousarray(v) for k, v in o.items()}


def build(nc, d, out, stages=None, h0=None):
    with ExitStack() as stack:
        sb, _ = bufs(nc, stack)
        h = sb("h", [TT, NT, D])
        xT = sb("xT", [P, KC, T + 1])
        ident = sb("ident", [P, P])
        with ExitStack() as s0:
            s = sems(nc, s0, "start_zero start_ident start_h0")
            block = s0.enter_context(nc.Block())

            @block.gpsimd
            def _(pool):
                nc.gpsimd.memset(xT[:, :, T:], 0.0)
                nc.gpsimd.memset(ident[:, :], 0.0).then_inc(s["start_zero"], 1)
                pool.wait_ge(s["start_zero"], 2)
                nc.gpsimd.affine_select(out=ident[:, :], in_=ident[:, :], compare_op=ALU.not_equal, fill=1.0,
                                        base=0, pattern=[[-1, P]], channel_multiplier=1).then_inc(s["start_ident"], 1)
                pool.wait_ge(s["start_ident"], 2)

            if h0 is not None:
                @block.sync
                def _(sp):
                    sp.dma_start(h[:, :, :], h0).then_inc(s["start_h0"], 16)
                    sp.wait_ge(s["start_h0"], 17)
        for n, stage in enumerate(STAGES):
            if stages is None or n in stages:
                stage(nc, d, h, xT, ident)
        with ExitStack() as s1:
            s = sems(nc, s1, "out_written")
            block = s1.enter_context(nc.Block())
            flat = out.rearrange("b s d -> (b s) d")

            @block.sync
            def _(sp):
                n = NT - 1
                sp.dma_start(flat[0:n * TT, :].rearrange("(t p) d -> p t d", p=TT), h[:, 0:n, :]
                             ).then_inc(s["out_written"], 16)
                rest = B * S - n * TT
                sp.dma_start(flat[n * TT:B * S, :], h[0:rest, n, :]).then_inc(s["out_written"], 16)
                sp.wait_ge(s["out_written"], 33)


def kernel(**inputs):
    import concourse.bacc as _bacc
    from concourse.bass_utils import run_bass_kernel_spmd as _run

    nc = _bacc.Bacc("TRN2", target_bir_lowering=False, num_devices=1)
    arrays, d = {}, {}
    for name, a in layout({k: np.asarray(v) for k, v in inputs.items()}).items():
        arrays[f"in_{name}"] = a
        d[name] = nc.dram_tensor(f"in_{name}", a.shape, mybir.dt.from_np(a.dtype), kind="ExternalInput").ap()
    out = nc.dram_tensor("out_0", (B, S, D), F32, kind="ExternalOutput").ap()
    build(nc, d, out)
    r = _run(nc, [arrays], core_ids=[0])
    return r.results[0]["out_0"]
```

```python
import math
from contextlib import ExitStack

import concourse.bass as bass
import numpy as np
from concourse import mybir

ALU = mybir.AluOpType
ACT = mybir.ActivationFunctionType
F32 = mybir.dt.float32
F32R = mybir.dt.float32r
BF16 = mybir.dt.bfloat16
U32 = mybir.dt.uint32
X = mybir.AxisListType.X

P = 128
B, S, D = 32, 37, 256
G = 3
TT = G * S
NT = 11
T = NT * TT
KC = D // P
NCH = 3
CH = T // NCH
BANK = 512
ROUND = 12582912.0


def sems(nc, stack, names):
    made = {n: nc.alloc_semaphore(n) for n in names.split()}
    for sem in made.values():
        nc.gpsimd.nop().then_inc(sem, 1)
    nc.all_engine_barrier()
    stack.callback(lambda: nc.clear_and_free_semaphores(list(made.values())))
    return made


def bufs(nc, stack):
    def sb(name, shape, dt=F32):
        return stack.enter_context(nc.sbuf_tensor(name, shape, dt))

    def ps(name, shape, dt=F32):
        return stack.enter_context(nc.psum_tensor(name, shape, dt))

    return sb, ps


def chain(eng, sem, at=0):
    n = [0]

    def link(ins):
        n[0] += 1
        ins.then_inc(sem, 1)
        eng.wait_ge(sem, at + n[0] + 1)

    link.count = lambda: n[0]
    return link


def flat2(ap):
    return ap.rearrange("p a d -> p (a d)")


def span(i, n):
    return slice(i * n, (i + 1) * n) if isinstance(i, int) else bass.ds(i * n if n > 1 else i, n)


def norm_transpose(nc, name, h, xT, ident, eps, center, w_dram=None, w_plus=0.0, x_tok=None, turn=True,
                   loads=()):
    with ExitStack() as stack:
        sb, ps = bufs(nc, stack)
        s = sems(nc, stack, " ".join(f"{name}_{x}" for x in (
            "w_loaded", "loaded", "w_ready", "v", "var_ready", "rstd_ready", "shift_ready", "x_dve", "x_act", "turned",
            "done")))
        s = {k[len(name) + 1:]: v for k, v in s.items()}
        xn = x_tok if x_tok is not None else sb(f"{name}_xn", [TT, NT, D])
        stats = sb(f"{name}_stats", [TT, NT, 6])
        mv = sb(f"{name}_mv", [TT, NT, 2])
        var = sb(f"{name}_var", [TT, NT])
        half = sb(f"{name}_half", [TT, NT])
        rstd = sb(f"{name}_rstd", [TT, NT])
        shift = sb(f"{name}_shift", [TT, NT])
        w = sb(f"{name}_w", [P, KC])
        pt = ps(f"{name}_pt", [P, KC * NCH, BANK])
        groups = [(0, 4), (4, 8), (8, NT)] if turn else []
        halves = [(0, 6), (6, NT)]
        ACT_TILES = (2, 5, 9)
        block = stack.enter_context(nc.Block())

        @block.sync
        def _(sp):
            if w_dram is not None:
                sp.dma_start(w[:, :], w_dram).then_inc(s["w_loaded"], 16)
            for dst, src in loads:
                sp.dma_start(dst, src).then_inc(s["loaded"], 16)
            if loads:
                sp.wait_ge(s["loaded"], 16 * len(loads) + 1)

        @block.vector
        def _(dve):
            link = chain(dve, s["v"])
            nc.vector.memset(half[:, :], -0.5)
            for a, b in halves:
                for t in range(a, b):
                    last = nc.vector.bn_stats(stats[:, t, :], h[:, t, :])
                link(last)
                for t in range(a, b):
                    last = nc.vector.bn_aggr(mv[:, t, :], stats[:, t, :])
                link(last)
                mean, v = (flat2(mv[:, a:b, k:k + 1]) for k in range(2))
                if center:
                    ins = nc.vector.tensor_scalar(var[:, a:b], v, 1.0, eps, ALU.mult, ALU.add)
                else:
                    link(nc.vector.tensor_tensor(shift[:, a:b], mean, mean, ALU.mult))
                    ins = nc.vector.scalar_tensor_tensor(var[:, a:b], v, eps, shift[:, a:b], ALU.add, ALU.add)
                ins.then_inc(s["var_ready"], 1)
            if w_dram is not None:
                dve.wait_ge(s["w_loaded"], 17)
                nc.vector.tensor_scalar(w[:, :], w[:, :], w_plus, None, ALU.add).then_inc(s["w_ready"], 1)
                dve.wait_ge(s["w_ready"], 2)
            for n, (a, b) in enumerate(halves):
                dve.wait_ge(s["rstd_ready"], n + 2)
                if center:
                    nc.vector.scalar_tensor_tensor(shift[:, a:b], flat2(mv[:, a:b, 0:1]), -1.0, rstd[:, a:b], ALU.mult,
                                                   ALU.mult).then_inc(s["shift_ready"], 1)
                for t in range(a, b):
                    if t in ACT_TILES:
                        continue
                    if center:
                        ins = nc.vector.tensor_scalar(xn[:, t, :], h[:, t, :], mv[:, t, 0:1], rstd[:, t:t + 1],
                                                      ALU.subtract, ALU.mult)
                    else:
                        ins = nc.vector.tensor_scalar(xn[:, t, :], h[:, t, :], rstd[:, t:t + 1], None, ALU.mult)
                    ins.then_inc(s["x_dve"], 1)
            for g, (a, b) in enumerate(groups):
                dve.wait_ge(s["turned"], KC * g + 2)
                nc.vector.tensor_scalar(xT[:, 0, a * TT:b * TT], pt[:, g, 0:(b - a) * TT],
                                        w[:, 0:1] if w_dram is not None else 1.0, None, ALU.mult
                                        ).then_inc(s["done"], 1)

        @block.gpsimd
        def _(pool):
            for n, (a, b) in enumerate(halves):
                pool.wait_ge(s["var_ready"], n + 2)
                nc.gpsimd.tensor_tensor(rstd[:, a:b], var[:, a:b], half[:, a:b], ALU.pow).then_inc(s["rstd_ready"], 1)

        @block.tensor
        def _(pe):
            for g, (a, b) in enumerate(groups):
                for k in range(KC):
                    for t in range(a, b):
                        if k == 0:
                            before = sum(x < t for x in ACT_TILES)
                            if t in ACT_TILES:
                                pe.wait_ge(s["x_act"], before + 2)
                            else:
                                pe.wait_ge(s["x_dve"], t - before + 2)
                        last = nc.tensor.transpose(pt[:, k * NCH + g, (t - a) * TT:(t - a + 1) * TT],
                                                   xn[:, t, k * P:(k + 1) * P], ident[0:TT, 0:TT])
                    last.then_inc(s["turned"], 1)

        @block.scalar
        def _(act):
            for t in ACT_TILES:
                n = sum(t >= b for _, b in halves)
                act.wait_ge(s["rstd_ready"], n + 2)
                if center:
                    act.wait_ge(s["shift_ready"], n + 2)
                if center:
                    ins = nc.scalar.activation(xn[:, t, :], h[:, t, :], ACT.Identity, scale=rstd[:, t:t + 1],
                                               bias=shift[:, t:t + 1])
                else:
                    ins = nc.scalar.activation(xn[:, t, :], h[:, t, :], ACT.Copy, scale=rstd[:, t:t + 1])
                ins.then_inc(s["x_act"], 1)
            if w_dram is not None:
                act.wait_ge(s["w_ready"], 2)
            for g, (a, b) in enumerate(groups):
                act.wait_ge(s["turned"], KC * g + 3)
                nc.scalar.activation(xT[:, 1, a * TT:b * TT], pt[:, NCH + g, 0:(b - a) * TT], ACT.Copy,
                                     scale=w[:, 1:2] if w_dram is not None else 1.0).then_inc(s["done"], 1)


def stage_tok(nc, d, h, ident):
    DIN = 768
    NK = DIN // P
    with ExitStack() as stack:
        sb, ps = bufs(nc, stack)
        s = sems(nc, stack, "tok_w_in tok_add_in tok_v tok_v2 tok_a tok_wsum tok_wtot tok_wq_ready tok_ss tok_ms "
                            "tok_r tok_xr tok_rounded tok_q_ready tok_turned tok_qT tok_mm tok_base tok_hdone "
                            "tok_half tok_x0 tok_x1 tok_x2")
        w = sb("tok_w", [P, NK, D])
        wa = sb("tok_wa", [P, NK * D])
        wq = sb("tok_wq", [P, NK, D], BF16)
        ones = sb("tok_ones", [P, P])
        wsum = sb("tok_wsum_b", [P, 1])
        wmean = sb("tok_wmean", [P, 1])
        wscale = sb("tok_wscale", [P, 1])
        x = sb("tok_x", [TT, NT, DIN])
        junk = sb("tok_junk", [TT, 2, DIN])
        add = sb("tok_addend", [TT, NT, D])
        pos = sb("tok_pos", [TT, D])
        ss = sb("tok_ssb", [TT, NT])
        ms = sb("tok_msb", [TT, NT])
        mx = sb("tok_mx", [TT, NT])
        half = sb("tok_halfb", [TT, NT])
        r = sb("tok_rb", [TT, NT])
        back = sb("tok_back", [TT, 1])
        sc = sb("tok_sc", [TT, NT])
        inv = sb("tok_inv", [TT, NT])
        qb = sb("tok_qb", [TT, NT, DIN], BF16)
        identb = sb("tok_identb", [P, P], BF16)
        qT = sb("tok_qTb", [P, NT, NK * TT], BF16)
        pw = ps("tok_pw", [P, BANK])
        pt = ps("tok_pt", [P, 2, 1024], BF16)
        po = ps("tok_po", [P, BANK])
        parts = [(0, 4), (4, 8), (8, NT)]
        AHEAD = 3
        block = stack.enter_context(nc.Block())

        @block.sync
        def _(sp):
            sp.dma_start(w[:, :, :], d["tok_w"]).then_inc(s["tok_w_in"], 16)
            for g, (a, b) in enumerate(parts):
                sp.dma_start(x[:, a:b, :], d["patches"][:, a:b, :]).then_inc(s[f"tok_x{g}"], 16)
            sp.dma_start(add[:, :, :], d["tok_addend"]).then_inc(s["tok_add_in"], 16)
            sp.dma_start(pos[:, :], d["tok_pos"]).then_inc(s["tok_add_in"], 16)

        @block.scalar
        def _(act):
            act.wait_ge(s["tok_w_in"], 17)
            nc.scalar.activation(wa[:, :], w[:, :, :].rearrange("p k d -> p (k d)"), ACT.Abs,
                                 accum_out=wsum[:, :]).then_inc(s["tok_wsum"], 1)
            for g, (a, b) in enumerate(parts):
                act.wait_ge(s[f"tok_x{g}"], 17)
                for t in range(a, b):
                    if t >= 2:
                        act.wait_ge(s["tok_ss"], t)
                    nc.scalar.activation(junk[:, t % 2, :], x[:, t, :], ACT.Square, accum_out=ss[:, t:t + 1]
                                         ).then_inc(s["tok_ss"], 1)

            def scaled(i):
                nc.scalar.activation(flat2(x[:, span(i, 1), :]), flat2(x[:, span(i, 1), :]), ACT.Copy,
                                     scale=r[:, span(i, 1)]).then_inc(s["tok_xr"], 1)

            def copy(i):
                act.wait_ge(s["tok_turned"], i + 2)
                nc.scalar.activation(flat2(qT[:, span(i, 1), :]).rearrange("p (k t) -> p k t", t=TT),
                                     pt[:, 0, 0:NK * P].rearrange("p (k t) -> p k t", t=P)[:, :, 0:TT], ACT.Copy
                                     ).then_inc(s["tok_qT"], 1)

            act.wait_ge(s["tok_r"], 2)
            for i in range(AHEAD):
                scaled(i)
            with act.Fori(AHEAD, NT) as i:
                scaled(i)
                copy(i - AHEAD)
            for i in range(NT - AHEAD, NT):
                copy(i)

        @block.gpsimd
        def _(pool):
            pool.wait_ge(s["tok_add_in"], 33)
            nc.gpsimd.tensor_tensor(h[:, :, :], add[:, :, :], pos[:, :].unsqueeze(1).broadcast_to([TT, NT, D]),
                                    ALU.add).then_inc(s["tok_base"], 1)
            pool.wait_ge(s["tok_ms"], 2)
            nc.gpsimd.tensor_tensor(r[:, :], ms[:, :], half[:, :], ALU.pow).then_inc(s["tok_r"], 1)
            with pool.Fori(0, NT) as i:
                pool.wait_ge(s["tok_rounded"], i + 2)
                nc.gpsimd.tensor_tensor(flat2(qb[:, bass.ds(i, 1), :]), flat2(x[:, bass.ds(i, 1), :]),
                                        back[:, :].broadcast_to([TT, DIN]), ALU.add).then_inc(s["tok_q_ready"], 1)

        @block.tensor
        def _(pe):
            pe.wait_ge(s["tok_half"], 2)
            pe.wait_ge(s["tok_wsum"], 2)
            nc.tensor.matmul(pw[:, 0:1], ones[:, :], wsum[:, :], start=True, stop=True).then_inc(s["tok_wtot"], 1)
            pe.wait_ge(s["tok_wq_ready"], 2)

            def turn(i):
                pe.wait_ge(s["tok_q_ready"], i + 2)
                pe.wait_ge(s["tok_qT"], i + 1)
                one = flat2(qb[:, span(i, 1), :])
                for k in range(NK):
                    last = nc.tensor.transpose(pt[:, 0, k * P:k * P + TT], one[:, k * P:(k + 1) * P],
                                               identb[0:TT, 0:TT])
                last.then_inc(s["tok_turned"], 1)

            def product(i):
                pe.wait_ge(s["tok_qT"], i + 2)
                pe.wait_ge(s["tok_hdone"], i + 1)
                one = flat2(qT[:, span(i, 1), :])
                for k in range(NK):
                    last = nc.tensor.matmul(po[0:TT, 0:D], one[:, k * TT:(k + 1) * TT], wq[:, k, :], start=(k == 0),
                                            stop=(k == NK - 1))
                last.then_inc(s["tok_mm"], 1)

            turn(0)
            with pe.Fori(1, NT) as i:
                turn(i)
                product(i - 1)
            product(NT - 1)

        @block.vector
        def _(dve):
            link = chain(dve, s["tok_v"])
            nc.vector.memset(half[:, :], -0.5)
            nc.vector.memset(back[:, :], -ROUND)
            nc.vector.tensor_copy(identb[:, :], ident[:, :])
            nc.vector.memset(ones[:, :], 1.0).then_inc(s["tok_half"], 1)
            dve.wait_ge(s["tok_wtot"], 2)
            link(nc.vector.tensor_scalar(wmean[:, :], pw[:, 0:1], 1.0 / (D * DIN), 1e-5, ALU.mult, ALU.max))
            link(nc.vector.reciprocal(wscale[:, :], wmean[:, :]))
            wf = w[:, :, :]
            link(nc.vector.tensor_scalar(wf, wf, wscale[:, 0:1], None, ALU.mult))
            link(nc.vector.tensor_scalar(wf, wf, ROUND, -ROUND, ALU.add, ALU.add))
            nc.vector.tensor_scalar(wq[:, :, :], wf, 1.0, -1.0, ALU.min, ALU.max).then_inc(s["tok_wq_ready"], 1)
            for g, (a, b) in enumerate(parts):
                dve.wait_ge(s[f"tok_x{g}"], 17)
                last = nc.vector.tensor_reduce(mx[:, a:b], x[:, a:b, :], X, ALU.max, apply_absolute_value=True)
            link(last)
            dve.wait_ge(s["tok_ss"], NT + 1)
            nc.vector.tensor_scalar(ms[:, :], ss[:, :], 1.0 / DIN, 1e-6, ALU.mult, ALU.add).then_inc(s["tok_ms"], 1)
            dve.wait_ge(s["tok_r"], 2)
            link(nc.vector.tensor_tensor(mx[:, :], mx[:, :], r[:, :], ALU.mult))
            link(nc.vector.tensor_scalar(mx[:, :], mx[:, :], 1e-5, None, ALU.max))
            link(nc.vector.reciprocal(sc[:, :], mx[:, :]))
            link(nc.vector.tensor_scalar(sc[:, :], sc[:, :], 127.0, None, ALU.mult))
            link(nc.vector.tensor_scalar(inv[:, :], mx[:, :], 1.0 / 127.0, wmean[0:TT, 0:1], ALU.mult, ALU.mult))

            def rounded(i):
                dve.wait_ge(s["tok_xr"], i + 2)
                one = flat2(x[:, span(i, 1), :])
                nc.vector.tensor_scalar(one, one, sc[:, span(i, 1)], 127.0, ALU.mult, ALU.min).then_inc(s["tok_v2"], 1)
                dve.wait_ge(s["tok_v2"], i + 2)
                nc.vector.tensor_scalar(one, one, -128.0, ROUND, ALU.max, ALU.add).then_inc(s["tok_rounded"], 1)

            def add(i):
                dve.wait_ge(s["tok_mm"], i + 2)
                ht = flat2(h[:, span(i, 1), :])
                nc.vector.scalar_tensor_tensor(ht, po[0:TT, 0:D], inv[:, span(i, 1)], ht, ALU.mult, ALU.add
                                               ).then_inc(s["tok_hdone"], 1)

            for i in range(AHEAD):
                rounded(i)
            dve.wait_ge(s["tok_base"], 2)
            with dve.Fori(AHEAD, NT) as i:
                rounded(i)
                add(i - AHEAD)
            for i in range(NT - AHEAD, NT):
                add(i)


def stage_attn0(nc, d, h, xT, ident):
    H, HG = 16, 8
    QG = 4
    NB = H // QG
    W = QG * S
    PG = (H + G - 1) // G
    with ExitStack() as stack:
        sb, ps = bufs(nc, stack)
        wq, wk, wv = (sb(f"a_w{n}", [P, KC, D]) for n in "qkv")
        wo = sb("a_wo", [G * 16, PG, D])
        bo = sb("a_bo", [TT, D])
        uv = sb("a_uv", [P, 2, KC])
        perm = sb("a_perm", [P, P])
        tab = sb("a_tab", [P, 4, TT])
        texp = sb("a_texp", [P, HG, S])
        hmask = sb("a_hmask", [P, HG])
        vmask = sb("a_vmask", [TT, D])
        band = sb("a_band", [TT, 2, S])
        norm_transpose(nc, "an", h, xT, ident, 1e-5, True, loads=[(x[:, :, :], d[f"a_{n}"]) for n, x in (
            ("wq", wq), ("wk", wk), ("wv", wv), ("wo", wo), ("tab", tab), ("texp", texp), ("band", band), ("uv", uv))]
            + [(x[:, :], d[f"a_{n}"]) for n, x in (("bo", bo), ("perm", perm), ("hmask", hmask), ("vmask", vmask))])
        s = sems(nc, stack, "a_zero a_qk_mm a_qk_done a_sw_mm a_sw_done a_qpad "
                            "a_qu_tile a_xrep a_kexp a_rot a_scores a_v_mm a_vexp a_probs a_max a_exp "
                            "a_turned a_summed a_pT a_pv a_oT a_out_mm a_hdone a_v1 a_v2")
        qu = sb("a_qu", [P, KC, T])
        qv = sb("a_qv", [P, KC, T + 1])
        sw = sb("a_sw", [P, KC, T + 1])
        kT = sb("a_kT", [P, KC, T])
        qum = sb("a_qum", [P, KC, G * TT])
        kexp = sb("a_kexp", [P, KC, G, HG, S])
        xrep = sb("a_xrep", [P, KC, G, G, S])
        r = [sb(f"a_r{n}", [P, KC, TT]) for n in (1, 2)]
        rt = [sb(f"a_rt{n}", [P, KC, TT]) for n in (1, 2)]
        m1 = sb("a_m1", [TT, NB, QG, S])
        m2 = sb("a_m2", [TT, NB, QG, S])
        e = sb("a_e", [TT, NB * QG, S])
        mx = sb("a_mx", [TT, H])
        sm = sb("a_sm", [TT, H])
        pT = sb("a_pTb", [TT, PG, TT])
        vexp = sb("a_vexpb", [TT, G, D])
        oT = sb("a_oTb", [G * 16, PG, TT])
        tmp = sb("a_tmp", [TT, D])
        psS = ps("a_psS", [P, NB, BANK])
        psT = ps("a_psT", [P, 2, BANK])
        psV = ps("a_psV", [P, 2, BANK])
        block = stack.enter_context(nc.Block())

        @block.tensor
        def _(pe):
            n = 0
            for w in (wq, wk):
                for c in range(KC):
                    for t in range(NCH):
                        if n >= 4:
                            pe.wait_ge(s["a_qk_done"], n - 2)
                        for k in range(KC):
                            last = nc.tensor.matmul(psS[:, n % 4, 0:CH], w[:, k, c * P:(c + 1) * P],
                                                    xT[:, k, t * CH:(t + 1) * CH], start=(k == 0), stop=(k == KC - 1))
                        last.then_inc(s["a_qk_mm"], 1)
                        n += 1
            pe.wait_ge(s["a_qk_done"], n + 1)
            for m in range(KC * NCH):
                if m >= 4:
                    pe.wait_ge(s["a_sw_done"], m - 2)
                c, t = divmod(m, NCH)
                nc.tensor.matmul(psS[:, m % 4, 0:CH], perm[:, :], qv[:, c, t * CH:(t + 1) * CH],
                                 start=True, stop=True).then_inc(s["a_sw_mm"], 1)
            pe.wait_ge(s["a_sw_done"], KC * NCH + 1)
            def scores(i):
                pe.wait_ge(s["a_qu_tile"], i + 2)
                pe.wait_ge(s["a_kexp"], i + 2)
                pe.wait_ge(s["a_rot"], i + 2)
                pe.wait_ge(s["a_summed"], i + 1)
                for g in range(NB):
                    c, o = divmod(g, 2)
                    for q in range(G):
                        nc.tensor.matmul(psS[0:TT, g, 0:W], qum[:, c, q * TT:(q + 1) * TT],
                                         kexp[:, c, q, o * QG:(o + 1) * QG, :].rearrange("p h j -> p (h j)"),
                                         start=(q == 0), stop=(q == G - 1))
                    for m in range(2):
                        last = nc.tensor.matmul(psS[0:TT, g, (m + 1) * W:(m + 2) * W], r[m][:, c, :],
                                                flat2(texp[:, o * QG:(o + 1) * QG, :]), start=True, stop=True)
                last.then_inc(s["a_scores"], 1)

            def values(i):
                pe.wait_ge(s["a_xrep"], i + 2)
                pe.wait_ge(s["a_vexp"], i + 1)
                for q in range(G):
                    for k in range(KC):
                        last = nc.tensor.matmul(psV[0:TT, q // 2, (q % 2) * D:(q % 2 + 1) * D],
                                                xrep[:, k, q, :, :].rearrange("p a j -> p (a j)"), wv[:, k, :],
                                                start=(k == 0), stop=(k == KC - 1))
                last.then_inc(s["a_v_mm"], 1)

            def turn(i):
                pe.wait_ge(s["a_probs"], i + 2)
                pe.wait_ge(s["a_hdone"], i + 1)
                for g in range(PG):
                    n = min(G, H - G * g) * S
                    last = nc.tensor.transpose(psT[0:n, g // 4, (g % 4) * TT:(g % 4 + 1) * TT],
                                               e[:, G * g:G * g + n // S, :].rearrange("p h j -> p (h j)"),
                                               ident[0:TT, 0:TT])
                last.then_inc(s["a_turned"], 1)

            def mix_values(i):
                pe.wait_ge(s["a_pT"], i + 2)
                pe.wait_ge(s["a_vexp"], i + 2)
                for g in range(PG):
                    m = min(G, H - G * g)
                    for q in range(G):
                        last = nc.tensor.matmul(psT[0:m * 16, g // 4, (g % 4) * TT + q * S:(g % 4) * TT + (q + 1) * S],
                                                vexp[0:m * S, q, g * 48:g * 48 + m * 16],
                                                pT[0:m * S, g, q * S:(q + 1) * S], start=True, stop=True)
                last.then_inc(s["a_pv"], 1)

            def project(i):
                pe.wait_ge(s["a_oT"], i + 2)
                for g in range(PG):
                    m = min(G, H - G * g) * 16
                    last = nc.tensor.matmul(psT[0:TT, 1, 0:D], oT[0:m, g, :], wo[0:m, g, :],
                                            start=(g == 0), stop=(g == PG - 1))
                last.then_inc(s["a_out_mm"], 1)

            scores(0)
            values(0)
            with pe.Fori(1, NT) as i:
                scores(i)
                turn(i - 1)
                mix_values(i - 1)
                values(i)
                project(i - 1)
            turn(NT - 1)
            mix_values(NT - 1)
            project(NT - 1)

        @block.scalar
        def _(act):
            act.wait_ge(s["a_qpad"], 2)
            for m in range(KC * NCH):
                c, t = divmod(m, NCH)
                act.wait_ge(s["a_sw_mm"], m + 2)
                nc.scalar.activation(sw[:, c, t * CH:(t + 1) * CH], psS[:, m % 4, 0:CH], ACT.Copy
                                     ).then_inc(s["a_sw_done"], 1)
            with act.Fori(0, NT) as i:
                act.wait_ge(s["a_max"], i + 2)
                act.wait_ge(s["a_turned"], i + 1)
                nc.scalar.activation(e[:, :, :], m1[:, :, :, :].rearrange("p b h j -> p (b h) j"), ACT.Exp,
                                     scale=0.25).then_inc(s["a_exp"], 1)
                act.wait_ge(s["a_turned"], i + 2)
                nc.scalar.activation(pT[:, 0:4, :].rearrange("p g t -> p (g t)"), psT[0:TT, 0, 0:4 * TT], ACT.Copy
                                     ).then_inc(s["a_v2"], 1)
                nc.scalar.activation(pT[:, 4, :], psT[0:TT, 1, 0:TT], ACT.Copy).then_inc(s["a_v2"], 1)
                nc.scalar.activation(pT[0:S, 5, :], psT[0:S, 1, TT:2 * TT], ACT.Copy).then_inc(s["a_v2"], 1)
                act.wait_ge(s["a_v2"], 3 * i + 4)
                nc.scalar.nop().then_inc(s["a_pT"], 1)
                act.wait_ge(s["a_pv"], i + 2)
                nc.scalar.activation(oT[:, 0:4, :].rearrange("p g t -> p (g t)"), psT[0:48, 0, 0:4 * TT], ACT.Copy)
                nc.scalar.activation(oT[:, 4, :], psT[0:48, 1, 0:TT], ACT.Copy)
                nc.scalar.activation(oT[0:16, 5, :], psT[0:16, 1, TT:2 * TT], ACT.Copy).then_inc(s["a_oT"], 1)

        @block.gpsimd
        def _(pool):
            nc.gpsimd.memset(qum[:, :, :], 0.0)
            nc.gpsimd.memset(qv[:, :, T:T + 1], 0.0).then_inc(s["a_zero"], 1)
            nc.gpsimd.memset(sw[:, :, T:T + 1], 0.0).then_inc(s["a_qpad"], 1)
            pool.wait_ge(s["a_zero"], 2)
            pool.wait_ge(s["a_qk_done"], 2 * KC * NCH + 1)
            with pool.Fori(0, NT) as i:
                pool.wait_ge(s["a_scores"], i + 1)
                for c in range(KC):
                    src = kT[:, c, bass.ds(i * TT, TT)].rearrange("p (q j) -> p q j", q=G)
                    for q in range(G):
                        last = nc.gpsimd.tensor_tensor(
                            kexp[:, c, q, :, :], src[:, q, :].unsqueeze(1).broadcast_to([P, HG, S]),
                            hmask[:, :].unsqueeze(2).broadcast_to([P, HG, S]), ALU.mult)
                last.then_inc(s["a_kexp"], 1)
                pool.wait_ge(s["a_v_mm"], i + 1)
                for c in range(KC):
                    for q in range(G):
                        last = nc.gpsimd.tensor_copy(xrep[:, c, q, :, :],
                                                     xT[:, c, bass.ds(i * TT + q * S, S)].unsqueeze(1)
                                                     .broadcast_to([P, G, S]))
                last.then_inc(s["a_xrep"], 1)

        @block.vector
        def _(dve):
            dve.wait_ge(s["a_zero"], 2)
            n = 0
            for w in range(2):
                for c in range(KC):
                    for t in range(NCH):
                        dve.wait_ge(s["a_qk_mm"], n + 2)
                        src = psS[:, n % 4, 0:CH]
                        at = slice(t * CH, (t + 1) * CH)
                        if w == 0:
                            nc.vector.tensor_scalar(qu[:, c, at], src, uv[:, 0, c:c + 1], None, ALU.add)
                            last = nc.vector.tensor_scalar(qv[:, c, at], src, uv[:, 1, c:c + 1], None, ALU.add)
                        else:
                            last = nc.vector.tensor_copy(kT[:, c, at], src)
                        last.then_inc(s["a_qk_done"], 1)
                        n += 1
            dve.wait_ge(s["a_qk_done"], n + 1)
            dve.wait_ge(s["a_sw_done"], KC * NCH + 1)
            def rotate(i):
                dve.wait_ge(s["a_scores"], i + 1)
                for c in range(KC):
                    for q in range(G):
                        last = nc.vector.tensor_copy(qum[:, c, q * (TT + S):q * (TT + S) + S],
                                                     qu[:, c, bass.ds(i * TT + q * S, S)])
                last.then_inc(s["a_qu_tile"], 1)
                for m in range(2):
                    at = bass.ds(i * TT + m, TT)
                    nc.vector.tensor_tensor(r[m][:, :, :], qv[:, :, at],
                                            tab[:, 2 * m:2 * m + 1, :].broadcast_to([P, KC, TT]), ALU.mult)
                    link(nc.vector.tensor_tensor(rt[m][:, :, :], sw[:, :, at],
                                                 tab[:, 2 * m + 1:2 * m + 2, :].broadcast_to([P, KC, TT]), ALU.mult))
                for m in range(2):
                    ins = nc.vector.tensor_tensor(r[m][:, :, :], r[m][:, :, :], rt[m][:, :, :], ALU.add)
                ins.then_inc(s["a_rot"], 1)

            def softmax(i):
                dve.wait_ge(s["a_scores"], i + 2)
                dve.wait_ge(s["a_exp"], i + 1)
                part = [psS[0:TT, :, m * W:(m + 1) * W].rearrange("p b (h j) -> p b h j", j=S) for m in range(3)]
                for m, dst in ((1, m1), (2, m2)):
                    last = nc.vector.tensor_tensor(dst[:, :, :, :], part[m],
                                                   band[:, m - 1:m, :].unsqueeze(1).broadcast_to([TT, NB, QG, S]),
                                                   ALU.mult)
                link(last)
                link(nc.vector.tensor_tensor(m2[:, :, :, :].rearrange("p b h j -> p b (h j)"),
                                             m2[:, :, :, :].rearrange("p b h j -> p b (h j)"),
                                             psS[0:TT, :, 0:W], ALU.add))
                nc.vector.nop().then_inc(s["a_summed"], 1)
                link(nc.vector.tensor_tensor(m1[:, :, :, :].rearrange("p b h j -> p (b h j)"),
                                             m1[:, :, :, :].rearrange("p b h j -> p (b h j)"),
                                             m2[:, :, :, :].rearrange("p b h j -> p (b h j)"), ALU.add))
                sc = m1[:, :, :, :].rearrange("p b h j -> p (b h) j")
                link(nc.vector.tensor_reduce(mx[:, :], sc, X, ALU.max))
                nc.vector.tensor_tensor(sc, sc, mx[:, :].unsqueeze(2).broadcast_to([TT, H, S]),
                                        ALU.subtract).then_inc(s["a_max"], 1)

            def probs(i):
                dve.wait_ge(s["a_exp"], i + 2)
                link(nc.vector.tensor_reduce(sm[:, :], e[:, :, :], X, ALU.add))
                link(nc.vector.reciprocal(sm[:, :], sm[:, :]))
                nc.vector.tensor_tensor(e[:, :, :], e[:, :, :], sm[:, :].unsqueeze(2).broadcast_to([TT, H, S]),
                                        ALU.mult).then_inc(s["a_probs"], 1)

            def values(i):
                dve.wait_ge(s["a_v_mm"], i + 2)
                dve.wait_ge(s["a_pv"], i + 1)
                for q in range(G):
                    last = nc.vector.tensor_tensor(vexp[:, q, :], psV[0:TT, q // 2, (q % 2) * D:(q % 2 + 1) * D],
                                                   vmask[:, :], ALU.mult)
                last.then_inc(s["a_vexp"], 1)

            def add(i):
                dve.wait_ge(s["a_out_mm"], i + 2)
                link(nc.vector.tensor_tensor(tmp[:, :], psT[0:TT, 1, 0:D], bo[:, :], ALU.add))
                ht = h[:, i, :] if isinstance(i, int) else flat2(h[:, bass.ds(i, 1), :])
                nc.vector.tensor_tensor(ht, ht, tmp[:, :], ALU.add).then_inc(s["a_hdone"], 1)

            link = chain(dve, s["a_v1"])
            rotate(0)
            ROT = link.count()
            softmax(0)
            rotate(1)
            probs(0)
            values(0)
            V0 = link.count()
            V1 = V0 - ROT + 1
            with dve.Fori(1, NT - 1) as i:
                link = chain(dve, s["a_v1"], (i - 1) * V1 + V0)
                softmax(i)
                rotate(i + 1)
                probs(i)
                values(i)
                add(i - 1)
            assert link.count() == V1, link.count()
            link = chain(dve, s["a_v1"], (NT - 2) * V1 + V0)
            softmax(NT - 1)
            probs(NT - 1)
            values(NT - 1)
            add(NT - 2)
            add(NT - 1)


def layout_attn0(i, o):
    f = np.float32
    for n in "qkv":
        o[f"a_w{n}"] = cols(i[f"L0_attn_W{n}"], KC)
    wo = np.zeros((6, 48, D), f)
    wo.reshape(288, D)[:D] = i["L0_attn_Wo"]
    o["a_wo"] = wo.transpose(1, 0, 2)
    o["a_bo"] = rep(i["L0_attn_bo"])
    o["a_uv"] = np.stack([i["L0_attn_u"].reshape(KC, P).T, i["L0_attn_v"].reshape(KC, P).T], 1)
    o["a_perm"] = np.eye(P, dtype=f)[np.arange(P) ^ 8]
    freq = 1.0 / 10000.0 ** (np.arange(0, 16, 2) / 16)
    w = np.tile(freq, P // 8)[:, None]
    sine = (np.arange(P) % 16 < 8)[:, None]
    pos = np.tile(np.arange(S), G)[None, :]
    tab = []
    for a in (pos, pos + S + 1):
        tab += [np.sin(a * w), np.where(sine, 1, -1) * np.cos(a * w)]
    o["a_tab"] = np.stack(tab, 1).astype(f)
    j = np.arange(S)[None, :]
    t = np.where(sine, np.cos(j * w), np.sin(j * w))
    own = (np.arange(P)[:, None] // 16 == np.arange(8)[None, :])
    o["a_texp"] = (own[:, :, None] * t[:, None, :]).astype(f)
    o["a_hmask"] = own.astype(f)
    o["a_vmask"] = (np.arange(TT)[:, None] // S == (np.arange(D)[None, :] // 16) % G).astype(f)
    q = np.tile(np.arange(S), G)[:, None]
    o["a_band"] = np.stack([j <= q, j >= q + 2], 1).astype(f)


def stage_ffn0(nc, d, h, xT, ident):
    F = 1024
    FC = F // P
    SP = S + 2
    with ExitStack() as stack:
        sb, ps = bufs(nc, stack)
        x = sb("f_x", [TT, NT, D])
        w1 = sb("f_w1", [P, KC * F])
        w2 = sb("f_w2", [P, FC * D])
        cw = sb("f_cw", [P, FC, 3])
        cb = sb("f_cb", [P, FC])
        norm_transpose(nc, "fn", h, xT, ident, 1e-5, True, x_tok=x, turn=False, loads=[
            (w1[:, :], d["f_w1"]), (w2[:, :], d["f_w2"]), (cw[:, :, :], d["f_cw"]), (cb[:, :], d["f_cb"])])
        s = sems(nc, stack, "f_v f_v2 f_v3 f_ones f_wsum f_wtot f_wq f_xq f_turned f_qT f_diag f_bc_mm f_bc "
                            "f_h_mm f_hp f_edge f_conv1 f_conv3 f_silu f_amax f_max_turned f_max f_diag2 f_bc2_mm "
                            "f_bc2 f_scaled f_hq f_out_mm f_hdone f_a")
        w1q = sb("f_w1q", [P, KC, F], BF16)
        w2q = sb("f_w2q", [P, FC, D], BF16)
        ones = sb("f_ones_b", [P, P])
        wsum = sb("f_wsum_b", [P, 2])
        wmean = sb("f_wmean", [P, 2])
        wscale = sb("f_wscale", [P, 2])
        mx = sb("f_mx", [TT, NT])
        sc = sb("f_sc", [TT, NT])
        inv = sb("f_inv", [TT, NT])
        xb = sb("f_xb", [TT, NT, D], BF16)
        identb = sb("f_identb", [P, P], BF16)
        qT = sb("f_qTb", [P, KC, T], BF16)
        diag = sb("f_diagb", [TT, NT, TT])
        bc = sb("f_bcb", [P, T])
        hp = [sb(f"f_hpb{u}", [P, B + 1, SP]) for u in range(2)]
        acc = [sb(f"f_acc{u}", [P, B + 1, S]) for u in range(2)]
        act1 = sb("f_act", [P, FC, T])
        amax = sb("f_amaxb", [P, T])
        hq = sb("f_hqb", [P, FC, T], BF16)
        pm = ps("f_pm", [P, NCH, BANK])
        pt = ps("f_pt", [P, 4, 2 * BANK], BF16)
        po = ps("f_po", [P, BANK])
        groups = [(0, 4), (4, 8), (8, NT)]
        SL = TT + 1
        ph = [(0, 9), (9, NT)]
        MP = 3
        block = stack.enter_context(nc.Block())

        @block.scalar
        def _(act):
            nc.scalar.activation(act1[:, 0:2, :].rearrange("p c t -> p (c t)")[:, 0:KC * F], w1[:, :], ACT.Abs,
                                 accum_out=wsum[:, 0:1])
            nc.scalar.activation(act1[:, 2:4, :].rearrange("p c t -> p (c t)")[:, 0:FC * D], w2[:, :], ACT.Abs,
                                 accum_out=wsum[:, 1:2]).then_inc(s["f_wsum"], 1)
            for g in range(4):
                act.wait_ge(s["f_turned"], g + 2)
                k, b = divmod(g, 2)
                lo, hi = ph[b]
                nc.scalar.activation(qT[:, k, lo * TT:hi * TT].rearrange("p (t x) -> p t x", x=TT),
                                     pt[:, g, 0:(hi - lo) * SL].rearrange("p (t x) -> p t x", x=SL)[:, :, 0:TT], ACT.Copy
                                     ).then_inc(s["f_qT"], 1)
            act.wait_ge(s["f_wsum"], 2)

            def first_tap(c, u):
                act.wait_ge(s["f_hp"], 3 * c + 4)
                act.wait_ge(s["f_silu"], c)
                nc.scalar.activation(acc[u][:, :, :], hp[u][:, :, 0:S], ACT.Identity, scale=flat2(cw[:, span(c, 1), 0:1]),
                                     bias=cb[:, span(c, 1)]).then_inc(s["f_conv1"], 1)

            def silu(c, u):
                act.wait_ge(s["f_conv3"], c + 2)
                nc.scalar.activation(flat2(act1[:, span(c, 1), :]), acc[u][:, :, :].rearrange("p b j -> p (b j)"),
                                     ACT.Silu).then_inc(s["f_silu"], 1)

            act.wait_ge(s["f_hp"], 4)
            nc.scalar.activation(acc[0][:, :, :], hp[0][:, :, 0:S], ACT.Identity, scale=cw[:, 0, 0:1],
                                 bias=cb[:, 0:1]).then_inc(s["f_conv1"], 1)
            first_tap(1, 1)
            silu(0, 0)
            with act.Fori(1, FC // 2) as i:
                for u in range(2):
                    first_tap(2 * i + u, u)
                    silu(2 * i + u - 1, 1 - u)
            silu(FC - 1, 1)

        @block.tensor
        def _(pe):
            pe.wait_ge(s["f_ones"], 2)
            pe.wait_ge(s["f_wsum"], 2)
            nc.tensor.matmul(po[:, 0:2], ones[:, :], wsum[:, :], start=True, stop=True).then_inc(s["f_wtot"], 1)
            pe.wait_ge(s["f_xq"], 2)
            for k in range(KC):
                for b, (lo, hi) in enumerate(ph):
                    for t in range(lo, hi):
                        last = nc.tensor.transpose(pt[:, 2 * k + b, (t - lo) * SL:(t - lo) * SL + TT],
                                                   xb[:, t, k * P:(k + 1) * P], identb[0:TT, 0:TT])
                    last.then_inc(s["f_turned"], 1)
            pe.wait_ge(s["f_diag"], 2)
            for g, (a, b) in enumerate(groups):
                last = nc.tensor.matmul(pm[:, g, 0:(b - a) * TT], ones[0:TT, :], flat2(diag[:, a:b, :]),
                                        start=True, stop=True)
            last.then_inc(s["f_bc_mm"], 1)
            pe.wait_ge(s["f_bc"], 2)
            pe.wait_ge(s["f_qT"], 5)
            with pe.Fori(0, FC) as c:
                for t in range(NCH):
                    pe.wait_ge(s["f_hp"], 3 * c + t + 1)
                    for k in range(KC):
                        last = nc.tensor.matmul(pm[:, t, 0:CH], w1q[:, k, bass.ds(c * P, P)],
                                                qT[:, k, t * CH:(t + 1) * CH], start=(k == 0), stop=(k == KC - 1))
                    last.then_inc(s["f_h_mm"], 1)
            pe.wait_ge(s["f_amax"], FC + 1)
            for g, (a, b) in enumerate(groups):
                pe.wait_ge(s["f_max"], g + 1)
                for t in range(a, b):
                    last = nc.tensor.transpose(pm[0:TT, 0, (t - a) * P:(t - a + 1) * P],
                                               amax[:, t * TT:(t + 1) * TT], ident[:, :])
                last.then_inc(s["f_max_turned"], 1)
            pe.wait_ge(s["f_diag2"], 2)
            for g, (a, b) in enumerate(groups):
                last = nc.tensor.matmul(pm[:, g, 0:(b - a) * TT], ones[0:TT, :], flat2(diag[:, a:b, :]),
                                        start=True, stop=True)
            last.then_inc(s["f_bc2_mm"], 1)
            pe.wait_ge(s["f_bc2"], NCH + 1)
            for g, (a, b) in enumerate(groups):
                pe.wait_ge(s["f_hq"], g + 2)
                for n in range(a, b):
                    if n >= NCH:
                        pe.wait_ge(s["f_hdone"], n - NCH + 2)
                    for k in range(FC):
                        last = nc.tensor.matmul(pm[0:TT, n % NCH, 0:D], hq[:, k, n * TT:(n + 1) * TT], w2q[:, k, :],
                                                start=(k == 0), stop=(k == FC - 1))
                    last.then_inc(s["f_out_mm"], 1)

        @block.gpsimd
        def _(pool):
            for u in range(2):
                nc.gpsimd.memset(hp[u][:, :, :], 0.0).then_inc(s["f_edge"], 1)
            for g, (a, b) in enumerate(groups):
                pool.wait_ge(s["f_bc2"], g + 2)
                nc.gpsimd.tensor_tensor(act1[:, 0:MP, a * TT:b * TT], act1[:, 0:MP, a * TT:b * TT],
                                        bc[:, a * TT:b * TT].unsqueeze(1).broadcast_to([P, MP, (b - a) * TT]), ALU.mult
                                        ).then_inc(s["f_scaled"], 1)

        @block.vector
        def _(dve):
            link = chain(dve, s["f_v"])
            nc.vector.memset(ones[:, :], 1.0).then_inc(s["f_ones"], 1)
            link(nc.vector.tensor_copy(identb[:, :], ident[:, :]))
            link(nc.vector.tensor_reduce(mx[:, :], x[:, :, :], X, ALU.max, apply_absolute_value=True))
            link(nc.vector.tensor_scalar(mx[:, :], mx[:, :], 1e-5, None, ALU.max))
            link(nc.vector.reciprocal(sc[:, :], mx[:, :]))
            link(nc.vector.tensor_scalar(sc[:, :], sc[:, :], 127.0, None, ALU.mult))
            link(nc.vector.tensor_tensor(x[:, :, :], x[:, :, :], sc[:, :].unsqueeze(2).broadcast_to([TT, NT, D]),
                                         ALU.mult))
            link(nc.vector.tensor_scalar(x[:, :, :], x[:, :, :], ROUND, -ROUND, ALU.add, ALU.add))
            nc.vector.tensor_scalar(xb[:, :, :], x[:, :, :], 127.0, -128.0, ALU.min, ALU.max).then_inc(s["f_xq"], 1)
            dve.wait_ge(s["f_wtot"], 2)
            link(nc.vector.tensor_scalar(wmean[:, :], po[:, 0:2], 1.0 / (F * D), 1e-5, ALU.mult, ALU.max))
            link(nc.vector.reciprocal(wscale[:, :], wmean[:, :]))
            for n, (w, wq) in enumerate(((w1, w1q), (w2, w2q))):
                link(nc.vector.tensor_scalar(w[:, :], w[:, :], wscale[:, n:n + 1], None, ALU.mult))
                link(nc.vector.tensor_scalar(w[:, :], w[:, :], ROUND, -ROUND, ALU.add, ALU.add))
                link(nc.vector.tensor_scalar(flat2(wq[:, :, :]), w[:, :], 1.0, -1.0, ALU.min, ALU.max))
            link(nc.vector.tensor_scalar(inv[:, :], mx[:, :], 1.0 / 127.0, wmean[0:TT, 0:1], ALU.mult, ALU.mult))
            eye = ident[0:TT, 0:TT].unsqueeze(1).broadcast_to([TT, NT, TT])
            nc.vector.tensor_tensor(diag[:, :, :], eye, inv[:, :].unsqueeze(2).broadcast_to([TT, NT, TT]), ALU.mult
                                    ).then_inc(s["f_diag"], 1)
            link(nc.vector.memset(amax[:, :], 0.0))
            dve.wait_ge(s["f_bc_mm"], 2)
            for g, (a, b) in enumerate(groups):
                last = nc.vector.tensor_copy(bc[:, a * TT:b * TT], pm[:, g, 0:(b - a) * TT])
            last.then_inc(s["f_bc"], 1)
            dve.wait_ge(s["f_bc"], 2)
            dve.wait_ge(s["f_edge"], 3)
            NB = (B + 1) // NCH

            def widened(c, u):
                if u is not None:
                    dve.wait_ge(s["f_conv3"], c)
                for t in range(NCH):
                    dve.wait_ge(s["f_h_mm"], 3 * c + t + 2)
                    nc.vector.tensor_tensor(hp[u or 0][:, t * NB:(t + 1) * NB, 1:S + 1],
                                            pm[:, t, 0:CH].rearrange("p (b j) -> p b j", j=S),
                                            bc[:, t * CH:(t + 1) * CH].rearrange("p (b j) -> p b j", j=S),
                                            ALU.mult).then_inc(s["f_hp"], 1)

            def taps(c, u):
                dve.wait_ge(s["f_conv1"], c + 2)
                dve.wait_ge(s["f_hp"], 3 * c + 4)
                tap = [flat2(cw[:, span(c, 1), n:n + 1]) for n in range(3)]
                link2(nc.vector.scalar_tensor_tensor(acc[u][:, :, :], hp[u][:, :, 1:S + 1], tap[1], acc[u][:, :, :],
                                                     ALU.mult, ALU.add))
                nc.vector.scalar_tensor_tensor(acc[u][:, :, :], hp[u][:, :, 2:S + 2], tap[2], acc[u][:, :, :],
                                               ALU.mult, ALU.add).then_inc(s["f_conv3"], 1)

            def largest(c):
                dve.wait_ge(s["f_silu"], c + 2)
                dve.wait_ge(s["f_amax"], c + 1)
                one = flat2(act1[:, span(c, 1), :])
                link2(nc.vector.scalar_tensor_tensor(amax[:, :], one, -1.0, amax[:, :], ALU.mult, ALU.max))
                nc.vector.tensor_tensor(amax[:, :], one, amax[:, :], ALU.max).then_inc(s["f_amax"], 1)

            link2 = chain(dve, s["f_v2"])
            widened(0, None)
            widened(1, 1)
            taps(0, 0)
            with dve.Fori(1, FC // 2) as i:
                link2 = chain(dve, s["f_v2"], 4 * (i - 1) + 1)
                for u in range(2):
                    widened(2 * i + u, u)
                    taps(2 * i + u - 1, 1 - u)
                    largest(2 * i + u - 2)
            link2 = chain(dve, s["f_v2"], 4 * (FC // 2 - 1) + 1)
            taps(FC - 1, 1)
            largest(FC - 2)
            largest(FC - 1)
            link3 = chain(dve, s["f_v3"])
            for g, (a, b) in enumerate(groups):
                dve.wait_ge(s["f_max_turned"], g + 2)
                nc.vector.tensor_reduce(mx[:, a:b], pm[0:TT, 0, 0:(b - a) * P].rearrange("p (t f) -> p t f", f=P),
                                        X, ALU.max).then_inc(s["f_max"], 1)
            dve.wait_ge(s["f_max"], 4)
            link3(nc.vector.tensor_scalar(mx[:, :], mx[:, :], 1e-5, None, ALU.max))
            link3(nc.vector.reciprocal(sc[:, :], mx[:, :]))
            link3(nc.vector.tensor_scalar(sc[:, :], sc[:, :], 127.0, None, ALU.mult))
            link3(nc.vector.tensor_scalar(inv[:, :], mx[:, :], 1.0 / 127.0, wmean[0:TT, 1:2], ALU.mult, ALU.mult))
            nc.vector.tensor_tensor(diag[:, :, :], eye, sc[:, :].unsqueeze(2).broadcast_to([TT, NT, TT]), ALU.mult
                                    ).then_inc(s["f_diag2"], 1)
            dve.wait_ge(s["f_bc2_mm"], 2)
            for g, (a, b) in enumerate(groups):
                nc.vector.tensor_copy(bc[:, a * TT:b * TT], pm[:, g, 0:(b - a) * TT]).then_inc(s["f_bc2"], 1)

            def add(g):
                for n in range(*groups[g]):
                    dve.wait_ge(s["f_out_mm"], n + 2)
                    nc.vector.scalar_tensor_tensor(h[:, n, :], pm[0:TT, n % NCH, 0:D], inv[:, n:n + 1], h[:, n, :],
                                                   ALU.mult, ALU.add).then_inc(s["f_hdone"], 1)

            for g, (a, b) in enumerate(groups):
                part = act1[:, :, a * TT:b * TT]
                dve.wait_ge(s["f_bc2"], g + 2)
                link3(nc.vector.tensor_tensor(part[:, MP:, :], part[:, MP:, :],
                                              bc[:, a * TT:b * TT].unsqueeze(1).broadcast_to([P, FC - MP, (b - a) * TT]),
                                              ALU.mult))
                dve.wait_ge(s["f_scaled"], g + 2)
                link3(nc.vector.tensor_scalar(part, part, ROUND, -ROUND, ALU.add, ALU.add))
                nc.vector.tensor_scalar(hq[:, :, a * TT:b * TT], part, 127.0, -128.0, ALU.min, ALU.max
                                        ).then_inc(s["f_hq"], 1)
                if g:
                    add(g - 1)
            add(NCH - 1)


def layout_ffn0(i, o):
    o["f_w1"] = cols(i["L0_ffn_w1"].T, KC).reshape(P, -1)
    o["f_w2"] = cols(i["L0_ffn_w2"].T, 8).reshape(P, -1)
    o["f_cw"] = cols(i["L0_ffn_conv_w"].reshape(-1, 3), 8)
    o["f_cb"] = i["L0_ffn_conv_b"].reshape(8, P).T


GROUPS = [(0, 4), (4, 8), (8, NT)]


def linear(sb, name, w_dram, n, bias_dram):
    w = sb(f"{name}_w", [P, KC, n])
    bias = sb(f"{name}_bias", [TT, n])
    return (w, bias, n), [(w[:, :, :], w_dram), (bias[:, :], bias_dram)]


def projected(nc, name, xT, layer, dst):
    w, bias, n = layer
    with ExitStack() as stack:
        _, ps = bufs(nc, stack)
        s = sems(nc, stack, f"{name}_mm {name}_done")
        s_mm, s_done = (s[f"{name}_{k}"] for k in ("mm", "done"))
        per = BANK // n
        parts = [(a, min(a + per, NT)) for a in range(0, NT, per)]
        NBK = min(4, len(parts))
        pp = ps(f"{name}_pp", [P, NBK, BANK])
        block = stack.enter_context(nc.Block())

        @block.tensor
        def _(pe):
            for m, (a, b) in enumerate(parts):
                if m >= NBK:
                    pe.wait_ge(s_done, m - NBK + 2)
                for t in range(a, b):
                    for k in range(KC):
                        last = nc.tensor.matmul(pp[0:TT, m % NBK, (t - a) * n:(t - a + 1) * n],
                                                xT[:, k, t * TT:(t + 1) * TT], w[:, k, :], start=(k == 0),
                                                stop=(k == KC - 1))
                last.then_inc(s_mm, 1)

        @block.vector
        def _(dve):
            for m, (a, b) in enumerate(parts):
                dve.wait_ge(s_mm, m + 2)
                nc.vector.tensor_tensor(dst[:, a:b, :],
                                        pp[0:TT, m % NBK, 0:(b - a) * n].rearrange("p (t n) -> p t n", n=n),
                                        bias[:, :].unsqueeze(1).broadcast_to([TT, b - a, n]), ALU.add
                                        ).then_inc(s_done, 1)


def stage_gate1(nc, d, h, xT, ident):
    N = 16
    W = D + 2 * N
    with ExitStack() as stack:
        sb, ps = bufs(nc, stack)
        x = sb("g_x", [TT, NT, D])
        pre = sb("g_pre", [TT, NT, W])
        layer, loads = linear(sb, "gp", d["g_w"], W, d["g_bias"])
        norm_transpose(nc, "gn", h, xT, ident, 1e-5, True, x_tok=x, loads=loads)
        projected(nc, "gp", xT, layer, pre)
        s = sems(nc, stack, "g_v g_abs g_exp g_ln")
        e = sb("g_e", [TT, NT, D])
        ln = sb("g_lnb", [TT, NT, D])
        u = sb("g_u", [TT, NT, D])
        bc = sb("g_bc", [TT, NT, N])
        sm = sb("g_sm", [TT, NT])
        block = stack.enter_context(nc.Block())

        @block.scalar
        def _(act):
            nc.scalar.activation(e[:, :, :], pre[:, :, 0:D], ACT.Abs).then_inc(s["g_abs"], 1)
            act.wait_ge(s["g_abs"], 2)
            nc.scalar.activation(e[:, :, :], e[:, :, :], ACT.Exp, scale=-1.0).then_inc(s["g_exp"], 1)
            act.wait_ge(s["g_exp"], 2)
            nc.scalar.activation(ln[:, :, :], e[:, :, :], ACT.Ln, bias=1.0).then_inc(s["g_ln"], 1)

        @block.vector
        def _(dve):
            link = chain(dve, s["g_v"])
            link(nc.vector.tensor_tensor(bc[:, :, :], pre[:, :, D:D + N], pre[:, :, D + N:W], ALU.mult))
            link(nc.vector.tensor_reduce(sm[:, :], bc[:, :, :], X, ALU.add))
            dve.wait_ge(s["g_exp"], 2)
            link(nc.vector.tensor_scalar(u[:, :, :], e[:, :, :], 1.0, None, ALU.add))
            link(nc.vector.scalar_tensor_tensor(u[:, :, :], u[:, :, :], -1.0, e[:, :, :], ALU.add, ALU.subtract))
            dve.wait_ge(s["g_ln"], 2)
            link(nc.vector.tensor_tensor(ln[:, :, :], ln[:, :, :], u[:, :, :], ALU.subtract))
            link(nc.vector.scalar_tensor_tensor(ln[:, :, :], pre[:, :, 0:D], 0.0, ln[:, :, :], ALU.max, ALU.add))
            link(nc.vector.tensor_tensor(ln[:, :, :], ln[:, :, :], x[:, :, :], ALU.mult))
            link(nc.vector.tensor_tensor(ln[:, :, :], ln[:, :, :], sm[:, :].unsqueeze(2).broadcast_to([TT, NT, D]),
                                         ALU.mult))
            link(nc.vector.tensor_tensor(h[:, :, :], h[:, :, :], ln[:, :, :], ALU.add))


def split_x(nc, name, xT, xh, xl):
    with ExitStack() as stack:
        s = sems(nc, stack, f"{name}_high {name}_low")
        block = stack.enter_context(nc.Block())

        @block.scalar
        def _(act):
            for k in range(KC):
                nc.scalar.activation(xh[:, k, :], xT[:, k, :], ACT.Copy).then_inc(s[f"{name}_high"], 1)

        @block.vector
        def _(dve):
            for k in range(KC):
                dve.wait_ge(s[f"{name}_high"], k + 2)
                nc.vector.tensor_tensor(xl[:, k, :], xT[:, k, :], xh[:, k, :].bitcast(F32), ALU.subtract
                                        ).then_inc(s[f"{name}_low"], 1)


def first_weights(sb, name, w_dram):
    w = sb(f"{name}_wb0", list(w_dram.shape[1:]))
    return w, [(w[:, :], w_dram[0])]


def experts(nc, name, w_dram, w0, gates, xh, xl, h, E, U, FC, gated, up_bias=None):
    I = FC * P
    NU = 2 if gated else 1
    UPW = NU * KC * I
    BW = UPW + FC * D
    biases = up_bias is not None
    WC = BW + (D if biases else 0)
    UP = 3 * FC
    NS = 3
    LAG = 1 if FC > 2 else 2
    RB = min(2, (U + 1) // 2)
    with ExitStack() as stack:
        sb, ps = bufs(nc, stack)
        names = ("up_mm act prod high low acc down_mm ones ones_r bias_in " +
                 " ".join(f"used{u}" for u in range(U)) + " " +
                 " ".join(f"w{r} wh{r} split{r}" for r in range(RB))).split()
        made = sems(nc, stack, " ".join(f"{name}_{k}" for k in names))
        s = {k[len(name) + 1:]: v for k, v in made.items()}
        w = [w0] + [sb(f"{name}_wb{r}", [P, WC]) for r in range(1, RB)]
        wh = [sb(f"{name}_whb{u}", [P, WC], F32R) for u in range(U)]
        wl = [sb(f"{name}_wlb{u}", [P, WC], F32R) for u in range(U)]
        HW = (LAG + 1) * 4 * TT if LAG == 1 else T
        hh = sb(f"{name}_hh", [P, FC, HW], F32R)
        hl = sb(f"{name}_hl", [P, FC, HW], F32R)
        sg = sb(f"{name}_sg", [P, NS, 4 * TT])
        pu = ps(f"{name}_pu", [P, 2, NU, BANK])
        po = ps(f"{name}_po", [P, 4, BANK])
        if biases:
            b1 = sb(f"{name}_b1", [P, E * FC])
            ones = sb(f"{name}_onesb", [1, TT])
            ones_r = sb(f"{name}_onesr", [1, TT], F32R)
        block = stack.enter_context(nc.Block())
        L = E // U - 1
        units = [(u, g) for u in range(U) for g in range(3)]
        LEAD = max(1, U // 2)

        def ahead(seq, i, j, n):
            r, k = divmod(j + n, len(seq))
            if r and isinstance(i, int) and i == L:
                return None
            return (i + r,) + seq[k]

        def raw(i, u):
            return u % RB, i * (U // RB) + u // RB

        def hid_at(u, g):
            return GROUPS[g][0] * TT if LAG == 2 else (u * 3 + g) % 2 * 4 * TT

        def slot(t, u, g):
            bank, half = divmod(t - GROUPS[g][0], 2)
            return po[0:TT, (u * 3 + g) % 2 * 2 + bank, half * D:(half + 1) * D]

        @block.sync
        def _(sp):
            if biases:
                sp.dma_start(b1[:, :], up_bias).then_inc(s["bias_in"], 16)

            def fetch(i, u):
                r, q = raw(i, u)
                sp.wait_ge(s[f"split{r}"], q + 1)
                sp.dma_start(w[r][:, :], w_dram[span(i * U + u, 1)].rearrange("a p w -> p (a w)")
                             ).then_inc(s[f"w{r}"], 16)

            for u in range(1, U):
                fetch(0, u)
            if L:
                with sp.Fori(1, L + 1) as i:
                    for u in range(U):
                        fetch(i, u)

        @block.gpsimd
        def _(pool):
            with pool.Fori(0, E // U) as i:
                for u in range(U):
                    r, q = raw(i, u)
                    pool.wait_ge(s[f"wh{r}"], q + 2)
                    nc.gpsimd.tensor_tensor(wl[u][:, :], w[r][:, :], wh[u][:, :].bitcast(F32), ALU.subtract
                                            ).then_inc(s[f"split{r}"], 1)

        @block.tensor
        def _(pe):
            def up(i, u, g):
                lo, hi = GROUPS[g]
                N = (hi - lo) * TT
                N += N % 2
                e = i * U + u
                if g == 0:
                    r, q = raw(i, u)
                    pe.wait_ge(s[f"split{r}"], q + 2)
                for f in range(FC):
                    n = g * FC + f
                    pe.wait_ge(s["prod"], e * UP + n + 1)
                    for m in range(NU):
                        dst = pu[:, (n + u * UP) % 2, m, 0:N]
                        for k in range(KC):
                            at = (m * KC + k) * I + f * P
                            w_hi, w_lo = wh[u][:, at:at + P], wl[u][:, at:at + P]
                            x_hi, x_lo = xh[:, k, lo * TT:lo * TT + N], xl[:, k, lo * TT:lo * TT + N]
                            nc.tensor.matmul(dst, w_lo, x_hi, start=(k == 0), stop=False)
                            nc.tensor.matmul(dst, w_hi, x_lo, start=False, stop=False)
                            last = nc.tensor.matmul(dst, w_hi, x_hi, start=False, stop=(k == KC - 1))
                    last.then_inc(s["up_mm"], 1)

            def down(i, u, g):
                lo, hi = GROUPS[g]
                e = i * U + u
                pe.wait_ge(s["low"], e * UP + (g + 1) * FC + 3)
                for t in range(lo, hi):
                    if (t - lo) % 2 == 0:
                        a, b = GROUPS[(g + 1) % 3]
                        pe.wait_ge(s["acc"], (e - (g < 2)) * NT + min(a + t - lo + 2, b) + 11)
                    o = slot(t, u, g)
                    if biases:
                        nc.tensor.matmul(o, ones_r[:, :], wh[u][0:1, BW:WC], start=True, stop=False)
                        nc.tensor.matmul(o, ones_r[:, :], wl[u][0:1, BW:WC], start=False, stop=False)
                    for f in range(FC):
                        at = UPW + f * D
                        w_hi, w_lo = wh[u][:, at:at + D], wl[u][:, at:at + D]
                        o_h = hid_at(u, g) + (t - lo) * TT
                        h_hi, h_lo = (x[:, f, o_h:o_h + TT] for x in (hh, hl))
                        nc.tensor.matmul(o, h_lo, w_hi, start=(f == 0 and not biases), stop=False)
                        nc.tensor.matmul(o, h_hi, w_lo, start=False, stop=False)
                        last = nc.tensor.matmul(o, h_hi, w_hi, start=False, stop=(f == FC - 1))
                    last.then_inc(s["down_mm"], 1)

            def turn(i):
                for j, (u, g) in enumerate(units):
                    nxt = ahead(units, i, j, 1)
                    if nxt is not None and LAG == 1:
                        up(*nxt)
                    down(i, u, g)
                    nxt = ahead(units, i, j, 2)
                    if nxt is not None and LAG == 2:
                        up(*nxt)

            if biases:
                pe.wait_ge(s["ones_r"], 2)
            up(0, 0, 0)
            if LAG == 2:
                up(0, 0, 1)
            if L:
                with pe.Fori(0, L) as i:
                    turn(i)
            turn(L)

        @block.scalar
        def _(act):
            def weights(i, u):
                r, q = raw(i, u)
                act.wait_ge(s[f"w{r}"], (q + (r > 0)) * 16 + 1)
                act.wait_ge(s[f"used{u}"], i + 1)
                nc.scalar.activation(wh[u][:, :], w[r][:, :], ACT.Copy).then_inc(s[f"wh{r}"], 1)

            def main(i, u, n):
                g, f = divmod(n, FC)
                lo, hi = GROUPS[g]
                N = (hi - lo) * TT
                e = i * U + u
                act.wait_ge(s["up_mm"], e * UP + n + 2)
                act.wait_ge(s["low"], e * UP + n + 1)
                src = pu[:, (n + u * UP) % 2, 0, 0:N]
                if gated:
                    nc.scalar.activation(sg[:, n % NS, 0:N], src, ACT.Silu).then_inc(s["act"], 1)
                else:
                    nc.scalar.activation(sg[:, n % NS, 0:N], src, ACT.Relu, bias=b1[:, span(e * FC + f, 1)]
                                         ).then_inc(s["prod"], 1)

            def high(i, u, n):
                g, f = divmod(n, FC)
                lo, hi = GROUPS[g]
                e = i * U + u
                act.wait_ge(s["prod"], e * UP + n + 3)
                at = hid_at(u, g)
                nc.scalar.activation(hh[:, f, at:at + (hi - lo) * TT], sg[:, n % NS, 0:(hi - lo) * TT], ACT.Copy
                                     ).then_inc(s["high"], 1)

            def unit(i, u, g):
                for n in range(g * FC, (g + 1) * FC):
                    main(i, u, n)
                    high(i, u, n)
                if g == (0 if U > 2 else 1):
                    nxt = ahead([(x,) for x in range(U)], i, u, LEAD)
                    if nxt is not None:
                        weights(*nxt)

            if biases:
                act.wait_ge(s["bias_in"], 17)
            for u in range(LEAD):
                weights(0, u)
            if L:
                with act.Fori(0, L) as i:
                    for u, g in units:
                        unit(i, u, g)
            for u, g in units:
                unit(L, u, g)

        @block.vector
        def _(dve):
            nc.vector.nop().then_inc(s["prod"], 1)
            nc.vector.nop().then_inc(s["low"], 2)
            nc.vector.nop().then_inc(s["acc"], 10)
            if biases:
                nc.vector.memset(ones[:, :], 1.0).then_inc(s["ones"], 1)
                dve.wait_ge(s["ones"], 2)
                nc.vector.tensor_copy(ones_r[:, :], ones[:, :]).then_inc(s["ones_r"], 1)

            def add(i, u, g):
                lo, hi = GROUPS[g]
                e = i * U + u
                dve.wait_ge(s["acc"], e * NT + hi)
                for t in range(lo, hi):
                    if (t - lo) % 2 == 0:
                        dve.wait_ge(s["down_mm"], e * NT + min(t + 2, hi) + 1)
                    nc.vector.scalar_tensor_tensor(h[:, t, :], slot(t, u, g), flat2(gates[:, t:t + 1, span(e, 1)]),
                                                   h[:, t, :], ALU.mult, ALU.add).then_inc(s["acc"], 1)
                if g == 2:
                    nc.vector.nop().then_inc(s[f"used{u}"], 1)

            def unit(i, u, g, before):
                lo, hi = GROUPS[g]
                N = (hi - lo) * TT
                for f in range(FC):
                    n = g * FC + f
                    m = (i * U + u) * UP + n
                    if gated:
                        dve.wait_ge(s["act"], m + 2)
                        nc.vector.tensor_tensor(sg[:, n % NS, 0:N], sg[:, n % NS, 0:N],
                                                pu[:, (n + u * UP) % 2, 1, 0:N], ALU.mult).then_inc(s["prod"], 1)
                    if f == 0 and before is not None and LAG == 2:
                        add(*before)
                    dve.wait_ge(s["high"], m + 2)
                    at = slice(hid_at(u, g), hid_at(u, g) + N)
                    nc.vector.tensor_tensor(hl[:, f, at], sg[:, n % NS, 0:N], hh[:, f, at].bitcast(F32), ALU.subtract
                                            ).then_inc(s["low"], 1)
                if before is not None and LAG == 1:
                    add(*before)

            def turn(i):
                for j, (u, g) in enumerate(units):
                    nxt = ahead(units, i, j, LAG)
                    if nxt is not None:
                        unit(*nxt, before=(i, u, g))
                    else:
                        add(i, u, g)

            unit(0, 0, 0, None)
            if LAG == 2:
                unit(0, 0, 1, None)
            if L:
                with dve.Fori(0, L) as i:
                    turn(i)
            turn(L)


def stage_ffn1(nc, d, h, xT, ident):
    E = 4
    with ExitStack() as stack:
        sb, ps = bufs(nc, stack)
        layer, loads = linear(sb, "ep", d["e_wu"], 1, d["e_bu"])
        w0, w_load = first_weights(sb, "e", d["e_w"])
        turn = sb("e_turn", [TT, E, E])
        norm_transpose(nc, "en", h, xT, ident, 1e-5, True,
                       loads=loads + [(turn[:, :, :], d["e_turn"])] + w_load)
        z = sb("e_z", [TT, NT, 1])
        gates = sb("e_gates", [TT, NT, E])
        projected(nc, "ep", xT, layer, z)
        with ExitStack() as inner:
            sb2, _ = bufs(nc, inner)
            s = sems(nc, inner, "e_u e_v")
            u = sb2("e_ub", [TT, NT, 1])
            w = sb2("e_w", [TT, NT, 1])
            t = sb2("e_t", [TT, NT, E])
            block = inner.enter_context(nc.Block())

            @block.scalar
            def _(act):
                nc.scalar.activation(u[:, :, :], z[:, :, :], ACT.Sigmoid).then_inc(s["e_u"], 1)

            @block.vector
            def _(dve):
                link = chain(dve, s["e_v"])
                dve.wait_ge(s["e_u"], 2)
                for r in range(E):
                    if r == 0:
                        link(nc.vector.tensor_copy(w[:, :, :], u[:, :, :]))
                    else:
                        link(nc.vector.tensor_scalar(w[:, :, :], u[:, :, :], float(E), float(r), ALU.mult, ALU.is_gt))
                        link(nc.vector.tensor_tensor(w[:, :, :], w[:, :, :], u[:, :, :], ALU.mult))
                        link(nc.vector.tensor_scalar(w[:, :, :], w[:, :, :], 1.0 / (r + 1), None, ALU.mult))
                    dst = gates if r == 0 else t
                    link(nc.vector.tensor_tensor(dst[:, :, :], w[:, :, :].broadcast_to([TT, NT, E]),
                                                 turn[:, r:r + 1, :].broadcast_to([TT, NT, E]), ALU.mult))
                    if r:
                        link(nc.vector.tensor_tensor(gates[:, :, :], gates[:, :, :], t[:, :, :], ALU.add))
        xh, xl = (sb(f"e_x{n}", [P, KC, T + 1], F32R) for n in "hl")
        split_x(nc, "ex", xT, xh, xl)
        experts(nc, "e", d["e_w"], w0, gates, xh, xl, h, E, 2, 8, False, d["e_b1"])


def layout_l1(i, o):
    o["g_w"] = cols(np.concatenate([i[f"L1_attn_W{n}"].T for n in (1, 2, 3)], 1), KC)
    o["g_bias"] = rep(np.concatenate([i[f"L1_attn_b{n}"] for n in (1, 2, 3)]))
    o["e_wu"] = cols(i["L1_ffn_Wu"], KC)
    o["e_bu"] = rep(i["L1_ffn_bu"])
    pos = np.tile(np.arange(S), G)[:, None, None]
    r, e = np.arange(4)[None, :, None], np.arange(4)[None, None, :]
    o["e_turn"] = ((pos + r) % 4 == e).astype(np.float32)
    b2 = np.zeros((4, P, D), np.float32)
    b2[:, 0] = i["L1_ffn_b2"]
    o["e_w"] = np.concatenate([up_cols(i["L1_ffn_W1"]), up_cols(i["L1_ffn_W2"]), b2], 2)
    o["e_b1"] = i["L1_ffn_b1"].reshape(4 * 8, P).T


def up_cols(w):
    e, k, n = w.shape
    return w.reshape(e, k // P, P, n).transpose(0, 2, 1, 3).reshape(e, P, -1)


def stage_scan(nc, d, h, xT, ident):
    DI, R, N, K = 512, 64, 16, 4
    C = DI // P
    SP = S + K - 1
    NB = (B + 1) // NCH
    W = C * CH
    with ExitStack() as stack:
        sb, ps = bufs(nc, stack)
        xc = sb("s_xc", [P, NCH, C, CH])
        res = sb("s_res", [P, NCH, C, CH])
        delta = sb("s_delta", [P, NCH, C, CH])
        a = sb("s_a", [P, N, C])
        dd = sb("s_d", [P, C])
        xdbl = sb("s_xdbl", [R + 2 * N, T])
        bc_dram = nc.dram_tensor("s_bc", (NCH, N, 2, CH), F32, kind="Internal").ap()
        with ExitStack() as inner:
            sb2, ps2 = bufs(nc, inner)
            w_in = sb2("s_w_in", [P, KC, 2 * DI])
            w_x = sb2("s_w_x", [P, C, R + 2 * N])
            w_dt = sb2("s_w_dt", [R, DI])
            cw = sb2("s_cw", [P, C, K])
            cb = sb2("s_cb", [P, C])
            b_dt = sb2("s_b_dt", [P, C])
            norm_transpose(nc, "sn", h, xT, ident, 1e-5, True, loads=[
                (w_in[:, :, :], d["s_w_in"]), (w_x[:, :, :], d["s_w_x"]), (w_dt[:, :], d["s_w_dt"]),
                (cw[:, :, :], d["s_cw"]), (cb[:, :], d["s_cb"]), (b_dt[:, :], d["s_b_dt"]),
                (a[:, :, :], d["s_a"]), (dd[:, :], d["s_d"])])
            s = sems(nc, inner, "s_edge s_u s_log s_px_mm s_x s_tap0 s_taps s_xc_done s_res_done s_dbl_mm s_dbl s_dt_mm "
                                "s_dt s_e s_ln s_v s_a_exp s_bc_out s_dve")
            xp = [sb2(f"s_xp{n}", [P, B + 1, SP]) for n in range(2)]
            acc = [sb2(f"s_acc{n}", [P, B + 1, S]) for n in range(2)]
            e = sb2("s_eb", [P, NCH, C, CH])
            ln = sb2("s_lnb", [P, NCH, C, CH])
            pp = ps2("s_pp", [P, 6, BANK])
            block = inner.enter_context(nc.Block())

            @block.sync
            def _(sp):
                sp.wait_ge(s["s_dbl"], NCH + 1)
                for t in range(NCH):
                    for m in range(2):
                        sp.dma_start(bc_dram[t, :, m, :], xdbl[R + m * N:R + (m + 1) * N, t * CH:(t + 1) * CH]
                                     ).then_inc(s["s_bc_out"], 16)
                sp.wait_ge(s["s_bc_out"], 6 * 16 + 1)

            @block.tensor
            def _(pe):
                for n in range(2 * C * NCH):
                    j, t = divmod(n, NCH)
                    if n >= 6:
                        m = n - 5
                        pe.wait_ge(s["s_x"], m + 1) if m <= C * NCH else pe.wait_ge(s["s_res_done"], m - C * NCH + 1)
                    for k in range(KC):
                        last = nc.tensor.matmul(pp[:, n % 6, 0:CH], w_in[:, k, j * P:(j + 1) * P],
                                                xT[:, k, t * CH:(t + 1) * CH], start=(k == 0), stop=(k == KC - 1))
                    last.then_inc(s["s_px_mm"], 1)
                pe.wait_ge(s["s_xc_done"], C + 1)
                pe.wait_ge(s["s_res_done"], C * NCH + 1)
                for t in range(NCH):
                    for c in range(C):
                        last = nc.tensor.matmul(pp[0:R + 2 * N, t, 0:CH], w_x[:, c, :], xc[:, t, c, :],
                                                start=(c == 0), stop=(c == C - 1))
                    last.then_inc(s["s_dbl_mm"], 1)
                for n in range(C * NCH):
                    t, c = divmod(n, C)
                    pe.wait_ge(s["s_dbl"], t + 2)
                    if n >= 3:
                        pe.wait_ge(s["s_dt"], n - 1)
                    nc.tensor.matmul(pp[:, 3 + n % 3, 0:CH], w_dt[:, c * P:(c + 1) * P], xdbl[0:R, t * CH:(t + 1) * CH],
                                     start=True, stop=True).then_inc(s["s_dt_mm"], 1)

            @block.scalar
            def _(act):
                nc.scalar.activation(a[:, :, :], a[:, :, :], ACT.Exp).then_inc(s["s_a_exp"], 1)

                def first_tap(c):
                    act.wait_ge(s["s_x"], 3 * c + 4)
                    if c >= 2:
                        act.wait_ge(s["s_xc_done"], c)
                    nc.scalar.activation(acc[c % 2][:, :, :], xp[c % 2][:, :, 0:S], ACT.Identity, scale=cw[:, c, 0:1],
                                         bias=cb[:, c:c + 1]).then_inc(s["s_tap0"], 1)

                first_tap(0)
                for c in range(C):
                    if c + 1 < C:
                        first_tap(c + 1)
                    act.wait_ge(s["s_taps"], c + 2)
                    nc.scalar.activation(xc[:, :, c, :], acc[c % 2][:, :, :].rearrange("p (t b) j -> p t (b j)", t=NCH),
                                         ACT.Silu).then_inc(s["s_xc_done"], 1)
                for n in range(C * NCH):
                    c, t = divmod(n, NCH)
                    act.wait_ge(s["s_px_mm"], C * NCH + n + 2)
                    nc.scalar.activation(res[:, t, c, :], pp[:, (C * NCH + n) % 6, 0:CH], ACT.Silu
                                         ).then_inc(s["s_res_done"], 1)
                for t in range(NCH):
                    act.wait_ge(s["s_dbl_mm"], t + 2)
                    nc.scalar.activation(xdbl[:, t * CH:(t + 1) * CH], pp[0:R + 2 * N, t, 0:CH], ACT.Copy
                                         ).then_inc(s["s_dbl"], 1)
                for t in range(NCH):
                    act.wait_ge(s["s_dt"], C * (t + 1) + 1)
                    nc.scalar.activation(e[:, t, :, :], delta[:, t, :, :], ACT.Abs).then_inc(s["s_e"], 1)
                for t in range(NCH):
                    act.wait_ge(s["s_e"], NCH + t + 1)
                    nc.scalar.activation(e[:, t, :, :], e[:, t, :, :], ACT.Exp, scale=-1.0).then_inc(s["s_e"], 1)
                    act.wait_ge(s["s_e"], NCH + t + 2)
                    nc.scalar.activation(ln[:, t, :, :], e[:, t, :, :], ACT.Ln, bias=1.0).then_inc(s["s_ln"], 1)

            @block.gpsimd
            def _(pool):
                for n in range(2):
                    nc.gpsimd.memset(xp[n][:, :, :], 0.0).then_inc(s["s_edge"], 1)
                for t in range(NCH):
                    pool.wait_ge(s["s_u"], t + 2)
                    lf, ef = (flat2(x[:, t, :, :]) for x in (ln, e))
                    nc.gpsimd.tensor_tensor(lf, lf, ef, ALU.subtract).then_inc(s["s_log"], 1)

            @block.vector
            def _(dve):
                link = chain(dve, s["s_v"])
                dve.wait_ge(s["s_edge"], 3)

                def widened(c):
                    if c >= 2:
                        dve.wait_ge(s["s_tap0"], c)
                        dve.wait_ge(s["s_taps"], c)
                    for t in range(NCH):
                        dve.wait_ge(s["s_px_mm"], 3 * c + t + 2)
                        nc.vector.tensor_copy(xp[c % 2][:, t * NB:(t + 1) * NB, K - 1:SP],
                                              pp[:, (3 * c + t) % 6, 0:CH].rearrange("p (b j) -> p b j", j=S)
                                              ).then_inc(s["s_x"], 1)

                def taps(c):
                    dve.wait_ge(s["s_x"], 3 * c + 4)
                    dve.wait_ge(s["s_tap0"], c + 2)
                    for k in range(1, K):
                        ins = nc.vector.scalar_tensor_tensor(acc[c % 2][:, :, :], xp[c % 2][:, :, k:k + S],
                                                             cw[:, c, k:k + 1], acc[c % 2][:, :, :], ALU.mult, ALU.add)
                        if k < K - 1:
                            link(ins)
                        else:
                            ins.then_inc(s["s_taps"], 1)

                widened(0)
                for c in range(C):
                    if c + 1 < C:
                        widened(c + 1)
                    taps(c)
                dve.wait_ge(s["s_a_exp"], 2)
                link(nc.vector.tensor_scalar(a[:, :, :], a[:, :, :], -1.0, None, ALU.mult))
                for n in range(C * NCH):
                    t, c = divmod(n, C)
                    dve.wait_ge(s["s_dt_mm"], n + 2)
                    nc.vector.tensor_scalar(delta[:, t, c, :], pp[:, 3 + n % 3, 0:CH], b_dt[:, c:c + 1], None, ALU.add
                                            ).then_inc(s["s_dt"], 1)
                tmp = flat2(acc[0][:, :, :])

                def corrected(t):
                    dve.wait_ge(s["s_ln"], t + 2)
                    for c in range(C):
                        one, ef = tmp[:, c % 3 * CH:(c % 3 + 1) * CH], e[:, t, c, :]
                        link(nc.vector.tensor_scalar(one, ef, 1.0, None, ALU.add))
                        last = nc.vector.scalar_tensor_tensor(ef, one, -1.0, ef, ALU.add, ALU.subtract)
                    last.then_inc(s["s_u"], 1)
                    dve.wait_ge(s["s_u"], t + 2)

                def softplus(t):
                    dve.wait_ge(s["s_log"], t + 2)
                    df, lf = flat2(delta[:, t, :, :]), flat2(ln[:, t, :, :])
                    link(nc.vector.scalar_tensor_tensor(df, df, 0.0, lf, ALU.max, ALU.add))

                for t in range(NCH):
                    corrected(t)
                    if t:
                        softplus(t - 1)
                softplus(NCH - 1)

        with ExitStack() as inner:
            sb2, ps2 = bufs(nc, inner)
            NBC = 4
            s = sems(nc, inner, "c_du c_exp c_start c_zero c_y_mm c_y c_ym c_w c_out_mm c_out " +
                     " ".join(f"c_da{u} c_dbu{u} c_scan{u} c_yt{u} c_sum{u}" for u in range(2)) +
                     "".join(f" c_bc{b}" for b in range(NBC)))
            v = s
            du = sb2("c_dub", [P, NCH, C, CH])
            bc = [sb2(f"c_bcb{b}", [P, 2, CH]) for b in range(NBC)]
            da = [sb2(f"c_dab{u}", [P, W]) for u in range(2)]
            dbu = [sb2(f"c_dbub{b}", [P, W]) for b in range(NBC)]
            st = [sb2(f"c_st{u}", [P, W]) for u in range(2)]
            zero = sb2("c_zerob", [P, CH], BF16)
            w_out = sb2("c_w_out", [P, C, D])
            ycol = sb2("c_ycol", [P, C, T])
            pc = ps2("c_pc", [P, C, BANK])
            po = ps2("c_po", [P, 2, BANK])
            block = inner.enter_context(nc.Block())
            done = [(t * CH) // TT for t in range(NCH + 1)]

            def slot(t, n):
                bank, half = divmod(n - done[t], 2)
                return po[0:TT, bank, half * D:(half + 1) * D]

            @block.sync
            def _(sp):
                sp.dma_start(w_out[:, :, :], d["s_w_out"]).then_inc(s["c_w"], 16)

                def load(t, i, b):
                    sp.dma_start(bc[b][:, :, :].rearrange("p m n -> p (m n)"),
                                 bc_dram[t, span(NBC * i + b, 1)].rearrange("a m n -> a (m n)")
                                 .broadcast_to([P, 2 * CH])).then_inc(s[f"c_bc{b}"], 16)

                for b in range(NBC):
                    load(0, 0, b)
                for t in range(NCH):
                    with sp.Fori(0 if t else 1, N // NBC) as i:
                        for b in range(NBC):
                            m = t * 8 + 2 * i + b // 2
                            sp.wait_ge(s[f"c_dbu{b % 2}"], m)
                            sp.wait_ge(s[f"c_yt{b % 2}"], m)
                            load(t, i, b)

            @block.scalar
            def _(act):
                act.wait_ge(s["c_zero"], 2)
                for t in range(NCH):
                    with act.Fori(0, N // 2) as i:
                        for u in range(2):
                            act.wait_ge(v[f"c_scan{u}"], t * 8 + i + 1)
                            for c in range(C):
                                last = nc.scalar.activation(da[u][:, c * CH:(c + 1) * CH], delta[:, t, c, :], ACT.Exp,
                                                            scale=flat2(a[:, bass.ds(2 * i + u, 1), c:c + 1]))
                            last.then_inc(s["c_exp"], 1)
                            act.wait_ge(s["c_exp"], t * 16 + 2 * i + u + 2)
                            nc.scalar.activation(da[u][:, :].rearrange("p (b j) -> p b j", j=S)[:, :, 0:1],
                                                 zero[:, 0:W // S].unsqueeze(2), ACT.Copy).then_inc(v[f"c_da{u}"], 1)

            @block.gpsimd
            def _(pool):
                pool.wait_ge(s["c_du"], 2)

                def inputs(t, i, b):
                    pool.wait_ge(s[f"c_bc{b}"], (t * (N // NBC) + i) * 16 + 17)
                    nc.gpsimd.tensor_tensor(dbu[b][:, :].rearrange("p (c n) -> p c n", c=C), du[:, t, :, :],
                                            bc[b][:, 0:1, :].broadcast_to([P, C, CH]), ALU.mult
                                            ).then_inc(s[f"c_dbu{b % 2}"], 1)

                for b in range(NBC):
                    inputs(0, 0, b)
                for t in range(NCH):
                    pool.wait_ge(s["c_du"], t + 2)
                    with pool.Fori(0 if t else 1, N // NBC) as i:
                        for b in range(NBC):
                            pool.wait_ge(s[f"c_scan{b % 2}"], t * 8 + 2 * i + b // 2)
                            inputs(t, i, b)

            @block.tensor
            def _(pe):
                def project(t):
                    pe.wait_ge(s["c_ym"], t + 2)
                    pe.wait_ge(s["c_out"], done[t] + 1)
                    for n in range(done[t], done[t + 1]):
                        for c in range(C):
                            last = nc.tensor.matmul(slot(t, n), ycol[:, c, n * TT:(n + 1) * TT], w_out[:, c, :],
                                                    start=(c == 0), stop=(c == C - 1))
                    last.then_inc(s["c_out_mm"], 1)

                pe.wait_ge(s["c_zero"], 2)
                pe.wait_ge(s["c_w"], 17)
                for t in range(NCH):
                    if t:
                        project(t - 1)
                    for c in range(C):
                        nc.tensor.matmul(pc[:, c, 0:CH], zero[:, 0:P], zero[:, :], start=True, stop=False,
                                         skip_group_check=True)
                    with pe.Fori(0, N // 2) as i:
                        for u in range(2):
                            pe.wait_ge(v[f"c_yt{u}"], t * 8 + i + 2)
                            for c in range(C):
                                last = nc.tensor.matmul(pc[:, c, 0:CH], ident[:, :], st[u][:, c * CH:(c + 1) * CH],
                                                        start=False, stop=False, skip_group_check=True)
                            last.then_inc(v[f"c_sum{u}"], 1)
                    for c in range(C):
                        last = nc.tensor.matmul(pc[:, c, 0:CH], zero[:, 0:P], zero[:, :], start=False, stop=True,
                                                skip_group_check=True)
                    last.then_inc(s["c_y_mm"], 1)
                project(NCH - 1)

            @block.vector
            def _(dve):
                def add(t):
                    dve.wait_ge(s["c_out_mm"], t + 2)
                    for n in range(done[t], done[t + 1]):
                        nc.vector.tensor_tensor(h[:, n, :], h[:, n, :], slot(t, n), ALU.add).then_inc(s["c_out"], 1)

                nc.vector.memset(zero[:, :], 0.0).then_inc(s["c_zero"], 1)
                for t in range(NCH):
                    nc.vector.tensor_tensor(du[:, t, :, :], delta[:, t, :, :], xc[:, t, :, :], ALU.mult
                                            ).then_inc(s["c_du"], 1)
                for t in range(NCH):
                    with dve.Fori(0, N // NBC) as i:
                        for b in range(NBC):
                            u = b % 2
                            m = t * 8 + 2 * i + b // 2
                            dve.wait_ge(v[f"c_da{u}"], m + 2)
                            dve.wait_ge(v[f"c_dbu{u}"], m + 2)
                            dve.wait_ge(v[f"c_sum{u}"], m + 1)
                            nc.vector.tensor_tensor_scan(st[u][:, :], da[u][:, :], dbu[b][:, :], 0.0, ALU.mult, ALU.add
                                                         ).then_inc(v[f"c_scan{u}"], 1)
                            dve.wait_ge(v[f"c_scan{u}"], m + 2)
                            dve.wait_ge(v[f"c_bc{b}"], (t * (N // NBC) + i) * 16 + 17)
                            nc.vector.tensor_tensor(st[u][:, :].rearrange("p (c n) -> p c n", c=C),
                                                    st[u][:, :].rearrange("p (c n) -> p c n", c=C),
                                                    bc[b][:, 1:2, :].broadcast_to([P, C, CH]), ALU.mult
                                                    ).then_inc(v[f"c_yt{u}"], 1)
                    if t:
                        add(t - 1)
                    dve.wait_ge(s["c_y_mm"], t + 2)
                    for c in range(C):
                        last = nc.vector.scalar_tensor_tensor(ycol[:, c, t * CH:(t + 1) * CH], xc[:, t, c, :],
                                                              dd[:, c:c + 1], pc[:, c, 0:CH], ALU.mult, ALU.add)
                    last.then_inc(s["c_y"], 1)
                    dve.wait_ge(s["c_y"], t + 2)
                    part = ycol[:, :, t * CH:(t + 1) * CH]
                    nc.vector.tensor_tensor(part, part, res[:, t, :, :], ALU.mult).then_inc(s["c_ym"], 1)
                add(NCH - 1)


def layout_scan(i, o):
    o["s_w_in"] = cols(i["L2_attn_W_in"], KC)
    o["s_w_x"] = cols(i["L2_attn_W_x"], 4)
    o["s_w_dt"] = i["L2_attn_W_dt"]
    o["s_cw"] = i["L2_attn_conv_w"].reshape(4, 4, P).transpose(2, 1, 0)
    o["s_cb"] = i["L2_attn_conv_b"].reshape(4, P).T
    o["s_b_dt"] = i["L2_attn_b_dt"].reshape(4, P).T
    o["s_a"] = i["L2_attn_A_log"].reshape(4, P, 16).transpose(1, 2, 0)
    o["s_d"] = i["L2_attn_D"].reshape(4, P).T
    o["s_w_out"] = cols(i["L2_attn_W_out"], 4)


def router(sb, name, w_dram, bias_dram, iota_dram, E):
    layer, loads = linear(sb, name, w_dram, E, bias_dram)
    iota = sb(f"{name}_iota", [TT, E])
    return layer, iota, loads + [(iota[:, :], iota_dram)]


def top2_gates(nc, name, logits, gates, iota, ident, E, capacity=None):
    with ExitStack() as stack:
        sb, ps = bufs(nc, stack)
        made = sems(nc, stack, " ".join(f"{name}_{k}" for k in "v max exp hot turned cum back m8 idx".split()))
        s = {k[len(name) + 1:]: x for k, x in made.items()}
        mx = sb(f"{name}_mx", [TT, NT])
        p = sb(f"{name}_p", [TT, NT, E])
        m8 = sb(f"{name}_m8b", [TT, NT, 8])
        idx = sb(f"{name}_idxb", [TT, NT, 8], U32)
        pick = sb(f"{name}_pick", [TT, NT, 2])
        hot = sb(f"{name}_hotb", [TT, NT, 2, E])
        hotT = sb(f"{name}_hotT", [2 * E, T])
        cum = sb(f"{name}_cumb", [2 * E, T])
        one = sb(f"{name}_one", [2 * E, T])
        pt = ps(f"{name}_pt", [P, NCH, BANK])
        pb = ps(f"{name}_pb", [P, BANK])
        block = stack.enter_context(nc.Block())

        @block.scalar
        def _(act):
            act.wait_ge(s["max"], 2)
            nc.scalar.activation(p[:, :, :], p[:, :, :], ACT.Exp).then_inc(s["exp"], 1)

        @block.tensor
        def _(pe):
            if capacity is not None:
                pe.wait_ge(s["hot"], 2)
                for g, (a, b) in enumerate(GROUPS):
                    for t in range(a, b):
                        last = nc.tensor.transpose(pt[0:2 * E, g, (t - a) * TT:(t - a + 1) * TT],
                                                   hot[:, t, :, :].rearrange("p k e -> p (k e)"), ident[0:TT, 0:TT])
                last.then_inc(s["turned"], 1)
                pe.wait_ge(s["cum"], 2)
                for t in range(NT):
                    last = nc.tensor.transpose(pb[0:TT, t * 2 * E:(t + 1) * 2 * E], cum[:, t * TT:(t + 1) * TT],
                                               ident[0:2 * E, 0:2 * E])
                last.then_inc(s["back"], 1)

        @block.vector
        def _(dve):
            link = chain(dve, s["v"])
            wide = [TT, NT, E]
            link(nc.vector.tensor_reduce(mx[:, :], logits[:, :, :], X, ALU.max))
            nc.vector.tensor_tensor(p[:, :, :], logits[:, :, :], mx[:, :].unsqueeze(2).broadcast_to(wide),
                                    ALU.subtract).then_inc(s["max"], 1)
            dve.wait_ge(s["exp"], 2)
            link(nc.vector.tensor_reduce(mx[:, :], p[:, :, :], X, ALU.add))
            link(nc.vector.reciprocal(mx[:, :], mx[:, :]))
            link(nc.vector.tensor_tensor(p[:, :, :], p[:, :, :], mx[:, :].unsqueeze(2).broadcast_to(wide), ALU.mult))
            for t in range(NT):
                last = nc.vector.max(m8[:, t, :], p[:, t, :])
            last.then_inc(s["m8"], 1)
            dve.wait_ge(s["m8"], 2)
            for t in range(NT):
                last = nc.vector.max_index(idx[:, t, :], m8[:, t, :], p[:, t, :])
            last.then_inc(s["idx"], 1)
            dve.wait_ge(s["idx"], 2)
            link(nc.vector.tensor_copy(pick[:, :, :], idx[:, :, 0:2]))
            for k in range(2):
                last = nc.vector.tensor_tensor(hot[:, :, k, :], pick[:, :, k:k + 1].broadcast_to(wide),
                                               iota[:, :].unsqueeze(1).broadcast_to(wide), ALU.is_equal)
            if capacity is None:
                link(last)
                link(nc.vector.tensor_tensor(mx[:, :].unsqueeze(2), m8[:, :, 0:1], m8[:, :, 1:2], ALU.add))
                link(nc.vector.reciprocal(mx[:, :], mx[:, :]))
                link(nc.vector.tensor_tensor(pick[:, :, :], m8[:, :, 0:2],
                                             mx[:, :].unsqueeze(2).broadcast_to([TT, NT, 2]), ALU.mult))
                w = pick
            else:
                last.then_inc(s["hot"], 1)
                link(nc.vector.memset(one[:, :], 1.0))
                dve.wait_ge(s["turned"], 2)
                for g, (a, b) in enumerate(GROUPS):
                    last = nc.vector.tensor_copy(hotT[:, a * TT:b * TT], pt[0:2 * E, g, 0:(b - a) * TT])
                link(last)
                link(nc.vector.tensor_tensor_scan(cum[:, :], one[:, :], hotT[:, :], 0.0, ALU.mult, ALU.add))
                nc.vector.scalar_tensor_tensor(cum[:, :], cum[:, :], float(capacity), hotT[:, :], ALU.is_le, ALU.mult
                                               ).then_inc(s["cum"], 1)
                dve.wait_ge(s["back"], 2)
                link(nc.vector.tensor_copy(hot[:, :, :, :].rearrange("p t k e -> p (t k e)"), pb[0:TT, 0:NT * 2 * E]))
                w = m8
            for k in range(2):
                last = nc.vector.tensor_tensor(hot[:, :, k, :], hot[:, :, k, :],
                                               w[:, :, k:k + 1].broadcast_to(wide), ALU.mult)
            link(last)
            link(nc.vector.tensor_tensor(gates[:, :, 0:E], hot[:, :, 0, :], hot[:, :, 1, :], ALU.add))
            if gates.shape[2] > E:
                link(nc.vector.memset(gates[:, :, E:], 1.0))


def stage_moe2(nc, d, h, xT, ident):
    E = 16
    capacity = max(1, math.ceil(B * S * 2 / E * 1.25))
    with ExitStack() as stack:
        sb, _ = bufs(nc, stack)
        w0, w_load = first_weights(sb, "m", d["m_w"])
        layer, iota, loads = router(sb, "mp", d["m_router"], d["m_zero"], d["m_iota"], E)
        norm_transpose(nc, "mn", h, xT, ident, 1e-5, True, loads=loads + w_load)
        logits = sb("m_logits", [TT, NT, E])
        gates = sb("m_gates", [TT, NT, E])
        projected(nc, "mp", xT, layer, logits)
        top2_gates(nc, "mt", logits, gates, iota, ident, E, capacity)
        xh, xl = (sb(f"m_x{n}", [P, KC, T + 1], F32R) for n in "hl")
        split_x(nc, "mx", xT, xh, xl)
        experts(nc, "m", d["m_w"], w0, gates, xh, xl, h, E, 4, 2, True)


def layout_moe2(i, o):
    o["m_router"] = cols(i["L2_ffn_router_w"], KC)
    o["m_zero"] = rep(np.zeros(16, np.float32))
    o["m_iota"] = rep(np.arange(16, dtype=np.float32))
    o["m_w"] = np.concatenate([up_cols(i[f"L2_ffn_{n}_w"]) for n in ("gate", "up", "down")], 2)


def stage_delta(nc, d, h, xT, ident):
    HK, HV, DK, K = 4, 8, 128, 4
    CV = 2 * HK + HV
    NB = (B + 1) // NCH
    SP = S + K - 1
    W2 = HK * TT
    with ExitStack() as stack:
        sb, ps = bufs(nc, stack)
        layer, loads = linear(sb, "dp", d["d_w_ba"], 2 * HV, d["d_b_ba"])
        norm_transpose(nc, "dn", h, xT, ident, 1e-6, False, w_dram=d["d_ln1"], w_plus=1.0, loads=loads)
        ba = sb("d_ba", [TT, NT, 2 * HV])
        projected(nc, "dp", xT, layer, ba)
        mix = sb("d_mix", [P, CV, T])
        beta = sb("d_beta", [TT, NT, HV])
        g = sb("d_g", [TT, NT, HV])
        pT = sb("d_pT", [TT, NT, HV, TT])
        a_dram = nc.dram_tensor("d_a", (B + 1, HV, S, S), F32, kind="Internal").ap()
        t_dram = nc.dram_tensor("d_t", (B + 1, HV, S, S), F32, kind="Internal").ap()

        with ExitStack() as inner:
            sb2, ps2 = bufs(nc, inner)
            s = sems(nc, inner, "dc_in dc_edge dc_v dc_v2 dc_beta dc_e dc_ln dc_al "
                                + " ".join(f"dc_w{u} dc_mm{u} dc_x{u} dc_tap{u} dc_taps{u} dc_done{u}" for u in range(2)))
            v = s
            w = [sb2(f"dc_wb{u}", [P, KC * P]) for u in range(2)]
            cw = sb2("dc_cw", [P, CV, K])
            xp = [sb2(f"dc_xp{u}", [P, B + 1, SP]) for u in range(2)]
            acc = [sb2(f"dc_acc{u}", [P, B + 1, S]) for u in range(2)]
            al = sb2("dc_alb", [TT, HV])
            e = sb2("dc_eb", [TT, NT, HV])
            ln = sb2("dc_lnb", [TT, NT, HV])
            uu = sb2("dc_u", [TT, NT, HV])
            pp = [ps2(f"dc_pp{u}", [P, NCH, BANK]) for u in range(2)]
            block = inner.enter_context(nc.Block())

            @block.sync
            def _(sp):
                sp.dma_start(al[:, :], d["d_a_log"]).then_inc(s["dc_in"], 16)
                sp.dma_start(cw[:, :, :], d["d_cw"]).then_inc(s["dc_in"], 16)
                with sp.Fori(0, CV // 2) as i:
                    for u in range(2):
                        sp.wait_ge(v[f"dc_mm{u}"], i + 1)
                        sp.dma_start(w[u][:, :], d["d_w_qkv"][bass.ds(2 * i + u, 1)].rearrange("a p n -> p (a n)")
                                     ).then_inc(v[f"dc_w{u}"], 16)

            @block.tensor
            def _(pe):
                with pe.Fori(0, CV // 2) as i:
                    for u in range(2):
                        pe.wait_ge(v[f"dc_w{u}"], i * 16 + 17)
                        pe.wait_ge(v[f"dc_x{u}"], i + 1)
                        for t in range(NCH):
                            for k in range(KC):
                                last = nc.tensor.matmul(pp[u][:, t, 0:CH], w[u][:, k * P:(k + 1) * P],
                                                        xT[:, k, t * CH:(t + 1) * CH], start=(k == 0),
                                                        stop=(k == KC - 1))
                        last.then_inc(v[f"dc_mm{u}"], 1)

            @block.scalar
            def _(act):
                act.wait_ge(s["dc_in"], 33)
                nc.scalar.activation(al[:, :], al[:, :], ACT.Exp).then_inc(s["dc_al"], 1)
                nc.scalar.activation(e[:, :, :], ba[:, :, HV:], ACT.Abs).then_inc(s["dc_e"], 1)
                act.wait_ge(s["dc_e"], 2)
                nc.scalar.activation(e[:, :, :], e[:, :, :], ACT.Exp, scale=-1.0).then_inc(s["dc_e"], 1)
                act.wait_ge(s["dc_e"], 3)
                nc.scalar.activation(ln[:, :, :], e[:, :, :], ACT.Ln, bias=1.0).then_inc(s["dc_ln"], 1)
                nc.scalar.activation(beta[:, :, :], ba[:, :, 0:HV], ACT.Sigmoid).then_inc(s["dc_beta"], 1)
                act.wait_ge(s["dc_edge"], 3)

                def first_tap(i, u):
                    act.wait_ge(v[f"dc_mm{u}"], i + 2)
                    act.wait_ge(v[f"dc_taps{u}"], i + 1)
                    nc.scalar.activation(xp[u][:, :, K - 1:SP].rearrange("p (t b) j -> p t b j", t=NCH),
                                         pp[u][:, :, 0:CH].rearrange("p t (b j) -> p t b j", j=S), ACT.Copy
                                         ).then_inc(v[f"dc_x{u}"], 1)
                    act.wait_ge(v[f"dc_x{u}"], i + 2)
                    act.wait_ge(v[f"dc_done{u}"], i + 1)
                    nc.scalar.activation(acc[u][:, :, :], xp[u][:, :, 0:S], ACT.Copy,
                                         scale=flat2(cw[:, span(2 * i + u, 1), 0:1])).then_inc(v[f"dc_tap{u}"], 1)

                def silu(i, u):
                    act.wait_ge(v[f"dc_taps{u}"], i + 2)
                    nc.scalar.activation(flat2(mix[:, span(2 * i + u, 1), :]), flat2(acc[u][:, :, :]), ACT.Silu
                                         ).then_inc(v[f"dc_done{u}"], 1)

                first_tap(0, 0)
                first_tap(0, 1)
                silu(0, 0)
                with act.Fori(1, CV // 2) as i:
                    first_tap(i, 0)
                    silu(i - 1, 1)
                    first_tap(i, 1)
                    silu(i, 0)
                silu(CV // 2 - 1, 1)

            @block.gpsimd
            def _(pool):
                for u in range(2):
                    nc.gpsimd.memset(xp[u][:, :, :], 0.0).then_inc(s["dc_edge"], 1)

            @block.vector
            def _(dve):
                link = chain(dve, s["dc_v"])
                dve.wait_ge(s["dc_ln"], 2)
                dve.wait_ge(s["dc_in"], 33)
                dve.wait_ge(s["dc_al"], 2)
                link(nc.vector.tensor_scalar(uu[:, :, :], e[:, :, :], 1.0, None, ALU.add))
                link(nc.vector.scalar_tensor_tensor(uu[:, :, :], uu[:, :, :], -1.0, e[:, :, :], ALU.add, ALU.subtract))
                link(nc.vector.tensor_tensor(ln[:, :, :], ln[:, :, :], uu[:, :, :], ALU.subtract))
                link(nc.vector.scalar_tensor_tensor(ln[:, :, :], ba[:, :, HV:], 0.0, ln[:, :, :], ALU.max, ALU.add))
                link(nc.vector.tensor_tensor(g[:, :, :], ln[:, :, :],
                                             al[:, :].unsqueeze(1).broadcast_to([TT, NT, HV]), ALU.mult))
                link(nc.vector.tensor_scalar(g[:, :, :], g[:, :, :], -1.0, None, ALU.mult))
                with dve.Fori(0, CV // 2) as i:
                    link2 = chain(dve, s["dc_v2"], 4 * i)
                    for u in range(2):
                        dve.wait_ge(v[f"dc_tap{u}"], i + 2)
                        for k in range(1, K):
                            ins = nc.vector.scalar_tensor_tensor(acc[u][:, :, :], xp[u][:, :, k:k + S],
                                                                 flat2(cw[:, span(2 * i + u, 1), k:k + 1]), acc[u][:, :, :], ALU.mult, ALU.add)
                            link2(ins) if k < K - 1 else ins.then_inc(v[f"dc_taps{u}"], 1)

        with ExitStack() as inner:
            sb2, ps2 = bufs(nc, inner)
            s = sems(nc, inner, "dl_in dl_sq dl_sum dl_ss dl_root dl_r dl_bc_mm dl_bc dl_v")
            sel = sb2("dl_sel", [P, 8, 8])
            spread = sb2("dl_spread", [8, 8, P])
            sq = sb2("dl_sqb", [P, 8, T])
            ss = sb2("dl_ssb", [8, T])
            root = sb2("dl_rootb", [8, T])
            r = sb2("dl_rb", [8, T])
            pp = ps2("dl_pp", [P, 3, BANK])
            pb = ps2("dl_pb", [P, 4, BANK])
            block = inner.enter_context(nc.Block())

            @block.sync
            def _(sp):
                sp.dma_start(sel[:, :, :], d["d_sel"]).then_inc(s["dl_in"], 16)
                sp.dma_start(spread[:, :, :], d["d_spread"]).then_inc(s["dl_in"], 16)

            @block.scalar
            def _(act):
                for c in range(8):
                    nc.scalar.activation(sq[:, c, :], mix[:, c, :], ACT.Square).then_inc(s["dl_sq"], 1)
                for t in range(NCH):
                    at = slice(t * CH, (t + 1) * CH)
                    act.wait_ge(s["dl_ss"], t + 2)
                    nc.scalar.activation(root[:, at], ss[:, at], ACT.Sqrt).then_inc(s["dl_root"], 1)

            @block.tensor
            def _(pe):
                pe.wait_ge(s["dl_in"], 33)
                for c in range(8):
                    pe.wait_ge(s["dl_sq"], c + 2)
                    for t in range(NCH):
                        last = nc.tensor.matmul(pp[0:8, t, 0:CH], sel[:, c, :], sq[:, c, t * CH:(t + 1) * CH],
                                                start=(c == 0), stop=(c == 7))
                last.then_inc(s["dl_sum"], 1)
                for n in range(8 * NCH):
                    t, c = divmod(n, 8)
                    if c == 0:
                        pe.wait_ge(s["dl_r"], t + 2)
                    if n >= 4:
                        pe.wait_ge(s["dl_bc"], n - 2)
                    nc.tensor.matmul(pb[:, n % 4, 0:CH], spread[:, c, :], r[:, t * CH:(t + 1) * CH], start=True,
                                     stop=True).then_inc(s["dl_bc_mm"], 1)

            @block.vector
            def _(dve):
                link = chain(dve, s["dl_v"])
                dve.wait_ge(s["dl_sum"], 2)
                for t in range(NCH):
                    nc.vector.tensor_scalar(ss[:, t * CH:(t + 1) * CH], pp[0:8, t, 0:CH], 1e-6, None, ALU.add
                                            ).then_inc(s["dl_ss"], 1)

                def inverse_root(t):
                    at = slice(t * CH, (t + 1) * CH)
                    dve.wait_ge(s["dl_root"], t + 2)
                    link(nc.vector.reciprocal(r[:, at], root[:, at]))
                    link(nc.vector.tensor_tensor(root[:, at], ss[:, at], r[:, at], ALU.mult))
                    link(nc.vector.tensor_tensor(root[:, at], root[:, at], r[:, at], ALU.mult))
                    link(nc.vector.tensor_scalar(root[:, at], root[:, at], -0.5, 1.5, ALU.mult, ALU.add))
                    nc.vector.tensor_tensor(r[:, at], r[:, at], root[:, at], ALU.mult).then_inc(s["dl_r"], 1)

                def scale(t):
                    for c in range(8):
                        n = 8 * t + c
                        dve.wait_ge(s["dl_bc_mm"], n + 2)
                        at = mix[:, c, t * CH:(t + 1) * CH]
                        nc.vector.tensor_tensor(at, at, pb[:, n % 4, 0:CH], ALU.mult).then_inc(s["dl_bc"], 1)

                inverse_root(0)
                for t in range(NCH):
                    if t + 1 < NCH:
                        inverse_root(t + 1)
                    scale(t)

        with ExitStack() as inner:
            sb2, ps2 = bufs(nc, inner)
            s = sems(nc, inner, "da_in da_gm da_ks da_dec_mm da_kk_mm da_exp da_kept da_v da_out da_p")
            m = sb2("da_masks", [TT, 3, TT])
            gm = sb2("da_gmb", [TT, 2, HV, TT])
            ks = sb2("da_ksb", [P, HK, TT])
            ex = sb2("da_ex", [TT, 2, HV, TT])
            am = sb2("da_am", [TT, HV, TT])
            pd = ps2("da_pd", [P, 4, BANK])
            pk = ps2("da_pk", [P, 2, BANK])
            block = inner.enter_context(nc.Block())
            wide = [TT, HV, TT]

            @block.sync
            def _(sp):
                sp.dma_start(m[:, :, :], d["d_masks"]).then_inc(s["da_in"], 16)
                with sp.Fori(0, NT) as i:
                    sp.wait_ge(s["da_kept"], i + 2)
                    for q in range(G):
                        at = slice(q * S, (q + 1) * S)
                        sp.dma_start(a_dram[bass.ds(i * G + q, 1)].rearrange("b h i j -> i (b h) j"), am[at, :, at]
                                     ).then_inc(s["da_out"], 16)
                sp.wait_ge(s["da_out"], NT * G * 16 + 1)

            @block.gpsimd
            def _(pool):
                pool.wait_ge(s["da_in"], 17)

                def masked_gates(i):
                    pool.wait_ge(s["da_dec_mm"], i + 1)
                    gt = flat2(g[:, span(i, 1), :]).unsqueeze(2).broadcast_to(wide)
                    for n in range(2):
                        last = nc.gpsimd.tensor_tensor(gm[:, n, :, :], gt, m[:, n:n + 1, :].broadcast_to(wide),
                                                       ALU.mult)
                    last.then_inc(s["da_gm"], 1)

                masked_gates(0)
                with pool.Fori(1, NT) as i:
                    masked_gates(i)

            @block.tensor
            def _(pe):
                pe.wait_ge(s["da_in"], 17)
                with pe.Fori(0, NT) as i:
                    pe.wait_ge(s["da_gm"], i + 2)
                    pe.wait_ge(s["da_exp"], 2 * i + 1)
                    for n in range(2):
                        for o in range(2):
                            last = nc.tensor.matmul(pd[0:TT, 2 * n + o, 0:W2], m[:, 1 - n, :],
                                                    flat2(gm[:, n, o * HK:(o + 1) * HK, :]), start=True, stop=True)
                    last.then_inc(s["da_dec_mm"], 1)
                    pe.wait_ge(s["da_ks"], i + 2)
                    pe.wait_ge(s["da_p"], i + 1)
                    for n in range(2):
                        for c in range(HK):
                            src = mix[:, n * HK + c, bass.ds(i * TT, TT)]
                            last = nc.tensor.matmul(pk[0:TT, n, c * TT:(c + 1) * TT], ks[:, c, :], src, start=True,
                                                    stop=True)
                    last.then_inc(s["da_kk_mm"], 1)

            @block.scalar
            def _(act):
                with act.Fori(0, NT) as i:
                    act.wait_ge(s["da_kk_mm"], i + 1)
                    nc.scalar.activation(ks[:, :, :], mix[:, HK:2 * HK, bass.ds(i * TT, TT)], ACT.Copy
                                         ).then_inc(s["da_ks"], 1)
                    act.wait_ge(s["da_dec_mm"], i + 2)
                    for n in (1, 0):
                        act.wait_ge(s["da_p" if n == 0 else "da_kept"], i + 1)
                        nc.scalar.activation(ex[:, n, :, :].rearrange("p (o h) x -> p o (h x)", o=2),
                                             pd[0:TT, 2 * n:2 * n + 2, 0:W2], ACT.Exp).then_inc(s["da_exp"], 1)

            @block.vector
            def _(dve):
                dve.wait_ge(s["da_in"], 17)
                V = 4
                with dve.Fori(0, NT) as i:
                    link = chain(dve, s["da_v"], V * i)
                    rep2 = [TT, HK, 2, TT]
                    kk = [pk[0:TT, n, 0:W2].rearrange("p (c x) -> p c x", x=TT).unsqueeze(2).broadcast_to(rep2)
                          for n in range(2)]
                    dve.wait_ge(s["da_exp"], 2 * i + 2)
                    link(nc.vector.tensor_tensor(ex[:, 1, :, :], ex[:, 1, :, :], m[:, 1:2, :].broadcast_to(wide),
                                                 ALU.mult))
                    dve.wait_ge(s["da_kk_mm"], i + 2)
                    one = ex[:, 1, :, :].rearrange("p (c r) x -> p c r x", r=2)
                    link(nc.vector.tensor_tensor(one, one, kk[1], ALU.mult))
                    dve.wait_ge(s["da_out"], i * G * 16 + 1)
                    nc.vector.tensor_tensor(am[:, :, :], ex[:, 1, :, :],
                                            flat2(beta[:, bass.ds(i, 1), :]).unsqueeze(2).broadcast_to(wide), ALU.mult
                                            ).then_inc(s["da_kept"], 1)
                    dve.wait_ge(s["da_exp"], 2 * i + 3)
                    link(nc.vector.tensor_tensor(ex[:, 0, :, :], ex[:, 0, :, :], m[:, 0:1, :].broadcast_to(wide),
                                                 ALU.mult))
                    link(nc.vector.tensor_tensor(pT[:, bass.ds(i, 1), :, :].rearrange("p a (c r) x -> p (a c) r x", r=2),
                                                 ex[:, 0, :, :].rearrange("p (c r) x -> p c r x", r=2), kk[0],
                                                 ALU.mult))
                    nc.vector.nop().then_inc(s["da_p"], 1)
                assert link.count() == V

        with ExitStack() as inner:
            sb2, ps2 = bufs(nc, inner)
            s = sems(nc, inner, "di_in di_zero di_v di_out")
            NG = B * HV // P
            a = sb2("di_a", [P, NG, S, S])
            tT = sb2("di_tT", [P, NG, S, S])
            pr = sb2("di_pr", [P, NG * S * S])
            block = inner.enter_context(nc.Block())
            split = [x[0:B].rearrange("b h i j -> (b h) (i j)").rearrange("(g p) n -> p g n", g=NG)
                     for x in (a_dram, t_dram)]

            @block.sync
            def _(sp):
                sp.dma_start(a[:, :, :, :].rearrange("p g i j -> p g (i j)"), split[0]).then_inc(s["di_in"], 16)
                sp.wait_ge(s["di_v"], 2 * S)
                sp.dma_start(split[1], tT[:, :, :, :].rearrange("p g i j -> p g (i j)")).then_inc(s["di_out"], 16)
                sp.dma_start(t_dram[B:B + 1].rearrange("b h i j -> (b h) (i j)"),
                             tT[0:HV, 0, :, :].rearrange("p i j -> p (i j)")).then_inc(s["di_out"], 16)
                sp.wait_ge(s["di_out"], 33)

            @block.gpsimd
            def _(pool):
                nc.gpsimd.memset(tT[:, :, :, :], 0.0).then_inc(s["di_zero"], 1)

            @block.vector
            def _(dve):
                link = chain(dve, s["di_v"])
                dve.wait_ge(s["di_zero"], 2)
                link(nc.vector.memset(tT[:, :, :, :].rearrange("p g i j -> p g (i j)")[:, :, 0:S * S:S + 1], 1.0))
                dve.wait_ge(s["di_in"], 17)
                for i in range(1, S):
                    half = i // 2 if i >= 16 else 0
                    blocks = [(0, half or i, 0), (half, i, half)][:2 if half else 1]
                    at, ones = 0, []
                    for lo, hi, j in blocks:
                        n = NG * (hi - lo) * (i - j)
                        one = pr[:, at:at + n].rearrange("p (g c j) -> p g c j", g=NG, c=hi - lo)
                        at += n
                        ones.append(one)
                        last = nc.vector.tensor_tensor(one, tT[:, :, lo:hi, j:i],
                                                       a[:, :, i:i + 1, j:i].broadcast_to([P, NG, hi - lo, i - j]),
                                                       ALU.mult)
                    link(last)
                    for (lo, hi, j), one in zip(blocks, ones):
                        last = nc.vector.tensor_reduce(tT[:, :, lo:hi, i:i + 1].rearrange("p g c a -> p g (c a)"), one,
                                                       X, ALU.add, negate=True)
                    link(last)


        with ExitStack() as inner:
            sb2, ps2 = bufs(nc, inner)
            s = sems(nc, inner, "do_in do_zero do_t do_vs do_ps do_xs do_v_mm do_vb do_u_mm do_u do_o_mm do_z_mm "
                                "do_sq do_ms do_r do_z do_g do_core do_c_mm do_c do_out_mm do_h do_v do_half")
            wz = sb2("do_wz", [P, KC, HV * DK])
            wo = sb2("do_wo", [P, HV, D])
            gw = sb2("do_gw", [TT, DK])
            tm = sb2("do_tm", [TT, HV, TT])
            vs = sb2("do_vsb", [P, HV, TT])
            pm = sb2("do_pm", [TT, HV, TT])
            xs = sb2("do_xsb", [P, KC, TT])
            vb = sb2("do_vbb", [TT, HV, DK])
            ub = sb2("do_ub", [TT, HV, DK])
            sq = sb2("do_sqb", [TT, HV, DK])
            ms = sb2("do_msb", [TT, HV])
            half = sb2("do_halfb", [TT, HV])
            zs = sb2("do_zs", [TT, HV, DK])
            core = sb2("do_coreb", [TT, HV, DK])
            cT = sb2("do_cT", [P, HV, TT])
            pv, pu, po, pz = (ps2(f"do_p{n}", [P, 2, BANK]) for n in "vuoz")
            block = inner.enter_context(nc.Block())
            wide = [TT, HV, DK]

            def heads(p):
                return p[0:TT, :, :].rearrange("p o (h x) -> p (o h) x", x=DK)

            @block.sync
            def _(sp):
                sp.dma_start(wz[:, :, :], d["d_w_z"]).then_inc(s["do_in"], 16)
                sp.dma_start(wo[:, :, :], d["d_w_out"]).then_inc(s["do_in"], 16)
                sp.dma_start(gw[:, :], d["d_gw"]).then_inc(s["do_in"], 16)
                sp.wait_ge(s["do_zero"], 2)
                with sp.Fori(0, NT) as i:
                    sp.wait_ge(s["do_u_mm"], i + 1)
                    for q in range(G):
                        at = slice(q * S, (q + 1) * S)
                        sp.dma_start(tm[at, :, at], t_dram[bass.ds(i * G + q, 1)].rearrange("b h i j -> i (b h) j")
                                     ).then_inc(s["do_t"], 16)

            @block.gpsimd
            def _(pool):
                nc.gpsimd.memset(tm[:, :, :], 0.0).then_inc(s["do_zero"], 1)
                pool.wait_ge(s["do_half"], 2)

                def stage_v(i):
                    pool.wait_ge(s["do_v_mm"], i + 1)
                    nc.gpsimd.tensor_copy(vs[:, :, :], mix[:, 2 * HK:CV, span(i, TT)]).then_inc(s["do_vs"], 1)

                def stage_x(i):
                    pool.wait_ge(s["do_z_mm"], i + 1)
                    nc.gpsimd.tensor_copy(xs[:, :, :], xT[:, :, span(i, TT)]).then_inc(s["do_xs"], 1)

                def stage_p(i):
                    pool.wait_ge(s["do_o_mm"], i + 1)
                    nc.gpsimd.tensor_copy(pm[:, :, :], pT[:, span(i, 1), :, :].rearrange("p a h x -> p (a h) x")
                                          ).then_inc(s["do_ps"], 1)

                def power(i):
                    pool.wait_ge(s["do_ms"], i + 2)
                    nc.gpsimd.tensor_tensor(ms[:, :], ms[:, :], half[:, :], ALU.pow).then_inc(s["do_r"], 1)

                stage_v(0)
                stage_x(0)
                stage_p(0)
                with pool.Fori(1, NT) as i:
                    stage_v(i)
                    stage_x(i)
                    power(i - 1)
                    stage_p(i)
                power(NT - 1)

            @block.tensor
            def _(pe):
                pe.wait_ge(s["do_in"], 49)

                def turn_v(i):
                    pe.wait_ge(s["do_vs"], i + 2)
                    for c in range(HV):
                        last = nc.tensor.transpose(pv[0:TT, c // 4, (c % 4) * DK:(c % 4 + 1) * DK], vs[:, c, :],
                                                   ident[:, :])
                    last.then_inc(s["do_v_mm"], 1)

                def gates_z(i):
                    pe.wait_ge(s["do_xs"], i + 2)
                    if not isinstance(i, int):
                        pe.wait_ge(s["do_h"], i)
                    for o in range(2):
                        for k in range(KC):
                            last = nc.tensor.matmul(pz[0:TT, o, :], xs[:, k, :], wz[:, k, o * BANK:(o + 1) * BANK],
                                                    start=(k == 0), stop=(k == KC - 1))
                    last.then_inc(s["do_z_mm"], 1)

                def updates(i):
                    pe.wait_ge(s["do_vb"], i + 2)
                    pe.wait_ge(s["do_t"], (i + 1) * G * 16 + 1)
                    pe.wait_ge(s["do_u"], i + 1)
                    for c in range(HV):
                        last = nc.tensor.matmul(pu[0:TT, c // 4, (c % 4) * DK:(c % 4 + 1) * DK], tm[:, c, :],
                                                vb[:, c, :], start=True, stop=True)
                    last.then_inc(s["do_u_mm"], 1)

                def outputs(i):
                    pe.wait_ge(s["do_u"], i + 2)
                    pe.wait_ge(s["do_ps"], i + 2)
                    pe.wait_ge(s["do_core"], i + 1)
                    for c in range(HV):
                        last = nc.tensor.matmul(po[0:TT, c // 4, (c % 4) * DK:(c % 4 + 1) * DK], pm[:, c, :],
                                                ub[:, c, :], start=True, stop=True)
                    last.then_inc(s["do_o_mm"], 1)

                def turn_core(i, ahead):
                    pe.wait_ge(s["do_core"], i + 2)
                    pe.wait_ge(s["do_vb"], i + ahead + 2)
                    for c in range(HV):
                        last = nc.tensor.transpose(pv[:, c // 4, (c % 4) * TT:(c % 4 + 1) * TT], core[:, c, :],
                                                   ident[0:TT, 0:TT])
                    last.then_inc(s["do_c_mm"], 1)

                def project(i, ahead):
                    pe.wait_ge(s["do_c"], i + 2)
                    pe.wait_ge(s["do_z"], i + ahead + 2)
                    for c in range(HV):
                        last = nc.tensor.matmul(pz[0:TT, 0, 0:D], cT[:, c, :], wo[:, c, :], start=(c == 0),
                                                stop=(c == HV - 1))
                    last.then_inc(s["do_out_mm"], 1)

                turn_v(0)
                gates_z(0)
                updates(0)
                outputs(0)
                with pe.Fori(1, NT) as i:
                    turn_v(i)
                    gates_z(i)
                    updates(i)
                    turn_core(i - 1, 1)
                    outputs(i)
                    project(i - 1, 1)
                turn_core(NT - 1, 0)
                project(NT - 1, 0)

            @block.scalar
            def _(act):
                def silu_z(i):
                    act.wait_ge(s["do_z_mm"], i + 2)
                    act.wait_ge(s["do_g"], i + 1)
                    nc.scalar.activation(zs[:, :, :], heads(pz), ACT.Silu).then_inc(s["do_z"], 1)

                def copy_u(i):
                    act.wait_ge(s["do_u_mm"], i + 2)
                    act.wait_ge(s["do_o_mm"], i + 1)
                    nc.scalar.activation(ub[:, :, :], heads(pu), ACT.Copy).then_inc(s["do_u"], 1)

                def squares(i):
                    act.wait_ge(s["do_o_mm"], i + 2)
                    act.wait_ge(s["do_ms"], i + 1)
                    nc.scalar.activation(sq[:, :, :], heads(po), ACT.Square).then_inc(s["do_sq"], 1)

                def copy_core(i):
                    act.wait_ge(s["do_c_mm"], i + 2)
                    act.wait_ge(s["do_out_mm"], i + 1)
                    nc.scalar.activation(cT[:, :, :].rearrange("p (o h) x -> p o (h x)", o=2), pv[:, :, 0:W2], ACT.Copy
                                         ).then_inc(s["do_c"], 1)

                silu_z(0)
                copy_u(0)
                squares(0)
                with act.Fori(1, NT) as i:
                    silu_z(i)
                    copy_u(i)
                    copy_core(i - 1)
                    squares(i)
                copy_core(NT - 1)

            @block.vector
            def _(dve):
                dve.wait_ge(s["do_in"], 49)
                nc.vector.memset(half[:, :], -0.5).then_inc(s["do_half"], 1)

                def beta_v(i):
                    dve.wait_ge(s["do_v_mm"], i + 2)
                    dve.wait_ge(s["do_u_mm"], i + 1)
                    nc.vector.tensor_tensor(vb[:, :, :], heads(pv),
                                            flat2(beta[:, span(i, 1), :]).unsqueeze(2).broadcast_to(wide), ALU.mult
                                            ).then_inc(s["do_vb"], 1)

                def gate(i):
                    dve.wait_ge(s["do_z"], i + 2)
                    dve.wait_ge(s["do_c_mm"], i + 1)
                    nc.vector.tensor_tensor(core[:, :, :], zs[:, :, :], gw[:, :].unsqueeze(1).broadcast_to(wide),
                                            ALU.mult).then_inc(s["do_g"], 1)

                def mean_square(i):
                    dve.wait_ge(s["do_sq"], i + 2)
                    dve.wait_ge(s["do_core"], i + 1)
                    link(nc.vector.tensor_reduce(ms[:, :], sq[:, :, :], X, ALU.add))
                    nc.vector.tensor_scalar(ms[:, :], ms[:, :], 1.0 / DK, 1e-6, ALU.mult, ALU.add).then_inc(s["do_ms"], 1)

                def norm(i):
                    dve.wait_ge(s["do_g"], i + 2)
                    link(nc.vector.tensor_tensor(core[:, :, :], core[:, :, :], heads(po), ALU.mult))
                    dve.wait_ge(s["do_r"], i + 2)
                    nc.vector.tensor_tensor(core[:, :, :], core[:, :, :], ms[:, :].unsqueeze(2).broadcast_to(wide),
                                            ALU.mult).then_inc(s["do_core"], 1)

                def add(i):
                    dve.wait_ge(s["do_out_mm"], i + 2)
                    ht = flat2(h[:, span(i, 1), :])
                    nc.vector.tensor_tensor(ht, ht, pz[0:TT, 0, 0:D], ALU.add).then_inc(s["do_h"], 1)

                beta_v(0)
                gate(0)
                with dve.Fori(1, NT) as i:
                    link = chain(dve, s["do_v"], (i - 1) * 2)
                    mean_square(i - 1)
                    beta_v(i)
                    norm(i - 1)
                    gate(i)
                    add(i - 1)
                link = chain(dve, s["do_v"], (NT - 1) * 2)
                mean_square(NT - 1)
                norm(NT - 1)
                add(NT - 1)


def stage_moe3(nc, d, h, xT, ident):
    with ExitStack() as stack:
        sb, ps = bufs(nc, stack)
        E = 8
        w0, w_load = first_weights(sb, "de", d["d_w_e"])
        layer, iota, loads = router(sb, "dr", d["d_router"], d["m_zero"][:, 0:E], d["m_iota"][:, 0:E], E)
        norm_transpose(nc, "dm", h, xT, ident, 1e-6, False, w_dram=d["d_ln2"], w_plus=1.0, loads=loads + w_load)
        logits = sb("d_logits", [TT, NT, E])
        gates = sb("d_gates", [TT, NT, E])
        projected(nc, "dr", xT, layer, logits)
        top2_gates(nc, "dt", logits, gates, iota, ident, E)
        xh, xl = (sb(f"d_x{n}", [P, KC, T + 1], F32R) for n in "hl")
        split_x(nc, "dx", xT, xh, xl)
        experts(nc, "de", d["d_w_e"], w0, gates, xh, xl, h, E, 4, 1, True)


def layout_delta(i, o):
    f = np.float32
    o["d_ln1"] = i["L3_attn_w_ln1"].reshape(KC, P).T
    o["d_ln2"] = i["L3_attn_w_ln2"].reshape(KC, P).T
    o["d_w_ba"] = cols(i["L3_attn_W_ba"], KC)
    o["d_b_ba"] = rep(np.concatenate([np.zeros(8, f), i["L3_attn_dt_bias"]]))
    w = i["L3_attn_W_qkvz"]
    o["d_w_qkv"] = w[:, :2048].reshape(KC, P, 16, P).transpose(2, 1, 0, 3).reshape(16, P, KC * P)
    o["d_w_z"] = cols(w[:, 2048:], KC)
    o["d_cw"] = i["L3_attn_conv_w"].reshape(16, P, 4).transpose(1, 0, 2)
    o["d_a_log"] = rep(i["L3_attn_A_log"])
    eye = np.eye(8, dtype=f)
    o["d_sel"] = np.broadcast_to(eye, (P, 8, 8))
    scale = np.where(np.arange(8) < 4, P ** -0.5, 1.0)
    o["d_spread"] = np.broadcast_to((eye * scale[None]).astype(f)[:, :, None], (8, 8, P))
    a = np.arange(TT)[:, None]
    b = np.arange(TT)[None, :]
    same = a // S == b // S
    o["d_masks"] = np.stack([same & (a <= b), same & (a > b), same & (a < b)], 1).astype(f)
    o["d_w_out"] = cols(i["L3_attn_W_out"], 8)
    o["d_gw"] = rep(i["L3_attn_gate_norm_w"])
    o["d_router"] = cols(i["L3_attn_W_router"], KC)
    o["d_w_e"] = np.concatenate([up_cols(i[f"L3_attn_W_{n}_e"]) for n in ("gate", "up", "down")], 2)


def stage_mla(nc, d, h, xT, ident):
    H, HD, NOPE = 16, 64, 32
    C = H * HD // P
    with ExitStack() as stack:
        sb, ps = bufs(nc, stack)
        q = sb("l_q", [P, C, T])
        kT = sb("l_kT", [P, C, T])
        ckv = sb("l_ckv", [HD, T])
        seqs = [P, T // S, S]

        with ExitStack() as inner:
            sb2, ps2 = bufs(nc, inner)
            wq = sb2("lp_wq", [P, KC, H * HD])
            wkva = sb2("lp_wkva", [P, KC, HD])
            wk = sb2("lp_wk", [HD, H * HD])
            perm = sb2("lp_perm", [P, P])
            tab = sb2("lp_tab", [P, 2, S])
            norm_transpose(nc, "ln", h, xT, ident, 1e-5, False, w_dram=d["l_ln1"], loads=[
                (wq[:, :, :], d["l_wq"]), (wkva[:, :, :], d["l_wkva"]), (wk[:, :], d["l_wk"]),
                (perm[:, :], d["l_perm"]), (tab[:, :, :], d["l_tab"])])
            s = sems(nc, inner, "lp_mm lp_raw lp_sw_mm lp_rot lp_v lp_k_mm lp_k lp_done")
            raw = [sb2(f"lp_raw{n}", [P, T]) for n in range(2)]
            sw = sb2("lp_sw", [P, T])
            pp = ps2("lp_pp", [P, NCH, BANK])
            pw = ps2("lp_pw", [P, NCH, BANK])
            block = inner.enter_context(nc.Block())
            jobs = [(wkva, HD, 0, ckv)] + [(wq, P, c * P, q[:, c, :]) for c in range(C)]

            @block.tensor
            def _(pe):
                def swap(n):
                    m = jobs[n][1]
                    pe.wait_ge(s["lp_raw"], n + 2)
                    if n:
                        pe.wait_ge(s["lp_rot"], n + 1)
                    for t in range(NCH):
                        last = nc.tensor.matmul(pw[0:m, t, 0:CH], perm[0:m, 0:m], raw[n % 2][0:m, t * CH:(t + 1) * CH],
                                                start=True, stop=True)
                    last.then_inc(s["lp_sw_mm"], 1)

                for n, (w, m, at, _) in enumerate(jobs):
                    if n:
                        pe.wait_ge(s["lp_raw"], n + 1)
                    for t in range(NCH):
                        for k in range(KC):
                            last = nc.tensor.matmul(pp[0:m, t, 0:CH], w[:, k, at:at + m],
                                                    xT[:, k, t * CH:(t + 1) * CH], start=(k == 0), stop=(k == KC - 1))
                    last.then_inc(s["lp_mm"], 1)
                    if n:
                        swap(n - 1)
                swap(len(jobs) - 1)
                pe.wait_ge(s["lp_rot"], len(jobs) + 1)
                for c in range(C):
                    if c >= 2:
                        pe.wait_ge(s["lp_k"], c)
                    for t in range(NCH):
                        last = nc.tensor.matmul((pp, pw)[c % 2][:, t, 0:CH], wk[:, c * P:(c + 1) * P],
                                                ckv[:, t * CH:(t + 1) * CH], start=True, stop=True)
                    last.then_inc(s["lp_k_mm"], 1)

            @block.scalar
            def _(act):
                for n, (_, m, _, _) in enumerate(jobs):
                    act.wait_ge(s["lp_mm"], n + 2)
                    if n >= 2:
                        act.wait_ge(s["lp_rot"], n)
                    nc.scalar.activation(raw[n % 2][0:m, :].rearrange("p (t n) -> p t n", t=NCH), pp[0:m, :, 0:CH],
                                         ACT.Copy).then_inc(s["lp_raw"], 1)
                for c in range(C):
                    act.wait_ge(s["lp_k_mm"], c + 2)
                    nc.scalar.activation(kT[:, c, :].rearrange("p (t n) -> p t n", t=NCH),
                                         (pp, pw)[c % 2][:, :, 0:CH], ACT.Copy).then_inc(s["lp_k"], 1)

            @block.vector
            def _(dve):
                link = chain(dve, s["lp_v"])
                for n, (_, m, _, dst) in enumerate(jobs):
                    one = dst if n else dst[:, :]
                    fac = [tab[0:m, k:k + 1, :].broadcast_to([m, T // S, S]) for k in range(2)]
                    dve.wait_ge(s["lp_sw_mm"], n + 2)
                    link(nc.vector.tensor_tensor(one.rearrange("p (b j) -> p b j", j=S),
                                                 raw[n % 2][0:m, :].rearrange("p (b j) -> p b j", j=S), fac[0],
                                                 ALU.mult))
                    for t in range(NCH):
                        last = nc.vector.tensor_tensor(
                            sw[0:m, t * CH:(t + 1) * CH].rearrange("p (b j) -> p b j", j=S),
                            pw[0:m, t, 0:CH].rearrange("p (b j) -> p b j", j=S), fac[1][:, 0:T // S // NCH, :],
                            ALU.mult)
                    link(last)
                    nc.vector.tensor_tensor(one, one, sw[0:m, :], ALU.add).then_inc(s["lp_rot"], 1)
                    dve.wait_ge(s["lp_rot"], n + 2)

        with ExitStack() as inner:
            sb2, ps2 = bufs(nc, inner)
            s = sems(nc, inner, "la_in la_zero la_qs la_kx la_lat la_s_mm la_sc la_max la_exp la_sum la_turned la_pT "
                                "la_v_mm la_vc la_mix la_o la_o_mm la_oT la_out_mm la_h la_v")
            QH = 4
            NQ = H // QH
            VD = NOPE * QH
            wv = sb2("la_wv", [NOPE, H * NOPE])
            wo = sb2("la_wo", [VD, NQ, D])
            neg = sb2("la_neg", [TT, TT])
            qs = sb2("la_qsb", [P, C, TT])
            kx = sb2("la_kxb", [P, C, 2, TT])
            lat = sb2("la_latb", [NOPE, TT])
            sc = sb2("la_scb", [TT, H, TT])
            e = sb2("la_e", [TT, H, TT])
            mx = sb2("la_mx", [TT, H])
            inv = sb2("la_inv", [TT, H])
            pT = sb2("la_pTb", [TT, H, TT])
            v = sb2("la_vb", [TT, H * NOPE])
            o = sb2("la_ob", [TT, H, NOPE])
            oT = sb2("la_oTb", [VD, NQ, TT])
            psS = ps2("la_psS", [P, 4, BANK])
            psT = ps2("la_psT", [P, 2, BANK])
            psV = ps2("la_psV", [P, BANK])
            psM = ps2("la_psM", [P, BANK])
            block = inner.enter_context(nc.Block())

            @block.sync
            def _(sp):
                for dst, src in ((wv[:, :], "l_wv"), (wo[:, :, :], "l_wo"), (neg[:, :], "l_neg")):
                    sp.dma_start(dst, d[src]).then_inc(s["la_in"], 16)

            @block.gpsimd
            def _(pool):
                nc.gpsimd.memset(kx[:, :, :, :], 0.0).then_inc(s["la_zero"], 1)
                with pool.Fori(0, NT) as i:
                    pool.wait_ge(s["la_s_mm"], i + 1)
                    nc.gpsimd.tensor_copy(qs[:, :, :], q[:, :, bass.ds(i * TT, TT)]).then_inc(s["la_qs"], 1)
                    pool.wait_ge(s["la_v_mm"], i + 1)
                    nc.gpsimd.tensor_copy(lat[:, :], ckv[0:NOPE, bass.ds(i * TT, TT)]).then_inc(s["la_lat"], 1)

            @block.scalar
            def _(act):
                act.wait_ge(s["la_zero"], 2)

                def keys(i):
                    act.wait_ge(s["la_s_mm"], i + 1)
                    for n in range(2):
                        at = slice(n * HD, (n + 1) * HD)
                        last = nc.scalar.activation(kx[at, :, n, :], kT[at, :, span(i, TT)], ACT.Copy)
                    last.then_inc(s["la_kx"], 1)

                def exponent(i):
                    act.wait_ge(s["la_max"], i + 2)
                    act.wait_ge(s["la_turned"], NQ * i + 1)
                    act.wait_ge(s["la_sum"], i + 1)
                    nc.scalar.activation(e[:, :, :], sc[:, :, :], ACT.Exp, scale=HD ** -0.5).then_inc(s["la_exp"], 1)

                def copy_turned(i):
                    for n in range(NQ):
                        act.wait_ge(s["la_turned"], NQ * i + n + 2)
                        nc.scalar.activation(pT[:, n * QH:(n + 1) * QH, :].rearrange("p h t -> p (h t)"),
                                             psT[0:TT, n % 2, 0:QH * TT], ACT.Copy).then_inc(s["la_pT"], 1)

                def copy_values(i):
                    act.wait_ge(s["la_v_mm"], i + 2)
                    act.wait_ge(s["la_mix"], i + 1)
                    nc.scalar.activation(v[:, :], psV[0:TT, :], ACT.Copy).then_inc(s["la_vc"], 1)

                def copy_outputs(i):
                    act.wait_ge(s["la_o_mm"], i + 2)
                    act.wait_ge(s["la_out_mm"], i + 1)
                    nc.scalar.activation(oT[:, :, :].rearrange("p g t -> p (g t)"), psT[0:VD, 0, 0:NQ * TT], ACT.Copy
                                         ).then_inc(s["la_oT"], 1)

                keys(0)
                keys(1)
                exponent(0)
                copy_values(0)
                copy_turned(0)
                keys(2)
                exponent(1)
                copy_values(1)
                with act.Fori(2, NT - 1) as i:
                    copy_outputs(i - 2)
                    copy_turned(i - 1)
                    keys(i + 1)
                    exponent(i)
                    copy_values(i)
                copy_outputs(NT - 3)
                copy_turned(NT - 2)
                exponent(NT - 1)
                copy_values(NT - 1)
                copy_outputs(NT - 2)
                copy_turned(NT - 1)
                copy_outputs(NT - 1)

            @block.tensor
            def _(pe):
                pe.wait_ge(s["la_in"], 49)

                def scores(i, part):
                    if part == 0:
                        pe.wait_ge(s["la_qs"], i + 2)
                        pe.wait_ge(s["la_kx"], i + 2)
                        pe.wait_ge(s["la_sc"], i + 1)
                    for c in range(part * C // 2, (part + 1) * C // 2):
                        last = nc.tensor.matmul(psS[0:TT, c // 2, (c % 2) * 2 * TT:(c % 2 + 1) * 2 * TT], qs[:, c, :],
                                                kx[:, c, :, :].rearrange("p a t -> p (a t)"), start=True, stop=True)
                    if part:
                        last.then_inc(s["la_s_mm"], 1)

                def values(i):
                    pe.wait_ge(s["la_lat"], i + 2)
                    pe.wait_ge(s["la_vc"], i + 1)
                    nc.tensor.matmul(psV[0:TT, :], lat[:, :], wv[:, :], start=True, stop=True).then_inc(s["la_v_mm"], 1)

                def turn(i, n):
                    if n == 0:
                        pe.wait_ge(s["la_exp"], i + 2)
                        pe.wait_ge(s["la_oT"], i + 1)
                    elif n == 1:
                        pe.wait_ge(s["la_h"], i + 1)
                    else:
                        pe.wait_ge(s["la_pT"], NQ * i + n)
                    for k in range(QH):
                        last = nc.tensor.transpose(psT[0:TT, n % 2, k * TT:(k + 1) * TT], e[:, n * QH + k, :],
                                                   ident[0:TT, 0:TT])
                    last.then_inc(s["la_turned"], 1)

                def mix_values(i, n):
                    pe.wait_ge(s["la_pT"], NQ * i + n + 2)
                    if n == 0:
                        pe.wait_ge(s["la_vc"], i + 2)
                        pe.wait_ge(s["la_o"], i + 1)
                    for k in range(n * QH, (n + 1) * QH):
                        last = nc.tensor.matmul(psM[0:TT, k * NOPE:(k + 1) * NOPE], pT[:, k, :],
                                                v[:, k * NOPE:(k + 1) * NOPE], start=True, stop=True)
                    if n == NQ - 1:
                        last.then_inc(s["la_mix"], 1)

                def turn_and_mix(i):
                    turn(i, 0)
                    turn(i, 1)
                    for n in range(NQ):
                        mix_values(i, n)
                        if n + 2 < NQ:
                            turn(i, n + 2)

                def turn_outputs(i):
                    pe.wait_ge(s["la_o"], i + 2)
                    for n in range(NQ):
                        last = nc.tensor.transpose(psT[0:VD, 0, n * TT:(n + 1) * TT],
                                                   o[:, n * QH:(n + 1) * QH, :].rearrange("p h x -> p (h x)"),
                                                   ident[0:TT, 0:TT])
                    last.then_inc(s["la_o_mm"], 1)

                def project(i):
                    pe.wait_ge(s["la_oT"], i + 2)
                    for n in range(NQ):
                        last = nc.tensor.matmul(psT[0:TT, 1, 0:D], oT[:, n, :], wo[:, n, :], start=(n == 0),
                                                stop=(n == NQ - 1))
                    last.then_inc(s["la_out_mm"], 1)

                scores(0, 0)
                scores(0, 1)
                values(0)
                scores(1, 0)
                scores(1, 1)
                turn_and_mix(0)
                values(1)
                with pe.Fori(2, NT) as i:
                    scores(i, 0)
                    turn_outputs(i - 2)
                    scores(i, 1)
                    project(i - 2)
                    turn_and_mix(i - 1)
                    values(i)
                turn_outputs(NT - 2)
                project(NT - 2)
                turn_and_mix(NT - 1)
                turn_outputs(NT - 1)
                project(NT - 1)

            @block.vector
            def _(dve):
                dve.wait_ge(s["la_in"], 49)

                def softmax(i):
                    dve.wait_ge(s["la_s_mm"], i + 2)
                    dve.wait_ge(s["la_exp"], i + 1)
                    nc.vector.tensor_tensor(sc[:, :, :].rearrange("p (b h) j -> p b h j", b=4),
                                            psS[0:TT, :, 0:QH * TT].rearrange("p b (h j) -> p b h j", j=TT),
                                            neg[:, :].unsqueeze(1).unsqueeze(1).broadcast_to([TT, 4, QH, TT]), ALU.add
                                            ).then_inc(s["la_sc"], 1)
                    dve.wait_ge(s["la_sc"], i + 2)
                    link(nc.vector.tensor_reduce(mx[:, :], sc[:, :, :], X, ALU.max))
                    nc.vector.tensor_tensor(sc[:, :, :], sc[:, :, :], mx[:, :].unsqueeze(2).broadcast_to([TT, H, TT]),
                                            ALU.subtract).then_inc(s["la_max"], 1)

                def add(i):
                    dve.wait_ge(s["la_out_mm"], i + 2)
                    ht = flat2(h[:, span(i, 1), :])
                    nc.vector.tensor_tensor(ht, ht, psT[0:TT, 1, 0:D], ALU.add).then_inc(s["la_h"], 1)

                def scale(i):
                    dve.wait_ge(s["la_mix"], i + 2)
                    dve.wait_ge(s["la_o_mm"], i + 1)
                    nc.vector.tensor_tensor(o[:, :, :], psM[0:TT, :].rearrange("p (h x) -> p h x", x=NOPE),
                                            inv[:, :].unsqueeze(2).broadcast_to([TT, H, NOPE]), ALU.mult
                                            ).then_inc(s["la_o"], 1)

                def sums(i):
                    dve.wait_ge(s["la_exp"], i + 2)
                    dve.wait_ge(s["la_o"], i + 1)
                    nc.vector.tensor_reduce(inv[:, :], e[:, :, :], X, ALU.add).then_inc(s["la_sum"], 1)
                    dve.wait_ge(s["la_sum"], i + 2)
                    link(nc.vector.reciprocal(inv[:, :], inv[:, :]))

                V = 2
                link = chain(dve, s["la_v"])
                softmax(0)
                sums(0)
                assert link.count() == V
                softmax(1)
                scale(0)
                sums(1)
                with dve.Fori(2, NT) as i:
                    link = chain(dve, s["la_v"], V * i)
                    add(i - 2)
                    softmax(i)
                    scale(i - 1)
                    sums(i)
                add(NT - 2)
                scale(NT - 1)
                add(NT - 1)


def stage_moe4(nc, d, h, xT, ident):
    with ExitStack() as stack:
        sb, ps = bufs(nc, stack)
        E = 8
        w0, w_load = first_weights(sb, "le", d["l_w_e"])
        ws0, ws_load = first_weights(sb, "ls", d["l_w_s"])
        layer, iota, loads = router(sb, "lr", d["l_router"], d["l_bias"], d["m_iota"][:, 0:E], E)
        norm_transpose(nc, "lm", h, xT, ident, 1e-5, False, w_dram=d["l_ln2"], loads=loads + w_load + ws_load)
        logits = sb("l_logits", [TT, NT, E])
        gates = sb("l_gates", [TT, NT, E])
        one = sb("l_one", [TT, NT, 1])
        projected(nc, "lr", xT, layer, logits)
        top2_gates(nc, "lt", logits, gates, iota, ident, E)
        xh, xl = (sb(f"l_x{n}", [P, KC, T + 1], F32R) for n in "hl")
        split_x(nc, "lx", xT, xh, xl)
        experts(nc, "le", d["l_w_e"], w0, gates, xh, xl, h, E, 4, 1, True)
        with ExitStack() as inner:
            s = sems(nc, inner, "l_one_set")
            block = inner.enter_context(nc.Block())

            @block.vector
            def _(dve):
                nc.vector.memset(one[:, :, :], 1.0).then_inc(s["l_one_set"], 1)
        experts(nc, "ls", d["l_w_s"], ws0, one, xh, xl, h, 1, 1, 1, True)


def layout_mla(i, o):
    f = np.float32
    o["l_ln1"] = i["L3_ffn_w_ln1"].reshape(KC, P).T
    o["l_ln2"] = i["L3_ffn_w_ln2"].reshape(KC, P).T
    o["l_wq"] = cols(i["L3_ffn_Wq"], KC)
    o["l_wkva"] = cols(i["L3_ffn_Wkva"], KC)
    wk = np.zeros((64, 16, 64), f)
    wk[:32, :, :32] = i["L3_ffn_Wkvb"].reshape(32, 16, 32)
    wk[32:, :, 32:] = np.eye(32, dtype=f)[:, None, :]
    o["l_wk"] = wk.reshape(64, 1024)
    o["l_wv"] = i["L3_ffn_Wkvb"]
    o["l_perm"] = np.eye(P, dtype=f)[np.arange(P) ^ 1]
    freq = 1.0 / 100000.0 ** (np.arange(0, 32, 2, dtype=np.float32) / 32)
    p = np.arange(P)
    rope = (p % 64 >= 32)[:, None]
    ang = np.arange(S)[None, :] * freq[(p % 32) // 2][:, None]
    sign = np.where(p % 2 == 0, -1, 1)[:, None]
    o["l_tab"] = np.stack([np.where(rope, np.cos(ang), 1), np.where(rope, sign * np.sin(ang), 0)], 1).astype(f)
    o["l_wo"] = i["L3_ffn_Wo"].reshape(16, 64, D)[:, :32].reshape(4, P, D).transpose(1, 0, 2)
    pos, seq = np.arange(TT) % S, np.arange(TT) // S
    counts = (seq[:, None] == seq[None, :]) & (pos[None, :] <= pos[:, None])
    o["l_neg"] = np.where(counts, 0, -1e30).astype(f)
    o["l_router"] = cols(i["L3_ffn_Wgate"], KC)
    o["l_bias"] = rep(i["L3_ffn_expert_bias"])
    o["l_w_e"] = np.concatenate([up_cols(i[f"L3_ffn_{n}"]) for n in ("Wg", "Wu", "Wd")], 2)
    o["l_w_s"] = np.concatenate([up_cols(i[f"L3_ffn_s{n}"]) for n in ("Wg", "Wu", "Wd")], 2)


def on_normed(name, *parts):
    def stage(nc, d, h, xT, ident):
        with ExitStack() as stack:
            sb, _ = bufs(nc, stack)
            r = sb(f"{name}_r", [TT, NT, D])
            norm_transpose(nc, f"{name}_ln", h, xT, ident, 1e-5, True, x_tok=r, turn=False)
            for part in parts:
                part(nc, d, r, xT, ident)
            s = sems(nc, stack, f"{name}_added")
            block = stack.enter_context(nc.Block())

            @block.vector
            def _(dve):
                nc.vector.tensor_tensor(h[:, :, :], h[:, :, :], r[:, :, :], ALU.add).then_inc(
                    s[f"{name}_added"], 1)
    return stage


STAGES = [lambda nc, d, h, xT, ident: stage_tok(nc, d, h, ident), stage_attn0, stage_ffn0, stage_gate1, stage_ffn1,
          stage_scan, stage_moe2, on_normed("l6", stage_delta, stage_moe3),
          on_normed("l7", stage_mla, stage_moe4)]
LAYOUTS = [layout_attn0, layout_ffn0, layout_l1, layout_scan, layout_moe2, layout_delta, layout_mla]


def cols(a, k):
    return a.reshape(k, -1, a.shape[1]).transpose(1, 0, 2)


def rep(a, n=TT):
    return np.broadcast_to(a.reshape(1, -1), (n, a.size))


def tiles(a):
    return a.reshape(NT, TT, -1).transpose(1, 0, 2)


def layout(i):
    f = np.float32
    o = {}
    pat = np.zeros((B + 1, S, 768), f)
    pat[:B, 1:] = i["x"].reshape(B, 3, 6, 16, 6, 16).transpose(0, 2, 4, 3, 5, 1).reshape(B, 36, 768)
    o["patches"] = tiles(pat.reshape(T, 768))
    add = np.zeros((B + 1, S, D), f)
    add[:B, 0] = i["L0_tok_class_token"].reshape(D)
    o["tok_addend"] = tiles(add.reshape(T, D))
    o["tok_pos"] = rep(i["L0_tok_pos_embedding"])
    o["tok_w"] = cols(i["L0_tok_weight"].T, 6)
    for g in LAYOUTS:
        g(i, o)
    return {k: np.ascontiguousarray(v) for k, v in o.items()}


def build(nc, d, out, stages=None, h0=None):
    with ExitStack() as stack:
        sb, _ = bufs(nc, stack)
        h = sb("h", [TT, NT, D])
        xT = sb("xT", [P, KC, T + 1])
        ident = sb("ident", [P, P])
        with ExitStack() as s0:
            s = sems(nc, s0, "start_zero start_ident start_h0")
            block = s0.enter_context(nc.Block())

            @block.gpsimd
            def _(pool):
                nc.gpsimd.memset(xT[:, :, T:], 0.0)
                nc.gpsimd.memset(ident[:, :], 0.0).then_inc(s["start_zero"], 1)
                pool.wait_ge(s["start_zero"], 2)
                nc.gpsimd.affine_select(out=ident[:, :], in_=ident[:, :], compare_op=ALU.not_equal, fill=1.0,
                                        base=0, pattern=[[-1, P]], channel_multiplier=1).then_inc(s["start_ident"], 1)
                pool.wait_ge(s["start_ident"], 2)

            if h0 is not None:
                @block.sync
                def _(sp):
                    sp.dma_start(h[:, :, :], h0).then_inc(s["start_h0"], 16)
                    sp.wait_ge(s["start_h0"], 17)
        for n, stage in enumerate(STAGES):
            if stages is None or n in stages:
                stage(nc, d, h, xT, ident)
        with ExitStack() as s1:
            s = sems(nc, s1, "out_written")
            block = s1.enter_context(nc.Block())
            flat = out.rearrange("b s d -> (b s) d")

            @block.sync
            def _(sp):
                n = NT - 1
                sp.dma_start(flat[0:n * TT, :].rearrange("(t p) d -> p t d", p=TT), h[:, 0:n, :]
                             ).then_inc(s["out_written"], 16)
                rest = B * S - n * TT
                sp.dma_start(flat[n * TT:B * S, :], h[0:rest, n, :]).then_inc(s["out_written"], 16)
                sp.wait_ge(s["out_written"], 33)


def kernel(**inputs):
    import concourse.bacc as _bacc
    from concourse.bass_utils import run_bass_kernel_spmd as _run

    nc = _bacc.Bacc("TRN2", target_bir_lowering=False, num_devices=1)
    arrays, d = {}, {}
    for name, a in layout({k: np.asarray(v) for k, v in inputs.items()}).items():
        arrays[f"in_{name}"] = a
        d[name] = nc.dram_tensor(f"in_{name}", a.shape, mybir.dt.from_np(a.dtype), kind="ExternalInput").ap()
    out = nc.dram_tensor("out_0", (B, S, D), F32, kind="ExternalOutput").ap()
    build(nc, d, out)
    r = _run(nc, [arrays], core_ids=[0])
    return r.results[0]["out_0"]
```
